# Optimizing a Trainium2 kernel written in Bass

```python
import numpy as np
import jax
import jax.numpy as jnp

def _softmax(x, axis=-1):
    return jax.nn.softmax(x, axis=axis)

def _gelu(x):
    return jax.nn.gelu(x, approximate=True)

def _silu(x):
    return jax.nn.silu(x)

def _sigmoid(x):
    return jax.nn.sigmoid(x)

def _layernorm(x, axis=-1, eps=1e-05):
    m = jnp.mean(x, axis=axis, keepdims=True)
    v = jnp.var(x, axis=axis, keepdims=True)
    return (x - m) / jnp.sqrt(v + eps)

def _scatter_add(tgt, idx, src, axis=0):
    return tgt.at[idx].add(src)

def _segment_sum(src, seg, n):
    return jax.ops.segment_sum(src, seg, n)
kernel_name = 'mk_audio_tower_d2_tok_audfeat512_r4_90b9fe'

def setup_inputs(seed: int=0):
    np.random.seed(seed)
    _w = jnp.asarray

    def _rec_inputs():
        import jax
        import jax.numpy as jnp
        _rk = jax.random.key(seed)
        x = 7.22013e-05 + 1.00017 * jax.random.normal(jax.random.fold_in(_rk, 1), (32, 1024, 32), jnp.float32)
        return x
    x = _rec_inputs()

    def _L0_tok_setup():
        import jax, jax.numpy as jnp
        import numpy as np
        PATCH_LEN = 16
        PATCH_STRIDE = 8
        D_MODEL = 128
        N_FEATURES = 32
        key = jax.random.key(seed)
        k_x, k_w, k_b = jax.random.split(key, 3)
        x = jax.random.normal(k_x, (64, 1024, N_FEATURES), dtype=jnp.float32)
        in_dim = PATCH_LEN * N_FEATURES
        bound = 1.0 / np.sqrt(in_dim)
        W = jax.random.uniform(k_w, (D_MODEL, in_dim), dtype=jnp.float32, minval=-bound, maxval=bound)
        b = jax.random.uniform(k_b, (D_MODEL,), dtype=jnp.float32, minval=-bound, maxval=bound)
        return {'x': x, 'W': W, 'b': b}
    _L0_tok_all = _L0_tok_setup()
    _L0_tok_in = {k: v for k, v in _L0_tok_all.items() if k in ('W', 'b')}
    del _L0_tok_all

    def _L0_attn_setup():
        import jax, jax.numpy as jnp
        import numpy as np
        B, N, D = (8, 128, 128)
        H = 8
        DK = D // H
        key = jax.random.key(seed)
        k1, k2, k3 = jax.random.split(key, 3)
        inputs = jax.random.normal(k1, (B, N, D), dtype=jnp.float32)
        W_qkv = jax.random.normal(k2, (D, 3 * DK), dtype=jnp.float32) * 0.02
        W_o = jax.random.normal(k3, (DK, D), dtype=jnp.float32) * 0.02
        return {'inputs': inputs, 'W_qkv': W_qkv, 'W_o': W_o}
    _L0_attn_all = _L0_attn_setup()
    _L0_attn_in = {k: v for k, v in _L0_attn_all.items() if k in ('W_qkv', 'W_o')}
    del _L0_attn_all

    def _L0_ffn_setup():
        import jax, jax.numpy as jnp
        import numpy as np
        B, T, C = (2, 512, 128)
        E, G, TG, K = (64, 8, 4, 6)
        H, HS = (160, 128)
        key = jax.random.key(seed)
        ks = jax.random.split(key, 9)
        s = 0.02
        return {'x': jax.random.normal(ks[0], (B, T, C), dtype=jnp.float32), 'router_w': jax.random.normal(ks[1], (E, C), dtype=jnp.float32) * s, 'bias_corr': jnp.zeros((E,), dtype=jnp.float32), 'Wg': jax.random.normal(ks[2], (E, C, H), dtype=jnp.float32) * s, 'Wu': jax.random.normal(ks[3], (E, C, H), dtype=jnp.float32) * s, 'Wd': jax.random.normal(ks[4], (E, H, C), dtype=jnp.float32) * s, 'sWg': jax.random.normal(ks[5], (C, HS), dtype=jnp.float32) * s, 'sWu': jax.random.normal(ks[6], (C, HS), dtype=jnp.float32) * s, 'sWd': jax.random.normal(ks[7], (HS, C), dtype=jnp.float32) * s}
    _L0_ffn_all = _L0_ffn_setup()
    _L0_ffn_in = {k: v for k, v in _L0_ffn_all.items() if k in ('router_w', 'bias_corr', 'Wg', 'Wu', 'Wd', 'sWg', 'sWu', 'sWd')}
    del _L0_ffn_all

    def _L1_attn_setup():
        import jax, jax.numpy as jnp
        import numpy as np
        B, S, D, H, N, SD, NH = (8, 256, 128, 64, 64, 128, 4)
        DH = H // NH

        def _ln(h, g, b):
            m = jnp.mean(h, -1, keepdims=True)
            v = jnp.var(h, -1, keepdims=True)
            return (h - m) * jax.lax.rsqrt(v + 1e-05) * g + b
        key = jax.random.key(seed)
        ks = iter(jax.random.split(key, 64))

        def w(*shape):
            return jax.random.normal(next(ks), shape, jnp.float32) * 0.02
        z = lambda *s: jnp.zeros(s, jnp.float32)
        o = lambda *s: jnp.ones(s, jnp.float32)
        return {'x': jax.random.normal(next(ks), (B, S, D), jnp.float32), 'sb_init': w(N, SD), 'sb_wq': w(D, SD), 'sb_bq': z(SD), 'sb_ww': w(D, SD), 'sb_bw': z(SD), 'sb_wo': w(SD, D), 'sb_bo': z(D), 'p_win': w(D, H), 'p_bin': z(H), 'b_wq': w(H, SD), 'b_bq': z(SD), 'b_keys': w(N, SD), 'bp_w': w(SD, H), 'bp_b': z(H), 'dn_wqkv': w(2, H, 3 * H), 'dn_bqkv': z(2, 3 * H), 'dn_wbeta': w(2, H, NH), 'dn_bbeta': z(2, NH), 'dn_wo': w(2, H, H), 'dn_bo': z(2, H), 'dn_lng': o(2, H), 'dn_lnb': z(2, H), 'sup_w': w(H, SD), 'sup_b': z(SD), 'op_w': w(H, D), 'op_b': z(D), 'oln_g': o(D), 'oln_b': z(D), 'ow': w(D, D), 'ob': z(D)}
    _L1_attn_all = _L1_attn_setup()
    _L1_attn_in = {k: v for k, v in _L1_attn_all.items() if k in ('sb_init', 'sb_wq', 'sb_bq', 'sb_ww', 'sb_bw', 'sb_wo', 'sb_bo', 'p_win', 'p_bin', 'b_wq', 'b_bq', 'b_keys', 'bp_w', 'bp_b', 'dn_wqkv', 'dn_bqkv', 'dn_wbeta', 'dn_bbeta', 'dn_wo', 'dn_bo', 'dn_lng', 'dn_lnb', 'sup_w', 'sup_b', 'op_w', 'op_b', 'oln_g', 'oln_b', 'ow', 'ob')}
    del _L1_attn_all

    def _L1_ffn_setup():
        import jax, jax.numpy as jnp
        import numpy as np
        EPS = 1e-05
        NUM_HEADS = 8
        TOP_K = 2
        CAP_FACTOR = 2

        def layernorm(x, g, b):
            m = jnp.mean(x, axis=-1, keepdims=True)
            v = jnp.var(x, axis=-1, keepdims=True)
            return (x - m) * jax.lax.rsqrt(v + EPS) * g + b
        key = jax.random.key(seed)
        ks = jax.random.split(key, 16)
        B, S, H, E, F = (2, 512, 128, 64, 512)
        s = 0.02
        return {'x': jax.random.normal(ks[0], (B, S, H), jnp.float32), 'ln1_g': jnp.ones((H,), jnp.float32), 'ln1_b': jnp.zeros((H,), jnp.float32), 'wq': jax.random.normal(ks[1], (H, H), jnp.float32) * s, 'wk': jax.random.normal(ks[2], (H, H), jnp.float32) * s, 'wv': jax.random.normal(ks[3], (H, H), jnp.float32) * s, 'wo': jax.random.normal(ks[4], (H, H), jnp.float32) * s, 'ln2_g': jnp.ones((H,), jnp.float32), 'ln2_b': jnp.zeros((H,), jnp.float32), 'wr': jax.random.normal(ks[5], (H, E), jnp.float32) * s, 'w1': jax.random.normal(ks[6], (E, H, F), jnp.float32) * s, 'b1': jnp.zeros((E, F), jnp.float32), 'w2': jax.random.normal(ks[7], (E, F, H), jnp.float32) * s, 'b2': jnp.zeros((E, H), jnp.float32)}
    _L1_ffn_all = _L1_ffn_setup()
    _L1_ffn_in = {k: v for k, v in _L1_ffn_all.items() if k in ('ln1_g', 'ln1_b', 'wq', 'wk', 'wv', 'wo', 'ln2_g', 'ln2_b', 'wr', 'w1', 'b1', 'w2', 'b2')}
    del _L1_ffn_all
    return {'x': x, 'L0_tok_W': _L0_tok_in['W'], 'L0_tok_b': _L0_tok_in['b'], 'L0_attn_W_qkv': _L0_attn_in['W_qkv'], 'L0_attn_W_o': _L0_attn_in['W_o'], 'L0_ffn_router_w': _L0_ffn_in['router_w'], 'L0_ffn_bias_corr': _L0_ffn_in['bias_corr'], 'L0_ffn_Wg': _L0_ffn_in['Wg'], 'L0_ffn_Wu': _L0_ffn_in['Wu'], 'L0_ffn_Wd': _L0_ffn_in['Wd'], 'L0_ffn_sWg': _L0_ffn_in['sWg'], 'L0_ffn_sWu': _L0_ffn_in['sWu'], 'L0_ffn_sWd': _L0_ffn_in['sWd'], 'L1_attn_sb_init': _L1_attn_in['sb_init'], 'L1_attn_sb_wq': _L1_attn_in['sb_wq'], 'L1_attn_sb_bq': _L1_attn_in['sb_bq'], 'L1_attn_sb_ww': _L1_attn_in['sb_ww'], 'L1_attn_sb_bw': _L1_attn_in['sb_bw'], 'L1_attn_sb_wo': _L1_attn_in['sb_wo'], 'L1_attn_sb_bo': _L1_attn_in['sb_bo'], 'L1_attn_p_win': _L1_attn_in['p_win'], 'L1_attn_p_bin': _L1_attn_in['p_bin'], 'L1_attn_b_wq': _L1_attn_in['b_wq'], 'L1_attn_b_bq': _L1_attn_in['b_bq'], 'L1_attn_b_keys': _L1_attn_in['b_keys'], 'L1_attn_bp_w': _L1_attn_in['bp_w'], 'L1_attn_bp_b': _L1_attn_in['bp_b'], 'L1_attn_dn_wqkv': _L1_attn_in['dn_wqkv'], 'L1_attn_dn_bqkv': _L1_attn_in['dn_bqkv'], 'L1_attn_dn_wbeta': _L1_attn_in['dn_wbeta'], 'L1_attn_dn_bbeta': _L1_attn_in['dn_bbeta'], 'L1_attn_dn_wo': _L1_attn_in['dn_wo'], 'L1_attn_dn_bo': _L1_attn_in['dn_bo'], 'L1_attn_dn_lng': _L1_attn_in['dn_lng'], 'L1_attn_dn_lnb': _L1_attn_in['dn_lnb'], 'L1_attn_sup_w': _L1_attn_in['sup_w'], 'L1_attn_sup_b': _L1_attn_in['sup_b'], 'L1_attn_op_w': _L1_attn_in['op_w'], 'L1_attn_op_b': _L1_attn_in['op_b'], 'L1_attn_oln_g': _L1_attn_in['oln_g'], 'L1_attn_oln_b': _L1_attn_in['oln_b'], 'L1_attn_ow': _L1_attn_in['ow'], 'L1_attn_ob': _L1_attn_in['ob'], 'L1_ffn_ln1_g': _L1_ffn_in['ln1_g'], 'L1_ffn_ln1_b': _L1_ffn_in['ln1_b'], 'L1_ffn_wq': _L1_ffn_in['wq'], 'L1_ffn_wk': _L1_ffn_in['wk'], 'L1_ffn_wv': _L1_ffn_in['wv'], 'L1_ffn_wo': _L1_ffn_in['wo'], 'L1_ffn_ln2_g': _L1_ffn_in['ln2_g'], 'L1_ffn_ln2_b': _L1_ffn_in['ln2_b'], 'L1_ffn_wr': _L1_ffn_in['wr'], 'L1_ffn_w1': _L1_ffn_in['w1'], 'L1_ffn_b1': _L1_ffn_in['b1'], 'L1_ffn_w2': _L1_ffn_in['w2'], 'L1_ffn_b2': _L1_ffn_in['b2']}

def reference(x, L0_tok_W, L0_tok_b, L0_attn_W_qkv, L0_attn_W_o, L0_ffn_router_w, L0_ffn_bias_corr, L0_ffn_Wg, L0_ffn_Wu, L0_ffn_Wd, L0_ffn_sWg, L0_ffn_sWu, L0_ffn_sWd, L1_attn_sb_init, L1_attn_sb_wq, L1_attn_sb_bq, L1_attn_sb_ww, L1_attn_sb_bw, L1_attn_sb_wo, L1_attn_sb_bo, L1_attn_p_win, L1_attn_p_bin, L1_attn_b_wq, L1_attn_b_bq, L1_attn_b_keys, L1_attn_bp_w, L1_attn_bp_b, L1_attn_dn_wqkv, L1_attn_dn_bqkv, L1_attn_dn_wbeta, L1_attn_dn_bbeta, L1_attn_dn_wo, L1_attn_dn_bo, L1_attn_dn_lng, L1_attn_dn_lnb, L1_attn_sup_w, L1_attn_sup_b, L1_attn_op_w, L1_attn_op_b, L1_attn_oln_g, L1_attn_oln_b, L1_attn_ow, L1_attn_ob, L1_ffn_ln1_g, L1_ffn_ln1_b, L1_ffn_wq, L1_ffn_wk, L1_ffn_wv, L1_ffn_wo, L1_ffn_ln2_g, L1_ffn_ln2_b, L1_ffn_wr, L1_ffn_w1, L1_ffn_b1, L1_ffn_w2, L1_ffn_b2):
    import jax
    import jax.numpy as jnp

    def _L0_tok_ref(x, W, b):
        import jax, jax.numpy as jnp
        import numpy as np
        PATCH_LEN = 16
        PATCH_STRIDE = 8
        D_MODEL = 128
        N_FEATURES = 32
        B, T, C = x.shape
        n_patches = (T - PATCH_LEN) // PATCH_STRIDE + 1
        idx = jnp.arange(n_patches)[:, None] * PATCH_STRIDE + jnp.arange(PATCH_LEN)[None, :]
        patches = x[:, idx, :]
        patches = patches.reshape(B, n_patches, PATCH_LEN * C)
        return jnp.einsum('bpf,df->bpd', patches, W) + b

    def _L0_attn_ref(inputs, W_qkv, W_o):
        import jax, jax.numpy as jnp
        import numpy as np
        B, N, D = (8, 128, 128)
        H = 8
        DK = D // H
        d_k = W_qkv.shape[1] // 3
        QKV = inputs @ W_qkv
        Q = QKV[:, :, 0 * d_k:1 * d_k]
        K = QKV[:, :, 1 * d_k:2 * d_k]
        V = QKV[:, :, 2 * d_k:3 * d_k]
        scale = 1.0 / jnp.sqrt(jnp.asarray(d_k, dtype=QKV.dtype))
        S = jnp.einsum('bnc,bmc->bcnm', Q, K) * scale
        A = jax.nn.softmax(S, axis=-1)
        SA = jnp.einsum('bcnm,bmc->bnc', A, V)
        return SA @ W_o

    def _L0_ffn_ref(x, router_w, bias_corr, Wg, Wu, Wd, sWg, sWu, sWd):
        import jax, jax.numpy as jnp
        import numpy as np
        B, T, C = (2, 512, 128)
        E, G, TG, K = (64, 8, 4, 6)
        H, HS = (160, 128)
        Bx, Tx, Cx = x.shape
        S = Bx * Tx
        xf = x.reshape(S, Cx)
        shared = jax.nn.silu(xf @ sWg) * (xf @ sWu) @ sWd
        logits = xf.astype(jnp.float32) @ router_w.T
        scores = jax.nn.sigmoid(logits).astype(x.dtype)
        biased = scores + bias_corr
        epg = E // G
        group_scores = biased.reshape(S, G, epg).max(axis=-1)
        _, sel_g = jax.lax.top_k(group_scores, TG)
        rows = jnp.arange(S)[:, None]
        group_mask = jnp.zeros((S, G), dtype=x.dtype).at[rows, sel_g].set(1.0)
        expert_mask = jnp.repeat(group_mask, epg, axis=1)
        masked = jnp.where(expert_mask > 0, biased, -jnp.inf)
        _, topk_idx = jax.lax.top_k(masked, K)
        w = jnp.take_along_axis(scores, topk_idx, axis=1)
        w = w / (w.sum(axis=-1, keepdims=True) + 1e-20)
        combine = jnp.zeros((S, E), dtype=x.dtype).at[rows, topk_idx].add(w)
        g = jnp.einsum('sc,ech->seh', xf, Wg)
        u = jnp.einsum('sc,ech->seh', xf, Wu)
        h = jax.nn.silu(g) * u
        hw = combine[:, :, None] * h
        routed = jnp.einsum('seh,ehc->sc', hw, Wd)
        return (shared + routed).reshape(Bx, Tx, Cx)

    def _L1_attn_ref(x, sb_init, sb_wq, sb_bq, sb_ww, sb_bw, sb_wo, sb_bo, p_win, p_bin, b_wq, b_bq, b_keys, bp_w, bp_b, dn_wqkv, dn_bqkv, dn_wbeta, dn_bbeta, dn_wo, dn_bo, dn_lng, dn_lnb, sup_w, sup_b, op_w, op_b, oln_g, oln_b, ow, ob):
        import jax, jax.numpy as jnp
        import numpy as np
        B, S, D, H, N, SD, NH = (8, 256, 128, 64, 64, 128, 4)
        DH = H // NH

        def _ln(h, g, b):
            m = jnp.mean(h, -1, keepdims=True)
            v = jnp.var(h, -1, keepdims=True)
            return (h - m) * jax.lax.rsqrt(v + 1e-05) * g + b
        Bv = x.shape[0]
        scale = SD ** 0.5
        slots0 = jnp.broadcast_to(sb_init, (Bv, N, SD))
        St0 = jnp.zeros((2, Bv, NH, DH, DH), x.dtype)

        def step(carry, tok):
            slots, St = carry
            q = tok @ sb_wq + sb_bq
            a = jax.nn.softmax(jnp.einsum('bd,bnd->bn', q, slots) / scale, -1)
            read = jnp.einsum('bn,bnd->bd', a, slots)
            slot_out = read @ sb_wo + sb_bo
            wr = tok @ sb_ww + sb_bw
            g = jax.nn.sigmoid(a)[..., None]
            slots = (1 - g) * slots + g * (a[..., None] * wr[:, None, :])
            xh = tok @ p_win + p_bin
            bq = xh @ b_wq + b_bq
            ba = jax.nn.softmax(bq @ b_keys.T / scale, -1)
            bindings = jnp.einsum('bn,bnd->bd', ba, slots)
            xh = xh + bindings @ bp_w + bp_b
            for l in range(2):
                qkv = xh @ dn_wqkv[l] + dn_bqkv[l]
                qh, kh, vh = [t.reshape(-1, NH, DH) for t in jnp.split(qkv, 3, -1)]
                kh = kh / (jnp.linalg.norm(kh, axis=-1, keepdims=True) + 1e-06)
                beta = jax.nn.sigmoid(xh @ dn_wbeta[l] + dn_bbeta[l])
                Sl = St[l]
                Sk = jnp.einsum('bhij,bhj->bhi', Sl, kh)
                Sl = Sl + (beta[..., None] * (vh - Sk))[..., None] * kh[:, :, None, :]
                o = jnp.einsum('bhij,bhj->bhi', Sl, qh).reshape(-1, H)
                xh = _ln(xh + o @ dn_wo[l] + dn_bo[l], dn_lng[l], dn_lnb[l])
                St = St.at[l].set(Sl)
            supd = ba[..., None] * xh[:, None, :] @ sup_w + sup_b
            g2 = jax.nn.sigmoid(ba)[..., None]
            slots = (1 - g2) * slots + g2 * supd
            out = slot_out + xh @ op_w + op_b
            return ((slots, St), out)
        (_, _), ys = jax.lax.scan(step, (slots0, St0), jnp.swapaxes(x, 0, 1))
        y = jnp.swapaxes(ys, 0, 1)
        return _ln(y, oln_g, oln_b) @ ow + ob

    def _L1_ffn_ref(x, ln1_g, ln1_b, wq, wk, wv, wo, ln2_g, ln2_b, wr, w1, b1, w2, b2):
        import jax, jax.numpy as jnp
        import numpy as np
        EPS = 1e-05
        NUM_HEADS = 8
        TOP_K = 2
        CAP_FACTOR = 2

        def layernorm(x, g, b):
            m = jnp.mean(x, axis=-1, keepdims=True)
            v = jnp.var(x, axis=-1, keepdims=True)
            return (x - m) * jax.lax.rsqrt(v + EPS) * g + b
        B, S, H = x.shape
        NH = NUM_HEADS
        dh = H // NH
        x1 = layernorm(x, ln1_g, ln1_b)
        q = (x1 @ wq).reshape(B, S, NH, dh)
        k = (x1 @ wk).reshape(B, S, NH, dh)
        v = (x1 @ wv).reshape(B, S, NH, dh)
        scores = jnp.einsum('bqhd,bkhd->bhqk', q, k) * dh ** (-0.5)
        p = jax.nn.softmax(scores, axis=-1)
        attn_out = jnp.einsum('bhqk,bkhd->bqhd', p, v).reshape(B, S, H) @ wo
        x = x + attn_out
        x2 = layernorm(x, ln2_g, ln2_b).reshape(B * S, H)
        T = B * S
        E = wr.shape[1]
        C = CAP_FACTOR * (T * TOP_K // E)
        probs = jax.nn.softmax(x2 @ wr, axis=-1)
        gate_v, gate_i = jax.lax.top_k(probs, TOP_K)
        gate_v = gate_v / jnp.sum(gate_v, axis=-1, keepdims=True)
        ef = gate_i.reshape(-1)
        gf = gate_v.reshape(-1)
        oh = jax.nn.one_hot(ef, E, dtype=x2.dtype)
        pos = jnp.sum((jnp.cumsum(oh, axis=0) - oh) * oh, axis=1).astype(jnp.int32)
        keep = (pos < C).astype(x2.dtype)
        posc = jnp.minimum(pos, C - 1)
        tok = jnp.repeat(x2, TOP_K, axis=0) * keep[:, None]
        buf = jnp.zeros((E, C, H), x2.dtype).at[ef, posc].add(tok)
        h = jax.nn.gelu(jnp.einsum('ech,ehf->ecf', buf, w1) + b1[:, None, :])
        y = jnp.einsum('ecf,efh->ech', h, w2) + b2[:, None, :]
        ys = y[ef, posc] * (gf * keep)[:, None]
        moe_out = ys.reshape(T, TOP_K, H).sum(axis=1).reshape(B, S, H)
        return x + moe_out
    h = _L0_tok_ref(x, L0_tok_W, L0_tok_b)
    h = h + _L0_attn_ref(_layernorm(h, axis=-1), L0_attn_W_qkv, L0_attn_W_o)
    h = h + _L0_ffn_ref(_layernorm(h, axis=-1), L0_ffn_router_w, L0_ffn_bias_corr, L0_ffn_Wg, L0_ffn_Wu, L0_ffn_Wd, L0_ffn_sWg, L0_ffn_sWu, L0_ffn_sWd)
    h = h + _L1_attn_ref(_layernorm(h, axis=-1), L1_attn_sb_init, L1_attn_sb_wq, L1_attn_sb_bq, L1_attn_sb_ww, L1_attn_sb_bw, L1_attn_sb_wo, L1_attn_sb_bo, L1_attn_p_win, L1_attn_p_bin, L1_attn_b_wq, L1_attn_b_bq, L1_attn_b_keys, L1_attn_bp_w, L1_attn_bp_b, L1_attn_dn_wqkv, L1_attn_dn_bqkv, L1_attn_dn_wbeta, L1_attn_dn_bbeta, L1_attn_dn_wo, L1_attn_dn_bo, L1_attn_dn_lng, L1_attn_dn_lnb, L1_attn_sup_w, L1_attn_sup_b, L1_attn_op_w, L1_attn_op_b, L1_attn_oln_g, L1_attn_oln_b, L1_attn_ow, L1_attn_ob)
    h = h + _L1_ffn_ref(_layernorm(h, axis=-1), L1_ffn_ln1_g, L1_ffn_ln1_b, L1_ffn_wq, L1_ffn_wk, L1_ffn_wv, L1_ffn_wo, L1_ffn_ln2_g, L1_ffn_ln2_b, L1_ffn_wr, L1_ffn_w1, L1_ffn_b1, L1_ffn_w2, L1_ffn_b2)
    return h

_drawn_inputs = setup_inputs


def setup_inputs(seed=0):
    import zlib

    import numpy as np

    out = dict(_drawn_inputs(seed))
    spreads = {'L0_ffn_bias_corr': (0.0, 0.8),
     'L1_attn_sb_bq': (0.0, 2.0),
     'L1_attn_sb_bw': (0.0, 2.0),
     'L1_attn_sb_bo': (0.0, 0.1),
     'L1_attn_p_bin': (0.0, 0.1),
     'L1_attn_b_bq': (0.0, 2.0),
     'L1_attn_bp_b': (0.0, 0.1),
     'L1_attn_dn_bqkv': (0.0, 0.8),
     'L1_attn_dn_bbeta': (0.0, 0.8),
     'L1_attn_dn_bo': (0.0, 0.291),
     'L1_attn_dn_lng': (1.0, 0.2),
     'L1_attn_dn_lnb': (0.0, 0.417),
     'L1_attn_sup_b': (0.0, 0.356),
     'L1_attn_op_b': (0.0, 0.1),
     'L1_attn_oln_g': (1.0, 0.2),
     'L1_attn_oln_b': (0.0, 0.468),
     'L1_attn_ob': (0.0, 0.1),
     'L1_ffn_ln1_g': (1.0, 0.6),
     'L1_ffn_ln1_b': (0.0, 0.8),
     'L1_ffn_ln2_g': (1.0, 0.2),
     'L1_ffn_ln2_b': (0.0, 0.334),
     'L1_ffn_b1': (0.0, 0.8),
     'L1_ffn_b2': (0.0, 0.428)}
    factors = {'L0_attn_W_qkv': 8.0,
     'L0_attn_W_o': 8.0,
     'L0_ffn_router_w': 8.0,
     'L0_ffn_Wg': 8.0,
     'L0_ffn_Wu': 8.0,
     'L0_ffn_Wd': 8.0,
     'L0_ffn_sWg': 5.097,
     'L0_ffn_sWu': 5.115,
     'L0_ffn_sWd': 4.993,
     'L1_attn_sb_init': 64.0,
     'L1_attn_sb_wq': 64.0,
     'L1_attn_sb_ww': 30.553,
     'L1_attn_b_wq': 64.0,
     'L1_attn_b_keys': 64.0,
     'L1_attn_bp_w': 5.698,
     'L1_attn_dn_wqkv': 8.0,
     'L1_attn_dn_wbeta': 8.0,
     'L1_attn_dn_wo': 8.0,
     'L1_attn_sup_w': 64.0,
     'L1_ffn_wq': 8.0,
     'L1_ffn_wk': 8.0,
     'L1_ffn_wv': 4.283,
     'L1_ffn_wo': 4.055,
     'L1_attn_sb_wo': 4.252,
     'L1_ffn_w1': 4.276}
    for name, (base, spread) in spreads.items():
        noise = np.random.default_rng([zlib.crc32(name.encode()), seed]).standard_normal(out[name].shape)
        drawn = base * np.exp(spread * noise) if base else spread * noise
        out[name] = jnp.asarray(drawn.astype(out[name].dtype))
    for name, factor in factors.items():
        out[name] = (out[name] * factor).astype(out[name].dtype)
    return out
```

```python
from contextlib import ExitStack

import concourse.bass as bass
from concourse import mybir

F32 = mybir.dt.float32
U32 = mybir.dt.uint32
I32 = mybir.dt.int32
ALU = mybir.AluOpType
ACT = mybir.ActivationFunctionType
X = mybir.AxisListType.X

P = 128
B = 32
T = 127
D = 128
GB = 4
NG = B // GB
EPS = 1e-5


class Chain:

    def __init__(self, eng, sem):
        self.eng, self.sem = eng, sem
        self.done, self.k, self.i, self.per = 0, 0, None, 0

    def enter(self, i, per):
        self.done += self.k
        self.i, self.per, self.k = i, per, 0

    def leave(self, times):
        assert self.k == self.per, (self.k, self.per)
        self.done += self.per * times
        self.i, self.per, self.k = None, 0, 0

    def value(self):
        return self.done + self.k + (0 if self.i is None else self.i * self.per)

    def tick(self, ins):
        self.k += 1
        ins.then_inc(self.sem, 1)

    def settle(self):
        self.eng.wait_ge(self.sem, self.value())

    def __call__(self, ins):
        self.tick(ins)
        self.settle()


class Core:

    def __init__(self, nc, ctx):
        self.nc, self.ctx, self.phase, self.sems = nc, ctx, "", []
        self.banks = self.psum("banks", [P, 8 * 512])
        self.bank = [self.banks[:, n * 512:(n + 1) * 512] for n in range(8)]
        self.hidden = self.sbuf("hidden", [P, B, D])
        self.ident = self.sbuf("ident", [P, P])
        self.minus_half = self.sbuf("minus_half", [P, B])

    def sbuf(self, name, shape, dt=F32, ctx=None):
        return (ctx or self.ctx).enter_context(self.nc.sbuf_tensor(self.phase + name, shape, dt))

    def psum(self, name, shape, dt=F32):
        return self.ctx.enter_context(self.nc.psum_tensor(name, shape, dt))

    def sem(self, name, ctx):
        if not self.sems:
            ctx.callback(self.clear_sems)
        self.sems.append(self.nc.alloc_semaphore(self.phase + name))
        return self.sems[-1]

    def clear_sems(self):
        self.nc.clear_and_free_semaphores(self.sems)
        self.nc.all_engine_barrier()
        self.sems = []


def across(ap, n):
    return ap.rearrange("(a d) -> a d", a=1).to_broadcast([n, ap.shape[0]])


def embed_patches(core, x, W, bias):
    nc = core.nc
    core.phase = "embed_"
    BLK = 8 * 32
    with ExitStack() as c:
        sb = lambda n, s, d=F32: core.sbuf(n, s, d, c)
        sem = lambda n: core.sem(n, c)
        w = sb("tok_w", [P, 4 * P])
        wT = sb("tok_wT", [P, 4, P])
        bias_all = sb("tok_bias", [P, D])
        xin = [sb(f"xin{n}", [P, GB, BLK]) for n in range(2)]
        xT = sb("xT", [P, 2, GB, P + 1])
        consts_ready, w_loaded = sem("consts_ready"), sem("tok_w_loaded")
        x_loaded = [sem(f"x_loaded{n}") for n in range(2)]
        x_free, xT_in_psum, xT_ready = sem("x_free"), sem("xT_in_psum"), sem("xT_ready")
        tok_done, acc_free, wT_in_psum, wT_ready = sem("tok_done"), sem("acc_free"), sem("wT_in_psum"), sem("wT_ready")
        pad_ready = sem("pad_ready")
        xg = x.rearrange("b (p r) c -> p b (r c)", r=8)
        with nc.Block() as block:

            @block.sync
            def _(sp):
                sp.dma_start(w[:, :], W).then_inc(w_loaded, 16)
                sp.dma_start(bias_all[:, :], across(bias, P)).then_inc(w_loaded, 16)
                for n in range(2):
                    sp.dma_start(xin[n][:, :, :], xg[:, n * GB:(n + 1) * GB, :]).then_inc(x_loaded[n], 16)
                with sp.Fori(0, NG // 2 - 1) as i:
                    for n in range(2):
                        sp.wait_ge(xT_in_psum, i * 2 + n + 1)
                        sp.dma_start(xin[n][:, :, :], xg[:, bass.ds(i * 2 * GB + (n + 2) * GB, GB), :]).then_inc(x_loaded[n], 16)

            @block.gpsimd
            def _(pool):
                pool.memset(core.ident[:, :], 0.0).then_inc(consts_ready, 1)
                pool.wait_ge(consts_ready, 1)
                pool.affine_select(out=core.ident[:, :], in_=core.ident[:, :], compare_op=ALU.not_equal, fill=1.0,
                                   base=0, pattern=[[-1, P]], channel_multiplier=1).then_inc(consts_ready, 1)
                pool.memset(core.minus_half[:, :], -0.5).then_inc(pad_ready, 1)
                pool.memset(xT[:, :, :, P:P + 1], 0.0).then_inc(pad_ready, 1)

            @block.tensor
            def _(pe):
                pe.wait_ge(consts_ready, 2)
                pe.wait_ge(w_loaded, 32)
                for k in range(4):
                    mm = pe.transpose(core.bank[0][:, k * P:(k + 1) * P], w[:, k * P:(k + 1) * P], core.ident[:, :])
                mm.then_inc(wT_in_psum, 1)
                pe.wait_ge(wT_ready, 1)
                pe.sem_inc(acc_free, 2)
                with pe.Fori(0, NG // 2) as i:
                    for n in range(2):
                        pe.wait_ge(x_loaded[n], i * 16 + 16)
                        for half in range(2):
                            for b in range(GB):
                                mm = pe.transpose(core.bank[half][:, b * P:(b + 1) * P],
                                                  xin[n][:, b, half * P:(half + 1) * P], core.ident[:, :])
                        mm.then_inc(xT_in_psum, 1)
                        pe.wait_ge(xT_ready, i * 2 + n + 1)
                        pe.wait_ge(acc_free, i * 2 + n + 1)
                        for b in range(GB):
                            for k in range(4):
                                mm = pe.matmul(core.bank[2 + n][:, b * P:(b + 1) * P],
                                               xT[:, k % 2, b, k // 2:k // 2 + P], wT[:, k, :],
                                               start=(k == 0), stop=(k == 3))
                        mm.then_inc(tok_done, 1)

            @block.scalar
            def _(act):
                act.wait_ge(wT_in_psum, 1)
                act.copy(wT[:, :, :].rearrange("p k d -> p (k d)"), core.bank[0][:, :]).then_inc(wT_ready, 1)
                act.wait_ge(pad_ready, 2)
                with act.Fori(0, NG // 2) as i:
                    for n in range(2):
                        act.wait_ge(xT_in_psum, i * 2 + n + 1)
                        for half in range(2):
                            cp = act.copy(xT[:, half, :, 0:P], core.bank[half][:, :].rearrange("p (b t) -> p b t", b=GB))
                        cp.then_inc(xT_ready, 1)

            @block.vector
            def _(dve):
                with dve.Fori(0, NG // 2) as i:
                    for n in range(2):
                        dve.wait_ge(tok_done, i * 2 + n + 1)
                        dve.tensor_tensor(core.hidden[:, bass.ds(i * 2 * GB + n * GB, GB), :],
                                          core.bank[2 + n][:, :].rearrange("p (b d) -> p b d", b=GB),
                                          bias_all[:, :].unsqueeze(1).to_broadcast([P, GB, D]),
                                          ALU.add).then_inc(acc_free, 1)


def normalize(core, name, src, out, sq):
    nc = core.nc
    core.phase = name + "_"
    with ExitStack() as c:
        mean = core.sbuf("mean", [P, B], F32, c)
        rstd = core.sbuf("rstd", [P, B], F32, c)
        chain = core.sem("chain", c)
        centred, squared, var_ready, rstd_ready = (core.sem(s, c) for s in ("centred", "squared", "var", "rstd"))
        with nc.Block() as block:

            @block.vector
            def _(dve):
                step = Chain(dve, chain)
                step(dve.tensor_reduce(mean[:, :], src[:, :, :], X, ALU.add))
                step(dve.tensor_scalar(mean[:, :], mean[:, :], 1.0 / D, None, ALU.mult))
                dve.tensor_tensor(out[:, :, :], src[:, :, :], mean[:, :].unsqueeze(2).to_broadcast([P, B, D]),
                                  ALU.subtract).then_inc(centred, 1)
                dve.wait_ge(squared, 1)
                step(dve.tensor_reduce(rstd[:, :], sq[:, :, :], X, ALU.add))
                dve.tensor_scalar(rstd[:, :], rstd[:, :], 1.0 / D, EPS, ALU.mult, ALU.add).then_inc(var_ready, 1)
                dve.wait_ge(rstd_ready, 1)
                step(dve.tensor_tensor(out[:, :, :], out[:, :, :], rstd[:, :].unsqueeze(2).to_broadcast([P, B, D]), ALU.mult))

            @block.scalar
            def _(act):
                act.wait_ge(centred, 1)
                act.activation(sq[:, :, :], out[:, :, :], ACT.Square).then_inc(squared, 1)

            @block.gpsimd
            def _(pool):
                pool.wait_ge(var_ready, 1)
                pool.tensor_tensor(rstd[:, :], rstd[:, :], core.minus_half[:, :], ALU.pow).then_inc(rstd_ready, 1)


def store_hidden(core, out):
    nc = core.nc
    with ExitStack() as c:
        stored = core.sem("stored", c)
        with nc.Block() as block:

            @block.sync
            def _(sp):
                sp.dma_start(out.rearrange("b t d -> t b d"), core.hidden[0:T, :, :]).then_inc(stored, 16)
                sp.wait_ge(stored, 16)


def channel_attention(core, xn, W_qkv, W_o):
    nc = core.nc
    core.phase = "attn0_"
    DK = 16
    R = 48
    SCALE = DK ** -0.5
    CH = 4 * P
    with ExitStack() as c:
        sb = lambda n, s, d=F32: core.sbuf(n, s, d, c)
        sem = lambda n: core.sem(n, c)
        wqkv = sb("wqkv", [P, 3 * DK])
        wq2, wk2 = sb("wq2", [P, R]), sb("wk2", [P, R])
        wo = sb("wo", [DK, D])
        chan = sb("chan", [P, DK])
        x_stage = [sb(f"x_stage{n}", [P, GB, D]) for n in range(2)]
        xT = sb("xT", [P, GB, P])
        kT = sb("kT", [P, GB, P])
        qT = sb("qT", [P, GB, P])
        v = sb("v", [P, GB, DK])
        kmax, kmin = sb("kmax", [R, GB]), sb("kmin", [R, GB])
        top = sb("top", [R, GB, P])
        qd = [sb(f"qd{n}", [P, DK, P]) for n in range(2)]
        vd = [sb(f"vd{n}", [P, DK, R]) for n in range(2)]
        probs = [sb(f"probs{n}", [P, DK, P]) for n in range(2)]
        rden = sb("rden", [DK, P])
        sa = sb("sa", [DK, GB, P])
        (w_loaded, consts_ready, w_ready, staged, xT_in_psum, xT_ready, q_in_psum, k_in_psum, v_in_psum, qk_copied,
         v_copied, qd_ready, scores_ready, probs_ready, sums_ready, sa_ready, out_in_psum,
         hidden_added, chain_sem) = (sem(n) for n in (
            "w_loaded", "consts_ready", "w_ready", "staged", "xT_in_psum", "xT_ready", "q_in_psum", "k_in_psum", "v_in_psum",
            "qk_copied", "v_copied", "qd_ready", "scores_ready", "probs_ready",
            "sums_ready", "sa_ready", "out_in_psum", "hidden_added", "chain"))
        xT_ps, q_ps, k_ps, sum_ps = core.bank[0], core.bank[1], core.bank[2], core.bank[3]
        v_ps, out_ps = xT_ps, q_ps
        with nc.Block() as block:

            @block.sync
            def _(sp):
                sp.dma_start(wqkv[:, :], W_qkv).then_inc(w_loaded, 16)
                sp.dma_start(wo[:, :], W_o).then_inc(w_loaded, 16)

            @block.gpsimd
            def _(pool):
                pool.memset(chan[:, :], 0.0).then_inc(consts_ready, 1)
                pool.wait_ge(consts_ready, 1)
                for n, base in enumerate((0, -32)):
                    pool.affine_select(out=chan[:, :], in_=chan[:, :], compare_op=ALU.not_equal, fill=1.0,
                                       base=base, pattern=[[-1, DK]], channel_multiplier=1).then_inc(consts_ready, 1)
                    pool.wait_ge(consts_ready, 2 + n)
                pool.memset(qT[:, :, :], 0.0).then_inc(consts_ready, 1)
                pool.memset(kT[:, :, :], -1.0).then_inc(consts_ready, 1)
                for n in range(2):
                    pool.memset(vd[n][:, :, 0:32], 0.0).then_inc(consts_ready, 1)
                    pool.memset(vd[n][:, :, 32:R], 0.0).then_inc(consts_ready, 1)
                pool.wait_ge(consts_ready, 9)
                for n in range(2):
                    flat = vd[n][:, :, :].rearrange("p c r -> p (c r)")
                    pool.memset(flat[:, 32::R + 1], 1.0).then_inc(consts_ready, 1)

            @block.tensor
            def _(pe):
                pe.sem_inc(v_copied, 1)
                pe.sem_inc(hidden_added, 1)
                pe.sem_inc(sa_ready, 1)
                pe.sem_inc(probs_ready, 2)
                pe.wait_ge(w_ready, 4)
                with pe.Fori(0, NG // 2) as i:
                    for g in range(2):
                        pe.wait_ge(staged, i * 2 + g + 1)
                        pe.wait_ge(v_copied, i * 2 + g + 1)
                        for b in range(GB):
                            mm = pe.transpose(xT_ps[:, b * P:(b + 1) * P], x_stage[g][:, b, :], core.ident[:, :])
                        mm.then_inc(xT_in_psum, 1)
                        pe.wait_ge(hidden_added, i * 2 + g + 1)
                        pe.wait_ge(xT_ready, i * 2 + g + 1)
                        rhs = xT[:, :, :].rearrange("p b t -> p (b t)")
                        pe.matmul(q_ps[0:R, :], wq2[:, :], rhs, start=True, stop=True).then_inc(q_in_psum, 1)
                        pe.matmul(k_ps[0:R, :], wk2[:, :], rhs, start=True, stop=True).then_inc(k_in_psum, 1)
                        for b in range(GB):
                            mm = pe.matmul(v_ps[:, b * DK:(b + 1) * DK], xT[:, b, :], wqkv[:, 2 * DK:3 * DK],
                                           start=True, stop=True)
                        mm.then_inc(v_in_psum, 1)
                        for b in range(GB + 1):
                            at = i * 2 * GB + g * GB + b
                            if b < GB:
                                pe.wait_ge(qd_ready, at + 1)
                                for half in range(2):
                                    pe.wait_ge(probs_ready, at * 2 + half + 1)
                                    for n in range(2):
                                        ch = half * 8 + n * 4
                                        mm = pe.matmul(core.bank[4 + 2 * half + n][0:T, :], kT[:, b, 0:T],
                                                       qd[b % 2][:, ch:ch + 4, :].rearrange("r c n -> r (c n)"),
                                                       start=True, stop=True)
                                    mm.then_inc(scores_ready, 1)
                            if b >= 1:
                                for half in range(2):
                                    pe.wait_ge(probs_ready, at * 2 + half + 1)
                                    if half == 0:
                                        pe.wait_ge(sa_ready, at)
                                    for ch in range(half * 8, half * 8 + 8):
                                        mm = pe.matmul(sum_ps[0:R, (b - 1) * P:b * P], vd[(b - 1) % 2][0:T, ch, :],
                                                       probs[(b - 1) % 2][0:T, ch, :], start=(ch == 0), stop=(ch == DK - 1))
                                mm.then_inc(sums_ready, 1)
                        pe.wait_ge(sa_ready, i * 2 * GB + (g + 1) * GB + 1)
                        for b in range(GB):
                            mm = pe.matmul(out_ps[:, b * P:(b + 1) * P], sa[:, b, :], wo[:, :], start=True, stop=True)
                        mm.then_inc(out_in_psum, 1)

            @block.scalar
            def _(act):
                with act.Fori(0, NG // 2) as i:
                    for g in range(2):
                        act.wait_ge(xT_in_psum, i * 2 + g + 1)
                        act.copy(xT[:, :, :].rearrange("p b t -> p (b t)"), xT_ps[:, :]).then_inc(xT_ready, 1)
                        act.wait_ge(q_in_psum, i * 2 + g + 1)
                        act.wait_ge(consts_ready, 11)
                        act.copy(qT[0:DK, :, :].rearrange("p b t -> p (b t)"), q_ps[0:DK, :]).then_inc(qk_copied, 1)
                        act.wait_ge(k_in_psum, i * 2 + g + 1)
                        act.copy(kT[0:DK, :, :].rearrange("p b t -> p (b t)"), k_ps[0:DK, :]).then_inc(qk_copied, 1)
                        act.wait_ge(v_in_psum, i * 2 + g + 1)
                        act.copy(v[:, :, :].rearrange("p b c -> p (b c)"), v_ps[:, 0:GB * DK]).then_inc(v_copied, 1)
                        for b in range(GB):
                            at = i * 2 * GB + g * GB + b
                            for half in range(2):
                                act.wait_ge(scores_ready, at * 2 + half + 1)
                                act.activation(probs[b % 2][0:T, half * 8:half * 8 + 8, :].rearrange("p c n -> p (c n)"),
                                               core.banks[0:T, (4 + 2 * half) * 512:(6 + 2 * half) * 512],
                                               ACT.Exp, scale=SCALE).then_inc(probs_ready, 1)

            @block.vector
            def _(dve):
                step = Chain(dve, chain_sem)
                dve.memset(wq2[:, :], 0.0).then_inc(w_ready, 1)
                dve.memset(wk2[:, :], 0.0).then_inc(w_ready, 1)
                dve.wait_ge(w_loaded, 32)
                dve.wait_ge(w_ready, 2)
                for w, col in ((wq2, 0), (wk2, DK)):
                    dve.tensor_copy(w[:, :].rearrange("p (a c) -> p a c", c=DK)[:, 0::2, :],
                                    wqkv[:, col:col + DK].unsqueeze(1).to_broadcast([P, 2, DK])).then_inc(w_ready, 1)
                with dve.Fori(0, NG // 2) as i:
                    step.enter(i, 2 * (5 + GB))
                    for g in range(2):
                        dve.tensor_copy(x_stage[g][:, :, :], xn[:, bass.ds(i * 2 * GB + g * GB, GB), :]).then_inc(staged, 1)
                        lo, hi = 32, R
                        q3 = q_ps[lo:hi, :].rearrange("p (b t) -> p b t", b=GB)
                        k3 = k_ps[lo:hi, :].rearrange("p (b t) -> p b t", b=GB)
                        dve.wait_ge(qk_copied, i * 4 + 2 * g + 2)
                        step.tick(dve.tensor_reduce(kmax[lo:hi, :], k3[:, :, 0:T], X, ALU.max))
                        step(dve.tensor_reduce(kmin[lo:hi, :], k3[:, :, 0:T], X, ALU.min))
                        step.tick(dve.tensor_tensor(top[lo:hi, :, :], q3, kmax[lo:hi, :].unsqueeze(2).to_broadcast([DK, GB, P]), ALU.mult))
                        step(dve.tensor_tensor(qT[lo:hi, :, :], q3, kmin[lo:hi, :].unsqueeze(2).to_broadcast([DK, GB, P]), ALU.mult))
                        step(dve.tensor_tensor(qT[lo:hi, :, :], qT[lo:hi, :, :], top[lo:hi, :, :], ALU.max))
                        dve.wait_ge(v_copied, i * 2 + g + 2)
                        for b in range(GB + 1):
                            at = i * 2 * GB + g * GB + b
                            if b < GB:
                                dve.tensor_copy(vd[b % 2][:, :, :].rearrange("p c r -> p (c r)")[:, 0::R + 1], v[:, b, :])
                                dve.tensor_tensor(qd[b % 2][:, :, :], qT[:, b, :].unsqueeze(1).to_broadcast([P, DK, P]),
                                                  chan[:, :].unsqueeze(2).to_broadcast([P, DK, P]), ALU.mult).then_inc(qd_ready, 1)
                            if b >= 1:
                                dve.wait_ge(sums_ready, at)
                                step(dve.reciprocal(rden[:, :], sum_ps[32:R, (b - 1) * P:b * P]))
                                dve.tensor_tensor(sa[:, b - 1, :], sum_ps[0:DK, (b - 1) * P:b * P], rden[:, :],
                                                  ALU.mult).then_inc(sa_ready, 1)
                        dve.wait_ge(out_in_psum, i * 2 + g + 1)
                        hid = core.hidden[:, bass.ds(i * 2 * GB + g * GB, GB), :]
                        dve.tensor_tensor(hid, out_ps[:, :].rearrange("p (b d) -> p b d", b=GB), hid, ALU.add).then_inc(hidden_added, 1)
                    step.leave(NG // 2)


def route_six_of_64(core, xn, combine, router_w, bias_corr):
    nc = core.nc
    core.phase = "route0_"
    E, G, TG, TOPK = 64, 8, 4, 6
    EPG = E // G
    W = E + 8 - TOPK
    FAR = 1e30
    with ExitStack() as c:
        sb = lambda n, s, d=F32: core.sbuf(n, s, d, c)
        sem = lambda n: core.sem(n, c)
        rw, rwT = sb("rw", [E, D]), sb("rwT", [D, E])
        bias = sb("bias", [P, E])
        lower = sb("lower", [P, G, G])
        sentinels = sb("sentinels", [P, 8 - TOPK])
        stage, xT = sb("stage", [P, GB, D]), sb("xT", [P, GB, P])
        expo, scores, biased = (sb(n, [P, GB, E]) for n in ("expo", "scores", "biased"))
        gs, rank, gmask, penalty = (sb(n, [P, GB, G]) for n in ("gs", "rank", "gmask", "penalty"))
        beats, ties = sb("beats", [P, GB, G, G]), sb("ties", [P, GB, G, G])
        masked, marked = sb("masked", [P, GB, W]), sb("marked", [P, GB, W])
        best = sb("best", [P, GB, 8])
        total = sb("total", [P, GB])
        waiter = sb("waiter", [1, 1])
        (w_loaded, consts_ready, rwT_in_psum, rwT_ready, staged, xT_in_psum, xT_ready, logits_ready, exp_ready,
         chain_sem) = (sem(n) for n in ("w_loaded", "consts_ready", "rwT_in_psum", "rwT_ready", "staged",
                                        "xT_in_psum", "xT_ready", "logits_ready", "exp_ready", "chain"))
        with nc.Block() as block:

            @block.sync
            def _(sp):
                sp.dma_start(rw[:, :], router_w).then_inc(w_loaded, 16)
                sp.dma_start(bias[:, :], across(bias_corr, P)).then_inc(w_loaded, 16)

            @block.gpsimd
            def _(pool):
                pool.memset(lower[:, :, :], 1.0).then_inc(consts_ready, 1)
                pool.wait_ge(consts_ready, 1)
                pool.affine_select(out=lower[:, :, :], in_=lower[:, :, :], compare_op=ALU.is_gt, fill=0.0, base=0,
                                   pattern=[[1, G], [-1, G]], channel_multiplier=0).then_inc(consts_ready, 1)
                for n in range(8 - TOPK):
                    pool.memset(sentinels[:, n:n + 1], -2 * FAR * (n + 1)).then_inc(consts_ready, 1)

            @block.tensor
            def _(pe):
                pe.wait_ge(w_loaded, 32)
                pe.transpose(core.bank[0][:, 0:E], rw[:, :], core.ident[0:E, 0:E]).then_inc(rwT_in_psum, 1)
                pe.wait_ge(rwT_ready, 1)
                with pe.Fori(0, NG) as g:
                    pe.wait_ge(staged, g + 1)
                    for b in range(GB):
                        mm = pe.transpose(core.bank[0][:, b * P:(b + 1) * P], stage[:, b, :], core.ident[:, :])
                    mm.then_inc(xT_in_psum, 1)
                    pe.wait_ge(xT_ready, g + 1)
                    for b in range(GB):
                        mm = pe.matmul(core.bank[1][:, b * E:(b + 1) * E], xT[:, b, :], rwT[:, :], start=True, stop=True)
                    mm.then_inc(logits_ready, 1)

            @block.scalar
            def _(act):
                act.wait_ge(rwT_in_psum, 1)
                act.copy(rwT[:, :], core.bank[0][:, 0:E]).then_inc(rwT_ready, 1)
                with act.Fori(0, NG) as g:
                    act.wait_ge(xT_in_psum, g + 1)
                    act.copy(xT[:, :, :].rearrange("p b t -> p (b t)"), core.bank[0][:, :]).then_inc(xT_ready, 1)
                    act.wait_ge(logits_ready, g + 1)
                    act.activation(expo[:, :, :].rearrange("p b e -> p (b e)"), core.bank[1][:, 0:GB * E], ACT.Exp,
                                   scale=-1.0).then_inc(exp_ready, 1)

            @block.vector
            def _(dve):
                step = Chain(dve, chain_sem)
                dve.wait_ge(consts_ready, 2 + 8 - TOPK)
                dve.wait_ge(w_loaded, 32)
                step(dve.tensor_copy(masked[:, :, E:W], sentinels[:, :].unsqueeze(1).to_broadcast([P, GB, W - E])))
                with dve.Fori(0, NG) as g:
                    step.enter(g, 28)
                    tiles = bass.ds(g * GB, GB)
                    dve.tensor_copy(stage[:, :, :], xn[:, tiles, :]).then_inc(staged, 1)
                    dve.wait_ge(exp_ready, g + 1)
                    step(dve.tensor_scalar(expo[:, :, :], expo[:, :, :], 1.0, None, ALU.add))
                    step(dve.reciprocal(scores[:, :, :], expo[:, :, :]))
                    step(dve.tensor_tensor(biased[:, :, :], scores[:, :, :], bias[:, :].unsqueeze(1).to_broadcast([P, GB, E]), ALU.add))
                    step(dve.tensor_reduce(gs[:, :, :].rearrange("p b g -> p (b g)"),
                                           biased[:, :, :].rearrange("p b (g e) -> p (b g) e", g=G), X, ALU.max))
                    other = gs[:, :, :].unsqueeze(2).to_broadcast([P, GB, G, G])
                    own = gs[:, :, :].unsqueeze(3).to_broadcast([P, GB, G, G])
                    step.tick(dve.tensor_tensor(beats[:, :, :, :], other, own, ALU.is_gt))
                    step(dve.tensor_tensor(ties[:, :, :, :], other, own, ALU.is_ge))
                    step(dve.tensor_tensor(ties[:, :, :, :].rearrange("p b g h -> p b (g h)"), ties[:, :, :, :].rearrange("p b g h -> p b (g h)"),
                                           lower[:, :, :].rearrange("p g h -> p (g h)").unsqueeze(1).to_broadcast([P, GB, G * G]), ALU.mult))
                    step(dve.tensor_tensor(beats[:, :, :, :], beats[:, :, :, :], ties[:, :, :, :], ALU.max))
                    step(dve.tensor_reduce(rank[:, :, :], beats[:, :, :, :], X, ALU.add))
                    step(dve.tensor_scalar(gmask[:, :, :], rank[:, :, :], float(TG), None, ALU.is_lt))
                    step(dve.tensor_scalar(penalty[:, :, :], gmask[:, :, :], -1.0, FAR, ALU.add, ALU.mult))
                    vals = masked[:, :, 0:E].rearrange("p b (g e) -> p b g e", g=G)
                    step(dve.tensor_tensor(vals, biased[:, :, :].rearrange("p b (g e) -> p b g e", g=G),
                                           gmask[:, :, :].unsqueeze(3).to_broadcast([P, GB, G, EPG]), ALU.mult))
                    step(dve.tensor_tensor(vals, vals, penalty[:, :, :].unsqueeze(3).to_broadcast([P, GB, G, EPG]), ALU.add))
                    dve.memset(waiter[:, :], 0.0)
                    for b in range(GB):
                        step.tick(dve.max(best[:, b, :], masked[:, b, 0:E]))
                    step.settle()
                    step(dve.tensor_copy(best[:, :, TOPK:8], sentinels[:, :].unsqueeze(1).to_broadcast([P, GB, 8 - TOPK])))
                    dve.memset(waiter[:, :], 0.0)
                    for b in range(GB):
                        step.tick(dve.match_replace(marked[:, b, :], best[:, b, :], masked[:, b, :], FAR))
                    step.settle()
                    step(dve.tensor_scalar(marked[:, :, 0:E], marked[:, :, 0:E], FAR, None, ALU.is_ge))
                    step(dve.tensor_tensor(expo[:, :, :], scores[:, :, :], marked[:, :, 0:E], ALU.mult))
                    step(dve.tensor_reduce(total[:, :], expo[:, :, :], X, ALU.add))
                    step(dve.tensor_scalar(total[:, :], total[:, :], 1e-20, None, ALU.add))
                    step(dve.reciprocal(total[:, :], total[:, :]))
                    step(dve.tensor_tensor(combine[:, tiles, :], expo[:, :, :], total[:, :].unsqueeze(2).to_broadcast([P, GB, E]), ALU.mult))
                    step.leave(NG)


def experts_dense(core, xn, combine, Wg, Wu, Wd, sWg, sWu, sWd):
    nc = core.nc
    core.phase = "experts0_"
    E, H, HS = 64, 160, 128
    HR = H - P
    with ExitStack() as c:
        sb = lambda n, s, d=F32: core.sbuf(n, s, d, c)
        sem = lambda n: core.sem(n, c)
        w_up = sb("w_up", [P, E, 2 * H])
        w_down, w_down_r = sb("w_down", [P, E, D]), sb("w_down_r", [HR, E, D])
        s_up, s_down = sb("s_up", [P, 2 * HS]), sb("s_down", [HS, D])
        x_tile, xT = sb("x_tile", [P, D]), sb("xT", [P, P])
        gate = [sb(f"gate{n}", [P, H]) for n in range(2)]
        h = [sb(f"h{n}", [P, H]) for n in range(2)]
        hT = [sb(f"hT{n}", [P, P]) for n in range(2)]
        hTr = [sb(f"hTr{n}", [HR, P]) for n in range(2)]
        (w_loaded, staged, xT_in_psum, xT_ready, up_ready, gate_ready, h_ready, hT_in_psum, hT_ready, tile_done,
         hidden_done) = (sem(n) for n in ("w_loaded", "staged", "xT_in_psum", "xT_ready", "up_ready", "gate_ready",
                                          "h_ready", "hT_in_psum", "hT_ready", "tile_done", "hidden_done"))
        up_ps, hT_ps, acc, x_ps = core.bank[0:2], core.bank[2:4], core.bank[4], core.bank[5]
        U = E + 1
        PAIRS = (U - 3) // 2

        with nc.Block() as block:

            @block.sync
            def _(sp):
                sp.dma_start(s_up[:, 0:HS], sWg).then_inc(w_loaded, 16)
                sp.dma_start(s_up[:, HS:2 * HS], sWu).then_inc(w_loaded, 16)
                sp.dma_start(s_down[:, :], sWd).then_inc(w_loaded, 16)
                sp.dma_start(w_up[:, :, 0:H], Wg.rearrange("e c h -> c e h")).then_inc(w_loaded, 16)
                sp.dma_start(w_up[:, :, H:2 * H], Wu.rearrange("e c h -> c e h")).then_inc(w_loaded, 16)
                sp.dma_start(w_down[:, :, :], Wd[:, 0:P, :].rearrange("e h c -> h e c")).then_inc(w_loaded, 16)
                sp.dma_start(w_down_r[:, :, :], Wd[:, P:H, :].rearrange("e h c -> h e c")).then_inc(w_loaded, 16)

            def pipeline(stages, t):
                last = len(stages) - 1

                def tick(s, j=None):
                    for n, stage in enumerate(stages):
                        if 0 <= s - n < U:
                            u = s - n
                            stage(u % 2, u if j is None else j * 2 + u, (u - 1) if j is None else j * 2 + u - 1, u == 0, u == U - 1)
                for s in range(3):
                    tick(s)
                return last, tick

            def run(eng, stages, t):
                last, tick = pipeline(stages, t)
                with eng.Fori(0, PAIRS) as j:
                    for s in (3, 4):
                        tick(s, j)
                for s in range(U, U + last):
                    tick(s)

            @block.tensor
            def _(pe):
                pe.wait_ge(w_loaded, 7 * 16)
                pe.sem_inc(hidden_done, 1)
                with pe.Fori(0, B) as t:
                    def up(par, u, e, first, end):
                        if first:
                            pe.matmul(up_ps[par][:, 0:2 * HS], xT[:, :], s_up[:, :], start=True, stop=True).then_inc(up_ready, 1)
                        else:
                            pe.matmul(up_ps[par][:, 0:2 * H], xT[:, :], w_up[:, bass.ds(e, 1), :].rearrange("p e h -> p (e h)"),
                                      start=True, stop=True).then_inc(up_ready, 1)

                    def turn(par, u, e, first, end):
                        pe.wait_ge(h_ready, t * U + u + 1)
                        mm = pe.transpose(hT_ps[par][:, 0:P], h[par][:, 0:P], core.ident[:, :])
                        if not first:
                            mm = pe.transpose(hT_ps[par][0:HR, P:2 * P], h[par][:, P:H], core.ident[:, :])
                        mm.then_inc(hT_in_psum, 1)

                    def down(par, u, e, first, end):
                        if first:
                            pe.wait_ge(hidden_done, t + 1)
                        pe.wait_ge(hT_ready, t * U + u + 1)
                        if first:
                            pe.matmul(acc[:, 0:D], hT[par][:, :], s_down[:, :], start=True, stop=False)
                        else:
                            pe.matmul(acc[:, 0:D], hT[par][:, :], w_down[:, bass.ds(e, 1), :].rearrange("p e h -> p (e h)"),
                                      start=False, stop=False)
                            pe.matmul(acc[:, 0:D], hTr[par][:, :], w_down_r[:, bass.ds(e, 1), :].rearrange("p e h -> p (e h)"),
                                      start=False, stop=end).then_inc(tile_done, 1)

                    pe.wait_ge(staged, t + 1)
                    pe.transpose(x_ps[:, 0:P], x_tile[:, :], core.ident[:, :]).then_inc(xT_in_psum, 1)
                    pe.wait_ge(xT_ready, t + 1)
                    run(pe, [up, turn, down], t)

            @block.scalar
            def _(act):
                with act.Fori(0, B) as t:
                    def silu(par, u, e, first, end):
                        act.wait_ge(up_ready, t * U + u + 1)
                        n = HS if first else H
                        act.activation(gate[par][:, 0:n], up_ps[par][:, 0:n], ACT.Silu).then_inc(gate_ready, 1)

                    def copy_turned(par, u, e, first, end):
                        act.wait_ge(hT_in_psum, t * U + u + 1)
                        cp = act.copy(hT[par][:, :], hT_ps[par][:, 0:P])
                        if not first:
                            cp = act.copy(hTr[par][:, :], hT_ps[par][0:HR, P:2 * P])
                        cp.then_inc(hT_ready, 1)

                    act.wait_ge(xT_in_psum, t + 1)
                    act.copy(xT[:, :], x_ps[:, 0:P]).then_inc(xT_ready, 1)
                    run(act, [silu, copy_turned], t)

            @block.vector
            def _(dve):
                with dve.Fori(0, B) as t:
                    def weigh(par, u, e, first, end):
                        dve.wait_ge(gate_ready, t * U + u + 1)
                        if first:
                            dve.tensor_tensor(h[par][:, 0:HS], gate[par][:, 0:HS], up_ps[par][:, HS:2 * HS], ALU.mult).then_inc(h_ready, 1)
                        else:
                            dve.scalar_tensor_tensor(out=h[par][:, :], in0=gate[par][:, :],
                                                     scalar=combine[:, bass.ds(t, 1), bass.ds(e, 1)].rearrange("p t e -> p (t e)"),
                                                     in1=up_ps[par][:, H:2 * H], op0=ALU.mult, op1=ALU.mult).then_inc(h_ready, 1)

                    dve.tensor_copy(x_tile[:, :], xn[:, bass.ds(t, 1), :].rearrange("p t d -> p (t d)")).then_inc(staged, 1)
                    run(dve, [weigh], t)
                    dve.wait_ge(tile_done, t * E + E)
                    hid = core.hidden[:, bass.ds(t, 1), :].rearrange("p t d -> p (t d)")
                    dve.tensor_tensor(hid, acc[:, 0:D], hid, ALU.add).then_inc(hidden_done, 1)


class ScanShapes:
    N, SD, H, NH, DH, L = 64, 128, 64, 4, 16, 2
    J = 4
    V = SD // J
    BA, OMG2, C2, G2, XH = 0, 64, 128, 192, 256
    F = 320


def scan_inputs(core, xn, w, record_part, record):
    nc = core.nc
    core.phase = "scan_in_"
    Z = ScanShapes
    SCALE = Z.SD ** -0.5
    with ExitStack() as c:
        sb = lambda n, s, d=F32: core.sbuf(n, s, d, c)
        sem = lambda n: core.sem(n, c)
        w_tok = sb("w_tok", [P, 2 * Z.SD + Z.H])
        b_tok = sb("b_tok", [P, 2 * Z.SD + Z.H])
        bp_b = sb("bp_b", [P, Z.H])
        b_wq = sb("b_wq", [Z.H, Z.SD])
        keys, keysT = sb("keys", [Z.N, Z.SD]), sb("keysT", [Z.SD, Z.N])
        b_in_col, b_bq_col = sb("b_in_col", [Z.H, 1]), sb("b_bq_col", [Z.SD, 1])
        stage, xT = sb("stage", [P, GB, D]), sb("xT", [P, GB, P])
        xhT = sb("xhT", [Z.H, GB, P])
        bqT = sb("bqT", [Z.SD, GB, P])
        rec = [sb(f"rec{n}", [P, GB, Z.F]) for n in range(2)]
        rec_part = [sb(f"rec_part{n}", [P, Z.J, GB, 2, Z.V]) for n in range(2)]
        top, total = sb("top", [P, GB]), sb("total", [P, GB])
        expo = sb("expo", [P, GB, Z.N])
        names = ("w_loaded", "keysT_in_psum", "keysT_ready", "staged", "xT_in_psum", "xT_ready", "tok_ready", "xhT_in_psum",
                 "xhT_ready", "bqT_in_psum", "bqT_ready", "logits_ready", "shifted", "exp_ready", "ba_ready", "exp2_ready",
                 "rec_ready", "chain")
        (w_loaded, keysT_in_psum, keysT_ready, staged, xT_in_psum, xT_ready, tok_ready, xhT_in_psum, xhT_ready, bqT_in_psum,
         bqT_ready, logits_ready, shifted, exp_ready, ba_ready, exp2_ready, rec_ready, chain_sem) = (sem(n) for n in names)
        rec_stored = [sem(f"rec_stored{n}") for n in range(2)]
        with nc.Block() as block:

            @block.sync
            def _(sp):
                o = 0
                for wn, bn in (("sb_wq", "sb_bq"), ("sb_ww", "sb_bw"), ("p_win", "p_bin")):
                    n = w[wn].shape[1]
                    sp.dma_start(w_tok[:, o:o + n], w[wn]).then_inc(w_loaded, 16)
                    sp.dma_start(b_tok[:, o:o + n], across(w[bn], P)).then_inc(w_loaded, 16)
                    o += n
                sp.dma_start(bp_b[:, :], across(w["bp_b"], P)).then_inc(w_loaded, 16)
                sp.dma_start(b_wq[:, :], w["b_wq"]).then_inc(w_loaded, 16)
                sp.dma_start(keys[:, :], w["b_keys"]).then_inc(w_loaded, 16)
                sp.dma_start(b_in_col[:, :], w["p_bin"].rearrange("(d a) -> d a", a=1)).then_inc(w_loaded, 16)
                sp.dma_start(b_bq_col[:, :], w["b_bq"].rearrange("(d a) -> d a", a=1)).then_inc(w_loaded, 16)
                for n in range(2):
                    sp.sem_inc(rec_stored[n], 32)
                with sp.Fori(0, NG // 2) as i:
                    for n in range(2):
                        sp.wait_ge(rec_ready, i * 2 + n + 1)
                        at = bass.ds(i * 2 * GB + n * GB, GB)
                        sp.dma_start(record[:, at, :], rec[n][:, :, :]).then_inc(rec_stored[n], 16)
                        sp.dma_start(record_part[:, :, at, :], rec_part[n][:, :, :, :, :].rearrange("p j b s d -> p j (b s d)")).then_inc(rec_stored[n], 16)
                for n in range(2):
                    sp.wait_ge(rec_stored[n], 32 * (NG // 2 + 1))

            @block.tensor
            def _(pe):
                pe.wait_ge(w_loaded, 11 * 16)
                pe.transpose(core.bank[0][:, 0:Z.N], keys[:, :], core.ident[0:Z.N, 0:Z.N]).then_inc(keysT_in_psum, 1)
                pe.wait_ge(keysT_ready, 1)
                with pe.Fori(0, NG // 2) as i:
                    for n in range(2):
                        g = i * 2 + n
                        pe.wait_ge(staged, g + 1)
                        for b in range(GB):
                            mm = pe.transpose(core.bank[0][:, b * P:(b + 1) * P], stage[:, b, :], core.ident[:, :])
                        mm.then_inc(xT_in_psum, 1)
                        pe.wait_ge(xT_ready, g + 1)
                        flat = xT[:, :, :].rearrange("p b t -> p (b t)")
                        pe.matmul(core.bank[1][0:Z.H, :], w_tok[:, 2 * Z.SD:], flat, start=True, stop=True).then_inc(xhT_in_psum, 1)
                        for b in range(GB):
                            mm = pe.matmul(core.bank[4 + b][:, 0:2 * Z.SD + Z.H], xT[:, b, :], w_tok[:, :], start=True, stop=True)
                        mm.then_inc(tok_ready, 1)
                        pe.wait_ge(xhT_ready, g + 1)
                        pe.matmul(core.bank[2][:, :], b_wq[:, :], xhT[:, :, :].rearrange("p b t -> p (b t)"), start=True, stop=True).then_inc(bqT_in_psum, 1)
                        pe.wait_ge(bqT_ready, g + 1)
                        for b in range(GB):
                            mm = pe.matmul(core.bank[3][:, b * Z.N:(b + 1) * Z.N], bqT[:, b, :], keysT[:, :], start=True, stop=True)
                        mm.then_inc(logits_ready, 1)

            @block.scalar
            def _(act):
                act.wait_ge(keysT_in_psum, 1)
                act.copy(keysT[:, :], core.bank[0][:, 0:Z.N]).then_inc(keysT_ready, 1)
                act.wait_ge(w_loaded, 11 * 16)
                with act.Fori(0, NG // 2) as i:
                    for n in range(2):
                        g = i * 2 + n
                        act.wait_ge(xT_in_psum, g + 1)
                        act.copy(xT[:, :, :].rearrange("p b t -> p (b t)"), core.bank[0][:, :]).then_inc(xT_ready, 1)
                        act.wait_ge(xhT_in_psum, g + 1)
                        act.activation(xhT[:, :, :].rearrange("p b t -> p (b t)"), core.bank[1][0:Z.H, :], ACT.Identity,
                                       bias=b_in_col[:, :]).then_inc(xhT_ready, 1)
                        act.wait_ge(bqT_in_psum, g + 1)
                        act.activation(bqT[:, :, :].rearrange("p b t -> p (b t)"), core.bank[2][:, :], ACT.Identity,
                                       bias=b_bq_col[:, :]).then_inc(bqT_ready, 1)
                        act.wait_ge(shifted, g + 1)
                        act.activation(expo[:, :, :], expo[:, :, :], ACT.Exp, scale=SCALE).then_inc(exp_ready, 1)
                        act.wait_ge(ba_ready, g + 1)
                        act.activation(expo[:, :, :], rec[n][:, :, Z.BA:Z.BA + Z.N], ACT.Exp, scale=-1.0).then_inc(exp2_ready, 1)

            @block.vector
            def _(dve):
                step = Chain(dve, chain_sem)
                dve.wait_ge(w_loaded, 11 * 16)
                with dve.Fori(0, NG // 2) as i:
                    step.enter(i, 2 * (3 * GB + 8))
                    for n in range(2):
                        g = i * 2 + n
                        cols = lambda a, k=Z.N: rec[n][:, :, a:a + k]
                        dve.tensor_copy(stage[:, :, :], xn[:, bass.ds(i * 2 * GB + n * GB, GB), :]).then_inc(staged, 1)
                        dve.wait_ge(tok_ready, g + 1)
                        dve.wait_ge(rec_stored[n], i * 32 + 32)
                        for b in range(GB):
                            for s in range(2):
                                cs = slice(s * Z.SD, (s + 1) * Z.SD)
                                part = lambda ap: ap.rearrange("p (j d) -> p j d", j=Z.J)
                                step.tick(dve.tensor_tensor(rec_part[n][:, :, b, s, :], part(core.bank[4 + b][:, cs]), part(b_tok[:, cs]), ALU.add))
                            step.tick(dve.tensor_tensor(rec[n][:, b, Z.XH:Z.XH + Z.H], core.bank[4 + b][:, 2 * Z.SD:2 * Z.SD + Z.H], b_tok[:, 2 * Z.SD:], ALU.add))
                        dve.wait_ge(logits_ready, g + 1)
                        lg = core.bank[3][:, 0:GB * Z.N].rearrange("p (b n) -> p b n", b=GB)
                        step(dve.tensor_reduce(top[:, :], lg, X, ALU.max))
                        dve.tensor_tensor(expo[:, :, :], lg, top[:, :].unsqueeze(2).to_broadcast([P, GB, Z.N]), ALU.subtract).then_inc(shifted, 1)
                        query = rec_part[n][:, :, :, 0, :].rearrange("p j b d -> p (j b) d")
                        step.tick(dve.tensor_scalar(query, query, SCALE, None, ALU.mult))
                        step(dve.tensor_tensor(cols(Z.XH), cols(Z.XH), bp_b[:, :].unsqueeze(1).to_broadcast([P, GB, Z.H]), ALU.add))
                        dve.wait_ge(exp_ready, g + 1)
                        step(dve.tensor_reduce(total[:, :], expo[:, :, :], X, ALU.add))
                        step(dve.reciprocal(total[:, :], total[:, :]))
                        dve.tensor_tensor(cols(Z.BA), expo[:, :, :], total[:, :].unsqueeze(2).to_broadcast([P, GB, Z.N]), ALU.mult).then_inc(ba_ready, 1)
                        dve.wait_ge(exp2_ready, g + 1)
                        step(dve.tensor_scalar(cols(Z.OMG2), expo[:, :, :], 1.0, None, ALU.add))
                        step(dve.reciprocal(cols(Z.G2), cols(Z.OMG2)))
                        step.tick(dve.tensor_tensor(cols(Z.C2), cols(Z.G2), cols(Z.BA), ALU.mult))
                        dve.tensor_tensor(cols(Z.OMG2), expo[:, :, :], cols(Z.G2), ALU.mult).then_inc(rec_ready, 1)
                    step.leave(NG // 2)


def scan_tokens(core, w, record_part, record, reads, states):
    nc = core.nc
    core.phase = "scan_"
    Z = ScanShapes
    N, H, J, DH = Z.N, Z.H, Z.J, Z.DH
    V = Z.SD // J
    M = N + 1
    LOADS = 2 + Z.L * (8 * J + 4) + 2 * J
    PER = 53
    STEPS = T + 1
    with ExitStack() as c:
        sb = lambda n, s, d=F32: core.sbuf(n, s, d, c)
        sem = lambda n: core.sem(n, c)
        slots = sb("slots", [P, M, V])
        prod, prod_r, outer_w = sb("prod", [P, M, V]), sb("prod_r", [P, M, V]), sb("outer_w", [P, N, V])
        delta = sb("delta", [P, N])
        same_b = sb("same_b", [P, P])
        part_of = sb("part_of", [P, J])
        bp_w = sb("bp_w", [Z.SD, H])
        w_qkv = sb("w_qkv", [H + 1, Z.L, J, 3 * DH + 1])
        w_o = sb("w_o", [H, Z.L, H])
        w_sup = sb("w_sup", [H + 1, Z.SD])
        bo, ln_g, ln_b = sb("bo", [P, Z.L, H]), sb("ln_g", [P, Z.L, H]), sb("ln_b", [P, Z.L, H])
        in_part = [sb(f"in_part{n}", [P, 2 * V]) for n in range(2)]
        in_q, in_wr = [p[:, 0:V] for p in in_part], [p[:, V:2 * V] for p in in_part]
        in_rep = [sb(f"in_rep{n}", [P, Z.F]) for n in range(2)]
        part, logits = sb("part", [P, M]), sb("logits", [P, N])
        nmax, den, rden = sb("nmax", [P, 1]), sb("den", [P, 1]), sb("rden", [P, 1])
        e_a, a, ea, g, omg, w2, keep, c1, gab = (sb(n, [P, M]) for n in ("e_a", "a", "ea", "g", "omg", "w2", "keep", "c1", "gab"))
        junk, cwr = sb("junk", [P, N]), sb("cwr", [P, 1])
        bind, bind_wide, bindT = sb("bind", [P, V]), sb("bind_wide", [P, J, V]), sb("bindT", [Z.SD, P])
        xh, xhb = sb("xh", [P, H]), sb("xhb", [P, H])
        xhT = sb("xhT", [H + 1, B])
        qkv = sb("qkv", [P, 3 * DH])
        eb, beta, ssq, kq, nrm, rk, rkq = (sb(n, [P, 1]) for n in ("eb", "beta", "ssq", "kq", "nrm", "rk", "rkq"))
        mem = [sb(f"mem{l}", [P, DH, DH]) for l in range(Z.L)]
        mprod = sb("mprod", [P, 2, DH, DH])
        msum = sb("msum", [P, 2, DH])
        kn, dv, no, no_wide = sb("kn", [P, DH]), sb("dv", [P, DH]), sb("no", [P, DH]), sb("no_wide", [P, J, DH])
        outer_m = sb("outer_m", [P, DH, DH])
        oT = sb("oT", [H, P])
        stats, mv, lnv, rstd = sb("stats", [P, 6]), sb("mv", [P, 2]), sb("lnv", [P, 1]), sb("rstd", [P, 1])
        waiter = sb("waiter", [1, 1])
        out_x = [sb(f"out_x{n}", [P, H]) for n in range(2)]
        out_r = [sb(f"out_r{n}", [P, V]) for n in range(2)]
        names = ("w_loaded", "consts_ready", "w_ready", "part_ready", "lg_in_psum", "nmax_ready", "exp_ready", "a_ready",
                 "ea_ready", "ax_ready", "prod_r_ready", "keep_ready", "bound", "decayed", "outer_w_ready", "bind_ready",
                 "bindT_in_psum", "bindT_ready", "xh_in_psum", "xh_ready", "xhT_in_psum", "xhT_ready", "qkv_in_psum",
                 "eb_ready", "ssq_ready", "nrm_ready", "kn_ready", "dv_ready", "mem_ready", "no_ready", "oT_in_psum",
                 "oT_ready", "o_in_psum", "mv_ready", "rstd_ready", "u_in_psum", "read_ready", "step_done", "chain", "act_chain",
                 "pool_chain")
        S = {n: sem(n) for n in names}
        loaded = [sem(f"loaded{n}") for n in range(2)]
        stored = [sem(f"stored{n}") for n in range(2)]
        A, BT, C_, D_, E_, F_, G_, U_ = core.bank

        def col(n, name, width=N):
            return in_rep[n][:, name:name + width]

        with nc.Block() as block:

            @block.sync
            def _(sp):
                loads = [(bp_w[:, :], w["bp_w"]),
                         (w_sup[0:H, :], w["sup_w"])]
                for l in range(Z.L):
                    loads += [(w_qkv[0:H, l, j, s * DH:(s + 1) * DH], w["dn_wqkv"][l][:, s * H + j * DH:s * H + (j + 1) * DH])
                              for s in range(3) for j in range(J)]
                    loads += [(w_qkv[H:H + 1, l, j, s * DH:(s + 1) * DH],
                               w["dn_bqkv"][l:l + 1, s * H + j * DH:s * H + (j + 1) * DH]) for s in range(3) for j in range(J)]
                    loads += [(w_qkv[0:H, l, j, 3 * DH:], w["dn_wbeta"][l][:, j:j + 1]) for j in range(J)]
                    loads += [(w_qkv[H:H + 1, l, j, 3 * DH:], w["dn_bbeta"][l:l + 1, j:j + 1]) for j in range(J)]
                    loads += [(w_o[:, l, :], w["dn_wo"][l])]
                    loads += [(dst[:, l, :], w[name][l:l + 1, :].to_broadcast([P, H]))
                              for dst, name in ((bo, "dn_bo"), (ln_g, "dn_lng"), (ln_b, "dn_lnb"))]
                for j in range(J):
                    loads += [(slots[32 * j:32 * j + 32, 0:N, :], w["sb_init"][:, V * j:V * j + V].unsqueeze(0).to_broadcast([B, N, V])),
                              (slots[32 * j:32 * j + 32, N, :], w["sup_b"][V * j:V * j + V].unsqueeze(0).to_broadcast([B, V]))]
                for dst, src in loads:
                    sp.dma_start(dst, src, allow_slow_non_contiguous=dst.shape[-1] == 1).then_inc(S["w_loaded"], 16)
                assert len(loads) == LOADS

                def load(t, n):
                    sp.dma_start(in_part[n][:, :], record_part[bass.ds(t, 1), :, :, :].rearrange("t j b f -> (t j b) f")).then_inc(loaded[n], 16)
                    for j in range(J):
                        sp.dma_start(in_rep[n][B * j:B * j + B, :], record[bass.ds(t, 1), :, :].rearrange("t b f -> (t b) f")).then_inc(loaded[n], 16)

                def store(t, n):
                    sp.wait_ge(S["read_ready"], t + 1)
                    sp.dma_start(reads[bass.ds(t, 1), :, :, :].rearrange("t j b d -> (t j b) d"), out_r[n][:, :]).then_inc(stored[n], 16)
                    sp.wait_ge(S["xh_ready"], t * 3 + 3)
                    sp.dma_start(states[bass.ds(t, 1), :, :].rearrange("t b f -> (t b) f"), out_x[n][0:B, :]).then_inc(stored[n], 16)

                for n in range(2):
                    sp.sem_inc(stored[n], 32)
                    load(n, n)
                with sp.Fori(0, STEPS // 2 - 1) as i:
                    for n in range(2):
                        store(i * 2 + n, n)
                        sp.wait_ge(S["step_done"], i * 2 + n + 1)
                        load(i * 2 + n + 2, n)
                for n in range(2):
                    store(STEPS - 2 + n, n)
                for n in range(2):
                    sp.wait_ge(stored[n], 32 * (STEPS // 2 + 1))

            @block.gpsimd
            def _(pool):
                step = Chain(pool, S["pool_chain"])
                step(pool.memset(same_b[:, :], 0.0))
                for s in range(1 - J, J):
                    step(pool.affine_select(out=same_b[:, :], in_=same_b[:, :], compare_op=ALU.not_equal, fill=1.0,
                                            base=B * s, pattern=[[-1, P]], channel_multiplier=1))
                step(pool.memset(part_of[:, :], 0.0))
                for j in range(J):
                    step(pool.memset(part_of[B * j:B * j + B, j:j + 1], 1.0))
                pool.memset(delta[:, :], 0.0).then_inc(S["consts_ready"], 1)
                pool.memset(xhT[:, :], 1.0).then_inc(S["consts_ready"], 1)
                pool.wait_ge(S["consts_ready"], 2)
                pool.memset(w_sup[H:H + 1, :], 0.0).then_inc(S["consts_ready"], 1)
                pool.wait_ge(S["consts_ready"], 3)
                for l in range(Z.L):
                    pool.memset(mem[l][:, :, :], 0.0).then_inc(S["consts_ready"], 1)
                pool.sem_inc(S["mem_ready"], 1)
                with pool.Fori(0, STEPS // 2) as i:
                    step.enter(i, 2 * Z.L)
                    for n in range(2):
                        t = i * 2 + n
                        pool.wait_ge(S["ax_ready"], t + 1)
                        pool.tensor_tensor(prod_r[:, :, :], slots[:, :, :], a[:, :].unsqueeze(2).to_broadcast([P, M, V]), ALU.mult).then_inc(S["prod_r_ready"], 1)
                        pool.wait_ge(S["prod_r_ready"], t + 1)
                        pool.wait_ge(S["bound"], t + 1)
                        pool.tensor_tensor(slots[:, 0:N, :], slots[:, 0:N, :], keep[:, 0:N].unsqueeze(2).to_broadcast([P, N, V]), ALU.mult).then_inc(S["decayed"], 1)
                        pool.wait_ge(loaded[n], i * 80 + 80)
                        pool.tensor_tensor(outer_w[:, :, :], in_wr[n].unsqueeze(1).to_broadcast([P, N, V]),
                                           c1[:, 0:N].unsqueeze(2).to_broadcast([P, N, V]), ALU.mult).then_inc(S["outer_w_ready"], 1)
                        for l in range(Z.L):
                            pool.wait_ge(S["dv_ready"], t * 2 + l + 1)
                            step(pool.tensor_tensor(outer_m[:, :, :], dv[:, :].unsqueeze(2).to_broadcast([P, DH, DH]),
                                                    kn[:, :].unsqueeze(1).to_broadcast([P, DH, DH]), ALU.mult))
                            pool.wait_ge(S["mem_ready"], t * 2 + l + 1)
                            pool.tensor_tensor(mem[l][:, :, :], mem[l][:, :, :], outer_m[:, :, :], ALU.subtract).then_inc(S["mem_ready"], 1)
                    step.leave(STEPS // 2)

            @block.tensor
            def _(pe):
                pe.wait_ge(S["pool_chain"], 3 * J + 1)
                pe.wait_ge(S["consts_ready"], 3 + Z.L)
                pe.wait_ge(S["w_ready"], 1)
                with pe.Fori(0, STEPS // 2) as i:
                    for n in range(2):
                        t = i * 2 + n

                        def turn_xh(which):
                            pe.wait_ge(S["xh_ready"], t * 3 + which + 1)
                            src = out_x[n] if which == 2 else xh
                            pe.matmul(D_[0:H, 0:B], src[0:B, :], core.ident[0:B, 0:B], start=True, stop=True).then_inc(S["xhT_in_psum"], 1)
                            pe.wait_ge(S["xhT_ready"], t * 3 + which + 1)

                        pe.wait_ge(S["part_ready"], t + 1)
                        pe.matmul(A[:, 0:M], same_b[:, :], part[:, :], start=True, stop=True).then_inc(S["lg_in_psum"], 1)
                        pe.wait_ge(S["bind_ready"], t + 1)
                        pe.matmul(BT[:, 0:P], bind_wide[:, :, :].rearrange("p j d -> p (j d)"), same_b[:, :], start=True, stop=True).then_inc(S["bindT_in_psum"], 1)
                        pe.wait_ge(S["bindT_ready"], t + 1)
                        pe.matmul(C_[:, 0:H], bindT[:, :], bp_w[:, :], start=True, stop=True).then_inc(S["xh_in_psum"], 1)
                        for l in range(Z.L):
                            turn_xh(l)
                            for j in range(J):
                                mm = pe.matmul(E_[B * j:B * j + B, 0:3 * DH + 1], xhT[:, :], w_qkv[:, l, j, :], start=True, stop=True)
                            mm.then_inc(S["qkv_in_psum"], 1)
                            pe.wait_ge(S["no_ready"], t * 2 + l + 1)
                            pe.matmul(F_[0:H, 0:P], no_wide[:, :, :].rearrange("p j d -> p (j d)"), same_b[:, :], start=True, stop=True).then_inc(S["oT_in_psum"], 1)
                            pe.wait_ge(S["oT_ready"], t * 2 + l + 1)
                            pe.matmul(G_[:, 0:H], oT[:, :], w_o[:, l, :], start=True, stop=True).then_inc(S["o_in_psum"], 1)
                        turn_xh(2)
                        for j in range(J):
                            mm = pe.matmul(U_[B * j:B * j + B, 0:V], xhT[:, :], w_sup[:, V * j:V * j + V], start=True, stop=True)
                        mm.then_inc(S["u_in_psum"], 1)

            @block.scalar
            def _(act):
                act.preload_act_table_set("natural_log_exp_and_others")
                step = Chain(act, S["act_chain"])
                act.wait_ge(S["consts_ready"], 3 + Z.L)
                with act.Fori(0, STEPS // 2) as i:
                    step.enter(i, 2 * Z.L * 2)
                    for n in range(2):
                        t = i * 2 + n

                        def copy_xhT(which):
                            act.wait_ge(S["xhT_in_psum"], t * 3 + which + 1)
                            act.copy(xhT[0:H, :], D_[0:H, 0:B]).then_inc(S["xhT_ready"], 1)

                        act.wait_ge(S["nmax_ready"], t + 1)
                        act.activation(e_a[:, 0:N], logits[:, :], ACT.Exp, bias=nmax[:, :], accum_out=den[:, :]).then_inc(S["exp_ready"], 1)
                        act.wait_ge(S["a_ready"], t + 1)
                        act.activation(ea[:, 0:N], a[:, 0:N], ACT.Exp, scale=-1.0).then_inc(S["ea_ready"], 1)
                        act.wait_ge(S["bindT_in_psum"], t + 1)
                        act.copy(bindT[:, :], BT[:, 0:P]).then_inc(S["bindT_ready"], 1)
                        for l in range(Z.L):
                            copy_xhT(l)
                            act.wait_ge(S["qkv_in_psum"], t * 2 + l + 1)
                            act.activation(eb[:, :], E_[:, 3 * DH:3 * DH + 1], ACT.Exp, scale=-1.0).then_inc(S["eb_ready"], 1)
                            act.wait_ge(S["ssq_ready"], t * 2 + l + 1)
                            step(act.activation(nrm[:, :], ssq[:, :], ACT.Ln))
                            act.activation(nrm[:, :], nrm[:, :], ACT.Exp, scale=0.5).then_inc(S["nrm_ready"], 1)
                            act.wait_ge(S["oT_in_psum"], t * 2 + l + 1)
                            act.copy(oT[:, :], F_[0:H, 0:P]).then_inc(S["oT_ready"], 1)
                            act.wait_ge(S["mv_ready"], t * 2 + l + 1)
                            step(act.activation(lnv[:, :], mv[:, 1:2], ACT.Ln, bias=EPS))
                            act.activation(rstd[:, :], lnv[:, :], ACT.Exp, scale=-0.5).then_inc(S["rstd_ready"], 1)
                        copy_xhT(2)
                    step.leave(STEPS // 2)

            @block.vector
            def _(dve):
                step = Chain(dve, S["chain"])
                dve.wait_ge(S["w_loaded"], 16 * LOADS)
                dve.wait_ge(S["consts_ready"], 3 + Z.L)
                dve.tensor_scalar(w_o[:, :, :], w_o[:, :, :], -1.0, None, ALU.mult).then_inc(S["w_ready"], 1)
                spread = lambda ap, k=N: ap[:, 0:k].unsqueeze(2).to_broadcast([P, k, V])
                with dve.Fori(0, STEPS // 2) as i:
                    step.enter(i, 2 * PER)
                    for n in range(2):
                        t = i * 2 + n
                        dve.wait_ge(loaded[n], i * 80 + 80)
                        step(dve.tensor_tensor(prod[:, :, :], slots[:, :, :], in_q[n].unsqueeze(1).to_broadcast([P, M, V]), ALU.mult))
                        dve.tensor_reduce(part[:, :], prod[:, :, :], X, ALU.add).then_inc(S["part_ready"], 1)
                        dve.wait_ge(S["lg_in_psum"], t + 1)
                        step(dve.tensor_copy(part[:, :], A[:, 0:M]))
                        step(dve.scalar_tensor_tensor(out=logits[:, :], in0=delta[:, :], scalar=part[:, N:M], in1=part[:, 0:N], op0=ALU.mult, op1=ALU.add))
                        dve.tensor_reduce(nmax[:, :], logits[:, :], X, ALU.max, negate=True).then_inc(S["nmax_ready"], 1)
                        dve.wait_ge(S["exp_ready"], t + 1)
                        step(dve.reciprocal(rden[:, :], den[:, :]))
                        dve.tensor_scalar(a[:, 0:N], e_a[:, 0:N], rden[:, :], None, ALU.mult).then_inc(S["a_ready"], 1)
                        dve.wait_ge(S["a_ready"], t + 1)
                        dve.tensor_tensor_reduce(junk[:, :], a[:, 0:N], delta[:, :], 1.0, 0.0, ALU.mult, ALU.add, a[:, N:M]).then_inc(S["ax_ready"], 1)
                        dve.wait_ge(S["ea_ready"], t + 1)
                        step(dve.tensor_scalar(g[:, 0:N], ea[:, 0:N], 1.0, None, ALU.add))
                        step(dve.reciprocal(g[:, 0:N], g[:, 0:N]))
                        step.tick(dve.tensor_tensor(omg[:, 0:N], ea[:, 0:N], g[:, 0:N], ALU.mult))
                        step(dve.tensor_tensor(gab[:, 0:N], g[:, 0:N], a[:, 0:N], ALU.mult))
                        step.tick(dve.tensor_tensor(w2[:, 0:N], omg[:, 0:N], col(n, Z.BA), ALU.mult))
                        step.tick(dve.tensor_tensor(keep[:, 0:N], omg[:, 0:N], col(n, Z.OMG2), ALU.mult))
                        step(dve.tensor_tensor(c1[:, 0:N], gab[:, 0:N], col(n, Z.OMG2), ALU.mult))
                        step.tick(dve.tensor_tensor_reduce(junk[:, :], gab[:, 0:N], col(n, Z.BA), 1.0, 0.0, ALU.mult, ALU.add, cwr[:, :]))
                        step(dve.tensor_tensor_reduce(e_a[:, 0:N], w2[:, 0:N], delta[:, :], 1.0, 0.0, ALU.mult, ALU.add, w2[:, N:M]))
                        dve.tensor_tensor(prod[:, :, :], slots[:, :, :], spread(w2, M), ALU.mult).then_inc(S["bound"], 1)
                        dve.wait_ge(S["bound"], t + 1)
                        step(dve.tensor_reduce(bind[:, :], prod[:, :, :].rearrange("p n d -> p d n"), X, ALU.add))
                        step(dve.scalar_tensor_tensor(out=bind[:, :], in0=in_wr[n], scalar=cwr[:, :], in1=bind[:, :], op0=ALU.mult, op1=ALU.add))
                        dve.tensor_tensor(bind_wide[:, :, :], bind[:, :].unsqueeze(1).to_broadcast([P, J, V]),
                                          part_of[:, :].unsqueeze(2).to_broadcast([P, J, V]), ALU.mult).then_inc(S["bind_ready"], 1)
                        step(dve.tensor_tensor(delta[:, :], delta[:, :], keep[:, 0:N], ALU.mult))
                        step.tick(dve.tensor_tensor(delta[:, :], delta[:, :], col(n, Z.G2), ALU.add))
                        dve.wait_ge(S["xh_in_psum"], t + 1)
                        dve.tensor_tensor(xh[:, :], C_[:, 0:H], col(n, Z.XH, H), ALU.add).then_inc(S["xh_ready"], 1)
                        dve.wait_ge(S["xh_ready"], t * 3 + 1)
                        for l in range(Z.L):
                            step(dve.tensor_tensor(xhb[:, :], xh[:, :], bo[:, l, :], ALU.add))
                            if l == 0:
                                dve.wait_ge(S["prod_r_ready"], t + 1)
                                dve.wait_ge(stored[n], i * 32 + 32)
                                dve.tensor_reduce(out_r[n][:, :], prod_r[:, :, :].rearrange("p n d -> p d n"), X, ALU.add).then_inc(S["read_ready"], 1)
                            dve.wait_ge(S["eb_ready"], t * 2 + l + 1)
                            step(dve.tensor_copy(qkv[:, :], E_[:, 0:3 * DH]))
                            q, k, v = (qkv[:, s * DH:(s + 1) * DH] for s in range(3))
                            step(dve.tensor_tensor_reduce(junk[:, 0:DH], k, k, 1.0, 1e-19, ALU.mult, ALU.add, ssq[:, :]))
                            dve.tensor_tensor_reduce(junk[:, 0:DH], k, q, 1.0, 0.0, ALU.mult, ALU.add, kq[:, :]).then_inc(S["ssq_ready"], 1)
                            dve.wait_ge(S["mem_ready"], t * 2 + l + 1)
                            step(dve.tensor_tensor(mprod[:, :, :, :], mem[l][:, :, :].unsqueeze(1).to_broadcast([P, 2, DH, DH]),
                                                   qkv[:, 0:2 * DH].rearrange("p (s j) -> p s j", s=2).unsqueeze(2).to_broadcast([P, 2, DH, DH]), ALU.mult))
                            step.tick(dve.tensor_reduce(msum[:, :, :], mprod[:, :, :, :], X, ALU.add))
                            step(dve.tensor_scalar(beta[:, :], eb[:, :], 1.0, None, ALU.add))
                            step(dve.reciprocal(beta[:, :], beta[:, :]))
                            dve.wait_ge(S["nrm_ready"], t * 2 + l + 1)
                            step(dve.tensor_scalar(nrm[:, :], nrm[:, :], 1e-6, None, ALU.add))
                            step(dve.reciprocal(rk[:, :], nrm[:, :]))
                            step.tick(dve.tensor_scalar(kn[:, :], k, rk[:, :], None, ALU.mult))
                            step.tick(dve.tensor_tensor(rkq[:, :], kq[:, :], rk[:, :], ALU.mult))
                            step(dve.scalar_tensor_tensor(out=dv[:, :], in0=msum[:, 1, :], scalar=rk[:, :], in1=v, op0=ALU.mult, op1=ALU.subtract))
                            dve.tensor_scalar(dv[:, :], dv[:, :], beta[:, :], None, ALU.mult).then_inc(S["dv_ready"], 1)
                            dve.wait_ge(S["dv_ready"], t * 2 + l + 1)
                            step(dve.scalar_tensor_tensor(out=no[:, :], in0=dv[:, :], scalar=rkq[:, :], in1=msum[:, 0, :], op0=ALU.mult, op1=ALU.subtract))
                            dve.tensor_tensor(no_wide[:, :, :], no[:, :].unsqueeze(1).to_broadcast([P, J, DH]),
                                              part_of[:, :].unsqueeze(2).to_broadcast([P, J, DH]), ALU.mult).then_inc(S["no_ready"], 1)
                            dve.wait_ge(S["o_in_psum"], t * 2 + l + 1)
                            step(dve.tensor_tensor(xhb[:, :], G_[:, 0:H], xhb[:, :], ALU.add))
                            step(dve.bn_stats(stats[:, :], xhb[:, :]))
                            dve.memset(waiter[:, :], 0.0)
                            dve.bn_aggr(mv[:, :], stats[:, :]).then_inc(S["mv_ready"], 1)
                            dve.wait_ge(S["rstd_ready"], t * 2 + l + 1)
                            step(dve.tensor_scalar(xhb[:, :], xhb[:, :], mv[:, 0:1], rstd[:, :], ALU.subtract, ALU.mult))
                            step(dve.tensor_tensor(xhb[:, :], xhb[:, :], ln_g[:, l, :], ALU.mult))
                            dst = xh if l == 0 else out_x[n]
                            dve.tensor_tensor(dst[:, :], xhb[:, :], ln_b[:, l, :], ALU.add).then_inc(S["xh_ready"], 1)
                            dve.wait_ge(S["xh_ready"], t * 3 + l + 2)
                        dve.wait_ge(S["outer_w_ready"], t + 1)
                        step(dve.tensor_tensor(slots[:, 0:N, :], slots[:, 0:N, :], outer_w[:, :, :], ALU.add))
                        dve.wait_ge(S["u_in_psum"], t + 1)
                        step(dve.tensor_tensor(prod[:, 0:N, :], U_[:, 0:V].unsqueeze(1).to_broadcast([P, N, V]), spread(col(n, Z.C2)), ALU.mult))
                        dve.tensor_tensor(slots[:, 0:N, :], slots[:, 0:N, :], prod[:, 0:N, :], ALU.add).then_inc(S["step_done"], 1)
                        dve.wait_ge(S["step_done"], t + 1)
                    step.leave(STEPS // 2)


def scan_outputs(core, w, reads, states):
    nc = core.nc
    core.phase = "after_scan_"
    Z = ScanShapes
    with ExitStack() as c:
        sb = lambda n, s, d=F32: core.sbuf(n, s, d, c)
        sem = lambda n: core.sem(n, c)
        wo, op_w, ow = sb("wo", [Z.SD, D]), sb("op_w", [Z.H, D]), sb("ow", [D, D])
        rows = {n: sb(n, [P, D]) for n in ("sb_bo", "op_b", "oln_g", "oln_b", "ob")}
        r = [sb(f"r{n}", [P, GB, Z.SD]) for n in range(2)]
        x = [sb(f"x{n}", [P, GB, Z.H]) for n in range(2)]
        rT, xT = sb("rT", [Z.SD, GB, P]), sb("xT", [Z.H, GB, P])
        y, sq, yT = sb("y", [P, GB, D]), sb("sq", [P, GB, D]), sb("yT", [D, GB, P])
        mean, var = sb("mean", [P, GB]), sb("var", [P, GB])
        names = ("w_loaded", "rT_in_psum", "xT_in_psum", "rT_ready", "xT_ready", "y_in_psum", "centred", "squared", "var_ready", "rstd_ready",
                 "y_ready", "yT_in_psum", "yT_ready", "out_in_psum", "hidden_added", "chain", "act_chain")
        S = {n: sem(n) for n in names}
        loaded = [sem(f"loaded{n}") for n in range(2)]
        flat = lambda ap: ap[:, :, :].rearrange("p b d -> p (b d)")
        with nc.Block() as block:

            @block.sync
            def _(sp):
                for dst, name in ((wo, "sb_wo"), (op_w, "op_w"), (ow, "ow")):
                    sp.dma_start(dst[:, :], w[name]).then_inc(S["w_loaded"], 16)
                for name, dst in rows.items():
                    sp.dma_start(dst[:, :], across(w[name], P)).then_inc(S["w_loaded"], 16)
                sp.sem_inc(S["xT_ready"], 2)
                with sp.Fori(0, NG // 2) as i:
                    for n in range(2):
                        at = bass.ds(i * 2 * GB + n * GB, GB)
                        sp.wait_ge(S["xT_ready"], i * 2 + n + 1)
                        for j in range(Z.J):
                            sp.dma_start(r[n][:, :, Z.V * j:Z.V * j + Z.V], reads[:, j, at, :]).then_inc(loaded[n], 16)
                        sp.dma_start(x[n][:, :, :], states[:, at, :]).then_inc(loaded[n], 16)

            @block.tensor
            def _(pe):
                pe.wait_ge(S["w_loaded"], 8 * 16)
                with pe.Fori(0, NG // 2) as i:
                    for n in range(2):
                        g = i * 2 + n
                        pe.wait_ge(loaded[n], i * 80 + 80)
                        for b in range(GB):
                            mm = pe.transpose(core.bank[0][:, b * P:(b + 1) * P], r[n][:, b, :], core.ident[:, :])
                        mm.then_inc(S["rT_in_psum"], 1)
                        for b in range(GB):
                            mm = pe.transpose(core.bank[1][0:Z.H, b * P:(b + 1) * P], x[n][:, b, :], core.ident[:, :])
                        mm.then_inc(S["xT_in_psum"], 1)
                        pe.wait_ge(S["rT_ready"], g + 1)
                        pe.wait_ge(S["xT_ready"], g + 3)
                        for b in range(GB):
                            pe.matmul(core.bank[2][:, b * P:(b + 1) * P], rT[:, b, :], wo[:, :], start=True, stop=False)
                            mm = pe.matmul(core.bank[2][:, b * P:(b + 1) * P], xT[:, b, :], op_w[:, :], start=False, stop=True)
                        mm.then_inc(S["y_in_psum"], 1)
                        pe.wait_ge(S["y_ready"], g + 1)
                        for b in range(GB):
                            mm = pe.transpose(core.bank[3][:, b * P:(b + 1) * P], y[:, b, :], core.ident[:, :])
                        mm.then_inc(S["yT_in_psum"], 1)
                        pe.wait_ge(S["yT_ready"], g + 1)
                        for b in range(GB):
                            mm = pe.matmul(core.bank[4][:, b * P:(b + 1) * P], yT[:, b, :], ow[:, :], start=True, stop=True)
                        mm.then_inc(S["out_in_psum"], 1)

            @block.scalar
            def _(act):
                act.preload_act_table_set("natural_log_exp_and_others")
                step = Chain(act, S["act_chain"])
                with act.Fori(0, NG // 2) as i:
                    step.enter(i, 2)
                    for n in range(2):
                        g = i * 2 + n
                        act.wait_ge(S["rT_in_psum"], g + 1)
                        act.copy(flat(rT), core.bank[0][:, :]).then_inc(S["rT_ready"], 1)
                        act.wait_ge(S["xT_in_psum"], g + 1)
                        act.copy(flat(xT), core.bank[1][0:Z.H, :]).then_inc(S["xT_ready"], 1)
                        act.wait_ge(S["centred"], g + 1)
                        act.activation(flat(sq), flat(y), ACT.Square).then_inc(S["squared"], 1)
                        act.wait_ge(S["var_ready"], g + 1)
                        step(act.activation(var[:, :], var[:, :], ACT.Ln))
                        act.activation(var[:, :], var[:, :], ACT.Exp, scale=-0.5).then_inc(S["rstd_ready"], 1)
                        act.wait_ge(S["yT_in_psum"], g + 1)
                        act.copy(flat(yT), core.bank[3][:, :]).then_inc(S["yT_ready"], 1)
                    step.leave(NG // 2)

            @block.vector
            def _(dve):
                step = Chain(dve, S["chain"])
                dve.wait_ge(S["w_loaded"], 8 * 16)
                step(dve.tensor_tensor(rows["sb_bo"][:, :], rows["sb_bo"][:, :], rows["op_b"][:, :], ALU.add))
                wide = lambda name: rows[name][:, :].unsqueeze(1).to_broadcast([P, GB, D])
                each = lambda ap: ap[:, :].unsqueeze(2).to_broadcast([P, GB, D])
                with dve.Fori(0, NG // 2) as i:
                    step.enter(i, 2 * 6 + 2)
                    for n in range(2):
                        g = i * 2 + n
                        y3 = y[:, :, :]
                        dve.wait_ge(S["y_in_psum"], g + 1)
                        step(dve.tensor_tensor(y3, core.bank[2][:, :].rearrange("p (b d) -> p b d", b=GB), wide("sb_bo"), ALU.add))
                        step(dve.tensor_reduce(mean[:, :], y3, X, ALU.add))
                        step(dve.tensor_scalar(mean[:, :], mean[:, :], 1.0 / D, None, ALU.mult))
                        dve.tensor_tensor(y3, y3, each(mean), ALU.subtract).then_inc(S["centred"], 1)
                        dve.wait_ge(S["squared"], g + 1)
                        step(dve.tensor_reduce(var[:, :], sq[:, :, :], X, ALU.add))
                        dve.tensor_scalar(var[:, :], var[:, :], 1.0 / D, EPS, ALU.mult, ALU.add).then_inc(S["var_ready"], 1)
                        dve.wait_ge(S["rstd_ready"], g + 1)
                        step(dve.tensor_tensor(y3, y3, each(var), ALU.mult))
                        step(dve.tensor_tensor(y3, y3, wide("oln_g"), ALU.mult))
                        dve.tensor_tensor(y3, y3, wide("oln_b"), ALU.add).then_inc(S["y_ready"], 1)
                        dve.wait_ge(S["out_in_psum"], g + 1)
                        step(dve.tensor_tensor(sq[:, :, :], core.bank[4][:, :].rearrange("p (b d) -> p b d", b=GB), wide("ob"), ALU.add))
                        hid = core.hidden[:, bass.ds(i * 2 * GB + n * GB, GB), :]
                        dve.tensor_tensor(hid, sq[:, :, :], hid, ALU.add).then_inc(S["hidden_added"], 1)
                    step.leave(NG // 2)


def self_attention(core, x, xn, g_row, b_row, wq, wk, wv, wo):
    nc = core.nc
    core.phase = "mha_"
    NH, DH = 8, 16
    SCALE = DH ** -0.5
    HALF = NH // 2 * P
    with ExitStack() as c:
        sb = lambda n, s, d=F32: core.sbuf(n, s, d, c)
        sem = lambda n: core.sem(n, c)
        W = {n: sb(n, [D, D]) for n in ("wq", "wk", "wv", "wo")}
        g_all, b_all = sb("g_all", [P, D]), sb("b_all", [P, D])
        head = sb("head", [P, NH])
        x1, xT, qT, kT, v = (sb(n, [P, GB, P]) for n in ("x1", "xT", "qT", "kT", "v"))
        kd = [sb(f"kd{n}", [P, NH, P]) for n in range(2)]
        probs = [sb(f"probs{n}", [P, NH, P]) for n in range(2)]
        pT = sb("pT", [P, NH, P])
        top, nmax, den, rden = (sb(n, [P, 2, NH]) for n in ("top", "nmax", "den", "rden"))
        o, oT = sb("o", [P, GB, D]), sb("oT", [D, GB, P])
        names = ("w_loaded", "consts_ready", "x1_ready", "xT_in_psum", "xT_ready", "q_in_psum", "k_in_psum", "v_in_psum", "q_ready", "k_ready",
                 "v_ready", "kd_ready", "scores_ready", "nmax_ready", "probs_ready", "pT_in_psum", "pT_ready", "o_in_psum", "o_ready",
                 "oT_in_psum", "oT_ready", "out_in_psum", "x_done", "chain")
        S = {n: sem(n) for n in names}
        flat = lambda ap: ap[:, :, :].rearrange("p b d -> p (b d)")
        bank = core.bank
        with nc.Block() as block:

            @block.sync
            def _(sp):
                for name, src in (("wq", wq), ("wk", wk), ("wv", wv), ("wo", wo)):
                    sp.dma_start(W[name][:, :], src).then_inc(S["w_loaded"], 16)
                sp.dma_start(g_all[:, :], across(g_row, P)).then_inc(S["w_loaded"], 16)
                sp.dma_start(b_all[:, :], across(b_row, P)).then_inc(S["w_loaded"], 16)

            @block.gpsimd
            def _(pool):
                pool.memset(head[:, :], 1.0).then_inc(S["consts_ready"], 1)
                pool.wait_ge(S["consts_ready"], 1)
                pool.affine_select(out=head[:, :], in_=head[:, :], compare_op=ALU.is_ge, fill=0.0, base=0,
                                   pattern=[[-DH, NH]], channel_multiplier=1).then_inc(S["consts_ready"], 1)
                pool.wait_ge(S["consts_ready"], 2)
                pool.affine_select(out=head[:, :], in_=head[:, :], compare_op=ALU.is_ge, fill=0.0, base=DH - 1,
                                   pattern=[[DH, NH]], channel_multiplier=-1).then_inc(S["consts_ready"], 1)

            @block.tensor
            def _(pe):
                pe.wait_ge(S["w_loaded"], 6 * 16)
                pe.sem_inc(S["x_done"], 1)
                pe.sem_inc(S["probs_ready"], 1)
                pe.sem_inc(S["o_ready"], 1)
                with pe.Fori(0, NG // 2) as i:
                    for n in range(2):
                        g = i * 2 + n
                        pe.wait_ge(S["x1_ready"], g + 1)
                        for b in range(GB):
                            mm = pe.transpose(bank[0][:, b * P:(b + 1) * P], x1[:, b, :], core.ident[:, :])
                        mm.then_inc(S["xT_in_psum"], 1)
                        pe.wait_ge(S["x_done"], g + 1)
                        pe.wait_ge(S["xT_ready"], g + 1)
                        pe.matmul(bank[1][:, :], W["wq"][:, :], flat(xT), start=True, stop=True).then_inc(S["q_in_psum"], 1)
                        pe.matmul(bank[2][:, :], W["wk"][:, :], flat(xT), start=True, stop=True).then_inc(S["k_in_psum"], 1)
                        for b in range(GB):
                            mm = pe.matmul(bank[3][:, b * P:(b + 1) * P], xT[:, b, :], W["wv"][:, :], start=True, stop=True)
                        mm.then_inc(S["v_in_psum"], 1)
                        pe.wait_ge(S["q_ready"], g + 1)
                        for b in range(GB + 1):
                            at = i * 2 * GB + n * GB + b
                            if b < GB:
                                pe.wait_ge(S["kd_ready"], at + 1)
                                pe.wait_ge(S["probs_ready"], at + 1)
                                for half in range(2):
                                    mm = pe.matmul(bank[4 + half][:, :], qT[:, b, :],
                                                   kd[b % 2][:, half * 4:half * 4 + 4, :].rearrange("p h m -> p (h m)"), start=True, stop=True)
                                mm.then_inc(S["scores_ready"], 1)
                            if b >= 1:
                                pe.wait_ge(S["probs_ready"], at + 1)
                                for h in range(NH):
                                    mm = pe.transpose(bank[6 + h // 4][0:T, h % 4 * P:(h % 4 + 1) * P], probs[(b - 1) % 2][:, h, 0:T], core.ident[:, :])
                                mm.then_inc(S["pT_in_psum"], 1)
                                pe.wait_ge(S["o_ready"], at)
                                pe.wait_ge(S["pT_ready"], at)
                                for h in range(NH):
                                    mm = pe.matmul(bank[0][:, (b - 1) * P + h * DH:(b - 1) * P + (h + 1) * DH], pT[0:T, h, :],
                                                   v[0:T, b - 1, h * DH:(h + 1) * DH], start=True, stop=True)
                                mm.then_inc(S["o_in_psum"], 1)
                        pe.wait_ge(S["o_ready"], i * 2 * GB + (n + 1) * GB + 1)
                        for b in range(GB):
                            mm = pe.transpose(bank[1][:, b * P:(b + 1) * P], o[:, b, :], core.ident[:, :])
                        mm.then_inc(S["oT_in_psum"], 1)
                        pe.wait_ge(S["oT_ready"], g + 1)
                        for b in range(GB):
                            mm = pe.matmul(bank[2][:, b * P:(b + 1) * P], oT[:, b, :], W["wo"][:, :], start=True, stop=True)
                        mm.then_inc(S["out_in_psum"], 1)

            @block.scalar
            def _(act):
                act.preload_act_table_set("exp_and_others")
                with act.Fori(0, NG // 2) as i:
                    for n in range(2):
                        g = i * 2 + n
                        for src, dst, ready, bk in (("xT_in_psum", xT, "xT_ready", 0), ("q_in_psum", qT, "q_ready", 1),
                                                    ("k_in_psum", kT, "k_ready", 2), ("v_in_psum", v, "v_ready", 3)):
                            act.wait_ge(S[src], g + 1)
                            act.copy(flat(dst), bank[bk][:, :]).then_inc(S[ready], 1)
                        for b in range(GB + 1):
                            at = i * 2 * GB + n * GB + b
                            if b >= 1:
                                act.wait_ge(S["pT_in_psum"], at)
                                act.copy(pT[0:T, :, :].rearrange("p h m -> p (h m)"), core.banks[0:T, 6 * 512:8 * 512]).then_inc(S["pT_ready"], 1)
                            if b < GB:
                                act.wait_ge(S["nmax_ready"], at + 1)
                                for h in range(NH):
                                    ex = act.activation(probs[b % 2][:, h, 0:T], bank[4 + h // 4][:, h % 4 * P:h % 4 * P + T], ACT.Exp,
                                                        bias=nmax[:, b % 2, h:h + 1], scale=SCALE, accum_out=den[:, b % 2, h:h + 1])
                                ex.then_inc(S["probs_ready"], 1)
                        act.wait_ge(S["oT_in_psum"], g + 1)
                        act.copy(flat(oT), bank[1][:, :]).then_inc(S["oT_ready"], 1)

            @block.vector
            def _(dve):
                step = Chain(dve, S["chain"])
                dve.wait_ge(S["w_loaded"], 6 * 16)
                dve.wait_ge(S["consts_ready"], 3)
                wide = lambda ap: ap[:, :].unsqueeze(1).to_broadcast([P, GB, D])
                with dve.Fori(0, NG // 2) as i:
                    step.enter(i, 2 * (1 + 2 * GB))
                    for n in range(2):
                        g = i * 2 + n
                        at3 = bass.ds(i * 2 * GB + n * GB, GB)
                        step(dve.tensor_tensor(x1[:, :, :], xn[:, at3, :], wide(g_all), ALU.mult))
                        dve.tensor_tensor(x1[:, :, :], x1[:, :, :], wide(b_all), ALU.add).then_inc(S["x1_ready"], 1)
                        dve.wait_ge(S["k_ready"], g + 1)
                        for b in range(GB + 1):
                            at = i * 2 * GB + n * GB + b
                            if b < GB:
                                dve.tensor_tensor(kd[b % 2][:, :, :], kT[:, b, :].unsqueeze(1).to_broadcast([P, NH, P]),
                                                  head[:, :].unsqueeze(2).to_broadcast([P, NH, P]), ALU.mult).then_inc(S["kd_ready"], 1)
                                dve.wait_ge(S["scores_ready"], at + 1)
                                step(dve.tensor_reduce(top[:, b % 2, :], core.banks[:, 4 * 512:6 * 512].rearrange("p (h m) -> p h m", h=NH)[:, :, 0:T], X, ALU.max))
                                dve.tensor_scalar(nmax[:, b % 2, :], top[:, b % 2, :], -SCALE, None, ALU.mult).then_inc(S["nmax_ready"], 1)
                            if b >= 1:
                                dve.wait_ge(S["o_in_psum"], at)
                                step(dve.reciprocal(rden[:, 0, :], den[:, (b - 1) % 2, :]))
                                dve.tensor_tensor(o[:, b - 1, :].rearrange("p (h d) -> p h d", h=NH), bank[0][:, (b - 1) * P:b * P].rearrange("p (h d) -> p h d", h=NH),
                                                  rden[:, 0, :].unsqueeze(2).to_broadcast([P, NH, DH]), ALU.mult).then_inc(S["o_ready"], 1)
                        dve.wait_ge(S["out_in_psum"], g + 1)
                        dve.tensor_tensor(x[:, at3, :], bank[2][:, :].rearrange("p (b d) -> p b d", b=GB), x[:, at3, :], ALU.add).then_inc(S["x_done"], 1)
                    step.leave(NG // 2)


class Dispatch:
    E, TOPK, C, CAP = 64, 2, 254, 256
    F = 512
    ROWS = E * CAP + TOPK * B * P


def route_two_of_64(core, xn, w, x2, put, take, gate, buf):
    nc = core.nc
    core.phase = "route1_"
    Z = Dispatch
    E, K = Z.E, Z.TOPK
    W = E + 8 - 1
    FAR = 1e30
    PER = 49
    with ExitStack() as c:
        sb = lambda n, s, d=F32: core.sbuf(n, s, d, c)
        sem = lambda n: core.sem(n, c)
        wr = sb("wr", [D, E])
        g_all, b_all = sb("g_all", [P, D]), sb("b_all", [P, D])
        zeros = sb("zeros", [P, D])
        before, ones = sb("before", [P, P]), sb("ones", [P, P])
        real = sb("real", [P, 1])
        base = sb("base", [P, E])
        spill = sb("spill", [P, B, K])
        sentinels = sb("sentinels", [P, 7])
        stage, xT = sb("stage", [P, GB, D]), sb("xT", [P, GB, P])
        probs, expo = sb("probs", [P, GB, W]), sb("expo", [P, GB, E])
        top, total = sb("top", [P, GB]), sb("total", [P, GB])
        best = sb("best", [P, GB, 8])
        v12 = sb("v12", [P, GB, K])
        marked = [sb(f"marked{k}", [P, GB, W]) for k in range(K)]
        sel = sb("sel", [P, GB, E])
        seen = sb("seen", [P, GB + 1, E])
        pos, row, prod = sb("pos", [P, GB, E]), sb("row", [P, GB, E]), sb("prod", [P, GB, E])
        p_k, r_k, keep, over = (sb(n, [P, GB, K]) for n in ("p_k", "r_k", "keep", "over"))
        waiter = sb("waiter", [1, 1])
        names = ("w_loaded", "zeroed", "consts_ready", "staged", "xT_in_psum", "xT_ready", "logits_ready", "shifted", "exp_ready",
                 "sel_ready", "pos_in_psum", "group_done", "chain", "pool_chain")
        S = {n: sem(n) for n in names}
        flat = lambda ap: ap[:, :, :].rearrange("p b d -> p (b d)")
        bank = core.bank
        with nc.Block() as block:

            @block.sync
            def _(sp):
                sp.dma_start(wr[:, :], w["wr"]).then_inc(S["w_loaded"], 16)
                sp.dma_start(g_all[:, :], across(w["ln2_g"], P)).then_inc(S["w_loaded"], 16)
                sp.dma_start(b_all[:, :], across(w["ln2_b"], P)).then_inc(S["w_loaded"], 16)
                sp.wait_ge(S["pool_chain"], 1)
                sp.dma_start(buf[0:E * Z.CAP, :].rearrange("(p r) d -> p r d", p=P),
                             zeros[:, :].unsqueeze(1).to_broadcast([P, E * Z.CAP // P, D])).then_inc(S["zeroed"], 16)
                sp.wait_ge(S["zeroed"], 16)

            @block.gpsimd
            def _(pool):
                step = Chain(pool, S["pool_chain"])
                step(pool.memset(zeros[:, :], 0.0))
                step(pool.memset(before[:, :], 1.0))
                step(pool.affine_select(out=before[:, :], in_=before[:, :], compare_op=ALU.is_gt, fill=0.0, base=0,
                                        pattern=[[1, P]], channel_multiplier=-1))
                step(pool.memset(ones[:, :], 1.0))
                step(pool.memset(real[:, :], 1.0))
                step(pool.affine_select(out=real[:, :], in_=real[:, :], compare_op=ALU.is_gt, fill=0.0, base=T,
                                        pattern=[[0, 1]], channel_multiplier=-1))
                step(pool.iota(base[:, :], pattern=[[Z.CAP, E]], base=0, channel_multiplier=0, allow_small_or_imprecise_dtypes=True))
                step(pool.iota(spill[:, :, :], pattern=[[K * P, B], [P, K]], base=E * Z.CAP, channel_multiplier=1, allow_small_or_imprecise_dtypes=True))
                for n in range(7):
                    step(pool.memset(sentinels[:, n:n + 1], -FAR * (n + 1)))
                pool.memset(seen[:, :, :], 0.0).then_inc(S["consts_ready"], 1)

            @block.tensor
            def _(pe):
                pe.wait_ge(S["w_loaded"], 3 * 16)
                pe.wait_ge(S["consts_ready"], 1)
                with pe.Fori(0, NG) as g:
                    pe.wait_ge(S["staged"], g + 1)
                    for b in range(GB):
                        mm = pe.transpose(bank[0][:, b * P:(b + 1) * P], stage[:, b, :], core.ident[:, :])
                    mm.then_inc(S["xT_in_psum"], 1)
                    pe.wait_ge(S["xT_ready"], g + 1)
                    for b in range(GB):
                        mm = pe.matmul(bank[1][:, b * E:(b + 1) * E], xT[:, b, :], wr[:, :], start=True, stop=True)
                    mm.then_inc(S["logits_ready"], 1)
                    pe.wait_ge(S["sel_ready"], g + 1)
                    pe.matmul(bank[2][:, 0:GB * E], before[:, :], flat(sel), start=True, stop=False)
                    pe.matmul(bank[2][:, 0:GB * E], ones[:, :], seen[:, 0:GB, :].rearrange("p b e -> p (b e)"), start=False, stop=True).then_inc(S["pos_in_psum"], 1)

            @block.scalar
            def _(act):
                act.preload_act_table_set("exp_and_others")
                with act.Fori(0, NG) as g:
                    act.wait_ge(S["xT_in_psum"], g + 1)
                    act.copy(flat(xT), bank[0][:, :]).then_inc(S["xT_ready"], 1)
                    act.wait_ge(S["shifted"], g + 1)
                    act.activation(flat(expo), flat(expo), ACT.Exp).then_inc(S["exp_ready"], 1)

            @block.vector
            def _(dve):
                step = Chain(dve, S["chain"])
                dve.wait_ge(S["w_loaded"], 3 * 16)
                dve.wait_ge(S["consts_ready"], 1)
                wide = lambda ap: ap[:, :].unsqueeze(1).to_broadcast([P, GB, D])
                each = lambda ap, n: ap.unsqueeze(2).to_broadcast([P, GB, n])
                step(dve.tensor_copy(probs[:, :, E:W], sentinels[:, :].unsqueeze(1).to_broadcast([P, GB, 7])))
                with dve.Fori(0, NG) as g:
                    step.enter(g, PER)
                    tiles = bass.ds(g * GB, GB)
                    step(dve.tensor_tensor(stage[:, :, :], xn[:, tiles, :], wide(g_all), ALU.mult))
                    dve.tensor_tensor(stage[:, :, :], stage[:, :, :], wide(b_all), ALU.add).then_inc(S["staged"], 1)
                    dve.wait_ge(S["staged"], g + 1)
                    step.tick(dve.tensor_copy(x2[:, tiles, :], stage[:, :, :]))
                    dve.wait_ge(S["logits_ready"], g + 1)
                    lg = bank[1][:, 0:GB * E].rearrange("p (b e) -> p b e", b=GB)
                    step(dve.tensor_reduce(top[:, :], lg, X, ALU.max))
                    dve.tensor_tensor(expo[:, :, :], lg, each(top[:, :], E), ALU.subtract).then_inc(S["shifted"], 1)
                    dve.wait_ge(S["exp_ready"], g + 1)
                    step(dve.tensor_reduce(total[:, :], expo[:, :, :], X, ALU.add))
                    step(dve.reciprocal(total[:, :], total[:, :]))
                    step(dve.tensor_tensor(probs[:, :, 0:E], expo[:, :, :], each(total[:, :], E), ALU.mult))
                    dve.memset(waiter[:, :], 0.0)
                    for b in range(GB):
                        step.tick(dve.max(best[:, b, :], probs[:, b, 0:E]))
                    step.settle()
                    step(dve.tensor_copy(v12[:, :, :], best[:, :, 0:K]))
                    for k in reversed(range(K)):
                        step(dve.tensor_copy(best[:, :, k + 1:8], sentinels[:, 0:7 - k].unsqueeze(1).to_broadcast([P, GB, 7 - k])))
                        dve.memset(waiter[:, :], 0.0)
                        for b in range(GB):
                            step.tick(dve.match_replace(marked[k][:, b, :], best[:, b, :], probs[:, b, :], FAR))
                        step.settle()
                    for k in range(K):
                        step.tick(dve.tensor_scalar(marked[k][:, :, 0:E], marked[k][:, :, 0:E], FAR, real[:, :], ALU.is_ge, ALU.mult))
                    step.settle()
                    step(dve.tensor_copy(sel[:, :, :], marked[1][:, :, 0:E]))
                    step.tick(dve.tensor_tensor(marked[1][:, :, 0:E], marked[1][:, :, 0:E], marked[0][:, :, 0:E], ALU.subtract))
                    for b in range(GB):
                        ins = dve.tensor_tensor(seen[:, b + 1, :], seen[:, b, :], sel[:, b, :], ALU.add)
                        if b < GB - 1:
                            step(ins)
                    ins.then_inc(S["sel_ready"], 1)
                    dve.wait_ge(S["pos_in_psum"], g + 1)
                    step.tick(dve.tensor_copy(seen[:, 0, :], seen[:, GB, :]))
                    step(dve.tensor_copy(pos[:, :, :], bank[2][:, 0:GB * E].rearrange("p (b e) -> p b e", b=GB)))
                    step(dve.tensor_tensor(row[:, :, :], pos[:, :, :], base[:, :].unsqueeze(1).to_broadcast([P, GB, E]), ALU.add))
                    for k in range(K):
                        for src, dst in ((pos, p_k), (row, r_k)):
                            step(dve.tensor_tensor(prod[:, :, :], marked[k][:, :, 0:E], src[:, :, :], ALU.mult))
                            step(dve.tensor_reduce(dst[:, :, k], prod[:, :, :], X, ALU.add))
                    step.tick(dve.tensor_scalar(keep[:, :, :], p_k[:, :, :], float(Z.C), real[:, :], ALU.is_lt, ALU.mult))
                    step(dve.tensor_scalar(over[:, :, :], p_k[:, :, :], float(1 - Z.C), 0.0, ALU.add, ALU.max))
                    step(dve.tensor_tensor(take[:, tiles, :], r_k[:, :, :], over[:, :, :], ALU.subtract))
                    step(dve.tensor_tensor(r_k[:, :, :], r_k[:, :, :], spill[:, tiles, :], ALU.subtract))
                    step(dve.tensor_tensor(r_k[:, :, :], r_k[:, :, :], keep[:, :, :], ALU.mult))
                    step(dve.tensor_tensor(put[:, tiles, :], r_k[:, :, :], spill[:, tiles, :], ALU.add))
                    step(dve.tensor_tensor(total[:, :], v12[:, :, 0], v12[:, :, 1], ALU.add))
                    step(dve.reciprocal(total[:, :], total[:, :]))
                    step(dve.tensor_tensor(v12[:, :, :], v12[:, :, :], each(total[:, :], K), ALU.mult))
                    step(dve.tensor_tensor(gate[:, tiles, :], v12[:, :, :], keep[:, :, :], ALU.mult))
                    step.leave(NG)


def experts_dispatched(core, x, x2, put, take, gate, w, buf, results):
    nc = core.nc
    core.phase = "experts1_"
    Z = Dispatch
    E, K, F = Z.E, Z.TOPK, Z.F
    FC = F // P
    R = Z.CAP // P
    with ExitStack() as c:
        sb = lambda n, s, d=F32: core.sbuf(n, s, d, c)
        sem = lambda n: core.sem(n, c)
        put_i, take_i = sb("put_i", [P, B, K], U32), sb("take_i", [P, B, K], U32)
        b1, b1T = sb("b1", [E, F]), sb("b1T", [P, FC, E])
        b2 = sb("b2", [1, E * D])
        ones = sb("ones", [1, P])
        w1 = [sb(f"w1_{n}", [D, F]) for n in range(2)]
        w2 = [sb(f"w2_{n}", [P, FC, D]) for n in range(2)]
        xe = [sb(f"xe{n}", [P, R, D]) for n in range(2)]
        xT = [sb(f"xT{n}", [D, R * P]) for n in range(2)]
        hT = [sb(f"hT{n}", [P, FC, R * P]) for n in range(2)]
        y = [sb(f"y{n}", [P, R, D]) for n in range(2)]
        back = [sb(f"back{n}", [P, K, D]) for n in range(4)]
        names = ("consts_loaded", "index_ready", "scattered", "b1T_in_psum", "b1T_ready", "ones_ready", "xT_in_psum", "xT_ready",
                 "up_in_psum", "h_ready", "y_in_psum", "y_ready", "chain")
        S = {n: sem(n) for n in names}
        w_loaded = [sem(f"w_loaded{n}") for n in range(2)]
        x_loaded = [sem(f"x_loaded{n}") for n in range(2)]
        y_stored = [sem(f"y_stored{n}") for n in range(2)]
        gathered = [sem(f"gathered{n}") for n in range(4)]
        bank = core.bank
        with nc.Block() as block:

            @block.gpsimd
            def _(pool):
                pool.wait_ge(S["index_ready"], 2)
                for b in range(B):
                    for k in range(K):
                        pool.indirect_dma_start(out=buf, out_offset=bass.IndirectOffsetOnAxis(ap=put_i[:, b, k:k + 1], axis=0),
                                                in_=x2[:, b, :], in_offset=None).then_inc(S["scattered"], 16)

            @block.sync
            def _(sp):
                sp.dma_start(b1[:, :], w["b1"]).then_inc(S["consts_loaded"], 16)
                sp.dma_start(b2[:, :], w["b2"].rearrange("(a e) d -> a (e d)", a=1)).then_inc(S["consts_loaded"], 16)

                def load_w(e, n):
                    sp.dma_start(w1[n][:, :], w["w1"][bass.ds(e, 1), :, :].rearrange("e c f -> (e c) f")).then_inc(w_loaded[n], 16)
                    sp.dma_start(w2[n][:, :, :], w["w2"][bass.ds(e, 1), :, :].rearrange("e (k f) c -> (e f) k c", k=FC)).then_inc(w_loaded[n], 16)

                def load_x(e, n):
                    sp.dma_start(xe[n][:, :, :], buf[bass.ds(e * Z.CAP, Z.CAP), :].rearrange("(p r) d -> p r d", r=R)).then_inc(x_loaded[n], 16)

                def store(e, n):
                    sp.wait_ge(S["y_ready"], e + 1)
                    sp.dma_start(results[bass.ds(e * Z.CAP, Z.CAP), :].rearrange("(p r) d -> p r d", r=R), y[n][:, :, :]).then_inc(y_stored[n], 16)

                for n in range(2):
                    sp.sem_inc(y_stored[n], 16)
                    load_w(n, n)
                sp.wait_ge(S["scattered"], 16 * B * K)
                for n in range(2):
                    load_x(n, n)
                with sp.Fori(0, E // 2 - 1) as i:
                    for n in range(2):
                        store(i * 2 + n, n)
                        load_w(i * 2 + n + 2, n)
                        load_x(i * 2 + n + 2, n)
                for n in range(2):
                    store(E - 2 + n, n)
                for n in range(2):
                    sp.wait_ge(y_stored[n], 16 * (E // 2 + 1))

            @block.tensor
            def _(pe):
                pe.wait_ge(S["consts_loaded"], 32)
                for k in range(FC):
                    mm = pe.transpose(bank[0][:, k * E:(k + 1) * E], b1[:, k * P:(k + 1) * P], core.ident[0:E, 0:E])
                mm.then_inc(S["b1T_in_psum"], 1)
                pe.wait_ge(S["b1T_ready"], 1)
                pe.wait_ge(S["ones_ready"], 1)
                with pe.Fori(0, E // 2) as i:
                    for n in range(2):
                        e = i * 2 + n
                        pe.wait_ge(x_loaded[n], i * 16 + 16)
                        for r in range(R):
                            mm = pe.transpose(bank[n][:, r * P:(r + 1) * P], xe[n][:, r, :], core.ident[:, :])
                        mm.then_inc(S["xT_in_psum"], 1)
                        pe.wait_ge(w_loaded[n], i * 32 + 32)
                        pe.wait_ge(S["xT_ready"], e + 1)
                        for k in range(FC):
                            mm = pe.matmul(bank[2 + 2 * n + k // 2][:, k % 2 * R * P:(k % 2 + 1) * R * P], w1[n][:, k * P:(k + 1) * P], xT[n][:, :],
                                           start=True, stop=True)
                            if k % 2 == 1:
                                mm.then_inc(S["up_in_psum"], 1)
                        for r in range(R):
                            pe.matmul(bank[6 + n][:, r * D:(r + 1) * D], ones[:, :], b2[:, bass.ds(e * D, D)], start=True, stop=False)
                            if r == 0:
                                pe.wait_ge(S["h_ready"], e + 1)
                            for k in range(FC):
                                mm = pe.matmul(bank[6 + n][:, r * D:(r + 1) * D], hT[n][:, k, r * P:(r + 1) * P], w2[n][:, k, :],
                                               start=False, stop=(k == FC - 1))
                        mm.then_inc(S["y_in_psum"], 1)

            @block.scalar
            def _(act):
                act.wait_ge(S["b1T_in_psum"], 1)
                act.copy(b1T[:, :, :].rearrange("p k e -> p (k e)"), bank[0][:, 0:FC * E]).then_inc(S["b1T_ready"], 1)
                act.wait_ge(S["b1T_ready"], 1)
                with act.Fori(0, E // 2) as i:
                    for n in range(2):
                        e = i * 2 + n
                        for k in range(FC):
                            act.wait_ge(S["up_in_psum"], i * 4 + n * 2 + k // 2 + 1)
                            ac = act.activation(hT[n][:, k, :], bank[2 + 2 * n + k // 2][:, k % 2 * R * P:(k % 2 + 1) * R * P], ACT.Gelu_apprx_tanh,
                                                bias=b1T[:, k, bass.ds(e, 1)])
                        ac.then_inc(S["h_ready"], 1)

            @block.vector
            def _(dve):
                dve.tensor_copy(put_i[:, :, :], put[:, :, :]).then_inc(S["index_ready"], 1)
                dve.tensor_copy(take_i[:, :, :], take[:, :, :]).then_inc(S["index_ready"], 1)
                dve.memset(ones[:, :], 1.0).then_inc(S["ones_ready"], 1)
                with dve.Fori(0, E // 2) as i:
                    for n in range(2):
                        e = i * 2 + n
                        dve.wait_ge(S["xT_in_psum"], e + 1)
                        dve.tensor_copy(xT[n][:, :], bank[n][:, 0:R * P]).then_inc(S["xT_ready"], 1)
                        dve.wait_ge(y_stored[n], i * 16 + 16)
                        dve.wait_ge(S["y_in_psum"], e + 1)
                        dve.tensor_copy(y[n][:, :, :].rearrange("p r d -> p (r d)"), bank[6 + n][:, 0:R * D]).then_inc(S["y_ready"], 1)

        with nc.Block() as block:

            @block.gpsimd
            def _(pool):
                for b in range(B):
                    if b >= 4:
                        pool.wait_ge(S["chain"], 3 * (b - 3))
                    for k in range(K):
                        pool.indirect_dma_start(out=back[b % 4][:, k, :], out_offset=None, in_=results,
                                                in_offset=bass.IndirectOffsetOnAxis(ap=take_i[:, b, k:k + 1], axis=0)).then_inc(gathered[b % 4], 16)

            @block.vector
            def _(dve):
                step = Chain(dve, S["chain"])
                for b in range(B):
                    step(dve.tensor_tensor(core.hidden[:, b, :], core.hidden[:, b, :], x[:, b, :], ALU.add))
                    dve.wait_ge(gathered[b % 4], 32 * (b // 4 + 1))
                    for k in range(K):
                        step(dve.scalar_tensor_tensor(out=core.hidden[:, b, :], in0=back[b % 4][:, k, :], scalar=gate[:, b, k:k + 1],
                                                      in1=core.hidden[:, b, :], op0=ALU.mult, op1=ALU.add))


def audio_tower(nc, w, out):
    l1 = {k[len("L1_attn_"):]: v for k, v in w.items() if k.startswith("L1_attn_")}
    record = nc.dram_tensor("record", (P, B, ScanShapes.F), F32, kind="Internal").ap()
    record_part = nc.dram_tensor("record_part", (P, ScanShapes.J, B, 2 * ScanShapes.V), F32, kind="Internal").ap()
    reads = nc.dram_tensor("reads", (P, ScanShapes.J, B, ScanShapes.V), F32, kind="Internal").ap()
    states = nc.dram_tensor("states", (P, B, ScanShapes.H), F32, kind="Internal").ap()
    buf = nc.dram_tensor("dispatched", (Dispatch.ROWS, D), F32, kind="Internal").ap()
    results = nc.dram_tensor("results", (Dispatch.E * Dispatch.CAP, D), F32, kind="Internal").ap()
    with ExitStack() as ctx:
        core = Core(nc, ctx)
        embed_patches(core, w["x"], w["L0_tok_W"], w["L0_tok_b"])
        with ExitStack() as c:
            core.phase = ""
            xn = core.sbuf("xn", [P, B, D], F32, c)
            with ExitStack() as cc:
                sq = core.sbuf("sq", [P, B, D], F32, cc)
                normalize(core, "ln0", core.hidden, xn, sq)
                channel_attention(core, xn, w["L0_attn_W_qkv"], w["L0_attn_W_o"])
                normalize(core, "ln1", core.hidden, xn, sq)
            with ExitStack() as cc:
                core.phase = ""
                combine = core.sbuf("combine", [P, B, 64], F32, cc)
                route_six_of_64(core, xn, combine, w["L0_ffn_router_w"], w["L0_ffn_bias_corr"])
                experts_dense(core, xn, combine, w["L0_ffn_Wg"], w["L0_ffn_Wu"], w["L0_ffn_Wd"], w["L0_ffn_sWg"],
                              w["L0_ffn_sWu"], w["L0_ffn_sWd"])
            with ExitStack() as cc:
                core.phase = ""
                sq = core.sbuf("sq2", [P, B, D], F32, cc)
                normalize(core, "ln2", core.hidden, xn, sq)
            scan_inputs(core, xn, l1, record_part, record)
        scan_tokens(core, l1, record_part, record, reads, states)
        scan_outputs(core, l1, reads, states)
        l1f = {k[len("L1_ffn_"):]: v for k, v in w.items() if k.startswith("L1_ffn_")}
        with ExitStack() as c:
            core.phase = ""
            x = core.sbuf("x", [P, B, D], F32, c)
            x2 = core.sbuf("x2", [P, B, D], F32, c)
            put, take, gate = (core.sbuf(n, [P, B, Dispatch.TOPK], F32, c) for n in ("put", "take", "gate"))
            with ExitStack() as cc:
                x1 = core.sbuf("x1", [P, B, D], F32, cc)
                normalize(core, "ln3", core.hidden, x, x2)
                normalize(core, "ln4", x, x1, x2)
                self_attention(core, x, x1, l1f["ln1_g"], l1f["ln1_b"], l1f["wq"], l1f["wk"], l1f["wv"], l1f["wo"])
                normalize(core, "ln5", x, x1, x2)
                route_two_of_64(core, x1, l1f, x2, put, take, gate, buf)
            experts_dispatched(core, x, x2, put, take, gate, l1f, buf, results)
        store_hidden(core, out)


def kernel(**inputs):
    import numpy as _np
    import concourse.bacc as _bacc
    from concourse import mybir as _mybir
    from concourse.bass_utils import run_bass_kernel_spmd as _run

    nc = _bacc.Bacc("TRN2", target_bir_lowering=False, num_devices=1)
    arrays, aps = {}, {}
    for name, value in inputs.items():
        a = _np.ascontiguousarray(value)
        arrays[f"in_{name}_dram"] = a
        aps[name] = nc.dram_tensor(f"in_{name}_dram", a.shape, _mybir.dt.from_np(a.dtype), kind="ExternalInput").ap()
    out = nc.dram_tensor("out_0_dram", (32, 127, 128), _mybir.dt.float32, kind="ExternalOutput").ap()
    audio_tower(nc, aps, out)
    r = _run(nc, [arrays], core_ids=[0])
    return r.results[0]["out_0_dram"]
```

```python
from contextlib import ExitStack

import concourse.bass as bass
from concourse import mybir

F32 = mybir.dt.float32
U32 = mybir.dt.uint32
I32 = mybir.dt.int32
ALU = mybir.AluOpType
ACT = mybir.ActivationFunctionType
X = mybir.AxisListType.X

P = 128
B = 32
T = 127
D = 128
GB = 4
NG = B // GB
EPS = 1e-5


class Chain:

    def __init__(self, eng, sem):
        self.eng, self.sem = eng, sem
        self.done, self.k, self.i, self.per = 0, 0, None, 0

    def enter(self, i, per):
        self.done += self.k
        self.i, self.per, self.k = i, per, 0

    def leave(self, times):
        assert self.k == self.per, (self.k, self.per)
        self.done += self.per * times
        self.i, self.per, self.k = None, 0, 0

    def value(self):
        return self.done + self.k + (0 if self.i is None else self.i * self.per)

    def tick(self, ins):
        self.k += 1
        ins.then_inc(self.sem, 1)

    def settle(self):
        self.eng.wait_ge(self.sem, self.value())

    def __call__(self, ins):
        self.tick(ins)
        self.settle()


class Core:

    def __init__(self, nc, ctx):
        self.nc, self.ctx, self.phase, self.sems = nc, ctx, "", []
        self.banks = self.psum("banks", [P, 8 * 512])
        self.bank = [self.banks[:, n * 512:(n + 1) * 512] for n in range(8)]
        self.hidden = self.sbuf("hidden", [P, B, D])
        self.ident = self.sbuf("ident", [P, P])
        self.minus_half = self.sbuf("minus_half", [P, B])

    def sbuf(self, name, shape, dt=F32, ctx=None):
        return (ctx or self.ctx).enter_context(self.nc.sbuf_tensor(self.phase + name, shape, dt))

    def psum(self, name, shape, dt=F32):
        return self.ctx.enter_context(self.nc.psum_tensor(name, shape, dt))

    def sem(self, name, ctx):
        if not self.sems:
            ctx.callback(self.clear_sems)
        self.sems.append(self.nc.alloc_semaphore(self.phase + name))
        return self.sems[-1]

    def clear_sems(self):
        self.nc.clear_and_free_semaphores(self.sems)
        self.nc.all_engine_barrier()
        self.sems = []


def across(ap, n):
    return ap.rearrange("(a d) -> a d", a=1).to_broadcast([n, ap.shape[0]])


def embed_patches(core, x, W, bias):
    nc = core.nc
    core.phase = "embed_"
    BLK = 8 * 32
    with ExitStack() as c:
        sb = lambda n, s, d=F32: core.sbuf(n, s, d, c)
        sem = lambda n: core.sem(n, c)
        w = sb("tok_w", [P, 4 * P])
        wT = sb("tok_wT", [P, 4, P])
        bias_all = sb("tok_bias", [P, D])
        xin = [sb(f"xin{n}", [P, GB, BLK]) for n in range(2)]
        xT = sb("xT", [P, 2, GB, P + 1])
        consts_ready, w_loaded = sem("consts_ready"), sem("tok_w_loaded")
        x_loaded = [sem(f"x_loaded{n}") for n in range(2)]
        x_free, xT_in_psum, xT_ready = sem("x_free"), sem("xT_in_psum"), sem("xT_ready")
        tok_done, acc_free, wT_in_psum, wT_ready = sem("tok_done"), sem("acc_free"), sem("wT_in_psum"), sem("wT_ready")
        pad_ready = sem("pad_ready")
        xg = x.rearrange("b (p r) c -> p b (r c)", r=8)
        with nc.Block() as block:

            @block.sync
            def _(sp):
                sp.dma_start(w[:, :], W).then_inc(w_loaded, 16)
                sp.dma_start(bias_all[:, :], across(bias, P)).then_inc(w_loaded, 16)
                for n in range(2):
                    sp.dma_start(xin[n][:, :, :], xg[:, n * GB:(n + 1) * GB, :]).then_inc(x_loaded[n], 16)
                with sp.Fori(0, NG // 2 - 1) as i:
                    for n in range(2):
                        sp.wait_ge(xT_in_psum, i * 2 + n + 1)
                        sp.dma_start(xin[n][:, :, :], xg[:, bass.ds(i * 2 * GB + (n + 2) * GB, GB), :]).then_inc(x_loaded[n], 16)

            @block.gpsimd
            def _(pool):
                pool.memset(core.ident[:, :], 0.0).then_inc(consts_ready, 1)
                pool.wait_ge(consts_ready, 1)
                pool.affine_select(out=core.ident[:, :], in_=core.ident[:, :], compare_op=ALU.not_equal, fill=1.0,
                                   base=0, pattern=[[-1, P]], channel_multiplier=1).then_inc(consts_ready, 1)
                pool.memset(core.minus_half[:, :], -0.5).then_inc(pad_ready, 1)
                pool.memset(xT[:, :, :, P:P + 1], 0.0).then_inc(pad_ready, 1)

            @block.tensor
            def _(pe):
                pe.wait_ge(consts_ready, 2)
                pe.wait_ge(w_loaded, 32)
                for k in range(4):
                    mm = pe.transpose(core.bank[0][:, k * P:(k + 1) * P], w[:, k * P:(k + 1) * P], core.ident[:, :])
                mm.then_inc(wT_in_psum, 1)
                pe.wait_ge(wT_ready, 1)
                pe.sem_inc(acc_free, 2)
                with pe.Fori(0, NG // 2) as i:
                    for n in range(2):
                        pe.wait_ge(x_loaded[n], i * 16 + 16)
                        for half in range(2):
                            for b in range(GB):
                                mm = pe.transpose(core.bank[half][:, b * P:(b + 1) * P],
                                                  xin[n][:, b, half * P:(half + 1) * P], core.ident[:, :])
                        mm.then_inc(xT_in_psum, 1)
                        pe.wait_ge(xT_ready, i * 2 + n + 1)
                        pe.wait_ge(acc_free, i * 2 + n + 1)
                        for b in range(GB):
                            for k in range(4):
                                mm = pe.matmul(core.bank[2 + n][:, b * P:(b + 1) * P],
                                               xT[:, k % 2, b, k // 2:k // 2 + P], wT[:, k, :],
                                               start=(k == 0), stop=(k == 3))
                        mm.then_inc(tok_done, 1)

            @block.scalar
            def _(act):
                act.wait_ge(wT_in_psum, 1)
                act.copy(wT[:, :, :].rearrange("p k d -> p (k d)"), core.bank[0][:, :]).then_inc(wT_ready, 1)
                act.wait_ge(pad_ready, 2)
                with act.Fori(0, NG // 2) as i:
                    for n in range(2):
                        act.wait_ge(xT_in_psum, i * 2 + n + 1)
                        for half in range(2):
                            cp = act.copy(xT[:, half, :, 0:P], core.bank[half][:, :].rearrange("p (b t) -> p b t", b=GB))
                        cp.then_inc(xT_ready, 1)

            @block.vector
            def _(dve):
                with dve.Fori(0, NG // 2) as i:
                    for n in range(2):
                        dve.wait_ge(tok_done, i * 2 + n + 1)
                        dve.tensor_tensor(core.hidden[:, bass.ds(i * 2 * GB + n * GB, GB), :],
                                          core.bank[2 + n][:, :].rearrange("p (b d) -> p b d", b=GB),
                                          bias_all[:, :].unsqueeze(1).to_broadcast([P, GB, D]),
                                          ALU.add).then_inc(acc_free, 1)


def normalize(core, name, src, out, sq):
    nc = core.nc
    core.phase = name + "_"
    with ExitStack() as c:
        mean = core.sbuf("mean", [P, B], F32, c)
        rstd = core.sbuf("rstd", [P, B], F32, c)
        chain = core.sem("chain", c)
        centred, squared, var_ready, rstd_ready = (core.sem(s, c) for s in ("centred", "squared", "var", "rstd"))
        with nc.Block() as block:

            @block.vector
            def _(dve):
                step = Chain(dve, chain)
                step(dve.tensor_reduce(mean[:, :], src[:, :, :], X, ALU.add))
                step(dve.tensor_scalar(mean[:, :], mean[:, :], 1.0 / D, None, ALU.mult))
                dve.tensor_tensor(out[:, :, :], src[:, :, :], mean[:, :].unsqueeze(2).to_broadcast([P, B, D]),
                                  ALU.subtract).then_inc(centred, 1)
                dve.wait_ge(squared, 1)
                step(dve.tensor_reduce(rstd[:, :], sq[:, :, :], X, ALU.add))
                dve.tensor_scalar(rstd[:, :], rstd[:, :], 1.0 / D, EPS, ALU.mult, ALU.add).then_inc(var_ready, 1)
                dve.wait_ge(rstd_ready, 1)
                step(dve.tensor_tensor(out[:, :, :], out[:, :, :], rstd[:, :].unsqueeze(2).to_broadcast([P, B, D]), ALU.mult))

            @block.scalar
            def _(act):
                act.wait_ge(centred, 1)
                act.activation(sq[:, :, :], out[:, :, :], ACT.Square).then_inc(squared, 1)

            @block.gpsimd
            def _(pool):
                pool.wait_ge(var_ready, 1)
                pool.tensor_tensor(rstd[:, :], rstd[:, :], core.minus_half[:, :], ALU.pow).then_inc(rstd_ready, 1)


def store_hidden(core, out):
    nc = core.nc
    with ExitStack() as c:
        stored = core.sem("stored", c)
        with nc.Block() as block:

            @block.sync
            def _(sp):
                sp.dma_start(out.rearrange("b t d -> t b d"), core.hidden[0:T, :, :]).then_inc(stored, 16)
                sp.wait_ge(stored, 16)


def channel_attention(core, xn, W_qkv, W_o, cleared):
    nc = core.nc
    core.phase = "attn0_"
    DK = 16
    R = 48
    SCALE = DK ** -0.5
    CH = 4 * P
    with ExitStack() as c:
        sb = lambda n, s, d=F32: core.sbuf(n, s, d, c)
        sem = lambda n: core.sem(n, c)
        wqkv = sb("wqkv", [P, 3 * DK])
        wq2, wk2 = sb("wq2", [P, R]), sb("wk2", [P, R])
        wo = sb("wo", [DK, D])
        chan = sb("chan", [P, DK])
        x_stage = [sb(f"x_stage{n}", [P, GB, D]) for n in range(2)]
        xT = sb("xT", [P, GB, P])
        kT = sb("kT", [P, GB, P])
        qT = sb("qT", [P, GB, P])
        v = sb("v", [P, GB, DK])
        kmax, kmin = sb("kmax", [R, GB]), sb("kmin", [R, GB])
        top = sb("top", [R, GB, P])
        qd = [sb(f"qd{n}", [P, DK, P]) for n in range(2)]
        vd = [sb(f"vd{n}", [P, DK, R]) for n in range(2)]
        probs = [sb(f"probs{n}", [P, DK, P]) for n in range(2)]
        rden = sb("rden", [DK, P])
        sa = sb("sa", [DK, GB, P])
        zeros = sb("zeros", [P, D])
        zeros_ready, zeros_stored = sem("zeros_ready"), sem("zeros_stored")
        (w_loaded, consts_ready, w_ready, staged, xT_in_psum, xT_ready, q_in_psum, k_in_psum, v_in_psum, qk_copied,
         v_copied, qd_ready, scores_ready, probs_ready, sums_ready, sa_ready, out_in_psum,
         hidden_added, chain_sem) = (sem(n) for n in (
            "w_loaded", "consts_ready", "w_ready", "staged", "xT_in_psum", "xT_ready", "q_in_psum", "k_in_psum", "v_in_psum",
            "qk_copied", "v_copied", "qd_ready", "scores_ready", "probs_ready",
            "sums_ready", "sa_ready", "out_in_psum", "hidden_added", "chain"))
        xT_ps, q_ps, k_ps, sum_ps = core.bank[0], core.bank[1], core.bank[2], core.bank[3]
        v_ps, out_ps = xT_ps, q_ps
        with nc.Block() as block:

            @block.sync
            def _(sp):
                sp.dma_start(wqkv[:, :], W_qkv).then_inc(w_loaded, 16)
                sp.dma_start(wo[:, :], W_o).then_inc(w_loaded, 16)
                sp.wait_ge(zeros_ready, 1)
                for rows in cleared:
                    n = rows.shape[0] // P
                    sp.dma_start(rows.rearrange("(p r) d -> p r d", p=P), zeros[:, :].unsqueeze(1).to_broadcast([P, n, D])).then_inc(zeros_stored, 16)
                sp.wait_ge(zeros_stored, 16 * len(cleared))

            @block.gpsimd
            def _(pool):
                pool.memset(zeros[:, :], 0.0).then_inc(zeros_ready, 1)
                pool.memset(chan[:, :], 0.0).then_inc(consts_ready, 1)
                pool.wait_ge(consts_ready, 1)
                for n, base in enumerate((0, -32)):
                    pool.affine_select(out=chan[:, :], in_=chan[:, :], compare_op=ALU.not_equal, fill=1.0,
                                       base=base, pattern=[[-1, DK]], channel_multiplier=1).then_inc(consts_ready, 1)
                    pool.wait_ge(consts_ready, 2 + n)
                pool.memset(qT[:, :, :], 0.0).then_inc(consts_ready, 1)
                pool.memset(kT[:, :, :], -1.0).then_inc(consts_ready, 1)
                for n in range(2):
                    pool.memset(vd[n][:, :, 0:32], 0.0).then_inc(consts_ready, 1)
                    pool.memset(vd[n][:, :, 32:R], 0.0).then_inc(consts_ready, 1)
                pool.wait_ge(consts_ready, 9)
                for n in range(2):
                    flat = vd[n][:, :, :].rearrange("p c r -> p (c r)")
                    pool.memset(flat[:, 32::R + 1], 1.0).then_inc(consts_ready, 1)

            @block.tensor
            def _(pe):
                pe.sem_inc(v_copied, 1)
                pe.sem_inc(hidden_added, 1)
                pe.sem_inc(sa_ready, 1)
                pe.sem_inc(probs_ready, 2)
                pe.wait_ge(w_ready, 4)
                with pe.Fori(0, NG // 2) as i:
                    for g in range(2):
                        pe.wait_ge(staged, i * 2 + g + 1)
                        pe.wait_ge(v_copied, i * 2 + g + 1)
                        for b in range(GB):
                            mm = pe.transpose(xT_ps[:, b * P:(b + 1) * P], x_stage[g][:, b, :], core.ident[:, :])
                        mm.then_inc(xT_in_psum, 1)
                        pe.wait_ge(hidden_added, i * 2 + g + 1)
                        pe.wait_ge(xT_ready, i * 2 + g + 1)
                        rhs = xT[:, :, :].rearrange("p b t -> p (b t)")
                        pe.matmul(q_ps[0:R, :], wq2[:, :], rhs, start=True, stop=True).then_inc(q_in_psum, 1)
                        pe.matmul(k_ps[0:R, :], wk2[:, :], rhs, start=True, stop=True).then_inc(k_in_psum, 1)
                        for b in range(GB):
                            mm = pe.matmul(v_ps[:, b * DK:(b + 1) * DK], xT[:, b, :], wqkv[:, 2 * DK:3 * DK],
                                           start=True, stop=True)
                        mm.then_inc(v_in_psum, 1)
                        for b in range(GB + 1):
                            at = i * 2 * GB + g * GB + b
                            if b < GB:
                                pe.wait_ge(qd_ready, at + 1)
                                for half in range(2):
                                    pe.wait_ge(probs_ready, at * 2 + half + 1)
                                    for n in range(2):
                                        ch = half * 8 + n * 4
                                        mm = pe.matmul(core.bank[4 + 2 * half + n][0:T, :], kT[:, b, 0:T],
                                                       qd[b % 2][:, ch:ch + 4, :].rearrange("r c n -> r (c n)"),
                                                       start=True, stop=True)
                                    mm.then_inc(scores_ready, 1)
                            if b >= 1:
                                for half in range(2):
                                    pe.wait_ge(probs_ready, at * 2 + half + 1)
                                    if half == 0:
                                        pe.wait_ge(sa_ready, at)
                                    for ch in range(half * 8, half * 8 + 8):
                                        mm = pe.matmul(sum_ps[0:R, (b - 1) * P:b * P], vd[(b - 1) % 2][0:T, ch, :],
                                                       probs[(b - 1) % 2][0:T, ch, :], start=(ch == 0), stop=(ch == DK - 1))
                                mm.then_inc(sums_ready, 1)
                        pe.wait_ge(sa_ready, i * 2 * GB + (g + 1) * GB + 1)
                        for b in range(GB):
                            mm = pe.matmul(out_ps[:, b * P:(b + 1) * P], sa[:, b, :], wo[:, :], start=True, stop=True)
                        mm.then_inc(out_in_psum, 1)

            @block.scalar
            def _(act):
                with act.Fori(0, NG // 2) as i:
                    for g in range(2):
                        act.wait_ge(xT_in_psum, i * 2 + g + 1)
                        act.copy(xT[:, :, :].rearrange("p b t -> p (b t)"), xT_ps[:, :]).then_inc(xT_ready, 1)
                        act.wait_ge(q_in_psum, i * 2 + g + 1)
                        act.wait_ge(consts_ready, 11)
                        act.copy(qT[0:DK, :, :].rearrange("p b t -> p (b t)"), q_ps[0:DK, :]).then_inc(qk_copied, 1)
                        act.wait_ge(k_in_psum, i * 2 + g + 1)
                        act.copy(kT[0:DK, :, :].rearrange("p b t -> p (b t)"), k_ps[0:DK, :]).then_inc(qk_copied, 1)
                        act.wait_ge(v_in_psum, i * 2 + g + 1)
                        act.copy(v[:, :, :].rearrange("p b c -> p (b c)"), v_ps[:, 0:GB * DK]).then_inc(v_copied, 1)
                        for b in range(GB):
                            at = i * 2 * GB + g * GB + b
                            for half in range(2):
                                act.wait_ge(scores_ready, at * 2 + half + 1)
                                act.activation(probs[b % 2][0:T, half * 8:half * 8 + 8, :].rearrange("p c n -> p (c n)"),
                                               core.banks[0:T, (4 + 2 * half) * 512:(6 + 2 * half) * 512],
                                               ACT.Exp, scale=SCALE).then_inc(probs_ready, 1)

            @block.vector
            def _(dve):
                step = Chain(dve, chain_sem)
                dve.memset(wq2[:, :], 0.0).then_inc(w_ready, 1)
                dve.memset(wk2[:, :], 0.0).then_inc(w_ready, 1)
                dve.wait_ge(w_loaded, 32)
                dve.wait_ge(w_ready, 2)
                for w, col in ((wq2, 0), (wk2, DK)):
                    dve.tensor_copy(w[:, :].rearrange("p (a c) -> p a c", c=DK)[:, 0::2, :],
                                    wqkv[:, col:col + DK].unsqueeze(1).to_broadcast([P, 2, DK])).then_inc(w_ready, 1)
                with dve.Fori(0, NG // 2) as i:
                    step.enter(i, 2 * (5 + GB))
                    for g in range(2):
                        dve.tensor_copy(x_stage[g][:, :, :], xn[:, bass.ds(i * 2 * GB + g * GB, GB), :]).then_inc(staged, 1)
                        lo, hi = 32, R
                        q3 = q_ps[lo:hi, :].rearrange("p (b t) -> p b t", b=GB)
                        k3 = k_ps[lo:hi, :].rearrange("p (b t) -> p b t", b=GB)
                        dve.wait_ge(qk_copied, i * 4 + 2 * g + 2)
                        step.tick(dve.tensor_reduce(kmax[lo:hi, :], k3[:, :, 0:T], X, ALU.max))
                        step(dve.tensor_reduce(kmin[lo:hi, :], k3[:, :, 0:T], X, ALU.min))
                        step.tick(dve.tensor_tensor(top[lo:hi, :, :], q3, kmax[lo:hi, :].unsqueeze(2).to_broadcast([DK, GB, P]), ALU.mult))
                        step(dve.tensor_tensor(qT[lo:hi, :, :], q3, kmin[lo:hi, :].unsqueeze(2).to_broadcast([DK, GB, P]), ALU.mult))
                        step(dve.tensor_tensor(qT[lo:hi, :, :], qT[lo:hi, :, :], top[lo:hi, :, :], ALU.max))
                        dve.wait_ge(v_copied, i * 2 + g + 2)
                        for b in range(GB + 1):
                            at = i * 2 * GB + g * GB + b
                            if b < GB:
                                dve.tensor_copy(vd[b % 2][:, :, :].rearrange("p c r -> p (c r)")[:, 0::R + 1], v[:, b, :])
                                dve.tensor_tensor(qd[b % 2][:, :, :], qT[:, b, :].unsqueeze(1).to_broadcast([P, DK, P]),
                                                  chan[:, :].unsqueeze(2).to_broadcast([P, DK, P]), ALU.mult).then_inc(qd_ready, 1)
                            if b >= 1:
                                dve.wait_ge(sums_ready, at)
                                step(dve.reciprocal(rden[:, :], sum_ps[32:R, (b - 1) * P:b * P]))
                                dve.tensor_tensor(sa[:, b - 1, :], sum_ps[0:DK, (b - 1) * P:b * P], rden[:, :],
                                                  ALU.mult).then_inc(sa_ready, 1)
                        dve.wait_ge(out_in_psum, i * 2 + g + 1)
                        hid = core.hidden[:, bass.ds(i * 2 * GB + g * GB, GB), :]
                        dve.tensor_tensor(hid, out_ps[:, :].rearrange("p (b d) -> p b d", b=GB), hid, ALU.add).then_inc(hidden_added, 1)
                    step.leave(NG // 2)


def route_six_of_64(core, xn, combine, router_w, bias_corr, loads, cleared):
    nc = core.nc
    core.phase = "route0_"
    E, G, TG, TOPK = 64, 8, 4, 6
    EPG = E // G
    W = E + 8 - TOPK
    FAR = 1e30
    with ExitStack() as c:
        sb = lambda n, s, d=F32: core.sbuf(n, s, d, c)
        sem = lambda n: core.sem(n, c)
        rw, rwT = sb("rw", [E, D]), sb("rwT", [D, E])
        bias = sb("bias", [P, E])
        lower = sb("lower", [P, G, G])
        sentinels = sb("sentinels", [P, 8 - TOPK])
        stage, xT = sb("stage", [P, GB, D]), sb("xT", [P, GB, P])
        expo, scores, biased = (sb(n, [P, GB, E]) for n in ("expo", "scores", "biased"))
        gs, rank, gmask, penalty = (sb(n, [P, GB, G]) for n in ("gs", "rank", "gmask", "penalty"))
        beats, ties = sb("beats", [P, GB, G, G]), sb("ties", [P, GB, G, G])
        masked, marked = sb("masked", [P, GB, W]), sb("marked", [P, GB, W])
        best = sb("best", [P, GB, 8])
        total = sb("total", [P, GB])
        waiter = sb("waiter", [1, 1])
        (w_loaded, consts_ready, rwT_in_psum, rwT_ready, staged, xT_in_psum, xT_ready, logits_ready, exp_ready,
         chain_sem, later_loaded) = (sem(n) for n in ("w_loaded", "consts_ready", "rwT_in_psum", "rwT_ready", "staged",
                                        "xT_in_psum", "xT_ready", "logits_ready", "exp_ready", "chain", "later_loaded"))
        with nc.Block() as block:

            @block.sync
            def _(sp):
                sp.dma_start(rw[:, :], router_w).then_inc(w_loaded, 16)
                sp.dma_start(bias[:, :], across(bias_corr, P)).then_inc(w_loaded, 16)
                for dst, src in loads:
                    sp.dma_start(dst, src).then_inc(later_loaded, 16)
                sp.wait_ge(later_loaded, 16 * len(loads))

            @block.gpsimd
            def _(pool):
                for ap in cleared:
                    pool.memset(ap, 0.0)
                pool.memset(lower[:, :, :], 1.0).then_inc(consts_ready, 1)
                pool.wait_ge(consts_ready, 1)
                pool.affine_select(out=lower[:, :, :], in_=lower[:, :, :], compare_op=ALU.is_gt, fill=0.0, base=0,
                                   pattern=[[1, G], [-1, G]], channel_multiplier=0).then_inc(consts_ready, 1)
                for n in range(8 - TOPK):
                    pool.memset(sentinels[:, n:n + 1], -2 * FAR * (n + 1)).then_inc(consts_ready, 1)

            @block.tensor
            def _(pe):
                pe.wait_ge(w_loaded, 32)
                pe.transpose(core.bank[0][:, 0:E], rw[:, :], core.ident[0:E, 0:E]).then_inc(rwT_in_psum, 1)
                pe.wait_ge(rwT_ready, 1)
                with pe.Fori(0, NG) as g:
                    pe.wait_ge(staged, g + 1)
                    for b in range(GB):
                        mm = pe.transpose(core.bank[0][:, b * P:(b + 1) * P], stage[:, b, :], core.ident[:, :])
                    mm.then_inc(xT_in_psum, 1)
                    pe.wait_ge(xT_ready, g + 1)
                    for b in range(GB):
                        mm = pe.matmul(core.bank[1][:, b * E:(b + 1) * E], xT[:, b, :], rwT[:, :], start=True, stop=True)
                    mm.then_inc(logits_ready, 1)

            @block.scalar
            def _(act):
                act.wait_ge(rwT_in_psum, 1)
                act.copy(rwT[:, :], core.bank[0][:, 0:E]).then_inc(rwT_ready, 1)
                with act.Fori(0, NG) as g:
                    act.wait_ge(xT_in_psum, g + 1)
                    act.copy(xT[:, :, :].rearrange("p b t -> p (b t)"), core.bank[0][:, :]).then_inc(xT_ready, 1)
                    act.wait_ge(logits_ready, g + 1)
                    act.activation(expo[:, :, :].rearrange("p b e -> p (b e)"), core.bank[1][:, 0:GB * E], ACT.Exp,
                                   scale=-1.0).then_inc(exp_ready, 1)

            @block.vector
            def _(dve):
                step = Chain(dve, chain_sem)
                dve.wait_ge(consts_ready, 2 + 8 - TOPK)
                dve.wait_ge(w_loaded, 32)
                step(dve.tensor_copy(masked[:, :, E:W], sentinels[:, :].unsqueeze(1).to_broadcast([P, GB, W - E])))
                with dve.Fori(0, NG) as g:
                    step.enter(g, 28)
                    tiles = bass.ds(g * GB, GB)
                    dve.tensor_copy(stage[:, :, :], xn[:, tiles, :]).then_inc(staged, 1)
                    dve.wait_ge(exp_ready, g + 1)
                    step(dve.tensor_scalar(expo[:, :, :], expo[:, :, :], 1.0, None, ALU.add))
                    step(dve.reciprocal(scores[:, :, :], expo[:, :, :]))
                    step(dve.tensor_tensor(biased[:, :, :], scores[:, :, :], bias[:, :].unsqueeze(1).to_broadcast([P, GB, E]), ALU.add))
                    step(dve.tensor_reduce(gs[:, :, :].rearrange("p b g -> p (b g)"),
                                           biased[:, :, :].rearrange("p b (g e) -> p (b g) e", g=G), X, ALU.max))
                    other = gs[:, :, :].unsqueeze(2).to_broadcast([P, GB, G, G])
                    own = gs[:, :, :].unsqueeze(3).to_broadcast([P, GB, G, G])
                    step.tick(dve.tensor_tensor(beats[:, :, :, :], other, own, ALU.is_gt))
                    step(dve.tensor_tensor(ties[:, :, :, :], other, own, ALU.is_ge))
                    step(dve.tensor_tensor(ties[:, :, :, :].rearrange("p b g h -> p b (g h)"), ties[:, :, :, :].rearrange("p b g h -> p b (g h)"),
                                           lower[:, :, :].rearrange("p g h -> p (g h)").unsqueeze(1).to_broadcast([P, GB, G * G]), ALU.mult))
                    step(dve.tensor_tensor(beats[:, :, :, :], beats[:, :, :, :], ties[:, :, :, :], ALU.max))
                    step(dve.tensor_reduce(rank[:, :, :], beats[:, :, :, :], X, ALU.add))
                    step(dve.tensor_scalar(gmask[:, :, :], rank[:, :, :], float(TG), None, ALU.is_lt))
                    step(dve.tensor_scalar(penalty[:, :, :], gmask[:, :, :], -1.0, FAR, ALU.add, ALU.mult))
                    vals = masked[:, :, 0:E].rearrange("p b (g e) -> p b g e", g=G)
                    step(dve.tensor_tensor(vals, biased[:, :, :].rearrange("p b (g e) -> p b g e", g=G),
                                           gmask[:, :, :].unsqueeze(3).to_broadcast([P, GB, G, EPG]), ALU.mult))
                    step(dve.tensor_tensor(vals, vals, penalty[:, :, :].unsqueeze(3).to_broadcast([P, GB, G, EPG]), ALU.add))
                    dve.memset(waiter[:, :], 0.0)
                    for b in range(GB):
                        step.tick(dve.max(best[:, b, :], masked[:, b, 0:E]))
                    step.settle()
                    step(dve.tensor_copy(best[:, :, TOPK:8], sentinels[:, :].unsqueeze(1).to_broadcast([P, GB, 8 - TOPK])))
                    dve.memset(waiter[:, :], 0.0)
                    for b in range(GB):
                        step.tick(dve.match_replace(marked[:, b, :], best[:, b, :], masked[:, b, :], FAR))
                    step.settle()
                    step(dve.tensor_scalar(marked[:, :, 0:E], marked[:, :, 0:E], FAR, None, ALU.is_ge))
                    step(dve.tensor_tensor(expo[:, :, :], scores[:, :, :], marked[:, :, 0:E], ALU.mult))
                    step(dve.tensor_reduce(total[:, :], expo[:, :, :], X, ALU.add))
                    step(dve.tensor_scalar(total[:, :], total[:, :], 1e-20, None, ALU.add))
                    step(dve.reciprocal(total[:, :], total[:, :]))
                    step(dve.tensor_tensor(combine[:, tiles, :], expo[:, :, :], total[:, :].unsqueeze(2).to_broadcast([P, GB, E]), ALU.mult))
                    step.leave(NG)




class Sparse:
    E, TOPK = 64, 6
    ROUTED = ((TOPK * B * T + E * (P - 1)) // P + 3) // 4 * 4
    TILES = ROUTED + B
    ROWS = TILES * P + TOPK * B * P
    H, HS = 160, 128


def dispatch_six(core, xn, combine, buf, take, weight, tile_expert):
    nc = core.nc
    core.phase = "dispatch0_"
    Z = Sparse
    E, K = Z.E, Z.TOPK
    PER = 17
    with ExitStack() as c:
        sb = lambda n, s, d=F32: core.sbuf(n, s, d, c)
        sem = lambda n: core.sem(n, c)
        before, ones = sb("before", [P, P]), sb("ones", [P, P])
        real = sb("real", [P, 1])
        spill = sb("spill", [P, B, K])
        tile_start = sb("tile_start", [P, B])
        index = sb("index", [P, 2])
        sel = sb("sel", [P, B, E])
        chosen, count, tiles_row, end = (sb(n, [P, E]) for n in ("chosen", "count", "tiles_row", "end"))
        more = sb("more", [P, E, B])
        base1 = sb("base1", [P, E])
        tiles_col, tiles_wide = sb("tiles_col", [E, 1]), sb("tiles_wide", [E, P])
        expert_col = sb("expert_col", [P, 2])
        seen = sb("seen", [P, GB + 1, E])
        key = sb("key", [P, GB, E])
        best = sb("best", [P, GB, 8])
        match = sb("match", [P, GB, K, E])
        row, valid, to = (sb(n, [P, GB, K]) for n in ("row", "valid", "to"))
        stage = [sb(f"stage{n}", [P, GB, D]) for n in range(2)]
        put = [sb(f"put{n}", [P, GB, K], U32) for n in range(2)]
        waiter, pool_waiter = sb("waiter", [1, 1]), sb("pool_waiter", [1, 1])
        names = ("consts_ready", "chosen_ready", "count_in_psum", "wide_ready", "base_in_psum", "expert_ready", "expert_in_psum",
                 "sel_ready", "pos_in_psum", "index_ready", "shared_sent", "chain", "pool_chain", "pool_waited")
        S = {n: sem(n) for n in names}
        sent = [sem(f"sent{n}") for n in range(2)]
        bank = core.bank
        with nc.Block() as block:

            @block.sync
            def _(sp):
                sp.dma_start(buf[Z.ROUTED * P:Z.TILES * P, :].rearrange("(b p) d -> p b d", p=P), xn[:, :, :]).then_inc(S["shared_sent"], 16)
                sp.wait_ge(S["shared_sent"], 16)

            @block.gpsimd
            def _(pool):
                step = Chain(pool, S["pool_chain"])
                iota = dict(allow_small_or_imprecise_dtypes=True)
                step(pool.memset(before[:, :], 1.0))
                step(pool.affine_select(out=before[:, :], in_=before[:, :], compare_op=ALU.is_gt, fill=0.0, base=0,
                                        pattern=[[1, P]], channel_multiplier=-1))
                step(pool.memset(ones[:, :], 1.0))
                step(pool.memset(real[:, :], 1.0))
                step(pool.affine_select(out=real[:, :], in_=real[:, :], compare_op=ALU.is_gt, fill=0.0, base=T,
                                        pattern=[[0, 1]], channel_multiplier=-1))
                step(pool.iota(spill[:, :, :], pattern=[[K * P, B], [P, K]], base=Z.TILES * P, channel_multiplier=1, **iota))
                step(pool.iota(tile_start[:, :], pattern=[[P, B]], base=0, channel_multiplier=0, **iota))
                step(pool.iota(index[:, :], pattern=[[P, 2]], base=0, channel_multiplier=1, **iota))
                step(pool.memset(tile_expert[:, :], E))
                step(pool.memset(pool_waiter[:, :], 0.0))
                pool.memset(seen[:, :, :], 0.0).then_inc(S["consts_ready"], 1)
                with pool.Fori(0, NG // 2) as i:
                    for n in range(2):
                        pool.wait_ge(S["index_ready"], i * 2 + n + 1)
                        pool.tensor_tensor(pool_waiter[:, :], pool_waiter[:, :], pool_waiter[:, :], ALU.add).then_inc(S["pool_waited"], 1)
                        for b in range(GB):
                            for k in range(K):
                                pool.indirect_dma_start(out=buf, out_offset=bass.IndirectOffsetOnAxis(ap=put[n][:, b, k:k + 1], axis=0),
                                                        in_=stage[n][:, b, :], in_offset=None).then_inc(sent[n], 16)
                        pool.wait_ge(S["pool_waited"], i * 2 + n + 1)
                for n in range(2):
                    pool.wait_ge(sent[n], 16 * GB * K * (NG // 2))

            @block.tensor
            def _(pe):
                pe.wait_ge(S["consts_ready"], 1)
                pe.wait_ge(S["chosen_ready"], 1)
                pe.matmul(bank[0][:, 0:E], ones[:, :], chosen[:, :], start=True, stop=True)
                pe.matmul(bank[0][0:E, E:E + 1], chosen[:, :], ones[:, 0:1], start=True, stop=True).then_inc(S["count_in_psum"], 1)
                pe.wait_ge(S["wide_ready"], 1)
                pe.matmul(bank[1][:, 0:E], tiles_wide[:, :], before[0:E, 0:E], start=True, stop=True).then_inc(S["base_in_psum"], 1)
                pe.wait_ge(S["expert_ready"], 1)
                for h in range(2):
                    mm = pe.matmul(bank[2][0:1, h * P:(h + 1) * P], expert_col[:, h:h + 1], core.ident[:, :], start=True, stop=True)
                mm.then_inc(S["expert_in_psum"], 1)
                with pe.Fori(0, NG) as g:
                    pe.wait_ge(S["sel_ready"], g + 1)
                    pe.matmul(bank[3][:, 0:GB * E], before[:, :], sel[:, bass.ds(g * GB, GB), :].rearrange("p b e -> p (b e)"), start=True, stop=False)
                    pe.matmul(bank[3][:, 0:GB * E], ones[:, :], seen[:, 0:GB, :].rearrange("p b e -> p (b e)"), start=False, stop=True).then_inc(S["pos_in_psum"], 1)

            @block.vector
            def _(dve):
                step = Chain(dve, S["chain"])
                dve.wait_ge(S["consts_ready"], 1)
                step(dve.tensor_scalar(sel[:, :, :], combine[:, :, :], 0.0, real[:, :], ALU.is_gt, ALU.mult))
                dve.tensor_reduce(chosen[:, :], sel[:, :, :].rearrange("p b e -> p e b"), X, ALU.add).then_inc(S["chosen_ready"], 1)
                dve.wait_ge(S["count_in_psum"], 1)
                step.tick(dve.tensor_copy(count[:, :], bank[0][:, 0:E]))
                step(dve.tensor_scalar(more[0:E, 0, :], tile_start[0:E, :], bank[0][0:E, E:E + 1], None, ALU.is_lt))
                step(dve.tensor_reduce(tiles_col[:, :], more[0:E, 0, :], X, ALU.add))
                dve.tensor_scalar(tiles_wide[:, :], ones[0:E, :], tiles_col[:, :], None, ALU.mult).then_inc(S["wide_ready"], 1)
                step(dve.tensor_tensor(more[:, :, :], count[:, :].unsqueeze(2).to_broadcast([P, E, B]),
                                       tile_start[:, :].unsqueeze(1).to_broadcast([P, E, B]), ALU.is_gt))
                step(dve.tensor_reduce(tiles_row[:, :], more[:, :, :], X, ALU.add))
                dve.wait_ge(S["base_in_psum"], 1)
                step.tick(dve.tensor_tensor(end[:, :], bank[1][:, 0:E], tiles_row[:, :], ALU.add))
                step(dve.tensor_scalar(base1[:, :], bank[1][:, 0:E], float(P), 1.0, ALU.mult, ALU.add))
                for h in range(2):
                    step(dve.tensor_scalar(count[:, :], end[:, :], index[:, h:h + 1], None, ALU.is_le))
                    ins = dve.tensor_reduce(expert_col[:, h:h + 1], count[:, :], X, ALU.add)
                    if h == 0:
                        step(ins)
                ins.then_inc(S["expert_ready"], 1)
                dve.wait_ge(S["expert_in_psum"], 1)
                step(dve.tensor_copy(tile_expert[:, 0:Z.ROUTED], bank[2][0:1, 0:Z.ROUTED]))
                with dve.Fori(0, NG // 2) as i:
                    step.enter(i, 2 * PER)
                    for n in range(2):
                        g = i * 2 + n
                        tiles = bass.ds(i * 2 * GB + n * GB, GB)
                        dve.wait_ge(sent[n], i * (16 * GB * K))
                        step.tick(dve.tensor_copy(stage[n][:, :, :], xn[:, tiles, :]))
                        for b in range(GB):
                            ins = dve.tensor_tensor(seen[:, b + 1, :], seen[:, b, :], sel[:, bass.ds(i * 2 * GB + n * GB + b, 1), :].rearrange("p b e -> p (b e)"), ALU.add)
                            if b < GB - 1:
                                step(ins)
                        ins.then_inc(S["sel_ready"], 1)
                        dve.wait_ge(S["pos_in_psum"], g + 1)
                        step.tick(dve.tensor_copy(seen[:, 0, :], seen[:, GB, :]))
                        step(dve.tensor_tensor(key[:, :, :], bank[3][:, 0:GB * E].rearrange("p (b e) -> p b e", b=GB),
                                               base1[:, :].unsqueeze(1).to_broadcast([P, GB, E]), ALU.add))
                        step(dve.tensor_tensor(key[:, :, :], key[:, :, :], sel[:, tiles, :], ALU.mult))
                        dve.memset(waiter[:, :], 0.0)
                        for b in range(GB):
                            step.tick(dve.max(best[:, b, :], key[:, b, :]))
                        step.settle()
                        best6 = best[:, :, 0:K]
                        step.tick(dve.tensor_tensor(match[:, :, :, :], key[:, :, :].unsqueeze(2).to_broadcast([P, GB, K, E]),
                                                    best6.unsqueeze(3).to_broadcast([P, GB, K, E]), ALU.is_equal))
                        step.tick(dve.tensor_scalar(valid[:, :, :], best6, 0.0, None, ALU.is_gt))
                        step.tick(dve.tensor_scalar(take[:, tiles, :], best6, -1.0, 0.0, ALU.add, ALU.max))
                        step(dve.scalar_tensor_tensor(out=row[:, :, :].rearrange("p b k -> p (b k)"), in0=best6, scalar=-1.0,
                                                      in1=spill[:, tiles, :], op0=ALU.add, op1=ALU.subtract))
                        step(dve.tensor_tensor(row[:, :, :], row[:, :, :], valid[:, :, :], ALU.mult))
                        dve.tensor_tensor(put[n][:, :, :], row[:, :, :], spill[:, tiles, :], ALU.add).then_inc(S["index_ready"], 1)
                        step(dve.tensor_tensor(match[:, :, :, :], match[:, :, :, :], combine[:, tiles, :].unsqueeze(2).to_broadcast([P, GB, K, E]), ALU.mult))
                        dve.tensor_reduce(weight[:, tiles, :], match[:, :, :, :], X, ALU.add)
                    step.leave(NG // 2)


def experts_sparse(core, w, w_up, buf, results, tile_expert):
    nc = core.nc
    core.phase = "experts0_"
    Z = Sparse
    H, HS, E, U = Z.H, Z.HS, Z.E, Z.TILES
    HR = H - P
    LAG = 4
    with ExitStack() as c:
        sb = lambda n, s, d=F32: core.sbuf(n, s, d, c)
        sem = lambda n: core.sem(n, c)
        w_down, w_down_r = sb("w_down", [P, E + 1, D]), sb("w_down_r", [HR, E + 1, D])
        x = [sb(f"x{n}", [P, D]) for n in range(4)]
        xT = [sb(f"xT{n}", [P, P]) for n in range(2)]
        gate = [sb(f"gate{n}", [P, H]) for n in range(2)]
        h = [sb(f"h{n}", [P, H]) for n in range(2)]
        hT = [sb(f"hT{n}", [P, P]) for n in range(2)]
        hTr = [sb(f"hTr{n}", [HR, P]) for n in range(2)]
        y = [sb(f"y{n}", [P, D]) for n in range(4)]
        names = ("w_loaded", "zeroed", "xT_in_psum", "xT_ready", "up_ready", "gate_ready", "h_ready", "hT_in_psum", "hT_ready",
                 "y_in_psum", "y_ready")
        S = {n: sem(n) for n in names}
        loaded = [sem(f"loaded{n}") for n in range(4)]
        stored = [sem(f"stored{n}") for n in range(4)]
        x_ps, up_ps, hT_ps, y_ps = (core.bank[n:n + 2] for n in (0, 2, 4, 6))
        one = lambda t, e: t[:, bass.ds(e, 1), :].rearrange("p e h -> p (e h)")

        def run(eng, stages):
            def tick(s, base):
                for lag, stage in stages:
                    if base is not None or 0 <= s - lag < U:
                        stage((s - lag) % 4, s - lag if base is None else base + (s - lag))
            for s in range(4):
                tick(s, None)
            with eng.Fori(0, U // 4 - 1) as i:
                for s in range(4, 8):
                    tick(s, i * 4)
            for s in range(U, U + LAG - 1):
                tick(s, None)

        with nc.Block() as block:

            @block.sync
            def _(sp):
                for n, dst, src in ((0, w_down[:, 0:E, :], w["Wd"][:, 0:P, :].rearrange("e h c -> h e c")),
                                    (1, w_down_r[:, 0:E, :], w["Wd"][:, P:H, :].rearrange("e h c -> h e c")),
                                    (2, w_down[:, E, :], w["sWd"])):
                    sp.dma_start(dst, src).then_inc(S["w_loaded"], 16)

                def load(n, u):
                    sp.dma_start(x[n][:, :], buf[bass.ds(u * P, P), :]).then_inc(loaded[n], 16)

                for n in range(4):
                    sp.sem_inc(stored[n], 16)
                    load(n, n)

                def store(n, u):
                    sp.wait_ge(S["y_ready"], u + 1)
                    sp.dma_start(results[bass.ds(u * P, P), :], y[n][:, :]).then_inc(stored[n], 16)

                with sp.Fori(0, U // 4 - 1) as i:
                    for n in range(4):
                        sp.wait_ge(S["xT_in_psum"], i * 4 + n + 1)
                        load(n, i * 4 + n + 4)
                        store(n, i * 4 + n)
                for n in range(4):
                    store(n, U - 4 + n)
                for n in range(4):
                    sp.wait_ge(stored[n], 16 * (U // 4 + 1))

            @block.gpsimd
            def _(pool):
                pool.memset(w_down_r[:, E, :], 0.0).then_inc(S["zeroed"], 1)

            @block.tensor
            def _(pe):
                pe.wait_ge(S["w_loaded"], 3 * 16)
                pe.wait_ge(S["zeroed"], 1)

                def turn_x(n, u):
                    pe.wait_ge(loaded[n], (u - n) * 4 + 16)
                    pe.transpose(x_ps[n % 2][:, 0:P], x[n][:, :], core.ident[:, :]).then_inc(S["xT_in_psum"], 1)

                def up(n, u):
                    e = pe.value_load(tile_expert[0:1, bass.ds(u, 1)], min_val=0, max_val=E)
                    pe.wait_ge(S["xT_ready"], u + 1)
                    pe.matmul(up_ps[n % 2][:, 0:2 * H], xT[n % 2][:, :], one(w_up, e), start=True, stop=True).then_inc(S["up_ready"], 1)

                def turn(n, u):
                    pe.wait_ge(S["h_ready"], u + 1)
                    pe.transpose(hT_ps[n % 2][:, 0:P], h[n % 2][:, 0:P], core.ident[:, :])
                    pe.transpose(hT_ps[n % 2][0:HR, P:2 * P], h[n % 2][:, P:H], core.ident[:, :]).then_inc(S["hT_in_psum"], 1)

                def down(n, u):
                    e = pe.value_load(tile_expert[0:1, bass.ds(u, 1)], min_val=0, max_val=E)
                    if isinstance(u, int) and u == U - 1:
                        pe.wait_ge(S["y_ready"], u - 1)
                    pe.wait_ge(S["hT_ready"], u + 1)
                    pe.matmul(y_ps[n % 2][:, 0:D], hT[n % 2][:, :], one(w_down, e), start=True, stop=False)
                    pe.matmul(y_ps[n % 2][:, 0:D], hTr[n % 2][:, :], one(w_down_r, e), start=False, stop=True).then_inc(S["y_in_psum"], 1)

                run(pe, [(0, turn_x), (1, up), (2, turn), (3, down)])

            @block.scalar
            def _(act):
                def silu(n, u):
                    act.wait_ge(S["up_ready"], u + 1)
                    act.activation(gate[n % 2][:, :], up_ps[n % 2][:, 0:H], ACT.Silu).then_inc(S["gate_ready"], 1)

                def copy_turned(n, u):
                    act.wait_ge(S["hT_in_psum"], u + 1)
                    act.copy(hT[n % 2][:, :], hT_ps[n % 2][:, 0:P])
                    act.copy(hTr[n % 2][:, :], hT_ps[n % 2][0:HR, P:2 * P]).then_inc(S["hT_ready"], 1)

                run(act, [(1, silu), (2, copy_turned)])

            @block.vector
            def _(dve):
                def copy_x(n, u):
                    dve.wait_ge(S["xT_in_psum"], u + 1)
                    dve.tensor_copy(xT[n % 2][:, :], x_ps[n % 2][:, 0:P]).then_inc(S["xT_ready"], 1)

                def multiply(n, u):
                    dve.wait_ge(S["gate_ready"], u + 1)
                    dve.tensor_tensor(h[n % 2][:, :], gate[n % 2][:, :], up_ps[n % 2][:, H:2 * H], ALU.mult).then_inc(S["h_ready"], 1)

                def copy_y(n, u):
                    dve.wait_ge(stored[n], (u - n) * 4 + 16)
                    dve.wait_ge(S["y_in_psum"], u + 1)
                    dve.tensor_copy(y[n][:, :], y_ps[n % 2][:, 0:D]).then_inc(S["y_ready"], 1)

                run(dve, [(0, copy_x), (1, multiply), (3, copy_y)])


def collect_six(core, take, weight, results):
    nc = core.nc
    core.phase = "collect0_"
    Z = Sparse
    K = Z.TOPK
    NB = 4
    with ExitStack() as c:
        sb = lambda n, s, d=F32: core.sbuf(n, s, d, c)
        sem = lambda n: core.sem(n, c)
        take_i = sb("take_i", [P, B, K], U32)
        back = [sb(f"back{n}", [P, K, D]) for n in range(NB)]
        shared = sb("shared", [P, B, D])
        index_ready, shared_loaded, chain = sem("index_ready"), sem("shared_loaded"), sem("chain")
        gathered = [sem(f"gathered{n}") for n in range(NB)]
        with nc.Block() as block:

            @block.sync
            def _(sp):
                sp.dma_start(shared[:, :, :], results[Z.ROUTED * P:Z.TILES * P, :].rearrange("(b p) d -> p b d", p=P)).then_inc(shared_loaded, 16)

            @block.gpsimd
            def _(pool):
                pool.wait_ge(index_ready, 1)
                for b in range(B):
                    if b >= NB:
                        pool.wait_ge(chain, 1 + K * (b - NB + 1))
                    for k in range(K):
                        pool.indirect_dma_start(out=back[b % NB][:, k, :], out_offset=None, in_=results,
                                                in_offset=bass.IndirectOffsetOnAxis(ap=take_i[:, b, k:k + 1], axis=0)).then_inc(gathered[b % NB], 16)

            @block.vector
            def _(dve):
                step = Chain(dve, chain)
                dve.tensor_copy(take_i[:, :, :], take[:, :, :]).then_inc(index_ready, 1)
                dve.wait_ge(shared_loaded, 16)
                step(dve.tensor_tensor(core.hidden[:, :, :], core.hidden[:, :, :], shared[:, :, :], ALU.add))
                for b in range(B):
                    dve.wait_ge(gathered[b % NB], 16 * K * (b // NB + 1))
                    for k in range(K):
                        step(dve.scalar_tensor_tensor(out=core.hidden[:, b, :], in0=back[b % NB][:, k, :], scalar=weight[:, b, k:k + 1],
                                                      in1=core.hidden[:, b, :], op0=ALU.mult, op1=ALU.add))


class ScanShapes:
    N, SD, H, NH, DH, L = 64, 128, 64, 4, 16, 2
    J = 4
    V = SD // J
    BA, OMG2, C2, G2, XH = 0, 64, 128, 192, 256
    F = 320


def scan_inputs(core, xn, w, record_part, record):
    nc = core.nc
    core.phase = "scan_in_"
    Z = ScanShapes
    SCALE = Z.SD ** -0.5
    with ExitStack() as c:
        sb = lambda n, s, d=F32: core.sbuf(n, s, d, c)
        sem = lambda n: core.sem(n, c)
        w_tok = sb("w_tok", [P, 2 * Z.SD + Z.H])
        b_tok = sb("b_tok", [P, 2 * Z.SD + Z.H])
        bp_b = sb("bp_b", [P, Z.H])
        b_wq = sb("b_wq", [Z.H, Z.SD])
        keys, keysT = sb("keys", [Z.N, Z.SD]), sb("keysT", [Z.SD, Z.N])
        b_in_col, b_bq_col = sb("b_in_col", [Z.H, 1]), sb("b_bq_col", [Z.SD, 1])
        stage, xT = sb("stage", [P, GB, D]), sb("xT", [P, GB, P])
        xhT = sb("xhT", [Z.H, GB, P])
        bqT = sb("bqT", [Z.SD, GB, P])
        rec = [sb(f"rec{n}", [P, GB, Z.F]) for n in range(2)]
        rec_part = [sb(f"rec_part{n}", [P, Z.J, GB, 2, Z.V]) for n in range(2)]
        top, total = sb("top", [P, GB]), sb("total", [P, GB])
        expo = sb("expo", [P, GB, Z.N])
        names = ("w_loaded", "keysT_in_psum", "keysT_ready", "staged", "xT_in_psum", "xT_ready", "tok_ready", "xhT_in_psum",
                 "xhT_ready", "bqT_in_psum", "bqT_ready", "logits_ready", "shifted", "exp_ready", "ba_ready", "exp2_ready",
                 "rec_ready", "chain")
        (w_loaded, keysT_in_psum, keysT_ready, staged, xT_in_psum, xT_ready, tok_ready, xhT_in_psum, xhT_ready, bqT_in_psum,
         bqT_ready, logits_ready, shifted, exp_ready, ba_ready, exp2_ready, rec_ready, chain_sem) = (sem(n) for n in names)
        rec_stored = [sem(f"rec_stored{n}") for n in range(2)]
        with nc.Block() as block:

            @block.sync
            def _(sp):
                o = 0
                for wn, bn in (("sb_wq", "sb_bq"), ("sb_ww", "sb_bw"), ("p_win", "p_bin")):
                    n = w[wn].shape[1]
                    sp.dma_start(w_tok[:, o:o + n], w[wn]).then_inc(w_loaded, 16)
                    sp.dma_start(b_tok[:, o:o + n], across(w[bn], P)).then_inc(w_loaded, 16)
                    o += n
                sp.dma_start(bp_b[:, :], across(w["bp_b"], P)).then_inc(w_loaded, 16)
                sp.dma_start(b_wq[:, :], w["b_wq"]).then_inc(w_loaded, 16)
                sp.dma_start(keys[:, :], w["b_keys"]).then_inc(w_loaded, 16)
                sp.dma_start(b_in_col[:, :], w["p_bin"].rearrange("(d a) -> d a", a=1)).then_inc(w_loaded, 16)
                sp.dma_start(b_bq_col[:, :], w["b_bq"].rearrange("(d a) -> d a", a=1)).then_inc(w_loaded, 16)
                for n in range(2):
                    sp.sem_inc(rec_stored[n], 32)
                with sp.Fori(0, NG // 2) as i:
                    for n in range(2):
                        sp.wait_ge(rec_ready, i * 2 + n + 1)
                        at = bass.ds(i * 2 * GB + n * GB, GB)
                        sp.dma_start(record[:, at, :], rec[n][:, :, :]).then_inc(rec_stored[n], 16)
                        sp.dma_start(record_part[:, :, at, :], rec_part[n][:, :, :, :, :].rearrange("p j b s d -> p j (b s d)")).then_inc(rec_stored[n], 16)
                for n in range(2):
                    sp.wait_ge(rec_stored[n], 32 * (NG // 2 + 1))

            @block.tensor
            def _(pe):
                pe.wait_ge(w_loaded, 11 * 16)
                pe.transpose(core.bank[0][:, 0:Z.N], keys[:, :], core.ident[0:Z.N, 0:Z.N]).then_inc(keysT_in_psum, 1)
                pe.wait_ge(keysT_ready, 1)
                with pe.Fori(0, NG // 2) as i:
                    for n in range(2):
                        g = i * 2 + n
                        pe.wait_ge(staged, g + 1)
                        for b in range(GB):
                            mm = pe.transpose(core.bank[0][:, b * P:(b + 1) * P], stage[:, b, :], core.ident[:, :])
                        mm.then_inc(xT_in_psum, 1)
                        pe.wait_ge(xT_ready, g + 1)
                        flat = xT[:, :, :].rearrange("p b t -> p (b t)")
                        pe.matmul(core.bank[1][0:Z.H, :], w_tok[:, 2 * Z.SD:], flat, start=True, stop=True).then_inc(xhT_in_psum, 1)
                        for b in range(GB):
                            mm = pe.matmul(core.bank[4 + b][:, 0:2 * Z.SD + Z.H], xT[:, b, :], w_tok[:, :], start=True, stop=True)
                        mm.then_inc(tok_ready, 1)
                        pe.wait_ge(xhT_ready, g + 1)
                        pe.matmul(core.bank[2][:, :], b_wq[:, :], xhT[:, :, :].rearrange("p b t -> p (b t)"), start=True, stop=True).then_inc(bqT_in_psum, 1)
                        pe.wait_ge(bqT_ready, g + 1)
                        for b in range(GB):
                            mm = pe.matmul(core.bank[3][:, b * Z.N:(b + 1) * Z.N], bqT[:, b, :], keysT[:, :], start=True, stop=True)
                        mm.then_inc(logits_ready, 1)

            @block.scalar
            def _(act):
                act.wait_ge(keysT_in_psum, 1)
                act.copy(keysT[:, :], core.bank[0][:, 0:Z.N]).then_inc(keysT_ready, 1)
                act.wait_ge(w_loaded, 11 * 16)
                with act.Fori(0, NG // 2) as i:
                    for n in range(2):
                        g = i * 2 + n
                        act.wait_ge(xT_in_psum, g + 1)
                        act.copy(xT[:, :, :].rearrange("p b t -> p (b t)"), core.bank[0][:, :]).then_inc(xT_ready, 1)
                        act.wait_ge(xhT_in_psum, g + 1)
                        act.activation(xhT[:, :, :].rearrange("p b t -> p (b t)"), core.bank[1][0:Z.H, :], ACT.Identity,
                                       bias=b_in_col[:, :]).then_inc(xhT_ready, 1)
                        act.wait_ge(bqT_in_psum, g + 1)
                        act.activation(bqT[:, :, :].rearrange("p b t -> p (b t)"), core.bank[2][:, :], ACT.Identity,
                                       bias=b_bq_col[:, :]).then_inc(bqT_ready, 1)
                        act.wait_ge(shifted, g + 1)
                        act.activation(expo[:, :, :], expo[:, :, :], ACT.Exp, scale=SCALE).then_inc(exp_ready, 1)
                        act.wait_ge(ba_ready, g + 1)
                        act.activation(expo[:, :, :], rec[n][:, :, Z.BA:Z.BA + Z.N], ACT.Exp, scale=-1.0).then_inc(exp2_ready, 1)

            @block.vector
            def _(dve):
                step = Chain(dve, chain_sem)
                dve.wait_ge(w_loaded, 11 * 16)
                with dve.Fori(0, NG // 2) as i:
                    step.enter(i, 2 * (3 * GB + 8))
                    for n in range(2):
                        g = i * 2 + n
                        cols = lambda a, k=Z.N: rec[n][:, :, a:a + k]
                        dve.tensor_copy(stage[:, :, :], xn[:, bass.ds(i * 2 * GB + n * GB, GB), :]).then_inc(staged, 1)
                        dve.wait_ge(tok_ready, g + 1)
                        dve.wait_ge(rec_stored[n], i * 32 + 32)
                        for b in range(GB):
                            for s in range(2):
                                cs = slice(s * Z.SD, (s + 1) * Z.SD)
                                part = lambda ap: ap.rearrange("p (j d) -> p j d", j=Z.J)
                                step.tick(dve.tensor_tensor(rec_part[n][:, :, b, s, :], part(core.bank[4 + b][:, cs]), part(b_tok[:, cs]), ALU.add))
                            step.tick(dve.tensor_tensor(rec[n][:, b, Z.XH:Z.XH + Z.H], core.bank[4 + b][:, 2 * Z.SD:2 * Z.SD + Z.H], b_tok[:, 2 * Z.SD:], ALU.add))
                        dve.wait_ge(logits_ready, g + 1)
                        lg = core.bank[3][:, 0:GB * Z.N].rearrange("p (b n) -> p b n", b=GB)
                        step(dve.tensor_reduce(top[:, :], lg, X, ALU.max))
                        dve.tensor_tensor(expo[:, :, :], lg, top[:, :].unsqueeze(2).to_broadcast([P, GB, Z.N]), ALU.subtract).then_inc(shifted, 1)
                        query = rec_part[n][:, :, :, 0, :].rearrange("p j b d -> p (j b) d")
                        step.tick(dve.tensor_scalar(query, query, SCALE, None, ALU.mult))
                        step(dve.tensor_tensor(cols(Z.XH), cols(Z.XH), bp_b[:, :].unsqueeze(1).to_broadcast([P, GB, Z.H]), ALU.add))
                        dve.wait_ge(exp_ready, g + 1)
                        step(dve.tensor_reduce(total[:, :], expo[:, :, :], X, ALU.add))
                        step(dve.reciprocal(total[:, :], total[:, :]))
                        dve.tensor_tensor(cols(Z.BA), expo[:, :, :], total[:, :].unsqueeze(2).to_broadcast([P, GB, Z.N]), ALU.mult).then_inc(ba_ready, 1)
                        dve.wait_ge(exp2_ready, g + 1)
                        step(dve.tensor_scalar(cols(Z.OMG2), expo[:, :, :], 1.0, None, ALU.add))
                        step(dve.reciprocal(cols(Z.G2), cols(Z.OMG2)))
                        step.tick(dve.tensor_tensor(cols(Z.C2), cols(Z.G2), cols(Z.BA), ALU.mult))
                        dve.tensor_tensor(cols(Z.OMG2), expo[:, :, :], cols(Z.G2), ALU.mult).then_inc(rec_ready, 1)
                    step.leave(NG // 2)


def scan_tokens(core, w, record_part, record, reads, states):
    nc = core.nc
    core.phase = "scan_"
    Z = ScanShapes
    N, H, J, DH = Z.N, Z.H, Z.J, Z.DH
    V = Z.SD // J
    M = N + 2
    LOADS = 2 + Z.L * (8 * J + 4) + 2 * J
    PER = 64
    STEPS = T + 1
    with ExitStack() as c:
        sb = lambda n, s, d=F32: core.sbuf(n, s, d, c)
        sem = lambda n: core.sem(n, c)
        slots = sb("slots", [P, M, V])
        prod, prod_r = sb("prod", [P, M, V]), sb("prod_r", [P, M, V])
        write, write_u = sb("write", [P, N, V]), sb("write_u", [P, N, V])
        delta = sb("delta", [P, N])
        same_b = sb("same_b", [P, P])
        part_of = sb("part_of", [P, J])
        bp_w = sb("bp_w", [Z.SD, H])
        w_qkv = sb("w_qkv", [H + 1, Z.L, J, 3 * DH + 1])
        w_o = sb("w_o", [H, Z.L, H])
        w_sup = sb("w_sup", [H + 1, Z.SD])
        bo, ln_g, ln_b = sb("bo", [P, Z.L, H]), sb("ln_g", [P, Z.L, H]), sb("ln_b", [P, Z.L, H])
        in_part = [sb(f"in_part{n}", [P, 2 * V]) for n in range(2)]
        in_q, in_wr = [p[:, 0:V] for p in in_part], [p[:, V:2 * V] for p in in_part]
        in_rep = [sb(f"in_rep{n}", [P, Z.F]) for n in range(2)]
        part, logits = sb("part", [P, M + 1]), sb("logits", [P, N])
        early, extra = sb("early", [P, N]), sb("extra", [P, 3])
        last, keep_last = sb("last", [P, N]), sb("keep_last", [P, N])
        qu = sb("qu", [P, 1])
        nmax, den, rden = sb("nmax", [P, 1]), sb("den", [P, 1]), sb("rden", [P, 1])
        e_a, a, ea, g, omg, w2, keep, c1, gab = (sb(n, [P, M]) for n in ("e_a", "a", "ea", "g", "omg", "w2", "keep", "c1", "gab"))
        junk, cwr = sb("junk", [P, N]), sb("cwr", [P, 1])
        bind, bind_wide, bindT = sb("bind", [P, V]), sb("bind_wide", [P, J, V]), sb("bindT", [Z.SD, P])
        xh, xhb = sb("xh", [P, H]), sb("xhb", [P, H])
        xhT = sb("xhT", [H + 1, B])
        qkv = sb("qkv", [P, 3 * DH + 1])
        eb, beta, ssq, kq, nrm, rk, rkq = (sb(n, [P, 1]) for n in ("eb", "beta", "ssq", "kq", "nrm", "rk", "rkq"))
        mem = [sb(f"mem{l}", [P, DH, DH]) for l in range(Z.L)]
        mprod = sb("mprod", [P, 2, DH, DH])
        msum = sb("msum", [P, 2, DH])
        kn, dv = ([sb(f"{n}{l}", [P, DH]) for l in range(Z.L)] for n in ("kn", "dv"))
        no, no_wide = sb("no", [P, DH]), sb("no_wide", [P, J, DH])
        outer_m = sb("outer_m", [P, DH, DH])
        oT = sb("oT", [H, P])
        stats, mv, lnv, rstd = sb("stats", [P, 6]), sb("mv", [P, 2]), sb("lnv", [P, 1]), sb("rstd", [P, 1])
        waiter = sb("waiter", [1, 1])
        out_x = [sb(f"out_x{n}", [P, H]) for n in range(2)]
        out_r = [sb(f"out_r{n}", [P, V]) for n in range(2)]
        names = ("w_loaded", "consts_ready", "w_ready", "part_ready", "lg_in_psum", "u_ready", "qu_ready", "qu_in_psum",
                 "nmax_ready", "exp_ready", "a_ready", "ea_ready", "ax_ready", "prod_r_ready", "coef_ready", "bound",
                 "write_ready", "bind_ready", "bindT_in_psum", "bindT_ready", "xh_in_psum", "xh_ready", "xhT_in_psum",
                 "xhT_ready", "qkv_in_psum", "qkv_ready", "eb_ready", "ssq_ready", "nrm_ready", "dv_ready", "mem_ready",
                 "no_ready", "oT_in_psum", "oT_ready", "o_in_psum", "mv_ready", "rstd_ready", "read_in_psum",
                 "read_ready", "step_done", "chain", "act_chain", "pool_chain")
        S = {n: sem(n) for n in names}
        loaded = [sem(f"loaded{n}") for n in range(2)]
        stored = [sem(f"stored{n}") for n in range(2)]
        A, QU, BT, D_, E_, F_, R_, U_ = core.bank
        C_, G_ = BT[:, P:2 * P], F_[:, P:2 * P]

        def col(n, name, width=N):
            return in_rep[n][:, name:name + width]

        with nc.Block() as block:

            @block.sync
            def _(sp):
                loads = [(bp_w[:, :], w["bp_w"]),
                         (w_sup[0:H, :], w["sup_w"])]
                for l in range(Z.L):
                    loads += [(w_qkv[0:H, l, j, s * DH:(s + 1) * DH], w["dn_wqkv"][l][:, s * H + j * DH:s * H + (j + 1) * DH])
                              for s in range(3) for j in range(J)]
                    loads += [(w_qkv[H:H + 1, l, j, s * DH:(s + 1) * DH],
                               w["dn_bqkv"][l:l + 1, s * H + j * DH:s * H + (j + 1) * DH]) for s in range(3) for j in range(J)]
                    loads += [(w_qkv[0:H, l, j, 3 * DH:], w["dn_wbeta"][l][:, j:j + 1]) for j in range(J)]
                    loads += [(w_qkv[H:H + 1, l, j, 3 * DH:], w["dn_bbeta"][l:l + 1, j:j + 1]) for j in range(J)]
                    loads += [(w_o[:, l, :], w["dn_wo"][l])]
                    loads += [(dst[:, l, :], w[name][l:l + 1, :].to_broadcast([P, H]))
                              for dst, name in ((bo, "dn_bo"), (ln_g, "dn_lng"), (ln_b, "dn_lnb"))]
                for j in range(J):
                    loads += [(slots[32 * j:32 * j + 32, 0:N, :], w["sb_init"][:, V * j:V * j + V].unsqueeze(0).to_broadcast([B, N, V])),
                              (slots[32 * j:32 * j + 32, N, :], w["sup_b"][V * j:V * j + V].unsqueeze(0).to_broadcast([B, V]))]
                for dst, src in loads:
                    sp.dma_start(dst, src, allow_slow_non_contiguous=dst.shape[-1] == 1).then_inc(S["w_loaded"], 16)
                assert len(loads) == LOADS

                def load(t, n):
                    sp.dma_start(in_part[n][:, :], record_part[bass.ds(t, 1), :, :, :].rearrange("t j b f -> (t j b) f")).then_inc(loaded[n], 16)
                    for j in range(J):
                        sp.dma_start(in_rep[n][B * j:B * j + B, :], record[bass.ds(t, 1), :, :].rearrange("t b f -> (t b) f")).then_inc(loaded[n], 16)

                def store(t, n):
                    sp.wait_ge(S["read_ready"], t + 1)
                    sp.dma_start(reads[bass.ds(t, 1), :, :, :].rearrange("t j b d -> (t j b) d"), out_r[n][:, :]).then_inc(stored[n], 16)
                    sp.wait_ge(S["xh_ready"], t * 3 + 3)
                    sp.dma_start(states[bass.ds(t, 1), :, :].rearrange("t b f -> (t b) f"), out_x[n][0:B, :]).then_inc(stored[n], 16)

                for n in range(2):
                    sp.sem_inc(stored[n], 32)
                    load(n, n)
                with sp.Fori(0, STEPS // 2 - 1) as i:
                    for n in range(2):
                        store(i * 2 + n, n)
                        sp.wait_ge(S["step_done"], i * 2 + n + 1)
                        load(i * 2 + n + 2, n)
                store(STEPS - 2, 0)
                sp.wait_ge(S["step_done"], STEPS - 1)
                load(STEPS - 1, 0)
                store(STEPS - 1, 1)
                sp.wait_ge(loaded[0], 80 * (STEPS // 2 + 1))
                for n in range(2):
                    sp.wait_ge(stored[n], 32 * (STEPS // 2 + 1))

            @block.gpsimd
            def _(pool):
                step = Chain(pool, S["pool_chain"])
                step(pool.memset(same_b[:, :], 0.0))
                for s in range(1 - J, J):
                    step(pool.affine_select(out=same_b[:, :], in_=same_b[:, :], compare_op=ALU.not_equal, fill=1.0,
                                            base=B * s, pattern=[[-1, P]], channel_multiplier=1))
                step(pool.memset(part_of[:, :], 0.0))
                for j in range(J):
                    step(pool.memset(part_of[B * j:B * j + B, j:j + 1], 1.0))
                step(pool.memset(last[:, :], 0.0))
                step(pool.memset(slots[:, N + 1, :], 0.0))
                pool.memset(delta[:, :], 0.0).then_inc(S["consts_ready"], 1)
                pool.memset(xhT[:, :], 1.0).then_inc(S["consts_ready"], 1)
                pool.wait_ge(S["consts_ready"], 2)
                pool.memset(w_sup[H:H + 1, :], 0.0).then_inc(S["consts_ready"], 1)
                pool.wait_ge(S["consts_ready"], 3)
                for l in range(Z.L):
                    pool.memset(mem[l][:, :, :], 0.0).then_inc(S["consts_ready"], 1)
                pool.sem_inc(S["mem_ready"], Z.L)
                with pool.Fori(0, STEPS // 2) as i:
                    step.enter(i, 2 * (Z.L + 2))
                    for n in range(2):
                        t = i * 2 + n
                        wide = lambda ap: ap[:, 0:N].unsqueeze(2).to_broadcast([P, N, V])
                        pool.wait_ge(S["ax_ready"], t + 1)
                        pool.tensor_tensor(prod_r[:, :, :], slots[:, :, :], a[:, :].unsqueeze(2).to_broadcast([P, M, V]), ALU.mult).then_inc(S["prod_r_ready"], 1)
                        pool.wait_ge(S["coef_ready"], t + 1)
                        step.tick(pool.tensor_tensor(write[:, :, :], in_wr[n].unsqueeze(1).to_broadcast([P, N, V]), wide(c1), ALU.mult))
                        step(pool.tensor_tensor(write_u[:, :, :], slots[:, N + 1:M, :].to_broadcast([P, N, V]), wide(keep_last), ALU.mult))
                        pool.tensor_tensor(write[:, :, :], write[:, :, :], write_u[:, :, :], ALU.add).then_inc(S["write_ready"], 1)
                        for l in range(Z.L):
                            pool.wait_ge(S["dv_ready"], t * 2 + l + 1)
                            step(pool.tensor_tensor(outer_m[:, :, :], dv[l][:, :].unsqueeze(2).to_broadcast([P, DH, DH]),
                                                    kn[l][:, :].unsqueeze(1).to_broadcast([P, DH, DH]), ALU.mult))
                            pool.tensor_tensor(mem[l][:, :, :], mem[l][:, :, :], outer_m[:, :, :], ALU.subtract).then_inc(S["mem_ready"], 1)
                            pool.wait_ge(S["mem_ready"], t * 2 + l + 1 + Z.L)
                    step.leave(STEPS // 2)

            @block.tensor
            def _(pe):
                pe.wait_ge(S["pool_chain"], 3 * J + 3)
                pe.wait_ge(S["consts_ready"], 3 + Z.L)
                pe.wait_ge(S["w_ready"], 1)
                pe.wait_ge(S["part_ready"], 1)
                pe.matmul(A[:, 0:M + 1], same_b[:, :], part[:, :], start=True, stop=True).then_inc(S["lg_in_psum"], 1)
                with pe.Fori(0, STEPS // 2) as i:
                    for n in range(2):
                        t = i * 2 + n

                        def turn_xh(which):
                            pe.wait_ge(S["xh_ready"], t * 3 + which + 1)
                            src = out_x[n] if which == 2 else xh
                            pe.matmul(D_[0:H, 0:B], src[0:B, :], core.ident[0:B, 0:B], start=True, stop=True).then_inc(S["xhT_in_psum"], 1)
                            pe.wait_ge(S["xhT_ready"], t * 3 + which + 1)

                        pe.wait_ge(S["qu_ready"], t + 1)
                        pe.matmul(QU[:, 0:1], same_b[:, :], qu[:, :], start=True, stop=True).then_inc(S["qu_in_psum"], 1)
                        pe.wait_ge(S["bind_ready"], t + 1)
                        pe.matmul(BT[:, 0:P], bind_wide[:, :, :].rearrange("p j d -> p (j d)"), same_b[:, :], start=True, stop=True).then_inc(S["bindT_in_psum"], 1)
                        pe.wait_ge(S["bindT_ready"], t + 1)
                        pe.matmul(C_[:, 0:H], bindT[:, :], bp_w[:, :], start=True, stop=True).then_inc(S["xh_in_psum"], 1)
                        for l in range(Z.L):
                            turn_xh(l)
                            for j in range(J):
                                mm = pe.matmul(E_[B * j:B * j + B, 0:3 * DH + 1], xhT[:, :], w_qkv[:, l, j, :], start=True, stop=True)
                            mm.then_inc(S["qkv_in_psum"], 1)
                            if l == 0:
                                pe.wait_ge(S["prod_r_ready"], t + 1)
                            for k in range(l * 2, l * 2 + 2):
                                pe.matmul(R_[:, :], core.ident[:, :], prod_r[:, 16 * k:16 * k + 16, :].rearrange("p n d -> p (n d)"), start=k == 0, stop=False)
                            if l == Z.L - 1:
                                pe.matmul(R_[:, 0:2 * V], core.ident[:, :], prod_r[:, N:M, :].rearrange("p n d -> p (n d)"), start=False, stop=True).then_inc(S["read_in_psum"], 1)
                            pe.wait_ge(S["no_ready"], t * 2 + l + 1)
                            pe.matmul(F_[0:H, 0:P], no_wide[:, :, :].rearrange("p j d -> p (j d)"), same_b[:, :], start=True, stop=True).then_inc(S["oT_in_psum"], 1)
                            pe.wait_ge(S["oT_ready"], t * 2 + l + 1)
                            pe.matmul(G_[:, 0:H], oT[:, :], w_o[:, l, :], start=True, stop=True).then_inc(S["o_in_psum"], 1)
                            if l == 0:
                                pe.wait_ge(S["part_ready"], t + 2)
                                pe.matmul(A[:, 0:M + 1], same_b[:, :], part[:, :], start=True, stop=True).then_inc(S["lg_in_psum"], 1)
                        turn_xh(2)
                        for j in range(J):
                            mm = pe.matmul(U_[B * j:B * j + B, 0:V], xhT[:, :], w_sup[:, V * j:V * j + V], start=True, stop=True)
                        mm.then_inc(S["u_ready"], 1)

            @block.scalar
            def _(act):
                act.preload_act_table_set("natural_log_exp_and_others")
                step = Chain(act, S["act_chain"])
                act.wait_ge(S["consts_ready"], 3 + Z.L)
                with act.Fori(0, STEPS // 2) as i:
                    step.enter(i, 2 * Z.L * 2)
                    for n in range(2):
                        t = i * 2 + n

                        def copy_xhT(which):
                            act.wait_ge(S["xhT_in_psum"], t * 3 + which + 1)
                            act.copy(xhT[0:H, :], D_[0:H, 0:B]).then_inc(S["xhT_ready"], 1)

                        act.wait_ge(S["nmax_ready"], t + 1)
                        act.activation(e_a[:, 0:N], logits[:, :], ACT.Exp, bias=nmax[:, :], accum_out=den[:, :]).then_inc(S["exp_ready"], 1)
                        act.wait_ge(S["a_ready"], t + 1)
                        act.activation(ea[:, 0:N], a[:, 0:N], ACT.Exp, scale=-1.0).then_inc(S["ea_ready"], 1)
                        act.wait_ge(S["bindT_in_psum"], t + 1)
                        act.copy(bindT[:, :], BT[:, 0:P]).then_inc(S["bindT_ready"], 1)
                        for l in range(Z.L):
                            copy_xhT(l)
                            act.wait_ge(S["qkv_ready"], t * 2 + l + 1)
                            act.activation(eb[:, :], qkv[:, 3 * DH:3 * DH + 1], ACT.Exp, scale=-1.0).then_inc(S["eb_ready"], 1)
                            act.wait_ge(S["ssq_ready"], t * 2 + l + 1)
                            step(act.activation(nrm[:, :], ssq[:, :], ACT.Ln))
                            act.activation(nrm[:, :], nrm[:, :], ACT.Exp, scale=0.5).then_inc(S["nrm_ready"], 1)
                            act.wait_ge(S["oT_in_psum"], t * 2 + l + 1)
                            act.copy(oT[:, :], F_[0:H, 0:P]).then_inc(S["oT_ready"], 1)
                            act.wait_ge(S["mv_ready"], t * 2 + l + 1)
                            step(act.activation(lnv[:, :], mv[:, 1:2], ACT.Ln, bias=EPS))
                            act.activation(rstd[:, :], lnv[:, :], ACT.Exp, scale=-0.5).then_inc(S["rstd_ready"], 1)
                        copy_xhT(2)
                    step.leave(STEPS // 2)

            @block.vector
            def _(dve):
                step = Chain(dve, S["chain"])
                dve.wait_ge(S["w_loaded"], 16 * LOADS)
                dve.wait_ge(S["consts_ready"], 3 + Z.L)
                dve.tensor_scalar(w_o[:, :, :], w_o[:, :, :], -1.0, None, ALU.mult).then_inc(S["w_ready"], 1)
                spread = lambda ap, k=N: ap[:, 0:k].unsqueeze(2).to_broadcast([P, k, V])
                half = lambda h: slice(h * N // 2, (h + 1) * N // 2)

                def query(q, rows):
                    return dve.tensor_tensor(prod[:, rows, :], slots[:, rows, :], q.unsqueeze(1).to_broadcast([P, rows.stop - rows.start, V]), ALU.mult)

                dve.wait_ge(loaded[0], 80)
                dve.memset(U_[:, 0:V], 0.0).then_inc(S["u_ready"], 1)
                step(query(in_q[0], slice(0, M)))
                step.tick(dve.memset(part[:, M:M + 1], 0.0))
                dve.tensor_reduce(part[:, 0:M], prod[:, :, :], X, ALU.add).then_inc(S["part_ready"], 1)
                dve.wait_ge(S["lg_in_psum"], 1)
                step(dve.tensor_copy(early[:, :], A[:, 0:N]))
                with dve.Fori(0, STEPS // 2) as i:
                    step.enter(i, 2 * PER)
                    for n in range(2):
                        t = i * 2 + n
                        m = 1 - n
                        dve.wait_ge(S["u_ready"], t + 1)
                        dve.tensor_tensor_reduce(junk[:, 0:V], U_[:, 0:V], in_q[n], 1.0, 0.0, ALU.mult, ALU.add, qu[:, :]).then_inc(S["qu_ready"], 1)
                        step.tick(dve.tensor_copy(slots[:, N + 1, :], U_[:, 0:V]))
                        dve.wait_ge(S["qu_in_psum"], t + 1)
                        step(dve.scalar_tensor_tensor(out=logits[:, :], in0=last[:, :], scalar=QU[:, 0:1], in1=early[:, :], op0=ALU.mult, op1=ALU.add))
                        dve.tensor_reduce(nmax[:, :], logits[:, :], X, ALU.max, negate=True).then_inc(S["nmax_ready"], 1)
                        dve.wait_ge(S["exp_ready"], t + 1)
                        step(dve.reciprocal(rden[:, :], den[:, :]))
                        dve.tensor_scalar(a[:, 0:N], e_a[:, 0:N], rden[:, :], None, ALU.mult).then_inc(S["a_ready"], 1)
                        dve.wait_ge(S["a_ready"], t + 1)
                        step(dve.tensor_tensor_reduce(junk[:, :], a[:, 0:N], delta[:, :], 1.0, 0.0, ALU.mult, ALU.add, a[:, N:N + 1]))
                        dve.tensor_tensor_reduce(junk[:, :], a[:, 0:N], last[:, :], 1.0, 0.0, ALU.mult, ALU.add, a[:, N + 1:M]).then_inc(S["ax_ready"], 1)
                        dve.wait_ge(S["ea_ready"], t + 1)
                        step(dve.tensor_scalar(g[:, 0:N], ea[:, 0:N], 1.0, None, ALU.add))
                        step(dve.reciprocal(g[:, 0:N], g[:, 0:N]))
                        step.tick(dve.tensor_tensor(omg[:, 0:N], ea[:, 0:N], g[:, 0:N], ALU.mult))
                        step(dve.tensor_tensor(gab[:, 0:N], g[:, 0:N], a[:, 0:N], ALU.mult))
                        step(dve.tensor_tensor(w2[:, 0:N], omg[:, 0:N], col(n, Z.BA), ALU.mult))
                        step(dve.tensor_tensor_reduce(junk[:, :], w2[:, 0:N], delta[:, :], 1.0, 0.0, ALU.mult, ALU.add, w2[:, N:N + 1]))
                        step(dve.tensor_tensor_reduce(junk[:, :], w2[:, 0:N], last[:, :], 1.0, 0.0, ALU.mult, ALU.add, w2[:, N + 1:M]))
                        step.tick(dve.tensor_tensor(prod[:, :, :], slots[:, :, :], spread(w2, M), ALU.mult))
                        step(dve.tensor_tensor_reduce(junk[:, :], gab[:, 0:N], col(n, Z.BA), 1.0, 0.0, ALU.mult, ALU.add, cwr[:, :]))
                        step(dve.tensor_reduce(bind[:, :], prod[:, :, :].rearrange("p n d -> p d n"), X, ALU.add))
                        step(dve.scalar_tensor_tensor(out=bind[:, :], in0=in_wr[n], scalar=cwr[:, :], in1=bind[:, :], op0=ALU.mult, op1=ALU.add))
                        dve.tensor_tensor(bind_wide[:, :, :], bind[:, :].unsqueeze(1).to_broadcast([P, J, V]),
                                          part_of[:, :].unsqueeze(2).to_broadcast([P, J, V]), ALU.mult).then_inc(S["bind_ready"], 1)
                        step.tick(dve.tensor_tensor(c1[:, 0:N], gab[:, 0:N], col(n, Z.OMG2), ALU.mult))
                        step(dve.tensor_tensor(keep[:, 0:N], omg[:, 0:N], col(n, Z.OMG2), ALU.mult))
                        dve.tensor_tensor(keep_last[:, :], keep[:, 0:N], last[:, :], ALU.mult).then_inc(S["coef_ready"], 1)
                        step(dve.tensor_tensor(delta[:, :], delta[:, :], keep[:, 0:N], ALU.mult))
                        step.tick(dve.tensor_tensor(delta[:, :], delta[:, :], col(n, Z.G2), ALU.add))
                        dve.wait_ge(S["coef_ready"], t + 1)
                        step.tick(dve.tensor_copy(last[:, :], col(n, Z.C2)))
                        dve.wait_ge(loaded[m], i * 80 + 80 + 80 * n)
                        step.tick(query(in_q[m], half(0)))
                        dve.wait_ge(S["xh_in_psum"], t + 1)
                        dve.tensor_tensor(xh[:, :], C_[:, 0:H], col(n, Z.XH, H), ALU.add).then_inc(S["xh_ready"], 1)
                        dve.wait_ge(S["xh_ready"], t * 3 + 1)
                        for l in range(Z.L):
                            step.tick(dve.tensor_tensor(xhb[:, :], xh[:, :], bo[:, l, :], ALU.add))
                            if l == 0:
                                step.tick(query(in_q[m], slice(N // 2, M)))
                            else:
                                dve.wait_ge(S["lg_in_psum"], t + 2)
                                step.tick(dve.tensor_copy(extra[:, :], A[:, N:M + 1]))
                                step(dve.tensor_tensor(early[:, :], A[:, 0:N], keep[:, 0:N], ALU.mult))
                                for k, coef in enumerate((delta, keep_last, c1)):
                                    step(dve.scalar_tensor_tensor(out=early[:, :], in0=coef[:, 0:N], scalar=extra[:, k:k + 1], in1=early[:, :], op0=ALU.mult, op1=ALU.add))
                                dve.wait_ge(S["prod_r_ready"], t + 1)
                                step.tick(dve.tensor_tensor(slots[:, half(0), :], slots[:, half(0), :], spread(keep)[:, half(0), :], ALU.mult))
                            dve.wait_ge(S["qkv_in_psum"], t * 2 + l + 1)
                            dve.tensor_copy(qkv[:, :], E_[:, 0:3 * DH + 1]).then_inc(S["qkv_ready"], 1)
                            dve.wait_ge(S["qkv_ready"], t * 2 + l + 1)
                            q, k, v = (qkv[:, s * DH:(s + 1) * DH] for s in range(3))
                            step(dve.tensor_tensor_reduce(junk[:, 0:DH], k, k, 1.0, 1e-19, ALU.mult, ALU.add, ssq[:, :]))
                            dve.tensor_tensor_reduce(junk[:, 0:DH], k, q, 1.0, 0.0, ALU.mult, ALU.add, kq[:, :]).then_inc(S["ssq_ready"], 1)
                            dve.wait_ge(S["mem_ready"], t * 2 + l + 1)
                            step(dve.tensor_tensor(mprod[:, :, :, :], mem[l][:, :, :].unsqueeze(1).to_broadcast([P, 2, DH, DH]),
                                                   qkv[:, 0:2 * DH].rearrange("p (s j) -> p s j", s=2).unsqueeze(2).to_broadcast([P, 2, DH, DH]), ALU.mult))
                            step.tick(dve.tensor_reduce(msum[:, :, :], mprod[:, :, :, :], X, ALU.add))
                            dve.wait_ge(S["eb_ready"], t * 2 + l + 1)
                            step(dve.tensor_scalar(beta[:, :], eb[:, :], 1.0, None, ALU.add))
                            dve.wait_ge(S["nrm_ready"], t * 2 + l + 1)
                            step(dve.tensor_scalar(nrm[:, :], nrm[:, :], 1e-6, None, ALU.add))
                            step.tick(dve.reciprocal(beta[:, :], beta[:, :]))
                            step(dve.reciprocal(rk[:, :], nrm[:, :]))
                            step.tick(dve.tensor_scalar(kn[l][:, :], k, rk[:, :], None, ALU.mult))
                            step.tick(dve.tensor_tensor(rkq[:, :], kq[:, :], rk[:, :], ALU.mult))
                            step(dve.scalar_tensor_tensor(out=dv[l][:, :], in0=msum[:, 1, :], scalar=rk[:, :], in1=v, op0=ALU.mult, op1=ALU.subtract))
                            dve.tensor_scalar(dv[l][:, :], dv[l][:, :], beta[:, :], None, ALU.mult).then_inc(S["dv_ready"], 1)
                            dve.wait_ge(S["dv_ready"], t * 2 + l + 1)
                            step(dve.scalar_tensor_tensor(out=no[:, :], in0=dv[l][:, :], scalar=rkq[:, :], in1=msum[:, 0, :], op0=ALU.mult, op1=ALU.subtract))
                            dve.tensor_tensor(no_wide[:, :, :], no[:, :].unsqueeze(1).to_broadcast([P, J, DH]),
                                              part_of[:, :].unsqueeze(2).to_broadcast([P, J, DH]), ALU.mult).then_inc(S["no_ready"], 1)
                            if l == 0:
                                step(dve.tensor_reduce(part[:, half(0)], prod[:, half(0), :], X, ALU.add))
                            else:
                                step(dve.tensor_tensor(slots[:, half(1), :], slots[:, half(1), :], spread(keep)[:, half(1), :], ALU.mult))
                            dve.wait_ge(S["o_in_psum"], t * 2 + l + 1)
                            step(dve.tensor_tensor(xhb[:, :], G_[:, 0:H], xhb[:, :], ALU.add))
                            step(dve.bn_stats(stats[:, :], xhb[:, :]))
                            dve.memset(waiter[:, :], 0.0)
                            dve.bn_aggr(mv[:, :], stats[:, :]).then_inc(S["mv_ready"], 1)
                            if l == 0:
                                step.tick(dve.tensor_tensor_reduce(junk[:, 0:V], in_wr[n], in_q[m], 1.0, 0.0, ALU.mult, ALU.add, part[:, M:M + 1]))
                                dve.tensor_reduce(part[:, N // 2:M], prod[:, N // 2:M, :], X, ALU.add).then_inc(S["part_ready"], 1)
                            else:
                                dve.wait_ge(S["write_ready"], t + 1)
                                step.tick(dve.tensor_tensor(slots[:, half(0), :], slots[:, half(0), :], write[:, half(0), :], ALU.add))
                            dve.wait_ge(S["rstd_ready"], t * 2 + l + 1)
                            step(dve.tensor_scalar(xhb[:, :], xhb[:, :], mv[:, 0:1], rstd[:, :], ALU.subtract, ALU.mult))
                            step(dve.tensor_tensor(xhb[:, :], xhb[:, :], ln_g[:, l, :], ALU.mult))
                            if l == Z.L - 1:
                                dve.wait_ge(stored[n], i * 32 + 32)
                            dst = xh if l == 0 else out_x[n]
                            dve.tensor_tensor(dst[:, :], xhb[:, :], ln_b[:, l, :], ALU.add).then_inc(S["xh_ready"], 1)
                            dve.wait_ge(S["xh_ready"], t * 3 + l + 2)
                        dve.wait_ge(S["read_in_psum"], t + 1)
                        dve.tensor_reduce(out_r[n][:, :], R_[:, :].rearrange("p (n d) -> p d n", d=V), X, ALU.add).then_inc(S["read_ready"], 1)
                        dve.tensor_tensor(slots[:, half(1), :], slots[:, half(1), :], write[:, half(1), :], ALU.add).then_inc(S["step_done"], 1)
                        dve.wait_ge(S["step_done"], t + 1)
                    step.leave(STEPS // 2)


def scan_outputs(core, w, reads, states):
    nc = core.nc
    core.phase = "after_scan_"
    Z = ScanShapes
    with ExitStack() as c:
        sb = lambda n, s, d=F32: core.sbuf(n, s, d, c)
        sem = lambda n: core.sem(n, c)
        wo, op_w, ow = sb("wo", [Z.SD, D]), sb("op_w", [Z.H, D]), sb("ow", [D, D])
        rows = {n: sb(n, [P, D]) for n in ("sb_bo", "op_b", "oln_g", "oln_b", "ob")}
        r = [sb(f"r{n}", [P, GB, Z.SD]) for n in range(2)]
        x = [sb(f"x{n}", [P, GB, Z.H]) for n in range(2)]
        rT, xT = sb("rT", [Z.SD, GB, P]), sb("xT", [Z.H, GB, P])
        y, sq, yT = sb("y", [P, GB, D]), sb("sq", [P, GB, D]), sb("yT", [D, GB, P])
        mean, var = sb("mean", [P, GB]), sb("var", [P, GB])
        names = ("w_loaded", "rT_in_psum", "xT_in_psum", "rT_ready", "xT_ready", "y_in_psum", "centred", "squared", "var_ready", "rstd_ready",
                 "y_ready", "yT_in_psum", "yT_ready", "out_in_psum", "hidden_added", "chain", "act_chain")
        S = {n: sem(n) for n in names}
        loaded = [sem(f"loaded{n}") for n in range(2)]
        flat = lambda ap: ap[:, :, :].rearrange("p b d -> p (b d)")
        with nc.Block() as block:

            @block.sync
            def _(sp):
                for dst, name in ((wo, "sb_wo"), (op_w, "op_w"), (ow, "ow")):
                    sp.dma_start(dst[:, :], w[name]).then_inc(S["w_loaded"], 16)
                for name, dst in rows.items():
                    sp.dma_start(dst[:, :], across(w[name], P)).then_inc(S["w_loaded"], 16)
                sp.sem_inc(S["xT_ready"], 2)
                with sp.Fori(0, NG // 2) as i:
                    for n in range(2):
                        at = bass.ds(i * 2 * GB + n * GB, GB)
                        sp.wait_ge(S["xT_ready"], i * 2 + n + 1)
                        for j in range(Z.J):
                            sp.dma_start(r[n][:, :, Z.V * j:Z.V * j + Z.V], reads[:, j, at, :]).then_inc(loaded[n], 16)
                        sp.dma_start(x[n][:, :, :], states[:, at, :]).then_inc(loaded[n], 16)

            @block.tensor
            def _(pe):
                pe.wait_ge(S["w_loaded"], 8 * 16)
                with pe.Fori(0, NG // 2) as i:
                    for n in range(2):
                        g = i * 2 + n
                        pe.wait_ge(loaded[n], i * 80 + 80)
                        for b in range(GB):
                            mm = pe.transpose(core.bank[0][:, b * P:(b + 1) * P], r[n][:, b, :], core.ident[:, :])
                        mm.then_inc(S["rT_in_psum"], 1)
                        for b in range(GB):
                            mm = pe.transpose(core.bank[1][0:Z.H, b * P:(b + 1) * P], x[n][:, b, :], core.ident[:, :])
                        mm.then_inc(S["xT_in_psum"], 1)
                        pe.wait_ge(S["rT_ready"], g + 1)
                        pe.wait_ge(S["xT_ready"], g + 3)
                        for b in range(GB):
                            pe.matmul(core.bank[2][:, b * P:(b + 1) * P], rT[:, b, :], wo[:, :], start=True, stop=False)
                            mm = pe.matmul(core.bank[2][:, b * P:(b + 1) * P], xT[:, b, :], op_w[:, :], start=False, stop=True)
                        mm.then_inc(S["y_in_psum"], 1)
                        pe.wait_ge(S["y_ready"], g + 1)
                        for b in range(GB):
                            mm = pe.transpose(core.bank[3][:, b * P:(b + 1) * P], y[:, b, :], core.ident[:, :])
                        mm.then_inc(S["yT_in_psum"], 1)
                        pe.wait_ge(S["yT_ready"], g + 1)
                        for b in range(GB):
                            mm = pe.matmul(core.bank[4][:, b * P:(b + 1) * P], yT[:, b, :], ow[:, :], start=True, stop=True)
                        mm.then_inc(S["out_in_psum"], 1)

            @block.scalar
            def _(act):
                act.preload_act_table_set("natural_log_exp_and_others")
                step = Chain(act, S["act_chain"])
                with act.Fori(0, NG // 2) as i:
                    step.enter(i, 2)
                    for n in range(2):
                        g = i * 2 + n
                        act.wait_ge(S["rT_in_psum"], g + 1)
                        act.copy(flat(rT), core.bank[0][:, :]).then_inc(S["rT_ready"], 1)
                        act.wait_ge(S["xT_in_psum"], g + 1)
                        act.copy(flat(xT), core.bank[1][0:Z.H, :]).then_inc(S["xT_ready"], 1)
                        act.wait_ge(S["centred"], g + 1)
                        act.activation(flat(sq), flat(y), ACT.Square).then_inc(S["squared"], 1)
                        act.wait_ge(S["var_ready"], g + 1)
                        step(act.activation(var[:, :], var[:, :], ACT.Ln))
                        act.activation(var[:, :], var[:, :], ACT.Exp, scale=-0.5).then_inc(S["rstd_ready"], 1)
                        act.wait_ge(S["yT_in_psum"], g + 1)
                        act.copy(flat(yT), core.bank[3][:, :]).then_inc(S["yT_ready"], 1)
                    step.leave(NG // 2)

            @block.vector
            def _(dve):
                step = Chain(dve, S["chain"])
                dve.wait_ge(S["w_loaded"], 8 * 16)
                step(dve.tensor_tensor(rows["sb_bo"][:, :], rows["sb_bo"][:, :], rows["op_b"][:, :], ALU.add))
                wide = lambda name: rows[name][:, :].unsqueeze(1).to_broadcast([P, GB, D])
                each = lambda ap: ap[:, :].unsqueeze(2).to_broadcast([P, GB, D])
                with dve.Fori(0, NG // 2) as i:
                    step.enter(i, 2 * 6 + 2)
                    for n in range(2):
                        g = i * 2 + n
                        y3 = y[:, :, :]
                        dve.wait_ge(S["y_in_psum"], g + 1)
                        step(dve.tensor_tensor(y3, core.bank[2][:, :].rearrange("p (b d) -> p b d", b=GB), wide("sb_bo"), ALU.add))
                        step(dve.tensor_reduce(mean[:, :], y3, X, ALU.add))
                        step(dve.tensor_scalar(mean[:, :], mean[:, :], 1.0 / D, None, ALU.mult))
                        dve.tensor_tensor(y3, y3, each(mean), ALU.subtract).then_inc(S["centred"], 1)
                        dve.wait_ge(S["squared"], g + 1)
                        step(dve.tensor_reduce(var[:, :], sq[:, :, :], X, ALU.add))
                        dve.tensor_scalar(var[:, :], var[:, :], 1.0 / D, EPS, ALU.mult, ALU.add).then_inc(S["var_ready"], 1)
                        dve.wait_ge(S["rstd_ready"], g + 1)
                        step(dve.tensor_tensor(y3, y3, each(var), ALU.mult))
                        step(dve.tensor_tensor(y3, y3, wide("oln_g"), ALU.mult))
                        dve.tensor_tensor(y3, y3, wide("oln_b"), ALU.add).then_inc(S["y_ready"], 1)
                        dve.wait_ge(S["out_in_psum"], g + 1)
                        step(dve.tensor_tensor(sq[:, :, :], core.bank[4][:, :].rearrange("p (b d) -> p b d", b=GB), wide("ob"), ALU.add))
                        hid = core.hidden[:, bass.ds(i * 2 * GB + n * GB, GB), :]
                        dve.tensor_tensor(hid, sq[:, :, :], hid, ALU.add).then_inc(S["hidden_added"], 1)
                    step.leave(NG // 2)


def self_attention(core, x, xn, g_row, b_row, wq, wk, wv, wo):
    nc = core.nc
    core.phase = "mha_"
    NH, DH = 8, 16
    SCALE = DH ** -0.5
    HALF = NH // 2 * P
    with ExitStack() as c:
        sb = lambda n, s, d=F32: core.sbuf(n, s, d, c)
        sem = lambda n: core.sem(n, c)
        W = {n: sb(n, [D, D]) for n in ("wq", "wk", "wv", "wo")}
        g_all, b_all = sb("g_all", [P, D]), sb("b_all", [P, D])
        head = sb("head", [P, NH])
        x1, xT, qT, kT, v = (sb(n, [P, GB, P]) for n in ("x1", "xT", "qT", "kT", "v"))
        kd = [sb(f"kd{n}", [P, NH, P]) for n in range(2)]
        probs = [sb(f"probs{n}", [P, NH, P]) for n in range(2)]
        pT = sb("pT", [P, NH, P])
        top, nmax, den, rden = (sb(n, [P, 2, NH]) for n in ("top", "nmax", "den", "rden"))
        o, oT = sb("o", [P, GB, D]), sb("oT", [D, GB, P])
        names = ("w_loaded", "consts_ready", "x1_ready", "xT_in_psum", "xT_ready", "q_in_psum", "k_in_psum", "v_in_psum", "q_ready", "k_ready",
                 "v_ready", "kd_ready", "scores_ready", "nmax_ready", "probs_ready", "pT_in_psum", "pT_ready", "o_in_psum", "o_ready",
                 "oT_in_psum", "oT_ready", "out_in_psum", "x_done", "chain")
        S = {n: sem(n) for n in names}
        flat = lambda ap: ap[:, :, :].rearrange("p b d -> p (b d)")
        bank = core.bank
        with nc.Block() as block:

            @block.sync
            def _(sp):
                for name, src in (("wq", wq), ("wk", wk), ("wv", wv), ("wo", wo)):
                    sp.dma_start(W[name][:, :], src).then_inc(S["w_loaded"], 16)
                sp.dma_start(g_all[:, :], across(g_row, P)).then_inc(S["w_loaded"], 16)
                sp.dma_start(b_all[:, :], across(b_row, P)).then_inc(S["w_loaded"], 16)

            @block.gpsimd
            def _(pool):
                pool.memset(head[:, :], 1.0).then_inc(S["consts_ready"], 1)
                pool.wait_ge(S["consts_ready"], 1)
                pool.affine_select(out=head[:, :], in_=head[:, :], compare_op=ALU.is_ge, fill=0.0, base=0,
                                   pattern=[[-DH, NH]], channel_multiplier=1).then_inc(S["consts_ready"], 1)
                pool.wait_ge(S["consts_ready"], 2)
                pool.affine_select(out=head[:, :], in_=head[:, :], compare_op=ALU.is_ge, fill=0.0, base=DH - 1,
                                   pattern=[[DH, NH]], channel_multiplier=-1).then_inc(S["consts_ready"], 1)

            @block.tensor
            def _(pe):
                pe.wait_ge(S["w_loaded"], 6 * 16)
                pe.sem_inc(S["x_done"], 1)
                pe.sem_inc(S["probs_ready"], 1)
                pe.sem_inc(S["o_ready"], 1)
                with pe.Fori(0, NG // 2) as i:
                    for n in range(2):
                        g = i * 2 + n
                        pe.wait_ge(S["x1_ready"], g + 1)
                        for b in range(GB):
                            mm = pe.transpose(bank[0][:, b * P:(b + 1) * P], x1[:, b, :], core.ident[:, :])
                        mm.then_inc(S["xT_in_psum"], 1)
                        pe.wait_ge(S["x_done"], g + 1)
                        pe.wait_ge(S["xT_ready"], g + 1)
                        pe.matmul(bank[1][:, :], W["wq"][:, :], flat(xT), start=True, stop=True).then_inc(S["q_in_psum"], 1)
                        pe.matmul(bank[2][:, :], W["wk"][:, :], flat(xT), start=True, stop=True).then_inc(S["k_in_psum"], 1)
                        for b in range(GB):
                            mm = pe.matmul(bank[3][:, b * P:(b + 1) * P], xT[:, b, :], W["wv"][:, :], start=True, stop=True)
                        mm.then_inc(S["v_in_psum"], 1)
                        pe.wait_ge(S["q_ready"], g + 1)
                        for b in range(GB + 1):
                            at = i * 2 * GB + n * GB + b
                            if b < GB:
                                pe.wait_ge(S["kd_ready"], at + 1)
                                pe.wait_ge(S["probs_ready"], at + 1)
                                for half in range(2):
                                    mm = pe.matmul(bank[4 + half][:, :], qT[:, b, :],
                                                   kd[b % 2][:, half * 4:half * 4 + 4, :].rearrange("p h m -> p (h m)"), start=True, stop=True)
                                mm.then_inc(S["scores_ready"], 1)
                            if b >= 1:
                                pe.wait_ge(S["probs_ready"], at + 1)
                                for h in range(NH):
                                    mm = pe.transpose(bank[6 + h // 4][0:T, h % 4 * P:(h % 4 + 1) * P], probs[(b - 1) % 2][:, h, 0:T], core.ident[:, :])
                                mm.then_inc(S["pT_in_psum"], 1)
                                pe.wait_ge(S["o_ready"], at)
                                pe.wait_ge(S["pT_ready"], at)
                                for h in range(NH):
                                    mm = pe.matmul(bank[0][:, (b - 1) * P + h * DH:(b - 1) * P + (h + 1) * DH], pT[0:T, h, :],
                                                   v[0:T, b - 1, h * DH:(h + 1) * DH], start=True, stop=True)
                                mm.then_inc(S["o_in_psum"], 1)
                        pe.wait_ge(S["o_ready"], i * 2 * GB + (n + 1) * GB + 1)
                        for b in range(GB):
                            mm = pe.transpose(bank[1][:, b * P:(b + 1) * P], o[:, b, :], core.ident[:, :])
                        mm.then_inc(S["oT_in_psum"], 1)
                        pe.wait_ge(S["oT_ready"], g + 1)
                        for b in range(GB):
                            mm = pe.matmul(bank[2][:, b * P:(b + 1) * P], oT[:, b, :], W["wo"][:, :], start=True, stop=True)
                        mm.then_inc(S["out_in_psum"], 1)

            @block.scalar
            def _(act):
                act.preload_act_table_set("exp_and_others")
                with act.Fori(0, NG // 2) as i:
                    for n in range(2):
                        g = i * 2 + n
                        for src, dst, ready, bk in (("xT_in_psum", xT, "xT_ready", 0), ("q_in_psum", qT, "q_ready", 1),
                                                    ("k_in_psum", kT, "k_ready", 2), ("v_in_psum", v, "v_ready", 3)):
                            act.wait_ge(S[src], g + 1)
                            act.copy(flat(dst), bank[bk][:, :]).then_inc(S[ready], 1)
                        for b in range(GB + 1):
                            at = i * 2 * GB + n * GB + b
                            if b >= 1:
                                act.wait_ge(S["pT_in_psum"], at)
                                act.copy(pT[0:T, :, :].rearrange("p h m -> p (h m)"), core.banks[0:T, 6 * 512:8 * 512]).then_inc(S["pT_ready"], 1)
                            if b < GB:
                                act.wait_ge(S["nmax_ready"], at + 1)
                                for h in range(NH):
                                    ex = act.activation(probs[b % 2][:, h, 0:T], bank[4 + h // 4][:, h % 4 * P:h % 4 * P + T], ACT.Exp,
                                                        bias=nmax[:, b % 2, h:h + 1], scale=SCALE, accum_out=den[:, b % 2, h:h + 1])
                                ex.then_inc(S["probs_ready"], 1)
                        act.wait_ge(S["oT_in_psum"], g + 1)
                        act.copy(flat(oT), bank[1][:, :]).then_inc(S["oT_ready"], 1)

            @block.vector
            def _(dve):
                step = Chain(dve, S["chain"])
                dve.wait_ge(S["w_loaded"], 6 * 16)
                dve.wait_ge(S["consts_ready"], 3)
                wide = lambda ap: ap[:, :].unsqueeze(1).to_broadcast([P, GB, D])
                with dve.Fori(0, NG // 2) as i:
                    step.enter(i, 2 * (1 + 2 * GB))
                    for n in range(2):
                        g = i * 2 + n
                        at3 = bass.ds(i * 2 * GB + n * GB, GB)
                        step(dve.tensor_tensor(x1[:, :, :], xn[:, at3, :], wide(g_all), ALU.mult))
                        dve.tensor_tensor(x1[:, :, :], x1[:, :, :], wide(b_all), ALU.add).then_inc(S["x1_ready"], 1)
                        dve.wait_ge(S["k_ready"], g + 1)
                        for b in range(GB + 1):
                            at = i * 2 * GB + n * GB + b
                            if b < GB:
                                dve.tensor_tensor(kd[b % 2][:, :, :], kT[:, b, :].unsqueeze(1).to_broadcast([P, NH, P]),
                                                  head[:, :].unsqueeze(2).to_broadcast([P, NH, P]), ALU.mult).then_inc(S["kd_ready"], 1)
                                dve.wait_ge(S["scores_ready"], at + 1)
                                step(dve.tensor_reduce(top[:, b % 2, :], core.banks[:, 4 * 512:6 * 512].rearrange("p (h m) -> p h m", h=NH)[:, :, 0:T], X, ALU.max))
                                dve.tensor_scalar(nmax[:, b % 2, :], top[:, b % 2, :], -SCALE, None, ALU.mult).then_inc(S["nmax_ready"], 1)
                            if b >= 1:
                                dve.wait_ge(S["o_in_psum"], at)
                                step(dve.reciprocal(rden[:, 0, :], den[:, (b - 1) % 2, :]))
                                dve.tensor_tensor(o[:, b - 1, :].rearrange("p (h d) -> p h d", h=NH), bank[0][:, (b - 1) * P:b * P].rearrange("p (h d) -> p h d", h=NH),
                                                  rden[:, 0, :].unsqueeze(2).to_broadcast([P, NH, DH]), ALU.mult).then_inc(S["o_ready"], 1)
                        dve.wait_ge(S["out_in_psum"], g + 1)
                        dve.tensor_tensor(x[:, at3, :], bank[2][:, :].rearrange("p (b d) -> p b d", b=GB), x[:, at3, :], ALU.add).then_inc(S["x_done"], 1)
                    step.leave(NG // 2)


class Dispatch:
    E, TOPK, C, CAP = 64, 2, 254, 256
    F = 512
    ROWS = E * CAP + TOPK * B * P


def route_two_of_64(core, xn, w, x2, put, take, gate):
    nc = core.nc
    core.phase = "route1_"
    Z = Dispatch
    E, K = Z.E, Z.TOPK
    W = E + 8 - 1
    FAR = 1e30
    PER = 49
    with ExitStack() as c:
        sb = lambda n, s, d=F32: core.sbuf(n, s, d, c)
        sem = lambda n: core.sem(n, c)
        wr = sb("wr", [D, E])
        g_all, b_all = sb("g_all", [P, D]), sb("b_all", [P, D])
        before, ones = sb("before", [P, P]), sb("ones", [P, P])
        real = sb("real", [P, 1])
        base = sb("base", [P, E])
        spill = sb("spill", [P, B, K])
        sentinels = sb("sentinels", [P, 7])
        stage, xT = sb("stage", [P, GB, D]), sb("xT", [P, GB, P])
        probs, expo = sb("probs", [P, GB, W]), sb("expo", [P, GB, E])
        top, total = sb("top", [P, GB]), sb("total", [P, GB])
        best = sb("best", [P, GB, 8])
        v12 = sb("v12", [P, GB, K])
        marked = [sb(f"marked{k}", [P, GB, W]) for k in range(K)]
        sel = sb("sel", [P, GB, E])
        seen = sb("seen", [P, GB + 1, E])
        pos, row, prod = sb("pos", [P, GB, E]), sb("row", [P, GB, E]), sb("prod", [P, GB, E])
        p_k, r_k, keep, over = (sb(n, [P, GB, K]) for n in ("p_k", "r_k", "keep", "over"))
        waiter = sb("waiter", [1, 1])
        names = ("w_loaded", "consts_ready", "staged", "xT_in_psum", "xT_ready", "logits_ready", "shifted", "exp_ready",
                 "sel_ready", "pos_in_psum", "group_done", "chain", "pool_chain")
        S = {n: sem(n) for n in names}
        flat = lambda ap: ap[:, :, :].rearrange("p b d -> p (b d)")
        bank = core.bank
        with nc.Block() as block:

            @block.sync
            def _(sp):
                sp.dma_start(wr[:, :], w["wr"]).then_inc(S["w_loaded"], 16)
                sp.dma_start(g_all[:, :], across(w["ln2_g"], P)).then_inc(S["w_loaded"], 16)
                sp.dma_start(b_all[:, :], across(w["ln2_b"], P)).then_inc(S["w_loaded"], 16)

            @block.gpsimd
            def _(pool):
                step = Chain(pool, S["pool_chain"])
                step(pool.memset(before[:, :], 1.0))
                step(pool.affine_select(out=before[:, :], in_=before[:, :], compare_op=ALU.is_gt, fill=0.0, base=0,
                                        pattern=[[1, P]], channel_multiplier=-1))
                step(pool.memset(ones[:, :], 1.0))
                step(pool.memset(real[:, :], 1.0))
                step(pool.affine_select(out=real[:, :], in_=real[:, :], compare_op=ALU.is_gt, fill=0.0, base=T,
                                        pattern=[[0, 1]], channel_multiplier=-1))
                step(pool.iota(base[:, :], pattern=[[Z.CAP, E]], base=0, channel_multiplier=0, allow_small_or_imprecise_dtypes=True))
                step(pool.iota(spill[:, :, :], pattern=[[K * P, B], [P, K]], base=E * Z.CAP, channel_multiplier=1, allow_small_or_imprecise_dtypes=True))
                for n in range(7):
                    step(pool.memset(sentinels[:, n:n + 1], -FAR * (n + 1)))
                pool.memset(seen[:, :, :], 0.0).then_inc(S["consts_ready"], 1)

            @block.tensor
            def _(pe):
                pe.wait_ge(S["w_loaded"], 3 * 16)
                pe.wait_ge(S["consts_ready"], 1)
                with pe.Fori(0, NG) as g:
                    pe.wait_ge(S["staged"], g + 1)
                    for b in range(GB):
                        mm = pe.transpose(bank[0][:, b * P:(b + 1) * P], stage[:, b, :], core.ident[:, :])
                    mm.then_inc(S["xT_in_psum"], 1)
                    pe.wait_ge(S["xT_ready"], g + 1)
                    for b in range(GB):
                        mm = pe.matmul(bank[1][:, b * E:(b + 1) * E], xT[:, b, :], wr[:, :], start=True, stop=True)
                    mm.then_inc(S["logits_ready"], 1)
                    pe.wait_ge(S["sel_ready"], g + 1)
                    pe.matmul(bank[2][:, 0:GB * E], before[:, :], flat(sel), start=True, stop=False)
                    pe.matmul(bank[2][:, 0:GB * E], ones[:, :], seen[:, 0:GB, :].rearrange("p b e -> p (b e)"), start=False, stop=True).then_inc(S["pos_in_psum"], 1)

            @block.scalar
            def _(act):
                act.preload_act_table_set("exp_and_others")
                with act.Fori(0, NG) as g:
                    act.wait_ge(S["xT_in_psum"], g + 1)
                    act.copy(flat(xT), bank[0][:, :]).then_inc(S["xT_ready"], 1)
                    act.wait_ge(S["shifted"], g + 1)
                    act.activation(flat(expo), flat(expo), ACT.Exp).then_inc(S["exp_ready"], 1)

            @block.vector
            def _(dve):
                step = Chain(dve, S["chain"])
                dve.wait_ge(S["w_loaded"], 3 * 16)
                dve.wait_ge(S["consts_ready"], 1)
                wide = lambda ap: ap[:, :].unsqueeze(1).to_broadcast([P, GB, D])
                each = lambda ap, n: ap.unsqueeze(2).to_broadcast([P, GB, n])
                step(dve.tensor_copy(probs[:, :, E:W], sentinels[:, :].unsqueeze(1).to_broadcast([P, GB, 7])))
                with dve.Fori(0, NG) as g:
                    step.enter(g, PER)
                    tiles = bass.ds(g * GB, GB)
                    step(dve.tensor_tensor(stage[:, :, :], xn[:, tiles, :], wide(g_all), ALU.mult))
                    dve.tensor_tensor(stage[:, :, :], stage[:, :, :], wide(b_all), ALU.add).then_inc(S["staged"], 1)
                    dve.wait_ge(S["staged"], g + 1)
                    step.tick(dve.tensor_copy(x2[:, tiles, :], stage[:, :, :]))
                    dve.wait_ge(S["logits_ready"], g + 1)
                    lg = bank[1][:, 0:GB * E].rearrange("p (b e) -> p b e", b=GB)
                    step(dve.tensor_reduce(top[:, :], lg, X, ALU.max))
                    dve.tensor_tensor(expo[:, :, :], lg, each(top[:, :], E), ALU.subtract).then_inc(S["shifted"], 1)
                    dve.wait_ge(S["exp_ready"], g + 1)
                    step(dve.tensor_reduce(total[:, :], expo[:, :, :], X, ALU.add))
                    step(dve.reciprocal(total[:, :], total[:, :]))
                    step(dve.tensor_tensor(probs[:, :, 0:E], expo[:, :, :], each(total[:, :], E), ALU.mult))
                    dve.memset(waiter[:, :], 0.0)
                    for b in range(GB):
                        step.tick(dve.max(best[:, b, :], probs[:, b, 0:E]))
                    step.settle()
                    step(dve.tensor_copy(v12[:, :, :], best[:, :, 0:K]))
                    for k in reversed(range(K)):
                        step(dve.tensor_copy(best[:, :, k + 1:8], sentinels[:, 0:7 - k].unsqueeze(1).to_broadcast([P, GB, 7 - k])))
                        dve.memset(waiter[:, :], 0.0)
                        for b in range(GB):
                            step.tick(dve.match_replace(marked[k][:, b, :], best[:, b, :], probs[:, b, :], FAR))
                        step.settle()
                    for k in range(K):
                        step.tick(dve.tensor_scalar(marked[k][:, :, 0:E], marked[k][:, :, 0:E], FAR, real[:, :], ALU.is_ge, ALU.mult))
                    step.settle()
                    step(dve.tensor_copy(sel[:, :, :], marked[1][:, :, 0:E]))
                    step.tick(dve.tensor_tensor(marked[1][:, :, 0:E], marked[1][:, :, 0:E], marked[0][:, :, 0:E], ALU.subtract))
                    for b in range(GB):
                        ins = dve.tensor_tensor(seen[:, b + 1, :], seen[:, b, :], sel[:, b, :], ALU.add)
                        if b < GB - 1:
                            step(ins)
                    ins.then_inc(S["sel_ready"], 1)
                    dve.wait_ge(S["pos_in_psum"], g + 1)
                    step.tick(dve.tensor_copy(seen[:, 0, :], seen[:, GB, :]))
                    step(dve.tensor_copy(pos[:, :, :], bank[2][:, 0:GB * E].rearrange("p (b e) -> p b e", b=GB)))
                    step(dve.tensor_tensor(row[:, :, :], pos[:, :, :], base[:, :].unsqueeze(1).to_broadcast([P, GB, E]), ALU.add))
                    for k in range(K):
                        for src, dst in ((pos, p_k), (row, r_k)):
                            step(dve.tensor_tensor(prod[:, :, :], marked[k][:, :, 0:E], src[:, :, :], ALU.mult))
                            step(dve.tensor_reduce(dst[:, :, k], prod[:, :, :], X, ALU.add))
                    step.tick(dve.tensor_scalar(keep[:, :, :], p_k[:, :, :], float(Z.C), real[:, :], ALU.is_lt, ALU.mult))
                    step(dve.tensor_scalar(over[:, :, :], p_k[:, :, :], float(1 - Z.C), 0.0, ALU.add, ALU.max))
                    step(dve.tensor_tensor(take[:, tiles, :], r_k[:, :, :], over[:, :, :], ALU.subtract))
                    step(dve.tensor_tensor(r_k[:, :, :], r_k[:, :, :], spill[:, tiles, :], ALU.subtract))
                    step(dve.tensor_tensor(r_k[:, :, :], r_k[:, :, :], keep[:, :, :], ALU.mult))
                    step(dve.tensor_tensor(put[:, tiles, :], r_k[:, :, :], spill[:, tiles, :], ALU.add))
                    step(dve.tensor_tensor(total[:, :], v12[:, :, 0], v12[:, :, 1], ALU.add))
                    step(dve.reciprocal(total[:, :], total[:, :]))
                    step(dve.tensor_tensor(v12[:, :, :], v12[:, :, :], each(total[:, :], K), ALU.mult))
                    step(dve.tensor_tensor(gate[:, tiles, :], v12[:, :, :], keep[:, :, :], ALU.mult))
                    step.leave(NG)


def experts_dispatched(core, x, x2, put, take, gate, w, buf, results):
    nc = core.nc
    core.phase = "experts1_"
    Z = Dispatch
    E, K, F = Z.E, Z.TOPK, Z.F
    FC = F // P
    R = Z.CAP // P
    with ExitStack() as c:
        sb = lambda n, s, d=F32: core.sbuf(n, s, d, c)
        sem = lambda n: core.sem(n, c)
        put_i, take_i = sb("put_i", [P, B, K], U32), sb("take_i", [P, B, K], U32)
        b1, b1T = sb("b1", [E, F]), sb("b1T", [P, FC, E])
        b2 = sb("b2", [1, E * D])
        ones = sb("ones", [1, P])
        w1 = [sb(f"w1_{n}", [D, F]) for n in range(2)]
        w2 = [sb(f"w2_{n}", [P, FC, D]) for n in range(2)]
        xe = [sb(f"xe{n}", [P, R, D]) for n in range(2)]
        xT = [sb(f"xT{n}", [D, R * P]) for n in range(2)]
        hT = [sb(f"hT{n}", [P, FC, R * P]) for n in range(2)]
        y = [sb(f"y{n}", [P, R, D]) for n in range(2)]
        back = [sb(f"back{n}", [P, K, D]) for n in range(4)]
        names = ("consts_loaded", "index_ready", "scattered", "b1T_in_psum", "b1T_ready", "ones_ready", "xT_in_psum", "xT_ready",
                 "up_in_psum", "h_ready", "y_in_psum", "y_ready", "chain")
        S = {n: sem(n) for n in names}
        w_loaded = [sem(f"w_loaded{n}") for n in range(2)]
        x_loaded = [sem(f"x_loaded{n}") for n in range(2)]
        y_stored = [sem(f"y_stored{n}") for n in range(2)]
        gathered = [sem(f"gathered{n}") for n in range(4)]
        bank = core.bank
        with nc.Block() as block:

            @block.gpsimd
            def _(pool):
                pool.wait_ge(S["index_ready"], 2)
                for b in range(B):
                    for k in range(K):
                        pool.indirect_dma_start(out=buf, out_offset=bass.IndirectOffsetOnAxis(ap=put_i[:, b, k:k + 1], axis=0),
                                                in_=x2[:, b, :], in_offset=None).then_inc(S["scattered"], 16)

            @block.sync
            def _(sp):
                sp.dma_start(b1[:, :], w["b1"]).then_inc(S["consts_loaded"], 16)
                sp.dma_start(b2[:, :], w["b2"].rearrange("(a e) d -> a (e d)", a=1)).then_inc(S["consts_loaded"], 16)

                def load_w(e, n):
                    sp.dma_start(w1[n][:, :], w["w1"][bass.ds(e, 1), :, :].rearrange("e c f -> (e c) f")).then_inc(w_loaded[n], 16)
                    sp.dma_start(w2[n][:, :, :], w["w2"][bass.ds(e, 1), :, :].rearrange("e (k f) c -> (e f) k c", k=FC)).then_inc(w_loaded[n], 16)

                def load_x(e, n):
                    sp.dma_start(xe[n][:, :, :], buf[bass.ds(e * Z.CAP, Z.CAP), :].rearrange("(p r) d -> p r d", r=R)).then_inc(x_loaded[n], 16)

                def store(e, n):
                    sp.wait_ge(S["y_ready"], e + 1)
                    sp.dma_start(results[bass.ds(e * Z.CAP, Z.CAP), :].rearrange("(p r) d -> p r d", r=R), y[n][:, :, :]).then_inc(y_stored[n], 16)

                for n in range(2):
                    sp.sem_inc(y_stored[n], 16)
                    load_w(n, n)
                sp.wait_ge(S["scattered"], 16 * B * K)
                for n in range(2):
                    load_x(n, n)
                with sp.Fori(0, E // 2 - 1) as i:
                    for n in range(2):
                        store(i * 2 + n, n)
                        load_w(i * 2 + n + 2, n)
                        load_x(i * 2 + n + 2, n)
                for n in range(2):
                    store(E - 2 + n, n)
                for n in range(2):
                    sp.wait_ge(y_stored[n], 16 * (E // 2 + 1))

            @block.tensor
            def _(pe):
                pe.wait_ge(S["consts_loaded"], 32)
                for k in range(FC):
                    mm = pe.transpose(bank[0][:, k * E:(k + 1) * E], b1[:, k * P:(k + 1) * P], core.ident[0:E, 0:E])
                mm.then_inc(S["b1T_in_psum"], 1)
                pe.wait_ge(S["b1T_ready"], 1)
                pe.wait_ge(S["ones_ready"], 1)
                with pe.Fori(0, E // 2) as i:
                    for n in range(2):
                        e = i * 2 + n
                        pe.wait_ge(x_loaded[n], i * 16 + 16)
                        for r in range(R):
                            mm = pe.transpose(bank[n][:, r * P:(r + 1) * P], xe[n][:, r, :], core.ident[:, :])
                        mm.then_inc(S["xT_in_psum"], 1)
                        pe.wait_ge(w_loaded[n], i * 32 + 32)
                        pe.wait_ge(S["xT_ready"], e + 1)
                        for k in range(FC):
                            mm = pe.matmul(bank[2 + 2 * n + k // 2][:, k % 2 * R * P:(k % 2 + 1) * R * P], w1[n][:, k * P:(k + 1) * P], xT[n][:, :],
                                           start=True, stop=True)
                            if k % 2 == 1:
                                mm.then_inc(S["up_in_psum"], 1)
                        for r in range(R):
                            pe.matmul(bank[6 + n][:, r * D:(r + 1) * D], ones[:, :], b2[:, bass.ds(e * D, D)], start=True, stop=False)
                            if r == 0:
                                pe.wait_ge(S["h_ready"], e + 1)
                            for k in range(FC):
                                mm = pe.matmul(bank[6 + n][:, r * D:(r + 1) * D], hT[n][:, k, r * P:(r + 1) * P], w2[n][:, k, :],
                                               start=False, stop=(k == FC - 1))
                        mm.then_inc(S["y_in_psum"], 1)

            @block.scalar
            def _(act):
                act.wait_ge(S["b1T_in_psum"], 1)
                act.copy(b1T[:, :, :].rearrange("p k e -> p (k e)"), bank[0][:, 0:FC * E]).then_inc(S["b1T_ready"], 1)
                act.wait_ge(S["b1T_ready"], 1)
                with act.Fori(0, E // 2) as i:
                    for n in range(2):
                        e = i * 2 + n
                        for k in range(FC):
                            act.wait_ge(S["up_in_psum"], i * 4 + n * 2 + k // 2 + 1)
                            ac = act.activation(hT[n][:, k, :], bank[2 + 2 * n + k // 2][:, k % 2 * R * P:(k % 2 + 1) * R * P], ACT.Gelu_apprx_tanh,
                                                bias=b1T[:, k, bass.ds(e, 1)])
                        ac.then_inc(S["h_ready"], 1)

            @block.vector
            def _(dve):
                dve.tensor_copy(put_i[:, :, :], put[:, :, :]).then_inc(S["index_ready"], 1)
                dve.tensor_copy(take_i[:, :, :], take[:, :, :]).then_inc(S["index_ready"], 1)
                dve.memset(ones[:, :], 1.0).then_inc(S["ones_ready"], 1)
                with dve.Fori(0, E // 2) as i:
                    for n in range(2):
                        e = i * 2 + n
                        dve.wait_ge(S["xT_in_psum"], e + 1)
                        dve.tensor_copy(xT[n][:, :], bank[n][:, 0:R * P]).then_inc(S["xT_ready"], 1)
                        dve.wait_ge(y_stored[n], i * 16 + 16)
                        dve.wait_ge(S["y_in_psum"], e + 1)
                        dve.tensor_copy(y[n][:, :, :].rearrange("p r d -> p (r d)"), bank[6 + n][:, 0:R * D]).then_inc(S["y_ready"], 1)

        with nc.Block() as block:

            @block.gpsimd
            def _(pool):
                for b in range(B):
                    if b >= 4:
                        pool.wait_ge(S["chain"], 3 * (b - 3))
                    for k in range(K):
                        pool.indirect_dma_start(out=back[b % 4][:, k, :], out_offset=None, in_=results,
                                                in_offset=bass.IndirectOffsetOnAxis(ap=take_i[:, b, k:k + 1], axis=0)).then_inc(gathered[b % 4], 16)

            @block.vector
            def _(dve):
                step = Chain(dve, S["chain"])
                for b in range(B):
                    step(dve.tensor_tensor(core.hidden[:, b, :], core.hidden[:, b, :], x[:, b, :], ALU.add))
                    dve.wait_ge(gathered[b % 4], 32 * (b // 4 + 1))
                    for k in range(K):
                        step(dve.scalar_tensor_tensor(out=core.hidden[:, b, :], in0=back[b % 4][:, k, :], scalar=gate[:, b, k:k + 1],
                                                      in1=core.hidden[:, b, :], op0=ALU.mult, op1=ALU.add))


def audio_tower(nc, w, out):
    l1 = {k[len("L1_attn_"):]: v for k, v in w.items() if k.startswith("L1_attn_")}
    record = nc.dram_tensor("record", (P, B, ScanShapes.F), F32, kind="Internal").ap()
    record_part = nc.dram_tensor("record_part", (P, ScanShapes.J, B, 2 * ScanShapes.V), F32, kind="Internal").ap()
    reads = nc.dram_tensor("reads", (P, ScanShapes.J, B, ScanShapes.V), F32, kind="Internal").ap()
    states = nc.dram_tensor("states", (P, B, ScanShapes.H), F32, kind="Internal").ap()
    buf = nc.dram_tensor("dispatched", (Dispatch.ROWS, D), F32, kind="Internal").ap()
    results = nc.dram_tensor("results", (Dispatch.E * Dispatch.CAP, D), F32, kind="Internal").ap()
    buf0 = nc.dram_tensor("dispatched0", (Sparse.ROWS, D), F32, kind="Internal").ap()
    results0 = nc.dram_tensor("results0", (Sparse.TILES * P, D), F32, kind="Internal").ap()
    with ExitStack() as ctx:
        core = Core(nc, ctx)
        embed_patches(core, w["x"], w["L0_tok_W"], w["L0_tok_b"])
        with ExitStack() as c:
            core.phase = ""
            xn = core.sbuf("xn", [P, B, D], F32, c)
            with ExitStack() as cc:
                sq = core.sbuf("sq", [P, B, D], F32, cc)
                normalize(core, "ln0", core.hidden, xn, sq)
                channel_attention(core, xn, w["L0_attn_W_qkv"], w["L0_attn_W_o"],
                                  [buf0[0:Sparse.ROUTED * P, :], buf[0:Dispatch.E * Dispatch.CAP, :]])
        core.phase = ""
        l0f = {k[len("L0_ffn_"):]: v for k, v in w.items() if k.startswith("L0_ffn_")}
        with ExitStack() as c:
            E, H, HS = Sparse.E, Sparse.H, Sparse.HS
            w_up = core.sbuf("w_up", [P, E + 1, 2 * H], F32, c)
            tile_expert = core.sbuf("tile_expert", [1, Sparse.TILES], I32, c)
            take = core.sbuf("take0", [P, B, Sparse.TOPK], F32, c)
            weight = core.sbuf("weight0", [P, B, Sparse.TOPK], F32, c)
            with ExitStack() as cc:
                xn = core.sbuf("xn0", [P, B, D], F32, cc)
                with ExitStack() as ccc:
                    sq = core.sbuf("sq1", [P, B, D], F32, ccc)
                    normalize(core, "ln1", core.hidden, xn, sq)
                core.phase = ""
                combine = core.sbuf("combine", [P, B, E], F32, cc)
                route_six_of_64(core, xn, combine, l0f["router_w"], l0f["bias_corr"],
                                [(w_up[:, 0:E, 0:H], l0f["Wg"].rearrange("e c h -> c e h")),
                                 (w_up[:, 0:E, H:2 * H], l0f["Wu"].rearrange("e c h -> c e h")),
                                 (w_up[:, E, 0:HS], l0f["sWg"]), (w_up[:, E, H:H + HS], l0f["sWu"])],
                                [w_up[:, E, HS:H], w_up[:, E, H + HS:2 * H]])
                dispatch_six(core, xn, combine, buf0, take, weight, tile_expert)
            experts_sparse(core, l0f, w_up, buf0, results0, tile_expert)
            collect_six(core, take, weight, results0)
        with ExitStack() as c:
            core.phase = ""
            xn = core.sbuf("xn2", [P, B, D], F32, c)
            with ExitStack() as cc:
                core.phase = ""
                sq = core.sbuf("sq2", [P, B, D], F32, cc)
                normalize(core, "ln2", core.hidden, xn, sq)
            scan_inputs(core, xn, l1, record_part, record)
        scan_tokens(core, l1, record_part, record, reads, states)
        scan_outputs(core, l1, reads, states)
        l1f = {k[len("L1_ffn_"):]: v for k, v in w.items() if k.startswith("L1_ffn_")}
        with ExitStack() as c:
            core.phase = ""
            x = core.sbuf("x", [P, B, D], F32, c)
            x2 = core.sbuf("x2", [P, B, D], F32, c)
            put, take, gate = (core.sbuf(n, [P, B, Dispatch.TOPK], F32, c) for n in ("put", "take", "gate"))
            with ExitStack() as cc:
                x1 = core.sbuf("x1", [P, B, D], F32, cc)
                normalize(core, "ln3", core.hidden, x, x2)
                normalize(core, "ln4", x, x1, x2)
                self_attention(core, x, x1, l1f["ln1_g"], l1f["ln1_b"], l1f["wq"], l1f["wk"], l1f["wv"], l1f["wo"])
                normalize(core, "ln5", x, x1, x2)
                route_two_of_64(core, x1, l1f, x2, put, take, gate)
            experts_dispatched(core, x, x2, put, take, gate, l1f, buf, results)
        store_hidden(core, out)


def kernel(**inputs):
    import numpy as _np
    import concourse.bacc as _bacc
    from concourse import mybir as _mybir
    from concourse.bass_utils import run_bass_kernel_spmd as _run

    nc = _bacc.Bacc("TRN2", target_bir_lowering=False, num_devices=1)
    arrays, aps = {}, {}
    for name, value in inputs.items():
        a = _np.ascontiguousarray(value)
        arrays[f"in_{name}_dram"] = a
        aps[name] = nc.dram_tensor(f"in_{name}_dram", a.shape, _mybir.dt.from_np(a.dtype), kind="ExternalInput").ap()
    out = nc.dram_tensor("out_0_dram", (32, 127, 128), _mybir.dt.float32, kind="ExternalOutput").ap()
    audio_tower(nc, aps, out)
    r = _run(nc, [arrays], core_ids=[0])
    return r.results[0]["out_0_dram"]
```

```python
from contextlib import ExitStack

import concourse.bass as bass
from concourse import mybir

F32 = mybir.dt.float32
U32 = mybir.dt.uint32
I32 = mybir.dt.int32
ALU = mybir.AluOpType
ACT = mybir.ActivationFunctionType
X = mybir.AxisListType.X

P = 128
B = 32
T = 127
D = 128
GB = 4
NG = B // GB
EPS = 1e-5


class Chain:

    def __init__(self, eng, sem):
        self.eng, self.sem = eng, sem
        self.done, self.k, self.i, self.per = 0, 0, None, 0

    def enter(self, i, per):
        self.done += self.k
        self.i, self.per, self.k = i, per, 0

    def leave(self, times):
        assert self.k == self.per, (self.k, self.per)
        self.done += self.per * times
        self.i, self.per, self.k = None, 0, 0

    def value(self):
        return self.done + self.k + (0 if self.i is None else self.i * self.per)

    def tick(self, ins):
        self.k += 1
        ins.then_inc(self.sem, 1)

    def settle(self):
        self.eng.wait_ge(self.sem, self.value())

    def __call__(self, ins):
        self.tick(ins)
        self.settle()


class Core:

    def __init__(self, nc, ctx):
        self.nc, self.ctx, self.phase, self.sems = nc, ctx, "", []
        self.banks = self.psum("banks", [P, 8 * 512])
        self.bank = [self.banks[:, n * 512:(n + 1) * 512] for n in range(8)]
        self.hidden = self.sbuf("hidden", [P, B, D])
        self.ident = self.sbuf("ident", [P, P])
        self.minus_half = self.sbuf("minus_half", [P, B])

    def sbuf(self, name, shape, dt=F32, ctx=None):
        return (ctx or self.ctx).enter_context(self.nc.sbuf_tensor(self.phase + name, shape, dt))

    def psum(self, name, shape, dt=F32):
        return self.ctx.enter_context(self.nc.psum_tensor(name, shape, dt))

    def sem(self, name, ctx):
        if not self.sems:
            ctx.callback(self.clear_sems)
        self.sems.append(self.nc.alloc_semaphore(self.phase + name))
        return self.sems[-1]

    def clear_sems(self):
        self.nc.clear_and_free_semaphores(self.sems)
        self.nc.all_engine_barrier()
        self.sems = []


def across(ap, n):
    return ap.rearrange("(a d) -> a d", a=1).to_broadcast([n, ap.shape[0]])


def embed_patches(core, x, W, bias):
    nc = core.nc
    core.phase = "embed_"
    BLK = 8 * 32
    with ExitStack() as c:
        sb = lambda n, s, d=F32: core.sbuf(n, s, d, c)
        sem = lambda n: core.sem(n, c)
        w = sb("tok_w", [P, 4 * P])
        wT = sb("tok_wT", [P, 4, P])
        bias_all = sb("tok_bias", [P, D])
        xin = [sb(f"xin{n}", [P, GB, BLK]) for n in range(2)]
        xT = sb("xT", [P, 2, GB, P + 1])
        consts_ready, w_loaded = sem("consts_ready"), sem("tok_w_loaded")
        x_loaded = [sem(f"x_loaded{n}") for n in range(2)]
        x_free, xT_in_psum, xT_ready = sem("x_free"), sem("xT_in_psum"), sem("xT_ready")
        tok_done, acc_free, wT_in_psum, wT_ready = sem("tok_done"), sem("acc_free"), sem("wT_in_psum"), sem("wT_ready")
        pad_ready = sem("pad_ready")
        xg = x.rearrange("b (p r) c -> p b (r c)", r=8)
        with nc.Block() as block:

            @block.sync
            def _(sp):
                sp.dma_start(w[:, :], W).then_inc(w_loaded, 16)
                sp.dma_start(bias_all[:, :], across(bias, P)).then_inc(w_loaded, 16)
                for n in range(2):
                    sp.dma_start(xin[n][:, :, :], xg[:, n * GB:(n + 1) * GB, :]).then_inc(x_loaded[n], 16)
                with sp.Fori(0, NG // 2 - 1) as i:
                    for n in range(2):
                        sp.wait_ge(xT_in_psum, i * 2 + n + 1)
                        sp.dma_start(xin[n][:, :, :], xg[:, bass.ds(i * 2 * GB + (n + 2) * GB, GB), :]).then_inc(x_loaded[n], 16)

            @block.gpsimd
            def _(pool):
                pool.memset(core.ident[:, :], 0.0).then_inc(consts_ready, 1)
                pool.wait_ge(consts_ready, 1)
                pool.affine_select(out=core.ident[:, :], in_=core.ident[:, :], compare_op=ALU.not_equal, fill=1.0,
                                   base=0, pattern=[[-1, P]], channel_multiplier=1).then_inc(consts_ready, 1)
                pool.memset(core.minus_half[:, :], -0.5).then_inc(pad_ready, 1)
                pool.memset(xT[:, :, :, P:P + 1], 0.0).then_inc(pad_ready, 1)

            @block.tensor
            def _(pe):
                pe.wait_ge(consts_ready, 2)
                pe.wait_ge(w_loaded, 32)
                for k in range(4):
                    mm = pe.transpose(core.bank[0][:, k * P:(k + 1) * P], w[:, k * P:(k + 1) * P], core.ident[:, :])
                mm.then_inc(wT_in_psum, 1)
                pe.wait_ge(wT_ready, 1)
                pe.sem_inc(acc_free, 2)
                with pe.Fori(0, NG // 2) as i:
                    for n in range(2):
                        pe.wait_ge(x_loaded[n], i * 16 + 16)
                        for half in range(2):
                            for b in range(GB):
                                mm = pe.transpose(core.bank[half][:, b * P:(b + 1) * P],
                                                  xin[n][:, b, half * P:(half + 1) * P], core.ident[:, :])
                        mm.then_inc(xT_in_psum, 1)
                        pe.wait_ge(xT_ready, i * 2 + n + 1)
                        pe.wait_ge(acc_free, i * 2 + n + 1)
                        for b in range(GB):
                            for k in range(4):
                                mm = pe.matmul(core.bank[2 + n][:, b * P:(b + 1) * P],
                                               xT[:, k % 2, b, k // 2:k // 2 + P], wT[:, k, :],
                                               start=(k == 0), stop=(k == 3))
                        mm.then_inc(tok_done, 1)

            @block.scalar
            def _(act):
                act.wait_ge(wT_in_psum, 1)
                act.copy(wT[:, :, :].rearrange("p k d -> p (k d)"), core.bank[0][:, :]).then_inc(wT_ready, 1)
                act.wait_ge(pad_ready, 2)
                with act.Fori(0, NG // 2) as i:
                    for n in range(2):
                        act.wait_ge(xT_in_psum, i * 2 + n + 1)
                        for half in range(2):
                            cp = act.copy(xT[:, half, :, 0:P], core.bank[half][:, :].rearrange("p (b t) -> p b t", b=GB))
                        cp.then_inc(xT_ready, 1)

            @block.vector
            def _(dve):
                with dve.Fori(0, NG // 2) as i:
                    for n in range(2):
                        dve.wait_ge(tok_done, i * 2 + n + 1)
                        dve.tensor_tensor(core.hidden[:, bass.ds(i * 2 * GB + n * GB, GB), :],
                                          core.bank[2 + n][:, :].rearrange("p (b d) -> p b d", b=GB),
                                          bias_all[:, :].unsqueeze(1).to_broadcast([P, GB, D]),
                                          ALU.add).then_inc(acc_free, 1)


def normalize(core, name, src, out, sq):
    nc = core.nc
    core.phase = name + "_"
    with ExitStack() as c:
        mean = core.sbuf("mean", [P, B], F32, c)
        rstd = core.sbuf("rstd", [P, B], F32, c)
        chain = core.sem("chain", c)
        centred, squared, var_ready, rstd_ready = (core.sem(s, c) for s in ("centred", "squared", "var", "rstd"))
        with nc.Block() as block:

            @block.vector
            def _(dve):
                step = Chain(dve, chain)
                step(dve.tensor_reduce(mean[:, :], src[:, :, :], X, ALU.add))
                step(dve.tensor_scalar(mean[:, :], mean[:, :], 1.0 / D, None, ALU.mult))
                dve.tensor_tensor(out[:, :, :], src[:, :, :], mean[:, :].unsqueeze(2).to_broadcast([P, B, D]),
                                  ALU.subtract).then_inc(centred, 1)
                dve.wait_ge(squared, 1)
                step(dve.tensor_reduce(rstd[:, :], sq[:, :, :], X, ALU.add))
                dve.tensor_scalar(rstd[:, :], rstd[:, :], 1.0 / D, EPS, ALU.mult, ALU.add).then_inc(var_ready, 1)
                dve.wait_ge(rstd_ready, 1)
                step(dve.tensor_tensor(out[:, :, :], out[:, :, :], rstd[:, :].unsqueeze(2).to_broadcast([P, B, D]), ALU.mult))

            @block.scalar
            def _(act):
                act.wait_ge(centred, 1)
                act.activation(sq[:, :, :], out[:, :, :], ACT.Square).then_inc(squared, 1)

            @block.gpsimd
            def _(pool):
                pool.wait_ge(var_ready, 1)
                pool.tensor_tensor(rstd[:, :], rstd[:, :], core.minus_half[:, :], ALU.pow).then_inc(rstd_ready, 1)


def store_hidden(core, out):
    nc = core.nc
    with ExitStack() as c:
        stored = core.sem("stored", c)
        with nc.Block() as block:

            @block.sync
            def _(sp):
                sp.dma_start(out.rearrange("b t d -> t b d"), core.hidden[0:T, :, :]).then_inc(stored, 16)
                sp.wait_ge(stored, 16)


def channel_attention(core, xn, W_qkv, W_o, cleared):
    nc = core.nc
    core.phase = "attn0_"
    DK = 16
    R = 48
    SCALE = DK ** -0.5
    CH = 4 * P
    with ExitStack() as c:
        sb = lambda n, s, d=F32: core.sbuf(n, s, d, c)
        sem = lambda n: core.sem(n, c)
        wqkv = sb("wqkv", [P, 3 * DK])
        wq2, wk2 = sb("wq2", [P, R]), sb("wk2", [P, R])
        wo = sb("wo", [DK, D])
        chan = sb("chan", [P, DK])
        x_stage = [sb(f"x_stage{n}", [P, GB, D]) for n in range(2)]
        xT = sb("xT", [P, GB, P])
        kT = sb("kT", [P, GB, P])
        qT = sb("qT", [P, GB, P])
        v = sb("v", [P, GB, DK])
        kmax, kmin = sb("kmax", [R, GB]), sb("kmin", [R, GB])
        top = sb("top", [R, GB, P])
        qd = [sb(f"qd{n}", [P, DK, P]) for n in range(2)]
        vd = [sb(f"vd{n}", [P, DK, R]) for n in range(2)]
        probs = [sb(f"probs{n}", [P, DK, P]) for n in range(2)]
        rden = sb("rden", [DK, P])
        sa = sb("sa", [DK, GB, P])
        zeros = sb("zeros", [P, D])
        zeros_ready, zeros_stored = sem("zeros_ready"), sem("zeros_stored")
        (w_loaded, consts_ready, w_ready, staged, xT_in_psum, xT_ready, q_in_psum, k_in_psum, v_in_psum, qk_copied,
         v_copied, qd_ready, scores_ready, probs_ready, sums_ready, sa_ready, out_in_psum,
         hidden_added, chain_sem) = (sem(n) for n in (
            "w_loaded", "consts_ready", "w_ready", "staged", "xT_in_psum", "xT_ready", "q_in_psum", "k_in_psum", "v_in_psum",
            "qk_copied", "v_copied", "qd_ready", "scores_ready", "probs_ready",
            "sums_ready", "sa_ready", "out_in_psum", "hidden_added", "chain"))
        xT_ps, q_ps, k_ps, sum_ps = core.bank[0], core.bank[1], core.bank[2], core.bank[3]
        v_ps, out_ps = xT_ps, q_ps
        with nc.Block() as block:

            @block.sync
            def _(sp):
                sp.dma_start(wqkv[:, :], W_qkv).then_inc(w_loaded, 16)
                sp.dma_start(wo[:, :], W_o).then_inc(w_loaded, 16)
                sp.wait_ge(zeros_ready, 1)
                for rows in cleared:
                    n = rows.shape[0] // P
                    sp.dma_start(rows.rearrange("(p r) d -> p r d", p=P), zeros[:, :].unsqueeze(1).to_broadcast([P, n, D])).then_inc(zeros_stored, 16)
                sp.wait_ge(zeros_stored, 16 * len(cleared))

            @block.gpsimd
            def _(pool):
                pool.memset(zeros[:, :], 0.0).then_inc(zeros_ready, 1)
                pool.memset(chan[:, :], 0.0).then_inc(consts_ready, 1)
                pool.wait_ge(consts_ready, 1)
                for n, base in enumerate((0, -32)):
                    pool.affine_select(out=chan[:, :], in_=chan[:, :], compare_op=ALU.not_equal, fill=1.0,
                                       base=base, pattern=[[-1, DK]], channel_multiplier=1).then_inc(consts_ready, 1)
                    pool.wait_ge(consts_ready, 2 + n)
                pool.memset(qT[:, :, :], 0.0).then_inc(consts_ready, 1)
                pool.memset(kT[:, :, :], -1.0).then_inc(consts_ready, 1)
                for n in range(2):
                    pool.memset(vd[n][:, :, 0:32], 0.0).then_inc(consts_ready, 1)
                    pool.memset(vd[n][:, :, 32:R], 0.0).then_inc(consts_ready, 1)
                pool.wait_ge(consts_ready, 9)
                for n in range(2):
                    flat = vd[n][:, :, :].rearrange("p c r -> p (c r)")
                    pool.memset(flat[:, 32::R + 1], 1.0).then_inc(consts_ready, 1)

            @block.tensor
            def _(pe):
                pe.sem_inc(v_copied, 1)
                pe.sem_inc(hidden_added, 1)
                pe.sem_inc(sa_ready, 1)
                pe.sem_inc(probs_ready, 2)
                pe.wait_ge(w_ready, 4)
                with pe.Fori(0, NG // 2) as i:
                    for g in range(2):
                        pe.wait_ge(staged, i * 2 + g + 1)
                        pe.wait_ge(v_copied, i * 2 + g + 1)
                        for b in range(GB):
                            mm = pe.transpose(xT_ps[:, b * P:(b + 1) * P], x_stage[g][:, b, :], core.ident[:, :])
                        mm.then_inc(xT_in_psum, 1)
                        pe.wait_ge(hidden_added, i * 2 + g + 1)
                        pe.wait_ge(xT_ready, i * 2 + g + 1)
                        rhs = xT[:, :, :].rearrange("p b t -> p (b t)")
                        pe.matmul(q_ps[0:R, :], wq2[:, :], rhs, start=True, stop=True).then_inc(q_in_psum, 1)
                        pe.matmul(k_ps[0:R, :], wk2[:, :], rhs, start=True, stop=True).then_inc(k_in_psum, 1)
                        for b in range(GB):
                            mm = pe.matmul(v_ps[:, b * DK:(b + 1) * DK], xT[:, b, :], wqkv[:, 2 * DK:3 * DK],
                                           start=True, stop=True)
                        mm.then_inc(v_in_psum, 1)
                        for b in range(GB + 1):
                            at = i * 2 * GB + g * GB + b
                            if b < GB:
                                pe.wait_ge(qd_ready, at + 1)
                                for half in range(2):
                                    pe.wait_ge(probs_ready, at * 2 + half + 1)
                                    for n in range(2):
                                        ch = half * 8 + n * 4
                                        mm = pe.matmul(core.bank[4 + 2 * half + n][0:T, :], kT[:, b, 0:T],
                                                       qd[b % 2][:, ch:ch + 4, :].rearrange("r c n -> r (c n)"),
                                                       start=True, stop=True)
                                    mm.then_inc(scores_ready, 1)
                            if b >= 1:
                                for half in range(2):
                                    pe.wait_ge(probs_ready, at * 2 + half + 1)
                                    if half == 0:
                                        pe.wait_ge(sa_ready, at)
                                    for ch in range(half * 8, half * 8 + 8):
                                        mm = pe.matmul(sum_ps[0:R, (b - 1) * P:b * P], vd[(b - 1) % 2][0:T, ch, :],
                                                       probs[(b - 1) % 2][0:T, ch, :], start=(ch == 0), stop=(ch == DK - 1))
                                mm.then_inc(sums_ready, 1)
                        pe.wait_ge(sa_ready, i * 2 * GB + (g + 1) * GB + 1)
                        for b in range(GB):
                            mm = pe.matmul(out_ps[:, b * P:(b + 1) * P], sa[:, b, :], wo[:, :], start=True, stop=True)
                        mm.then_inc(out_in_psum, 1)

            @block.scalar
            def _(act):
                with act.Fori(0, NG // 2) as i:
                    for g in range(2):
                        act.wait_ge(xT_in_psum, i * 2 + g + 1)
                        act.copy(xT[:, :, :].rearrange("p b t -> p (b t)"), xT_ps[:, :]).then_inc(xT_ready, 1)
                        act.wait_ge(q_in_psum, i * 2 + g + 1)
                        act.wait_ge(consts_ready, 11)
                        act.copy(qT[0:DK, :, :].rearrange("p b t -> p (b t)"), q_ps[0:DK, :]).then_inc(qk_copied, 1)
                        act.wait_ge(k_in_psum, i * 2 + g + 1)
                        act.copy(kT[0:DK, :, :].rearrange("p b t -> p (b t)"), k_ps[0:DK, :]).then_inc(qk_copied, 1)
                        act.wait_ge(v_in_psum, i * 2 + g + 1)
                        act.copy(v[:, :, :].rearrange("p b c -> p (b c)"), v_ps[:, 0:GB * DK]).then_inc(v_copied, 1)
                        for b in range(GB):
                            at = i * 2 * GB + g * GB + b
                            for half in range(2):
                                act.wait_ge(scores_ready, at * 2 + half + 1)
                                act.activation(probs[b % 2][0:T, half * 8:half * 8 + 8, :].rearrange("p c n -> p (c n)"),
                                               core.banks[0:T, (4 + 2 * half) * 512:(6 + 2 * half) * 512],
                                               ACT.Exp, scale=SCALE).then_inc(probs_ready, 1)

            @block.vector
            def _(dve):
                step = Chain(dve, chain_sem)
                dve.memset(wq2[:, :], 0.0).then_inc(w_ready, 1)
                dve.memset(wk2[:, :], 0.0).then_inc(w_ready, 1)
                dve.wait_ge(w_loaded, 32)
                dve.wait_ge(w_ready, 2)
                for w, col in ((wq2, 0), (wk2, DK)):
                    dve.tensor_copy(w[:, :].rearrange("p (a c) -> p a c", c=DK)[:, 0::2, :],
                                    wqkv[:, col:col + DK].unsqueeze(1).to_broadcast([P, 2, DK])).then_inc(w_ready, 1)
                with dve.Fori(0, NG // 2) as i:
                    step.enter(i, 2 * (5 + GB))
                    for g in range(2):
                        dve.tensor_copy(x_stage[g][:, :, :], xn[:, bass.ds(i * 2 * GB + g * GB, GB), :]).then_inc(staged, 1)
                        lo, hi = 32, R
                        q3 = q_ps[lo:hi, :].rearrange("p (b t) -> p b t", b=GB)
                        k3 = k_ps[lo:hi, :].rearrange("p (b t) -> p b t", b=GB)
                        dve.wait_ge(qk_copied, i * 4 + 2 * g + 2)
                        step.tick(dve.tensor_reduce(kmax[lo:hi, :], k3[:, :, 0:T], X, ALU.max))
                        step(dve.tensor_reduce(kmin[lo:hi, :], k3[:, :, 0:T], X, ALU.min))
                        step.tick(dve.tensor_tensor(top[lo:hi, :, :], q3, kmax[lo:hi, :].unsqueeze(2).to_broadcast([DK, GB, P]), ALU.mult))
                        step(dve.tensor_tensor(qT[lo:hi, :, :], q3, kmin[lo:hi, :].unsqueeze(2).to_broadcast([DK, GB, P]), ALU.mult))
                        step(dve.tensor_tensor(qT[lo:hi, :, :], qT[lo:hi, :, :], top[lo:hi, :, :], ALU.max))
                        dve.wait_ge(v_copied, i * 2 + g + 2)
                        for b in range(GB + 1):
                            at = i * 2 * GB + g * GB + b
                            if b < GB:
                                dve.tensor_copy(vd[b % 2][:, :, :].rearrange("p c r -> p (c r)")[:, 0::R + 1], v[:, b, :])
                                dve.tensor_tensor(qd[b % 2][:, :, :], qT[:, b, :].unsqueeze(1).to_broadcast([P, DK, P]),
                                                  chan[:, :].unsqueeze(2).to_broadcast([P, DK, P]), ALU.mult).then_inc(qd_ready, 1)
                            if b >= 1:
                                dve.wait_ge(sums_ready, at)
                                step(dve.reciprocal(rden[:, :], sum_ps[32:R, (b - 1) * P:b * P]))
                                dve.tensor_tensor(sa[:, b - 1, :], sum_ps[0:DK, (b - 1) * P:b * P], rden[:, :],
                                                  ALU.mult).then_inc(sa_ready, 1)
                        dve.wait_ge(out_in_psum, i * 2 + g + 1)
                        hid = core.hidden[:, bass.ds(i * 2 * GB + g * GB, GB), :]
                        dve.tensor_tensor(hid, out_ps[:, :].rearrange("p (b d) -> p b d", b=GB), hid, ALU.add).then_inc(hidden_added, 1)
                    step.leave(NG // 2)


def route_six_of_64(core, xn, combine, router_w, bias_corr, loads, cleared):
    nc = core.nc
    core.phase = "route0_"
    E, G, TG, TOPK = 64, 8, 4, 6
    EPG = E // G
    W = E + 8 - TOPK
    FAR = 1e30
    with ExitStack() as c:
        sb = lambda n, s, d=F32: core.sbuf(n, s, d, c)
        sem = lambda n: core.sem(n, c)
        rw, rwT = sb("rw", [E, D]), sb("rwT", [D, E])
        bias = sb("bias", [P, E])
        lower = sb("lower", [P, G, G])
        sentinels = sb("sentinels", [P, 8 - TOPK])
        stage, xT = sb("stage", [P, GB, D]), sb("xT", [P, GB, P])
        expo, scores, biased = (sb(n, [P, GB, E]) for n in ("expo", "scores", "biased"))
        gs, rank, gmask, penalty = (sb(n, [P, GB, G]) for n in ("gs", "rank", "gmask", "penalty"))
        beats, ties = sb("beats", [P, GB, G, G]), sb("ties", [P, GB, G, G])
        masked, marked = sb("masked", [P, GB, W]), sb("marked", [P, GB, W])
        best = sb("best", [P, GB, 8])
        total = sb("total", [P, GB])
        waiter = sb("waiter", [1, 1])
        (w_loaded, consts_ready, rwT_in_psum, rwT_ready, staged, xT_in_psum, xT_ready, logits_ready, exp_ready,
         chain_sem, later_loaded) = (sem(n) for n in ("w_loaded", "consts_ready", "rwT_in_psum", "rwT_ready", "staged",
                                        "xT_in_psum", "xT_ready", "logits_ready", "exp_ready", "chain", "later_loaded"))
        with nc.Block() as block:

            @block.sync
            def _(sp):
                sp.dma_start(rw[:, :], router_w).then_inc(w_loaded, 16)
                sp.dma_start(bias[:, :], across(bias_corr, P)).then_inc(w_loaded, 16)
                for dst, src in loads:
                    sp.dma_start(dst, src).then_inc(later_loaded, 16)
                sp.wait_ge(later_loaded, 16 * len(loads))

            @block.gpsimd
            def _(pool):
                for ap in cleared:
                    pool.memset(ap, 0.0)
                pool.memset(lower[:, :, :], 1.0).then_inc(consts_ready, 1)
                pool.wait_ge(consts_ready, 1)
                pool.affine_select(out=lower[:, :, :], in_=lower[:, :, :], compare_op=ALU.is_gt, fill=0.0, base=0,
                                   pattern=[[1, G], [-1, G]], channel_multiplier=0).then_inc(consts_ready, 1)
                for n in range(8 - TOPK):
                    pool.memset(sentinels[:, n:n + 1], -2 * FAR * (n + 1)).then_inc(consts_ready, 1)

            @block.tensor
            def _(pe):
                pe.wait_ge(w_loaded, 32)
                pe.transpose(core.bank[0][:, 0:E], rw[:, :], core.ident[0:E, 0:E]).then_inc(rwT_in_psum, 1)
                pe.wait_ge(rwT_ready, 1)
                with pe.Fori(0, NG) as g:
                    pe.wait_ge(staged, g + 1)
                    for b in range(GB):
                        mm = pe.transpose(core.bank[0][:, b * P:(b + 1) * P], stage[:, b, :], core.ident[:, :])
                    mm.then_inc(xT_in_psum, 1)
                    pe.wait_ge(xT_ready, g + 1)
                    for b in range(GB):
                        mm = pe.matmul(core.bank[1][:, b * E:(b + 1) * E], xT[:, b, :], rwT[:, :], start=True, stop=True)
                    mm.then_inc(logits_ready, 1)

            @block.scalar
            def _(act):
                act.wait_ge(rwT_in_psum, 1)
                act.copy(rwT[:, :], core.bank[0][:, 0:E]).then_inc(rwT_ready, 1)
                with act.Fori(0, NG) as g:
                    act.wait_ge(xT_in_psum, g + 1)
                    act.copy(xT[:, :, :].rearrange("p b t -> p (b t)"), core.bank[0][:, :]).then_inc(xT_ready, 1)
                    act.wait_ge(logits_ready, g + 1)
                    act.activation(expo[:, :, :].rearrange("p b e -> p (b e)"), core.bank[1][:, 0:GB * E], ACT.Exp,
                                   scale=-1.0).then_inc(exp_ready, 1)

            @block.vector
            def _(dve):
                step = Chain(dve, chain_sem)
                dve.wait_ge(consts_ready, 2 + 8 - TOPK)
                dve.wait_ge(w_loaded, 32)
                step(dve.tensor_copy(masked[:, :, E:W], sentinels[:, :].unsqueeze(1).to_broadcast([P, GB, W - E])))
                with dve.Fori(0, NG) as g:
                    step.enter(g, 28)
                    tiles = bass.ds(g * GB, GB)
                    dve.tensor_copy(stage[:, :, :], xn[:, tiles, :]).then_inc(staged, 1)
                    dve.wait_ge(exp_ready, g + 1)
                    step(dve.tensor_scalar(expo[:, :, :], expo[:, :, :], 1.0, None, ALU.add))
                    step(dve.reciprocal(scores[:, :, :], expo[:, :, :]))
                    step(dve.tensor_tensor(biased[:, :, :], scores[:, :, :], bias[:, :].unsqueeze(1).to_broadcast([P, GB, E]), ALU.add))
                    step(dve.tensor_reduce(gs[:, :, :].rearrange("p b g -> p (b g)"),
                                           biased[:, :, :].rearrange("p b (g e) -> p (b g) e", g=G), X, ALU.max))
                    other = gs[:, :, :].unsqueeze(2).to_broadcast([P, GB, G, G])
                    own = gs[:, :, :].unsqueeze(3).to_broadcast([P, GB, G, G])
                    step.tick(dve.tensor_tensor(beats[:, :, :, :], other, own, ALU.is_gt))
                    step(dve.tensor_tensor(ties[:, :, :, :], other, own, ALU.is_ge))
                    step(dve.tensor_tensor(ties[:, :, :, :].rearrange("p b g h -> p b (g h)"), ties[:, :, :, :].rearrange("p b g h -> p b (g h)"),
                                           lower[:, :, :].rearrange("p g h -> p (g h)").unsqueeze(1).to_broadcast([P, GB, G * G]), ALU.mult))
                    step(dve.tensor_tensor(beats[:, :, :, :], beats[:, :, :, :], ties[:, :, :, :], ALU.max))
                    step(dve.tensor_reduce(rank[:, :, :], beats[:, :, :, :], X, ALU.add))
                    step(dve.tensor_scalar(gmask[:, :, :], rank[:, :, :], float(TG), None, ALU.is_lt))
                    step(dve.tensor_scalar(penalty[:, :, :], gmask[:, :, :], -1.0, FAR, ALU.add, ALU.mult))
                    vals = masked[:, :, 0:E].rearrange("p b (g e) -> p b g e", g=G)
                    step(dve.tensor_tensor(vals, biased[:, :, :].rearrange("p b (g e) -> p b g e", g=G),
                                           gmask[:, :, :].unsqueeze(3).to_broadcast([P, GB, G, EPG]), ALU.mult))
                    step(dve.tensor_tensor(vals, vals, penalty[:, :, :].unsqueeze(3).to_broadcast([P, GB, G, EPG]), ALU.add))
                    dve.memset(waiter[:, :], 0.0)
                    for b in range(GB):
                        step.tick(dve.max(best[:, b, :], masked[:, b, 0:E]))
                    step.settle()
                    step(dve.tensor_copy(best[:, :, TOPK:8], sentinels[:, :].unsqueeze(1).to_broadcast([P, GB, 8 - TOPK])))
                    dve.memset(waiter[:, :], 0.0)
                    for b in range(GB):
                        step.tick(dve.match_replace(marked[:, b, :], best[:, b, :], masked[:, b, :], FAR))
                    step.settle()
                    step(dve.tensor_scalar(marked[:, :, 0:E], marked[:, :, 0:E], FAR, None, ALU.is_ge))
                    step(dve.tensor_tensor(expo[:, :, :], scores[:, :, :], marked[:, :, 0:E], ALU.mult))
                    step(dve.tensor_reduce(total[:, :], expo[:, :, :], X, ALU.add))
                    step(dve.tensor_scalar(total[:, :], total[:, :], 1e-20, None, ALU.add))
                    step(dve.reciprocal(total[:, :], total[:, :]))
                    step(dve.tensor_tensor(combine[:, tiles, :], expo[:, :, :], total[:, :].unsqueeze(2).to_broadcast([P, GB, E]), ALU.mult))
                    step.leave(NG)




class Sparse:
    E, TOPK = 64, 6
    ROUTED = ((TOPK * B * T + E * (P - 1)) // P + 3) // 4 * 4
    TILES = ROUTED + B
    ROWS = TILES * P + TOPK * B * P
    H, HS = 160, 128


def dispatch_six(core, xn, combine, buf, take, weight, tile_expert):
    nc = core.nc
    core.phase = "dispatch0_"
    Z = Sparse
    E, K = Z.E, Z.TOPK
    PER = 17
    with ExitStack() as c:
        sb = lambda n, s, d=F32: core.sbuf(n, s, d, c)
        sem = lambda n: core.sem(n, c)
        before, ones = sb("before", [P, P]), sb("ones", [P, P])
        real = sb("real", [P, 1])
        spill = sb("spill", [P, B, K])
        tile_start = sb("tile_start", [P, B])
        index = sb("index", [P, 2])
        sel = sb("sel", [P, B, E])
        chosen, count, tiles_row, end = (sb(n, [P, E]) for n in ("chosen", "count", "tiles_row", "end"))
        more = sb("more", [P, E, B])
        base1 = sb("base1", [P, E])
        tiles_col, tiles_wide = sb("tiles_col", [E, 1]), sb("tiles_wide", [E, P])
        expert_col = sb("expert_col", [P, 2])
        seen = sb("seen", [P, GB + 1, E])
        key = sb("key", [P, GB, E])
        best = sb("best", [P, GB, 8])
        match = sb("match", [P, GB, K, E])
        row, valid, to = (sb(n, [P, GB, K]) for n in ("row", "valid", "to"))
        stage = [sb(f"stage{n}", [P, GB, D]) for n in range(2)]
        put = [sb(f"put{n}", [P, GB, K], U32) for n in range(2)]
        waiter, pool_waiter = sb("waiter", [1, 1]), sb("pool_waiter", [1, 1])
        names = ("consts_ready", "chosen_ready", "count_in_psum", "wide_ready", "base_in_psum", "expert_ready", "expert_in_psum",
                 "sel_ready", "pos_in_psum", "index_ready", "shared_sent", "chain", "pool_chain", "pool_waited")
        S = {n: sem(n) for n in names}
        sent = [sem(f"sent{n}") for n in range(2)]
        bank = core.bank
        with nc.Block() as block:

            @block.sync
            def _(sp):
                sp.dma_start(buf[Z.ROUTED * P:Z.TILES * P, :].rearrange("(b p) d -> p b d", p=P), xn[:, :, :]).then_inc(S["shared_sent"], 16)
                sp.wait_ge(S["shared_sent"], 16)

            @block.gpsimd
            def _(pool):
                step = Chain(pool, S["pool_chain"])
                iota = dict(allow_small_or_imprecise_dtypes=True)
                step(pool.memset(before[:, :], 1.0))
                step(pool.affine_select(out=before[:, :], in_=before[:, :], compare_op=ALU.is_gt, fill=0.0, base=0,
                                        pattern=[[1, P]], channel_multiplier=-1))
                step(pool.memset(ones[:, :], 1.0))
                step(pool.memset(real[:, :], 1.0))
                step(pool.affine_select(out=real[:, :], in_=real[:, :], compare_op=ALU.is_gt, fill=0.0, base=T,
                                        pattern=[[0, 1]], channel_multiplier=-1))
                step(pool.iota(spill[:, :, :], pattern=[[K * P, B], [P, K]], base=Z.TILES * P, channel_multiplier=1, **iota))
                step(pool.iota(tile_start[:, :], pattern=[[P, B]], base=0, channel_multiplier=0, **iota))
                step(pool.iota(index[:, :], pattern=[[P, 2]], base=0, channel_multiplier=1, **iota))
                step(pool.memset(tile_expert[:, :], E))
                step(pool.memset(pool_waiter[:, :], 0.0))
                pool.memset(seen[:, :, :], 0.0).then_inc(S["consts_ready"], 1)
                with pool.Fori(0, NG // 2) as i:
                    for n in range(2):
                        pool.wait_ge(S["index_ready"], i * 2 + n + 1)
                        pool.tensor_tensor(pool_waiter[:, :], pool_waiter[:, :], pool_waiter[:, :], ALU.add).then_inc(S["pool_waited"], 1)
                        for b in range(GB):
                            for k in range(K):
                                pool.indirect_dma_start(out=buf, out_offset=bass.IndirectOffsetOnAxis(ap=put[n][:, b, k:k + 1], axis=0),
                                                        in_=stage[n][:, b, :], in_offset=None).then_inc(sent[n], 16)
                        pool.wait_ge(S["pool_waited"], i * 2 + n + 1)
                for n in range(2):
                    pool.wait_ge(sent[n], 16 * GB * K * (NG // 2))

            @block.tensor
            def _(pe):
                pe.wait_ge(S["consts_ready"], 1)
                pe.wait_ge(S["chosen_ready"], 1)
                pe.matmul(bank[0][:, 0:E], ones[:, :], chosen[:, :], start=True, stop=True)
                pe.matmul(bank[0][0:E, E:E + 1], chosen[:, :], ones[:, 0:1], start=True, stop=True).then_inc(S["count_in_psum"], 1)
                pe.wait_ge(S["wide_ready"], 1)
                pe.matmul(bank[1][:, 0:E], tiles_wide[:, :], before[0:E, 0:E], start=True, stop=True).then_inc(S["base_in_psum"], 1)
                pe.wait_ge(S["expert_ready"], 1)
                for h in range(2):
                    mm = pe.matmul(bank[2][0:1, h * P:(h + 1) * P], expert_col[:, h:h + 1], core.ident[:, :], start=True, stop=True)
                mm.then_inc(S["expert_in_psum"], 1)
                with pe.Fori(0, NG) as g:
                    pe.wait_ge(S["sel_ready"], g + 1)
                    pe.matmul(bank[3][:, 0:GB * E], before[:, :], sel[:, bass.ds(g * GB, GB), :].rearrange("p b e -> p (b e)"), start=True, stop=False)
                    pe.matmul(bank[3][:, 0:GB * E], ones[:, :], seen[:, 0:GB, :].rearrange("p b e -> p (b e)"), start=False, stop=True).then_inc(S["pos_in_psum"], 1)

            @block.vector
            def _(dve):
                step = Chain(dve, S["chain"])
                dve.wait_ge(S["consts_ready"], 1)
                step(dve.tensor_scalar(sel[:, :, :], combine[:, :, :], 0.0, real[:, :], ALU.is_gt, ALU.mult))
                dve.tensor_reduce(chosen[:, :], sel[:, :, :].rearrange("p b e -> p e b"), X, ALU.add).then_inc(S["chosen_ready"], 1)
                dve.wait_ge(S["count_in_psum"], 1)
                step.tick(dve.tensor_copy(count[:, :], bank[0][:, 0:E]))
                step(dve.tensor_scalar(more[0:E, 0, :], tile_start[0:E, :], bank[0][0:E, E:E + 1], None, ALU.is_lt))
                step(dve.tensor_reduce(tiles_col[:, :], more[0:E, 0, :], X, ALU.add))
                dve.tensor_scalar(tiles_wide[:, :], ones[0:E, :], tiles_col[:, :], None, ALU.mult).then_inc(S["wide_ready"], 1)
                step(dve.tensor_tensor(more[:, :, :], count[:, :].unsqueeze(2).to_broadcast([P, E, B]),
                                       tile_start[:, :].unsqueeze(1).to_broadcast([P, E, B]), ALU.is_gt))
                step(dve.tensor_reduce(tiles_row[:, :], more[:, :, :], X, ALU.add))
                dve.wait_ge(S["base_in_psum"], 1)
                step.tick(dve.tensor_tensor(end[:, :], bank[1][:, 0:E], tiles_row[:, :], ALU.add))
                step(dve.tensor_scalar(base1[:, :], bank[1][:, 0:E], float(P), 1.0, ALU.mult, ALU.add))
                for h in range(2):
                    step(dve.tensor_scalar(count[:, :], end[:, :], index[:, h:h + 1], None, ALU.is_le))
                    ins = dve.tensor_reduce(expert_col[:, h:h + 1], count[:, :], X, ALU.add)
                    if h == 0:
                        step(ins)
                ins.then_inc(S["expert_ready"], 1)
                dve.wait_ge(S["expert_in_psum"], 1)
                step(dve.tensor_copy(tile_expert[:, 0:Z.ROUTED], bank[2][0:1, 0:Z.ROUTED]))
                with dve.Fori(0, NG // 2) as i:
                    step.enter(i, 2 * PER)
                    for n in range(2):
                        g = i * 2 + n
                        tiles = bass.ds(i * 2 * GB + n * GB, GB)
                        dve.wait_ge(sent[n], i * (16 * GB * K))
                        step.tick(dve.tensor_copy(stage[n][:, :, :], xn[:, tiles, :]))
                        for b in range(GB):
                            ins = dve.tensor_tensor(seen[:, b + 1, :], seen[:, b, :], sel[:, bass.ds(i * 2 * GB + n * GB + b, 1), :].rearrange("p b e -> p (b e)"), ALU.add)
                            if b < GB - 1:
                                step(ins)
                        ins.then_inc(S["sel_ready"], 1)
                        dve.wait_ge(S["pos_in_psum"], g + 1)
                        step.tick(dve.tensor_copy(seen[:, 0, :], seen[:, GB, :]))
                        step(dve.tensor_tensor(key[:, :, :], bank[3][:, 0:GB * E].rearrange("p (b e) -> p b e", b=GB),
                                               base1[:, :].unsqueeze(1).to_broadcast([P, GB, E]), ALU.add))
                        step(dve.tensor_tensor(key[:, :, :], key[:, :, :], sel[:, tiles, :], ALU.mult))
                        dve.memset(waiter[:, :], 0.0)
                        for b in range(GB):
                            step.tick(dve.max(best[:, b, :], key[:, b, :]))
                        step.settle()
                        best6 = best[:, :, 0:K]
                        step.tick(dve.tensor_tensor(match[:, :, :, :], key[:, :, :].unsqueeze(2).to_broadcast([P, GB, K, E]),
                                                    best6.unsqueeze(3).to_broadcast([P, GB, K, E]), ALU.is_equal))
                        step.tick(dve.tensor_scalar(valid[:, :, :], best6, 0.0, None, ALU.is_gt))
                        step.tick(dve.tensor_scalar(take[:, tiles, :], best6, -1.0, 0.0, ALU.add, ALU.max))
                        step(dve.scalar_tensor_tensor(out=row[:, :, :].rearrange("p b k -> p (b k)"), in0=best6, scalar=-1.0,
                                                      in1=spill[:, tiles, :], op0=ALU.add, op1=ALU.subtract))
                        step(dve.tensor_tensor(row[:, :, :], row[:, :, :], valid[:, :, :], ALU.mult))
                        dve.tensor_tensor(put[n][:, :, :], row[:, :, :], spill[:, tiles, :], ALU.add).then_inc(S["index_ready"], 1)
                        step(dve.tensor_tensor(match[:, :, :, :], match[:, :, :, :], combine[:, tiles, :].unsqueeze(2).to_broadcast([P, GB, K, E]), ALU.mult))
                        dve.tensor_reduce(weight[:, tiles, :], match[:, :, :, :], X, ALU.add)
                    step.leave(NG // 2)


def experts_sparse(core, w, w_up, buf, results, tile_expert):
    nc = core.nc
    core.phase = "experts0_"
    Z = Sparse
    H, HS, E, U = Z.H, Z.HS, Z.E, Z.TILES
    HR = H - P
    LAG = 4
    with ExitStack() as c:
        sb = lambda n, s, d=F32: core.sbuf(n, s, d, c)
        sem = lambda n: core.sem(n, c)
        w_down, w_down_r = sb("w_down", [P, E + 1, D]), sb("w_down_r", [HR, E + 1, D])
        x = [sb(f"x{n}", [P, D]) for n in range(4)]
        xT = [sb(f"xT{n}", [P, P]) for n in range(2)]
        gate = [sb(f"gate{n}", [P, H]) for n in range(2)]
        h = [sb(f"h{n}", [P, H]) for n in range(2)]
        hT = [sb(f"hT{n}", [P, P]) for n in range(2)]
        hTr = [sb(f"hTr{n}", [HR, P]) for n in range(2)]
        y = [sb(f"y{n}", [P, D]) for n in range(4)]
        names = ("w_loaded", "zeroed", "xT_in_psum", "xT_ready", "up_ready", "gate_ready", "h_ready", "hT_in_psum", "hT_ready",
                 "y_in_psum", "y_ready")
        S = {n: sem(n) for n in names}
        loaded = [sem(f"loaded{n}") for n in range(4)]
        stored = [sem(f"stored{n}") for n in range(4)]
        x_ps, up_ps, hT_ps, y_ps = (core.bank[n:n + 2] for n in (0, 2, 4, 6))
        one = lambda t, e: t[:, bass.ds(e, 1), :].rearrange("p e h -> p (e h)")

        def run(eng, stages, enter=None, prepare=None):
            def tick(s, base):
                for lag, stage in stages:
                    if prepare and s == 7 and lag == stages[-1][0]:
                        prepare(base + 4)
                    if base is not None or 0 <= s - lag < U:
                        stage(s - lag if base is not None else (s - lag) % 4, s - lag if base is None else base + (s - lag))
            if prepare:
                prepare(0)
                enter()
            for s in range(4):
                tick(s, None)
            with eng.Fori(0, U // 4 - 1) as i:
                if enter:
                    enter()
                for s in range(4, 8):
                    tick(s, i * 4)
            if enter:
                enter()
            for s in range(U, U + LAG - 1):
                tick(s, None)

        with nc.Block() as block:

            @block.sync
            def _(sp):
                for n, dst, src in ((0, w_down[:, 0:E, :], w["Wd"][:, 0:P, :].rearrange("e h c -> h e c")),
                                    (1, w_down_r[:, 0:E, :], w["Wd"][:, P:H, :].rearrange("e h c -> h e c")),
                                    (2, w_down[:, E, :], w["sWd"])):
                    sp.dma_start(dst, src).then_inc(S["w_loaded"], 16)

                def load(n, u):
                    sp.dma_start(x[n][:, :], buf[bass.ds(u * P, P), :]).then_inc(loaded[n], 16)

                for n in range(4):
                    sp.sem_inc(stored[n], 16)
                    load(n, n)

                def load_next(n, u):
                    sp.wait_ge(S["xT_in_psum"], u - 3)
                    load(n, u)

                def store(n, u):
                    sp.wait_ge(S["y_ready"], u + 1)
                    sp.dma_start(results[bass.ds(u * P, P), :], y[n][:, :]).then_inc(stored[n], 16)

                for n in range(4):
                    load_next(n, 4 + n)
                with sp.Fori(0, U // 4 - 2) as i:
                    for n in range(4):
                        load_next(n, i * 4 + n + 8)
                        store(n, i * 4 + n)
                for n in range(8):
                    store(n % 4, U - 8 + n)
                for n in range(4):
                    sp.wait_ge(stored[n], 16 * (U // 4 + 1))

            @block.gpsimd
            def _(pool):
                pool.memset(w_down_r[:, E, :], 0.0).then_inc(S["zeroed"], 1)

            @block.tensor
            def _(pe):
                pe.wait_ge(S["w_loaded"], 3 * 16)
                pe.wait_ge(S["zeroed"], 1)

                numbers = [pe.alloc_register(f"expert{k}") for k in range(8)]
                experts = []

                def load_experts(u):
                    pe.load(numbers, tile_expert[0:1, bass.ds(u, 8)])

                def take_experts():
                    experts[:] = [pe.snap(r, min_val=0, max_val=E) for r in numbers]

                def turn_x(n, u):
                    n %= 4
                    pe.wait_ge(loaded[n], (u - n) * 4 + 16)
                    pe.transpose(x_ps[n % 2][:, 0:P], x[n][:, :], core.ident[:, :]).then_inc(S["xT_in_psum"], 1)

                def up(n, u):
                    e = experts[n]
                    n %= 4
                    pe.wait_ge(S["xT_ready"], u + 1)
                    pe.matmul(up_ps[n % 2][:, 0:2 * H], xT[n % 2][:, :], one(w_up, e), start=True, stop=True).then_inc(S["up_ready"], 1)

                def turn(n, u):
                    n %= 4
                    pe.wait_ge(S["h_ready"], u + 1)
                    pe.transpose(hT_ps[n % 2][:, 0:P], h[n % 2][:, 0:P], core.ident[:, :])
                    pe.transpose(hT_ps[n % 2][0:HR, P:2 * P], h[n % 2][:, P:H], core.ident[:, :]).then_inc(S["hT_in_psum"], 1)

                def down(n, u):
                    e = experts[n]
                    n %= 4
                    if isinstance(u, int) and u == U - 1:
                        pe.wait_ge(S["y_ready"], u - 1)
                    pe.wait_ge(S["hT_ready"], u + 1)
                    pe.matmul(y_ps[n % 2][:, 0:D], hT[n % 2][:, :], one(w_down, e), start=True, stop=False)
                    pe.matmul(y_ps[n % 2][:, 0:D], hTr[n % 2][:, :], one(w_down_r, e), start=False, stop=True).then_inc(S["y_in_psum"], 1)

                run(pe, [(0, turn_x), (1, up), (2, turn), (3, down)], take_experts, load_experts)

            @block.scalar
            def _(act):
                def silu(n, u):
                    n %= 4
                    act.wait_ge(S["up_ready"], u + 1)
                    act.activation(gate[n % 2][:, :], up_ps[n % 2][:, 0:H], ACT.Silu).then_inc(S["gate_ready"], 1)

                def copy_turned(n, u):
                    n %= 4
                    act.wait_ge(S["hT_in_psum"], u + 1)
                    act.copy(hT[n % 2][:, :], hT_ps[n % 2][:, 0:P])
                    act.copy(hTr[n % 2][:, :], hT_ps[n % 2][0:HR, P:2 * P]).then_inc(S["hT_ready"], 1)

                run(act, [(1, silu), (2, copy_turned)])

            @block.vector
            def _(dve):
                def copy_x(n, u):
                    n %= 4
                    dve.wait_ge(S["xT_in_psum"], u + 1)
                    dve.tensor_copy(xT[n % 2][:, :], x_ps[n % 2][:, 0:P]).then_inc(S["xT_ready"], 1)

                def multiply(n, u):
                    n %= 4
                    dve.wait_ge(S["gate_ready"], u + 1)
                    dve.tensor_tensor(h[n % 2][:, :], gate[n % 2][:, :], up_ps[n % 2][:, H:2 * H], ALU.mult).then_inc(S["h_ready"], 1)

                def copy_y(n, u):
                    n %= 4
                    dve.wait_ge(stored[n], (u - n) * 4 + 16)
                    dve.wait_ge(S["y_in_psum"], u + 1)
                    dve.tensor_copy(y[n][:, :], y_ps[n % 2][:, 0:D]).then_inc(S["y_ready"], 1)

                run(dve, [(0, copy_x), (1, multiply), (3, copy_y)])


def collect_six(core, take, weight, results):
    nc = core.nc
    core.phase = "collect0_"
    Z = Sparse
    K = Z.TOPK
    NB = 4
    with ExitStack() as c:
        sb = lambda n, s, d=F32: core.sbuf(n, s, d, c)
        sem = lambda n: core.sem(n, c)
        take_i = sb("take_i", [P, B, K], U32)
        back = [sb(f"back{n}", [P, K, D]) for n in range(NB)]
        shared = sb("shared", [P, B, D])
        index_ready, shared_loaded, chain = sem("index_ready"), sem("shared_loaded"), sem("chain")
        gathered = [sem(f"gathered{n}") for n in range(NB)]
        with nc.Block() as block:

            @block.sync
            def _(sp):
                sp.dma_start(shared[:, :, :], results[Z.ROUTED * P:Z.TILES * P, :].rearrange("(b p) d -> p b d", p=P)).then_inc(shared_loaded, 16)

            @block.gpsimd
            def _(pool):
                pool.wait_ge(index_ready, 1)
                for b in range(B):
                    if b >= NB:
                        pool.wait_ge(chain, 1 + K * (b - NB + 1))
                    for k in range(K):
                        pool.indirect_dma_start(out=back[b % NB][:, k, :], out_offset=None, in_=results,
                                                in_offset=bass.IndirectOffsetOnAxis(ap=take_i[:, b, k:k + 1], axis=0)).then_inc(gathered[b % NB], 16)

            @block.vector
            def _(dve):
                step = Chain(dve, chain)
                dve.tensor_copy(take_i[:, :, :], take[:, :, :]).then_inc(index_ready, 1)
                dve.wait_ge(shared_loaded, 16)
                step(dve.tensor_tensor(core.hidden[:, :, :], core.hidden[:, :, :], shared[:, :, :], ALU.add))
                for b in range(B):
                    dve.wait_ge(gathered[b % NB], 16 * K * (b // NB + 1))
                    for k in range(K):
                        step(dve.scalar_tensor_tensor(out=core.hidden[:, b, :], in0=back[b % NB][:, k, :], scalar=weight[:, b, k:k + 1],
                                                      in1=core.hidden[:, b, :], op0=ALU.mult, op1=ALU.add))


class ScanShapes:
    N, SD, H, NH, DH, L = 64, 128, 64, 4, 16, 2
    J = 4
    V = SD // J
    BA, OMG2, C2, G2, XH = 0, 64, 128, 192, 256
    F = 320


def scan_inputs(core, xn, w, record_part, record):
    nc = core.nc
    core.phase = "scan_in_"
    Z = ScanShapes
    SCALE = Z.SD ** -0.5
    with ExitStack() as c:
        sb = lambda n, s, d=F32: core.sbuf(n, s, d, c)
        sem = lambda n: core.sem(n, c)
        w_tok = sb("w_tok", [P, 2 * Z.SD + Z.H])
        b_tok = sb("b_tok", [P, 2 * Z.SD + Z.H])
        bp_b = sb("bp_b", [P, Z.H])
        b_wq = sb("b_wq", [Z.H, Z.SD])
        keys, keysT = sb("keys", [Z.N, Z.SD]), sb("keysT", [Z.SD, Z.N])
        b_in_col, b_bq_col = sb("b_in_col", [Z.H, 1]), sb("b_bq_col", [Z.SD, 1])
        stage, xT = sb("stage", [P, GB, D]), sb("xT", [P, GB, P])
        xhT = sb("xhT", [Z.H, GB, P])
        bqT = sb("bqT", [Z.SD, GB, P])
        rec = [sb(f"rec{n}", [P, GB, Z.F]) for n in range(2)]
        rec_part = [sb(f"rec_part{n}", [P, Z.J, GB, 2, Z.V]) for n in range(2)]
        top, total = sb("top", [P, GB]), sb("total", [P, GB])
        expo = sb("expo", [P, GB, Z.N])
        names = ("w_loaded", "keysT_in_psum", "keysT_ready", "staged", "xT_in_psum", "xT_ready", "tok_ready", "xhT_in_psum",
                 "xhT_ready", "bqT_in_psum", "bqT_ready", "logits_ready", "shifted", "exp_ready", "ba_ready", "exp2_ready",
                 "rec_ready", "chain")
        (w_loaded, keysT_in_psum, keysT_ready, staged, xT_in_psum, xT_ready, tok_ready, xhT_in_psum, xhT_ready, bqT_in_psum,
         bqT_ready, logits_ready, shifted, exp_ready, ba_ready, exp2_ready, rec_ready, chain_sem) = (sem(n) for n in names)
        rec_stored = [sem(f"rec_stored{n}") for n in range(2)]
        with nc.Block() as block:

            @block.sync
            def _(sp):
                o = 0
                for wn, bn in (("sb_wq", "sb_bq"), ("sb_ww", "sb_bw"), ("p_win", "p_bin")):
                    n = w[wn].shape[1]
                    sp.dma_start(w_tok[:, o:o + n], w[wn]).then_inc(w_loaded, 16)
                    sp.dma_start(b_tok[:, o:o + n], across(w[bn], P)).then_inc(w_loaded, 16)
                    o += n
                sp.dma_start(bp_b[:, :], across(w["bp_b"], P)).then_inc(w_loaded, 16)
                sp.dma_start(b_wq[:, :], w["b_wq"]).then_inc(w_loaded, 16)
                sp.dma_start(keys[:, :], w["b_keys"]).then_inc(w_loaded, 16)
                sp.dma_start(b_in_col[:, :], w["p_bin"].rearrange("(d a) -> d a", a=1)).then_inc(w_loaded, 16)
                sp.dma_start(b_bq_col[:, :], w["b_bq"].rearrange("(d a) -> d a", a=1)).then_inc(w_loaded, 16)
                for n in range(2):
                    sp.sem_inc(rec_stored[n], 32)
                with sp.Fori(0, NG // 2) as i:
                    for n in range(2):
                        sp.wait_ge(rec_ready, i * 2 + n + 1)
                        at = bass.ds(i * 2 * GB + n * GB, GB)
                        sp.dma_start(record[:, at, :], rec[n][:, :, :]).then_inc(rec_stored[n], 16)
                        sp.dma_start(record_part[:, :, at, :], rec_part[n][:, :, :, :, :].rearrange("p j b s d -> p j (b s d)")).then_inc(rec_stored[n], 16)
                for n in range(2):
                    sp.wait_ge(rec_stored[n], 32 * (NG // 2 + 1))

            @block.tensor
            def _(pe):
                pe.wait_ge(w_loaded, 11 * 16)
                pe.transpose(core.bank[0][:, 0:Z.N], keys[:, :], core.ident[0:Z.N, 0:Z.N]).then_inc(keysT_in_psum, 1)
                pe.wait_ge(keysT_ready, 1)
                with pe.Fori(0, NG // 2) as i:
                    for n in range(2):
                        g = i * 2 + n
                        pe.wait_ge(staged, g + 1)
                        for b in range(GB):
                            mm = pe.transpose(core.bank[0][:, b * P:(b + 1) * P], stage[:, b, :], core.ident[:, :])
                        mm.then_inc(xT_in_psum, 1)
                        pe.wait_ge(xT_ready, g + 1)
                        flat = xT[:, :, :].rearrange("p b t -> p (b t)")
                        pe.matmul(core.bank[1][0:Z.H, :], w_tok[:, 2 * Z.SD:], flat, start=True, stop=True).then_inc(xhT_in_psum, 1)
                        for b in range(GB):
                            mm = pe.matmul(core.bank[4 + b][:, 0:2 * Z.SD + Z.H], xT[:, b, :], w_tok[:, :], start=True, stop=True)
                        mm.then_inc(tok_ready, 1)
                        pe.wait_ge(xhT_ready, g + 1)
                        pe.matmul(core.bank[2][:, :], b_wq[:, :], xhT[:, :, :].rearrange("p b t -> p (b t)"), start=True, stop=True).then_inc(bqT_in_psum, 1)
                        pe.wait_ge(bqT_ready, g + 1)
                        for b in range(GB):
                            mm = pe.matmul(core.bank[3][:, b * Z.N:(b + 1) * Z.N], bqT[:, b, :], keysT[:, :], start=True, stop=True)
                        mm.then_inc(logits_ready, 1)

            @block.scalar
            def _(act):
                act.wait_ge(keysT_in_psum, 1)
                act.copy(keysT[:, :], core.bank[0][:, 0:Z.N]).then_inc(keysT_ready, 1)
                act.wait_ge(w_loaded, 11 * 16)
                with act.Fori(0, NG // 2) as i:
                    for n in range(2):
                        g = i * 2 + n
                        act.wait_ge(xT_in_psum, g + 1)
                        act.copy(xT[:, :, :].rearrange("p b t -> p (b t)"), core.bank[0][:, :]).then_inc(xT_ready, 1)
                        act.wait_ge(xhT_in_psum, g + 1)
                        act.activation(xhT[:, :, :].rearrange("p b t -> p (b t)"), core.bank[1][0:Z.H, :], ACT.Identity,
                                       bias=b_in_col[:, :]).then_inc(xhT_ready, 1)
                        act.wait_ge(bqT_in_psum, g + 1)
                        act.activation(bqT[:, :, :].rearrange("p b t -> p (b t)"), core.bank[2][:, :], ACT.Identity,
                                       bias=b_bq_col[:, :]).then_inc(bqT_ready, 1)
                        act.wait_ge(shifted, g + 1)
                        act.activation(expo[:, :, :], expo[:, :, :], ACT.Exp, scale=SCALE).then_inc(exp_ready, 1)
                        act.wait_ge(ba_ready, g + 1)
                        act.activation(expo[:, :, :], rec[n][:, :, Z.BA:Z.BA + Z.N], ACT.Exp, scale=-1.0).then_inc(exp2_ready, 1)

            @block.vector
            def _(dve):
                step = Chain(dve, chain_sem)
                dve.wait_ge(w_loaded, 11 * 16)
                with dve.Fori(0, NG // 2) as i:
                    step.enter(i, 2 * (3 * GB + 8))
                    for n in range(2):
                        g = i * 2 + n
                        cols = lambda a, k=Z.N: rec[n][:, :, a:a + k]
                        dve.tensor_copy(stage[:, :, :], xn[:, bass.ds(i * 2 * GB + n * GB, GB), :]).then_inc(staged, 1)
                        dve.wait_ge(tok_ready, g + 1)
                        dve.wait_ge(rec_stored[n], i * 32 + 32)
                        for b in range(GB):
                            for s in range(2):
                                cs = slice(s * Z.SD, (s + 1) * Z.SD)
                                part = lambda ap: ap.rearrange("p (j d) -> p j d", j=Z.J)
                                step.tick(dve.tensor_tensor(rec_part[n][:, :, b, s, :], part(core.bank[4 + b][:, cs]), part(b_tok[:, cs]), ALU.add))
                            step.tick(dve.tensor_tensor(rec[n][:, b, Z.XH:Z.XH + Z.H], core.bank[4 + b][:, 2 * Z.SD:2 * Z.SD + Z.H], b_tok[:, 2 * Z.SD:], ALU.add))
                        dve.wait_ge(logits_ready, g + 1)
                        lg = core.bank[3][:, 0:GB * Z.N].rearrange("p (b n) -> p b n", b=GB)
                        step(dve.tensor_reduce(top[:, :], lg, X, ALU.max))
                        dve.tensor_tensor(expo[:, :, :], lg, top[:, :].unsqueeze(2).to_broadcast([P, GB, Z.N]), ALU.subtract).then_inc(shifted, 1)
                        query = rec_part[n][:, :, :, 0, :].rearrange("p j b d -> p (j b) d")
                        step.tick(dve.tensor_scalar(query, query, SCALE, None, ALU.mult))
                        step(dve.tensor_tensor(cols(Z.XH), cols(Z.XH), bp_b[:, :].unsqueeze(1).to_broadcast([P, GB, Z.H]), ALU.add))
                        dve.wait_ge(exp_ready, g + 1)
                        step(dve.tensor_reduce(total[:, :], expo[:, :, :], X, ALU.add))
                        step(dve.reciprocal(total[:, :], total[:, :]))
                        dve.tensor_tensor(cols(Z.BA), expo[:, :, :], total[:, :].unsqueeze(2).to_broadcast([P, GB, Z.N]), ALU.mult).then_inc(ba_ready, 1)
                        dve.wait_ge(exp2_ready, g + 1)
                        step(dve.tensor_scalar(cols(Z.OMG2), expo[:, :, :], 1.0, None, ALU.add))
                        step(dve.reciprocal(cols(Z.G2), cols(Z.OMG2)))
                        step.tick(dve.tensor_tensor(cols(Z.C2), cols(Z.G2), cols(Z.BA), ALU.mult))
                        dve.tensor_tensor(cols(Z.OMG2), expo[:, :, :], cols(Z.G2), ALU.mult).then_inc(rec_ready, 1)
                    step.leave(NG // 2)


def scan_tokens(core, w, record_part, record, reads, states):
    nc = core.nc
    core.phase = "scan_"
    Z = ScanShapes
    N, H, J, DH = Z.N, Z.H, Z.J, Z.DH
    V = Z.SD // J
    M = N + 2
    LOADS = 2 + Z.L * (8 * J + 4) + 2 * J
    PER = 61
    R1, R2 = N // 4, N * 5 // 8
    STEPS = T + 1
    with ExitStack() as c:
        sb = lambda n, s, d=F32: core.sbuf(n, s, d, c)
        sem = lambda n: core.sem(n, c)
        slots = sb("slots", [P, M, V])
        prod, prod_r, prod_q = (sb(n, [P, M, V]) for n in ("prod", "prod_r", "prod_q"))
        write, write_u = sb("write", [P, N, V]), sb("write_u", [P, N, V])
        delta = sb("delta", [P, N])
        same_b = sb("same_b", [P, P])
        part_of = sb("part_of", [P, J])
        bp_w = sb("bp_w", [Z.SD, H])
        w_qkv = sb("w_qkv", [H + 1, Z.L, J, 3 * DH + 1])
        w_o = sb("w_o", [H, Z.L, H])
        w_sup = sb("w_sup", [H + 1, Z.SD])
        bo, ln_g, ln_b = sb("bo", [P, Z.L, H]), sb("ln_g", [P, Z.L, H]), sb("ln_b", [P, Z.L, H])
        in_part = [sb(f"in_part{n}", [P, 2 * V]) for n in range(2)]
        in_q, in_wr = [p[:, 0:V] for p in in_part], [p[:, V:2 * V] for p in in_part]
        in_rep = [sb(f"in_rep{n}", [P, Z.F]) for n in range(2)]
        part, logits = sb("part", [P, M + 1]), sb("logits", [P, N])
        early, extra = sb("early", [P, N]), sb("extra", [P, 3])
        last, keep_last = sb("last", [P, N]), sb("keep_last", [P, N])
        qu = sb("qu", [P, 1])
        nmax, den, rden = sb("nmax", [P, 1]), sb("den", [P, 1]), sb("rden", [P, 1])
        e_a, a, ea, g, omg, w2, keep, c1, gab = (sb(n, [P, M]) for n in ("e_a", "a", "ea", "g", "omg", "w2", "keep", "c1", "gab"))
        junk, junk2, cwr = sb("junk", [P, N]), sb("junk2", [P, N]), sb("cwr", [P, 1])
        bind, bind_wide, bindT = sb("bind", [P, V]), sb("bind_wide", [P, J, V]), sb("bindT", [Z.SD, P])
        xh, xhb = sb("xh", [P, H]), sb("xhb", [P, H])
        xhT = sb("xhT", [H + 1, B])
        qkv = sb("qkv", [P, 3 * DH + 1])
        eb, beta, ssq, kq, nrm, rk, rkq, rb = (sb(n, [P, 1]) for n in ("eb", "beta", "ssq", "kq", "nrm", "rk", "rkq", "rb"))
        vb = sb("vb", [P, DH])
        mem = [sb(f"mem{l}", [P, DH, DH]) for l in range(Z.L)]
        mprod = sb("mprod", [P, 2, DH, DH])
        msum = sb("msum", [P, 2, DH])
        kn, dv = ([sb(f"{n}{l}", [P, DH]) for l in range(Z.L)] for n in ("kn", "dv"))
        no, no_wide = sb("no", [P, DH]), sb("no_wide", [P, J, DH])
        outer_m = sb("outer_m", [P, DH, DH])
        oT = sb("oT", [H, P])
        stats, mv, lnv, rstd = sb("stats", [P, 6]), sb("mv", [P, 2]), sb("lnv", [P, 1]), sb("rstd", [P, 1])
        waiter = sb("waiter", [1, 1])
        out_x = [sb(f"out_x{n}", [P, H]) for n in range(2)]
        out_r = [sb(f"out_r{n}", [P, V]) for n in range(2)]
        names = ("w_loaded", "consts_ready", "w_ready", "part_ready", "lg_in_psum", "u_ready", "qu_ready", "qu_in_psum",
                 "nmax_ready", "exp_ready", "a_ready", "ea_ready", "ax_ready", "prod_r_ready", "coef_ready", "outer_done",
                 "queried", "slots_ready", "bind_ready", "bindT_in_psum", "bindT_ready", "xh_in_psum", "xh_ready", "xhT_in_psum",
                 "xhT_ready", "qkv_in_psum", "qkv_ready", "eb_ready", "ssq_ready", "nrm_ready", "dv_ready", "mem_ready",
                 "no_ready", "oT_in_psum", "oT_ready", "o_in_psum", "mv_ready", "rstd_ready", "read_in_psum",
                 "read_ready", "step_done", "chain", "act_chain", "pool_chain")
        S = {n: sem(n) for n in names}
        loaded = [sem(f"loaded{n}") for n in range(2)]
        stored = [sem(f"stored{n}") for n in range(2)]
        A, QU, BT, D_, E_, F_, R_, U_ = core.bank
        C_, G_ = BT[:, P:2 * P], F_[:, P:2 * P]

        def col(n, name, width=N):
            return in_rep[n][:, name:name + width]

        with nc.Block() as block:

            @block.sync
            def _(sp):
                loads = [(bp_w[:, :], w["bp_w"]),
                         (w_sup[0:H, :], w["sup_w"])]
                for l in range(Z.L):
                    loads += [(w_qkv[0:H, l, j, s * DH:(s + 1) * DH], w["dn_wqkv"][l][:, s * H + j * DH:s * H + (j + 1) * DH])
                              for s in range(3) for j in range(J)]
                    loads += [(w_qkv[H:H + 1, l, j, s * DH:(s + 1) * DH],
                               w["dn_bqkv"][l:l + 1, s * H + j * DH:s * H + (j + 1) * DH]) for s in range(3) for j in range(J)]
                    loads += [(w_qkv[0:H, l, j, 3 * DH:], w["dn_wbeta"][l][:, j:j + 1]) for j in range(J)]
                    loads += [(w_qkv[H:H + 1, l, j, 3 * DH:], w["dn_bbeta"][l:l + 1, j:j + 1]) for j in range(J)]
                    loads += [(w_o[:, l, :], w["dn_wo"][l])]
                    loads += [(dst[:, l, :], w[name][l:l + 1, :].to_broadcast([P, H]))
                              for dst, name in ((bo, "dn_bo"), (ln_g, "dn_lng"), (ln_b, "dn_lnb"))]
                for j in range(J):
                    loads += [(slots[32 * j:32 * j + 32, 0:N, :], w["sb_init"][:, V * j:V * j + V].unsqueeze(0).to_broadcast([B, N, V])),
                              (slots[32 * j:32 * j + 32, N, :], w["sup_b"][V * j:V * j + V].unsqueeze(0).to_broadcast([B, V]))]
                for dst, src in loads:
                    sp.dma_start(dst, src, allow_slow_non_contiguous=dst.shape[-1] == 1).then_inc(S["w_loaded"], 16)
                assert len(loads) == LOADS

                def load(t, n):
                    sp.dma_start(in_part[n][:, :], record_part[bass.ds(t, 1), :, :, :].rearrange("t j b f -> (t j b) f")).then_inc(loaded[n], 16)
                    for j in range(J):
                        sp.dma_start(in_rep[n][B * j:B * j + B, :], record[bass.ds(t, 1), :, :].rearrange("t b f -> (t b) f")).then_inc(loaded[n], 16)

                def store(t, n):
                    sp.wait_ge(S["read_ready"], t + 1)
                    sp.dma_start(reads[bass.ds(t, 1), :, :, :].rearrange("t j b d -> (t j b) d"), out_r[n][:, :]).then_inc(stored[n], 16)
                    sp.wait_ge(S["xh_ready"], t * 3 + 3)
                    sp.dma_start(states[bass.ds(t, 1), :, :].rearrange("t b f -> (t b) f"), out_x[n][0:B, :]).then_inc(stored[n], 16)

                for n in range(2):
                    sp.sem_inc(stored[n], 32)
                    load(n, n)
                with sp.Fori(0, STEPS // 2 - 1) as i:
                    for n in range(2):
                        store(i * 2 + n, n)
                        sp.wait_ge(S["step_done"], i * 2 + n + 1)
                        load(i * 2 + n + 2, n)
                store(STEPS - 2, 0)
                sp.wait_ge(S["step_done"], STEPS - 1)
                load(STEPS - 1, 0)
                store(STEPS - 1, 1)
                sp.wait_ge(loaded[0], 80 * (STEPS // 2 + 1))
                for n in range(2):
                    sp.wait_ge(stored[n], 32 * (STEPS // 2 + 1))

            @block.gpsimd
            def _(pool):
                step = Chain(pool, S["pool_chain"])
                step(pool.memset(same_b[:, :], 0.0))
                for s in range(1 - J, J):
                    step(pool.affine_select(out=same_b[:, :], in_=same_b[:, :], compare_op=ALU.not_equal, fill=1.0,
                                            base=B * s, pattern=[[-1, P]], channel_multiplier=1))
                step(pool.memset(part_of[:, :], 0.0))
                for j in range(J):
                    step(pool.memset(part_of[B * j:B * j + B, j:j + 1], 1.0))
                step(pool.memset(last[:, :], 0.0))
                step(pool.memset(slots[:, N + 1, :], 0.0))
                pool.memset(delta[:, :], 0.0).then_inc(S["consts_ready"], 1)
                pool.memset(xhT[:, :], 1.0).then_inc(S["consts_ready"], 1)
                pool.wait_ge(S["consts_ready"], 2)
                pool.memset(w_sup[H:H + 1, :], 0.0).then_inc(S["consts_ready"], 1)
                pool.wait_ge(S["consts_ready"], 3)
                for l in range(Z.L):
                    pool.memset(mem[l][:, :, :], 0.0).then_inc(S["consts_ready"], 1)
                pool.sem_inc(S["mem_ready"], Z.L)
                pool.sem_inc(S["slots_ready"], 1)
                with pool.Fori(0, STEPS // 2) as i:
                    step.enter(i, 2 * (Z.L + 3))
                    for n in range(2):
                        t = i * 2 + n
                        wide = lambda ap: ap[:, 0:N].unsqueeze(2).to_broadcast([P, N, V])

                        def update_memory(l):
                            pool.wait_ge(S["dv_ready"], t * 2 + l + 1)
                            step(pool.tensor_tensor(outer_m[:, :, :], dv[l][:, :].unsqueeze(2).to_broadcast([P, DH, DH]),
                                                    kn[l][:, :].unsqueeze(1).to_broadcast([P, DH, DH]), ALU.mult))
                            pool.tensor_tensor(mem[l][:, :, :], mem[l][:, :, :], outer_m[:, :, :], ALU.subtract).then_inc(S["mem_ready"], 1)
                            pool.wait_ge(S["mem_ready"], t * 2 + l + 1 + Z.L)

                        pool.wait_ge(S["ax_ready"], t + 1)
                        pool.tensor_tensor(prod_r[:, :, :], slots[:, :, :], a[:, :].unsqueeze(2).to_broadcast([P, M, V]), ALU.mult).then_inc(S["prod_r_ready"], 1)
                        pool.wait_ge(S["coef_ready"], t + 1)
                        step(pool.tensor_tensor(write[:, :, :], in_wr[n].unsqueeze(1).to_broadcast([P, N, V]), wide(c1), ALU.mult))
                        pool.tensor_tensor(write_u[:, :, :], slots[:, N + 1:M, :].to_broadcast([P, N, V]), wide(keep_last), ALU.mult).then_inc(S["outer_done"], 1)
                        pool.wait_ge(S["outer_done"], t + 1)
                        step(pool.tensor_tensor(write[:, :, :], write[:, :, :], write_u[:, :, :], ALU.add))
                        update_memory(0)
                        pool.wait_ge(S["queried"], t + 1)
                        step(pool.tensor_tensor(slots[:, 0:N, :], slots[:, 0:N, :], wide(keep), ALU.mult))
                        pool.tensor_tensor(slots[:, 0:N, :], slots[:, 0:N, :], write[:, :, :], ALU.add).then_inc(S["slots_ready"], 1)
                        pool.wait_ge(S["slots_ready"], t + 2)
                        update_memory(1)
                    step.leave(STEPS // 2)

            @block.tensor
            def _(pe):
                pe.wait_ge(S["pool_chain"], 3 * J + 3)
                pe.wait_ge(S["consts_ready"], 3 + Z.L)
                pe.wait_ge(S["w_ready"], 1)
                pe.wait_ge(S["part_ready"], 1)
                pe.matmul(A[:, 0:M + 1], same_b[:, :], part[:, :], start=True, stop=True).then_inc(S["lg_in_psum"], 1)
                with pe.Fori(0, STEPS // 2) as i:
                    for n in range(2):
                        t = i * 2 + n

                        def turn_xh(which):
                            pe.wait_ge(S["xh_ready"], t * 3 + which + 1)
                            src = out_x[n] if which == 2 else xh
                            pe.matmul(D_[0:H, 0:B], src[0:B, :], core.ident[0:B, 0:B], start=True, stop=True).then_inc(S["xhT_in_psum"], 1)
                            pe.wait_ge(S["xhT_ready"], t * 3 + which + 1)

                        pe.wait_ge(S["qu_ready"], t + 1)
                        pe.matmul(QU[:, 0:1], same_b[:, :], qu[:, :], start=True, stop=True).then_inc(S["qu_in_psum"], 1)
                        pe.wait_ge(S["bind_ready"], t + 1)
                        pe.matmul(BT[:, 0:P], bind_wide[:, :, :].rearrange("p j d -> p (j d)"), same_b[:, :], start=True, stop=True).then_inc(S["bindT_in_psum"], 1)
                        pe.wait_ge(S["bindT_ready"], t + 1)
                        pe.matmul(C_[:, 0:H], bindT[:, :], bp_w[:, :], start=True, stop=True).then_inc(S["xh_in_psum"], 1)
                        for l in range(Z.L):
                            turn_xh(l)
                            for j in range(J):
                                mm = pe.matmul(E_[B * j:B * j + B, 0:3 * DH + 1], xhT[:, :], w_qkv[:, l, j, :], start=True, stop=True)
                            mm.then_inc(S["qkv_in_psum"], 1)
                            if l == 0:
                                pe.wait_ge(S["prod_r_ready"], t + 1)
                            for k in range(l * 2, l * 2 + 2):
                                pe.matmul(R_[:, :], core.ident[:, :], prod_r[:, 16 * k:16 * k + 16, :].rearrange("p n d -> p (n d)"), start=k == 0, stop=False)
                            if l == Z.L - 1:
                                pe.matmul(R_[:, 0:2 * V], core.ident[:, :], prod_r[:, N:M, :].rearrange("p n d -> p (n d)"), start=False, stop=True).then_inc(S["read_in_psum"], 1)
                            pe.wait_ge(S["no_ready"], t * 2 + l + 1)
                            pe.matmul(F_[0:H, 0:P], no_wide[:, :, :].rearrange("p j d -> p (j d)"), same_b[:, :], start=True, stop=True).then_inc(S["oT_in_psum"], 1)
                            pe.wait_ge(S["oT_ready"], t * 2 + l + 1)
                            pe.matmul(G_[:, 0:H], oT[:, :], w_o[:, l, :], start=True, stop=True).then_inc(S["o_in_psum"], 1)
                            if l == Z.L - 1:
                                pe.wait_ge(S["part_ready"], t + 2)
                                pe.matmul(A[:, 0:M + 1], same_b[:, :], part[:, :], start=True, stop=True).then_inc(S["lg_in_psum"], 1)
                        turn_xh(2)
                        for j in range(J):
                            mm = pe.matmul(U_[B * j:B * j + B, 0:V], xhT[:, :], w_sup[:, V * j:V * j + V], start=True, stop=True)
                        mm.then_inc(S["u_ready"], 1)

            @block.scalar
            def _(act):
                act.preload_act_table_set("natural_log_exp_and_others")
                step = Chain(act, S["act_chain"])
                act.wait_ge(S["consts_ready"], 3 + Z.L)
                with act.Fori(0, STEPS // 2) as i:
                    step.enter(i, 2 * Z.L * 2)
                    for n in range(2):
                        t = i * 2 + n

                        def copy_xhT(which):
                            act.wait_ge(S["xhT_in_psum"], t * 3 + which + 1)
                            act.copy(xhT[0:H, :], D_[0:H, 0:B]).then_inc(S["xhT_ready"], 1)

                        act.wait_ge(S["nmax_ready"], t + 1)
                        act.activation(e_a[:, 0:N], logits[:, :], ACT.Exp, bias=nmax[:, :], accum_out=den[:, :]).then_inc(S["exp_ready"], 1)
                        act.wait_ge(S["a_ready"], t + 1)
                        act.activation(ea[:, 0:N], a[:, 0:N], ACT.Exp, scale=-1.0).then_inc(S["ea_ready"], 1)
                        act.wait_ge(S["bindT_in_psum"], t + 1)
                        act.copy(bindT[:, :], BT[:, 0:P]).then_inc(S["bindT_ready"], 1)
                        for l in range(Z.L):
                            copy_xhT(l)
                            act.wait_ge(S["qkv_ready"], t * 2 + l + 1)
                            act.activation(eb[:, :], qkv[:, 3 * DH:3 * DH + 1], ACT.Exp, scale=-1.0).then_inc(S["eb_ready"], 1)
                            act.wait_ge(S["ssq_ready"], t * 2 + l + 1)
                            step(act.activation(nrm[:, :], ssq[:, :], ACT.Ln))
                            act.activation(nrm[:, :], nrm[:, :], ACT.Exp, scale=0.5).then_inc(S["nrm_ready"], 1)
                            act.wait_ge(S["oT_in_psum"], t * 2 + l + 1)
                            act.copy(oT[:, :], F_[0:H, 0:P]).then_inc(S["oT_ready"], 1)
                            act.wait_ge(S["mv_ready"], t * 2 + l + 1)
                            step(act.activation(lnv[:, :], mv[:, 1:2], ACT.Ln, bias=EPS))
                            act.activation(rstd[:, :], lnv[:, :], ACT.Exp, scale=-0.5).then_inc(S["rstd_ready"], 1)
                        copy_xhT(2)
                    step.leave(STEPS // 2)

            @block.vector
            def _(dve):
                step = Chain(dve, S["chain"])
                dve.wait_ge(S["w_loaded"], 16 * LOADS)
                dve.wait_ge(S["consts_ready"], 3 + Z.L)
                dve.tensor_scalar(w_o[:, :, :], w_o[:, :, :], -1.0, None, ALU.mult).then_inc(S["w_ready"], 1)
                spread = lambda ap, k=N: ap[:, 0:k].unsqueeze(2).to_broadcast([P, k, V])
                def query(q, first, end):
                    return dve.tensor_tensor(prod_q[:, first:end, :], slots[:, first:end, :], q.unsqueeze(1).to_broadcast([P, end - first, V]), ALU.mult)

                def summed(first, end):
                    return dve.tensor_reduce(part[:, first:end], prod_q[:, first:end, :], X, ALU.add)

                dve.wait_ge(loaded[0], 80)
                dve.memset(U_[:, 0:V], 0.0).then_inc(S["u_ready"], 1)
                step(query(in_q[0], 0, M))
                step.tick(dve.memset(part[:, M:M + 1], 0.0))
                summed(0, M).then_inc(S["part_ready"], 1)
                dve.wait_ge(S["lg_in_psum"], 1)
                step(dve.tensor_copy(early[:, :], A[:, 0:N]))
                with dve.Fori(0, STEPS // 2) as i:
                    step.enter(i, 2 * PER)
                    for n in range(2):
                        t = i * 2 + n
                        m = 1 - n
                        dve.wait_ge(S["u_ready"], t + 1)
                        dve.tensor_tensor_reduce(junk[:, 0:V], U_[:, 0:V], in_q[n], 1.0, 0.0, ALU.mult, ALU.add, qu[:, :]).then_inc(S["qu_ready"], 1)
                        step.tick(dve.tensor_copy(slots[:, N + 1, :], U_[:, 0:V]))
                        dve.wait_ge(S["qu_in_psum"], t + 1)
                        step(dve.scalar_tensor_tensor(out=logits[:, :], in0=last[:, :], scalar=QU[:, 0:1], in1=early[:, :], op0=ALU.mult, op1=ALU.add))
                        dve.tensor_reduce(nmax[:, :], logits[:, :], X, ALU.max, negate=True).then_inc(S["nmax_ready"], 1)
                        dve.wait_ge(S["exp_ready"], t + 1)
                        step(dve.reciprocal(rden[:, :], den[:, :]))
                        dve.tensor_scalar(a[:, 0:N], e_a[:, 0:N], rden[:, :], None, ALU.mult).then_inc(S["a_ready"], 1)
                        dve.wait_ge(S["a_ready"], t + 1)
                        step.tick(dve.tensor_tensor_reduce(junk[:, :], a[:, 0:N], delta[:, :], 1.0, 0.0, ALU.mult, ALU.add, a[:, N:N + 1]))
                        dve.tensor_tensor_reduce(junk2[:, :], a[:, 0:N], last[:, :], 1.0, 0.0, ALU.mult, ALU.add, a[:, N + 1:M]).then_inc(S["ax_ready"], 1)
                        dve.wait_ge(S["ea_ready"], t + 1)
                        step(dve.tensor_scalar(g[:, 0:N], ea[:, 0:N], 1.0, None, ALU.add))
                        step(dve.reciprocal(g[:, 0:N], g[:, 0:N]))
                        step.tick(dve.tensor_tensor(omg[:, 0:N], ea[:, 0:N], g[:, 0:N], ALU.mult))
                        step(dve.tensor_tensor(gab[:, 0:N], g[:, 0:N], a[:, 0:N], ALU.mult))
                        step.tick(dve.tensor_tensor(w2[:, 0:N], omg[:, 0:N], col(n, Z.BA), ALU.mult))
                        dve.wait_ge(S["slots_ready"], t + 1)
                        step(dve.tensor_tensor(keep[:, 0:N], omg[:, 0:N], col(n, Z.OMG2), ALU.mult))
                        step.tick(dve.tensor_tensor_reduce(junk[:, :], w2[:, 0:N], delta[:, :], 1.0, 0.0, ALU.mult, ALU.add, w2[:, N:N + 1]))
                        step.tick(dve.tensor_tensor_reduce(junk2[:, :], w2[:, 0:N], last[:, :], 1.0, 0.0, ALU.mult, ALU.add, w2[:, N + 1:M]))
                        step.tick(dve.tensor_tensor(c1[:, 0:N], gab[:, 0:N], col(n, Z.OMG2), ALU.mult))
                        dve.tensor_tensor(keep_last[:, :], keep[:, 0:N], last[:, :], ALU.mult).then_inc(S["coef_ready"], 1)
                        step.settle()
                        step.tick(dve.tensor_tensor(prod[:, :, :], slots[:, :, :], spread(w2, M), ALU.mult))
                        step(dve.tensor_tensor_reduce(junk[:, :], gab[:, 0:N], col(n, Z.BA), 1.0, 0.0, ALU.mult, ALU.add, cwr[:, :]))
                        step(dve.tensor_reduce(bind[:, :], prod[:, :, :].rearrange("p n d -> p d n"), X, ALU.add))
                        step(dve.scalar_tensor_tensor(out=bind[:, :], in0=in_wr[n], scalar=cwr[:, :], in1=bind[:, :], op0=ALU.mult, op1=ALU.add))
                        dve.tensor_tensor(bind_wide[:, :, :], bind[:, :].unsqueeze(1).to_broadcast([P, J, V]),
                                          part_of[:, :].unsqueeze(2).to_broadcast([P, J, V]), ALU.mult).then_inc(S["bind_ready"], 1)
                        step.tick(dve.tensor_tensor(delta[:, :], delta[:, :], keep[:, 0:N], ALU.mult))
                        dve.wait_ge(S["coef_ready"], t + 1)
                        step(dve.tensor_copy(last[:, :], col(n, Z.C2)))
                        step.tick(dve.tensor_tensor(delta[:, :], delta[:, :], col(n, Z.G2), ALU.add))
                        dve.wait_ge(loaded[m], i * 80 + 80 + 80 * n)
                        step.tick(query(in_q[m], 0, R1))
                        dve.wait_ge(S["xh_in_psum"], t + 1)
                        dve.tensor_tensor(xh[:, :], C_[:, 0:H], col(n, Z.XH, H), ALU.add).then_inc(S["xh_ready"], 1)
                        dve.wait_ge(S["xh_ready"], t * 3 + 1)
                        for l in range(Z.L):
                            step.tick(dve.tensor_tensor(xhb[:, :], xh[:, :], bo[:, l, :], ALU.add))
                            if l == 0:
                                step.tick(query(in_q[m], R1, R2))
                            else:
                                step.tick(summed(R1, R2))
                            dve.wait_ge(S["qkv_in_psum"], t * 2 + l + 1)
                            dve.tensor_copy(qkv[:, :], E_[:, 0:3 * DH + 1]).then_inc(S["qkv_ready"], 1)
                            dve.wait_ge(S["qkv_ready"], t * 2 + l + 1)
                            q, k, v = (qkv[:, s * DH:(s + 1) * DH] for s in range(3))
                            step.tick(dve.tensor_tensor_reduce(junk[:, 0:DH], k, k, 1.0, 1e-19, ALU.mult, ALU.add, ssq[:, :]))
                            dve.tensor_tensor_reduce(junk2[:, 0:DH], k, q, 1.0, 0.0, ALU.mult, ALU.add, kq[:, :]).then_inc(S["ssq_ready"], 1)
                            dve.wait_ge(S["mem_ready"], t * 2 + l + 1)
                            step.tick(dve.tensor_tensor(mprod[:, :, :, :], mem[l][:, :, :].unsqueeze(1).to_broadcast([P, 2, DH, DH]),
                                                        qkv[:, 0:2 * DH].rearrange("p (s j) -> p s j", s=2).unsqueeze(2).to_broadcast([P, 2, DH, DH]), ALU.mult))
                            dve.wait_ge(S["eb_ready"], t * 2 + l + 1)
                            step.tick(dve.tensor_scalar(beta[:, :], eb[:, :], 1.0, None, ALU.add))
                            dve.wait_ge(S["nrm_ready"], t * 2 + l + 1)
                            step(dve.tensor_scalar(nrm[:, :], nrm[:, :], 1e-6, None, ALU.add))
                            step.tick(dve.reciprocal(beta[:, :], beta[:, :]))
                            step.tick(dve.reciprocal(rk[:, :], nrm[:, :]))
                            step(dve.tensor_reduce(msum[:, :, :], mprod[:, :, :, :], X, ALU.add))
                            step.tick(dve.tensor_tensor(rb[:, :], rk[:, :], beta[:, :], ALU.mult))
                            step.tick(dve.tensor_scalar(vb[:, :], v, beta[:, :], None, ALU.mult))
                            step.tick(dve.tensor_tensor(rkq[:, :], kq[:, :], rk[:, :], ALU.mult))
                            step(dve.tensor_scalar(kn[l][:, :], k, rk[:, :], None, ALU.mult))
                            dve.scalar_tensor_tensor(out=dv[l][:, :], in0=msum[:, 1, :], scalar=rb[:, :], in1=vb[:, :], op0=ALU.mult, op1=ALU.subtract).then_inc(S["dv_ready"], 1)
                            dve.wait_ge(S["dv_ready"], t * 2 + l + 1)
                            step(dve.scalar_tensor_tensor(out=no[:, :], in0=dv[l][:, :], scalar=rkq[:, :], in1=msum[:, 0, :], op0=ALU.mult, op1=ALU.subtract))
                            dve.tensor_tensor(no_wide[:, :, :], no[:, :].unsqueeze(1).to_broadcast([P, J, DH]),
                                              part_of[:, :].unsqueeze(2).to_broadcast([P, J, DH]), ALU.mult).then_inc(S["no_ready"], 1)
                            if l == 0:
                                query(in_q[m], R2, M).then_inc(S["queried"], 1)
                                step.tick(summed(0, R1))
                            else:
                                step.tick(dve.tensor_tensor_reduce(junk[:, 0:V], in_wr[n], in_q[m], 1.0, 0.0, ALU.mult, ALU.add, part[:, M:M + 1]))
                                dve.wait_ge(S["queried"], t + 1)
                                summed(R2, M).then_inc(S["part_ready"], 1)
                                dve.wait_ge(S["read_in_psum"], t + 1)
                                dve.wait_ge(stored[n], i * 32 + 32)
                                dve.tensor_reduce(out_r[n][:, :], R_[:, :].rearrange("p (n d) -> p d n", d=V), X, ALU.add).then_inc(S["read_ready"], 1)
                            dve.wait_ge(S["o_in_psum"], t * 2 + l + 1)
                            step(dve.tensor_tensor(xhb[:, :], G_[:, 0:H], xhb[:, :], ALU.add))
                            step(dve.bn_stats(stats[:, :], xhb[:, :]))
                            dve.memset(waiter[:, :], 0.0)
                            dve.bn_aggr(mv[:, :], stats[:, :]).then_inc(S["mv_ready"], 1)
                            dve.wait_ge(S["mv_ready"], t * 2 + l + 1)
                            step(dve.scalar_tensor_tensor(out=xhb[:, :], in0=xhb[:, :], scalar=mv[:, 0:1], in1=ln_g[:, l, :], op0=ALU.subtract, op1=ALU.mult))
                            dve.wait_ge(S["rstd_ready"], t * 2 + l + 1)
                            dst = xh if l == 0 else out_x[n]
                            dve.scalar_tensor_tensor(out=dst[:, :], in0=xhb[:, :], scalar=rstd[:, :], in1=ln_b[:, l, :], op0=ALU.mult, op1=ALU.add).then_inc(S["xh_ready"], 1)
                            dve.wait_ge(S["xh_ready"], t * 3 + l + 2)
                        dve.wait_ge(S["lg_in_psum"], t + 2)
                        step.tick(dve.tensor_copy(extra[:, :], A[:, N:M + 1]))
                        dve.wait_ge(S["outer_done"], t + 1)
                        step(dve.tensor_tensor(early[:, :], A[:, 0:N], keep[:, 0:N], ALU.mult))
                        for k, coef in enumerate((delta, keep_last, c1)):
                            ins = dve.scalar_tensor_tensor(out=early[:, :], in0=coef[:, 0:N], scalar=extra[:, k:k + 1], in1=early[:, :], op0=ALU.mult, op1=ALU.add)
                            if k < 2:
                                step(ins)
                        ins.then_inc(S["step_done"], 1)
                        dve.wait_ge(S["step_done"], t + 1)
                    step.leave(STEPS // 2)


def scan_outputs(core, w, reads, states):
    nc = core.nc
    core.phase = "after_scan_"
    Z = ScanShapes
    with ExitStack() as c:
        sb = lambda n, s, d=F32: core.sbuf(n, s, d, c)
        sem = lambda n: core.sem(n, c)
        wo, op_w, ow = sb("wo", [Z.SD, D]), sb("op_w", [Z.H, D]), sb("ow", [D, D])
        rows = {n: sb(n, [P, D]) for n in ("sb_bo", "op_b", "oln_g", "oln_b", "ob")}
        r = [sb(f"r{n}", [P, GB, Z.SD]) for n in range(2)]
        x = [sb(f"x{n}", [P, GB, Z.H]) for n in range(2)]
        rT, xT = sb("rT", [Z.SD, GB, P]), sb("xT", [Z.H, GB, P])
        y, sq, yT = sb("y", [P, GB, D]), sb("sq", [P, GB, D]), sb("yT", [D, GB, P])
        mean, var = sb("mean", [P, GB]), sb("var", [P, GB])
        names = ("w_loaded", "rT_in_psum", "xT_in_psum", "rT_ready", "xT_ready", "y_in_psum", "centred", "squared", "var_ready", "rstd_ready",
                 "y_ready", "yT_in_psum", "yT_ready", "out_in_psum", "hidden_added", "chain", "act_chain")
        S = {n: sem(n) for n in names}
        loaded = [sem(f"loaded{n}") for n in range(2)]
        flat = lambda ap: ap[:, :, :].rearrange("p b d -> p (b d)")
        with nc.Block() as block:

            @block.sync
            def _(sp):
                for dst, name in ((wo, "sb_wo"), (op_w, "op_w"), (ow, "ow")):
                    sp.dma_start(dst[:, :], w[name]).then_inc(S["w_loaded"], 16)
                for name, dst in rows.items():
                    sp.dma_start(dst[:, :], across(w[name], P)).then_inc(S["w_loaded"], 16)
                sp.sem_inc(S["xT_ready"], 2)
                with sp.Fori(0, NG // 2) as i:
                    for n in range(2):
                        at = bass.ds(i * 2 * GB + n * GB, GB)
                        sp.wait_ge(S["xT_ready"], i * 2 + n + 1)
                        for j in range(Z.J):
                            sp.dma_start(r[n][:, :, Z.V * j:Z.V * j + Z.V], reads[:, j, at, :]).then_inc(loaded[n], 16)
                        sp.dma_start(x[n][:, :, :], states[:, at, :]).then_inc(loaded[n], 16)

            @block.tensor
            def _(pe):
                pe.wait_ge(S["w_loaded"], 8 * 16)
                with pe.Fori(0, NG // 2) as i:
                    for n in range(2):
                        g = i * 2 + n
                        pe.wait_ge(loaded[n], i * 80 + 80)
                        for b in range(GB):
                            mm = pe.transpose(core.bank[0][:, b * P:(b + 1) * P], r[n][:, b, :], core.ident[:, :])
                        mm.then_inc(S["rT_in_psum"], 1)
                        for b in range(GB):
                            mm = pe.transpose(core.bank[1][0:Z.H, b * P:(b + 1) * P], x[n][:, b, :], core.ident[:, :])
                        mm.then_inc(S["xT_in_psum"], 1)
                        pe.wait_ge(S["rT_ready"], g + 1)
                        pe.wait_ge(S["xT_ready"], g + 3)
                        for b in range(GB):
                            pe.matmul(core.bank[2][:, b * P:(b + 1) * P], rT[:, b, :], wo[:, :], start=True, stop=False)
                            mm = pe.matmul(core.bank[2][:, b * P:(b + 1) * P], xT[:, b, :], op_w[:, :], start=False, stop=True)
                        mm.then_inc(S["y_in_psum"], 1)
                        pe.wait_ge(S["y_ready"], g + 1)
                        for b in range(GB):
                            mm = pe.transpose(core.bank[3][:, b * P:(b + 1) * P], y[:, b, :], core.ident[:, :])
                        mm.then_inc(S["yT_in_psum"], 1)
                        pe.wait_ge(S["yT_ready"], g + 1)
                        for b in range(GB):
                            mm = pe.matmul(core.bank[4][:, b * P:(b + 1) * P], yT[:, b, :], ow[:, :], start=True, stop=True)
                        mm.then_inc(S["out_in_psum"], 1)

            @block.scalar
            def _(act):
                act.preload_act_table_set("natural_log_exp_and_others")
                step = Chain(act, S["act_chain"])
                with act.Fori(0, NG // 2) as i:
                    step.enter(i, 2)
                    for n in range(2):
                        g = i * 2 + n
                        act.wait_ge(S["rT_in_psum"], g + 1)
                        act.copy(flat(rT), core.bank[0][:, :]).then_inc(S["rT_ready"], 1)
                        act.wait_ge(S["xT_in_psum"], g + 1)
                        act.copy(flat(xT), core.bank[1][0:Z.H, :]).then_inc(S["xT_ready"], 1)
                        act.wait_ge(S["centred"], g + 1)
                        act.activation(flat(sq), flat(y), ACT.Square).then_inc(S["squared"], 1)
                        act.wait_ge(S["var_ready"], g + 1)
                        step(act.activation(var[:, :], var[:, :], ACT.Ln))
                        act.activation(var[:, :], var[:, :], ACT.Exp, scale=-0.5).then_inc(S["rstd_ready"], 1)
                        act.wait_ge(S["yT_in_psum"], g + 1)
                        act.copy(flat(yT), core.bank[3][:, :]).then_inc(S["yT_ready"], 1)
                    step.leave(NG // 2)

            @block.vector
            def _(dve):
                step = Chain(dve, S["chain"])
                dve.wait_ge(S["w_loaded"], 8 * 16)
                step(dve.tensor_tensor(rows["sb_bo"][:, :], rows["sb_bo"][:, :], rows["op_b"][:, :], ALU.add))
                wide = lambda name: rows[name][:, :].unsqueeze(1).to_broadcast([P, GB, D])
                each = lambda ap: ap[:, :].unsqueeze(2).to_broadcast([P, GB, D])
                with dve.Fori(0, NG // 2) as i:
                    step.enter(i, 2 * 6 + 2)
                    for n in range(2):
                        g = i * 2 + n
                        y3 = y[:, :, :]
                        dve.wait_ge(S["y_in_psum"], g + 1)
                        step(dve.tensor_tensor(y3, core.bank[2][:, :].rearrange("p (b d) -> p b d", b=GB), wide("sb_bo"), ALU.add))
                        step(dve.tensor_reduce(mean[:, :], y3, X, ALU.add))
                        step(dve.tensor_scalar(mean[:, :], mean[:, :], 1.0 / D, None, ALU.mult))
                        dve.tensor_tensor(y3, y3, each(mean), ALU.subtract).then_inc(S["centred"], 1)
                        dve.wait_ge(S["squared"], g + 1)
                        step(dve.tensor_reduce(var[:, :], sq[:, :, :], X, ALU.add))
                        dve.tensor_scalar(var[:, :], var[:, :], 1.0 / D, EPS, ALU.mult, ALU.add).then_inc(S["var_ready"], 1)
                        dve.wait_ge(S["rstd_ready"], g + 1)
                        step(dve.tensor_tensor(y3, y3, each(var), ALU.mult))
                        step(dve.tensor_tensor(y3, y3, wide("oln_g"), ALU.mult))
                        dve.tensor_tensor(y3, y3, wide("oln_b"), ALU.add).then_inc(S["y_ready"], 1)
                        dve.wait_ge(S["out_in_psum"], g + 1)
                        step(dve.tensor_tensor(sq[:, :, :], core.bank[4][:, :].rearrange("p (b d) -> p b d", b=GB), wide("ob"), ALU.add))
                        hid = core.hidden[:, bass.ds(i * 2 * GB + n * GB, GB), :]
                        dve.tensor_tensor(hid, sq[:, :, :], hid, ALU.add).then_inc(S["hidden_added"], 1)
                    step.leave(NG // 2)


def self_attention(core, x, xn, g_row, b_row, wq, wk, wv, wo):
    nc = core.nc
    core.phase = "mha_"
    NH, DH = 8, 16
    SCALE = DH ** -0.5
    HALF = NH // 2 * P
    with ExitStack() as c:
        sb = lambda n, s, d=F32: core.sbuf(n, s, d, c)
        sem = lambda n: core.sem(n, c)
        W = {n: sb(n, [D, D]) for n in ("wq", "wk", "wv", "wo")}
        g_all, b_all = sb("g_all", [P, D]), sb("b_all", [P, D])
        head = sb("head", [P, NH])
        x1, xT = ([sb(f"{name}{n}", [P, GB, P]) for n in range(2)] for name in ("x1", "xT"))
        qT, kT, v = (sb(n, [P, B, P]) for n in ("qT", "kT", "v"))
        q = [sb(f"q{n}", [P, P]) for n in range(2)]
        kd = [sb(f"kd{n}", [P, NH, P]) for n in range(2)]
        probs = [sb(f"probs{n}", [P, NH, P]) for n in range(2)]
        pT = sb("pT", [P, NH, P])
        top, nmax, rden = sb("top", [P, NH]), sb("nmax", [P, 2, NH]), sb("rden", [P, NH])
        den = sb("den", [P, 4, NH])
        o, oT = ([sb(f"{name}{n}", [P, P]) for n in range(2)] for name in ("o", "oT"))
        names = ("w_loaded", "consts_ready", "x1_ready", "xT_in_psum", "xT_ready", "q_in_psum", "k_in_psum", "v_in_psum", "q_ready", "k_ready",
                 "v_ready", "kd_ready", "scores_ready", "top_ready", "rden_ready", "nmax_ready", "probs_ready", "pT_in_psum", "pT_ready", "o_in_psum", "o_ready",
                 "oT_in_psum", "oT_ready", "out_in_psum", "x_done", "chain")
        S = {n: sem(n) for n in names}
        LAG = 5

        def run(eng, stages):
            def tick(s, base):
                for lag, stage in stages:
                    if base is not None or 0 <= s - lag < B:
                        stage((s - lag) % 4, s - lag if base is None else base + (s - lag))
            for s in range(8):
                tick(s, None)
            with eng.Fori(0, B // 4 - 2) as i:
                for s in range(8, 12):
                    tick(s, i * 4)
            for s in range(B, B + LAG):
                tick(s, None)

        flat = lambda ap: ap[:, :, :].rearrange("p b d -> p (b d)")
        bank = core.bank
        with nc.Block() as block:

            @block.sync
            def _(sp):
                for name, src in (("wq", wq), ("wk", wk), ("wv", wv), ("wo", wo)):
                    sp.dma_start(W[name][:, :], src).then_inc(S["w_loaded"], 16)
                sp.dma_start(g_all[:, :], across(g_row, P)).then_inc(S["w_loaded"], 16)
                sp.dma_start(b_all[:, :], across(b_row, P)).then_inc(S["w_loaded"], 16)

            @block.gpsimd
            def _(pool):
                pool.memset(head[:, :], 1.0).then_inc(S["consts_ready"], 1)
                pool.wait_ge(S["consts_ready"], 1)
                pool.affine_select(out=head[:, :], in_=head[:, :], compare_op=ALU.is_ge, fill=0.0, base=0,
                                   pattern=[[-DH, NH]], channel_multiplier=1).then_inc(S["consts_ready"], 1)
                pool.wait_ge(S["consts_ready"], 2)
                pool.affine_select(out=head[:, :], in_=head[:, :], compare_op=ALU.is_ge, fill=0.0, base=DH - 1,
                                   pattern=[[DH, NH]], channel_multiplier=-1).then_inc(S["consts_ready"], 1)

            @block.tensor
            def _(pe):
                pe.wait_ge(S["w_loaded"], 6 * 16)
                pe.sem_inc(S["xT_in_psum"], 2)
                pe.sem_inc(S["v_ready"], 2)

                def turn_x(g, n):
                    pe.wait_ge(S["x1_ready"], g + 1)
                    for b in range(GB):
                        mm = pe.transpose(bank[n][:, b * P:(b + 1) * P], x1[n][:, b, :], core.ident[:, :])
                    mm.then_inc(S["xT_in_psum"], 1)

                def project(g, n):
                    pe.wait_ge(S["v_ready"], g + 1)
                    pe.wait_ge(S["xT_ready"], g + 1)
                    pe.matmul(bank[2 + 3 * n][:, :], W["wq"][:, :], flat(xT[n]), start=True, stop=True).then_inc(S["q_in_psum"], 1)
                    pe.matmul(bank[3 + 3 * n][:, :], W["wk"][:, :], flat(xT[n]), start=True, stop=True).then_inc(S["k_in_psum"], 1)
                    for b in range(GB):
                        mm = pe.matmul(bank[4 + 3 * n][:, b * P:(b + 1) * P], xT[n][:, b, :], W["wv"][:, :], start=True, stop=True)
                    mm.then_inc(S["v_in_psum"], 1)

                turn_x(0, 0)
                with pe.Fori(0, NG // 2 - 1) as i:
                    for n in range(2):
                        turn_x(i * 2 + n + 1, 1 - n)
                        project(i * 2 + n, n)
                turn_x(NG - 1, 1)
                project(NG - 2, 0)
                project(NG - 1, 1)
                pe.wait_ge(S["v_ready"], NG + 2)

                def out_proj(n, u):
                    pe.wait_ge(S["oT_ready"], u + 1)
                    pe.matmul(bank[3][:, P:2 * P], oT[n % 2][:, :], W["wo"][:, :], start=True, stop=True).then_inc(S["out_in_psum"], 1)

                def values(n, u):
                    pe.wait_ge(S["pT_ready"], u + 1)
                    if not (isinstance(u, int) and u == 0):
                        pe.wait_ge(S["o_ready"], u)
                    for h in range(NH):
                        mm = pe.matmul(bank[0][:, h * DH:(h + 1) * DH], pT[0:T, h, :], v[0:T, bass.ds(u, 1), h * DH:(h + 1) * DH].rearrange("p a d -> p (a d)"),
                                       start=True, stop=True)
                    mm.then_inc(S["o_in_psum"], 1)

                def turn_probs(n, u):
                    pe.wait_ge(S["probs_ready"], u + 1)
                    for h in range(NH):
                        mm = pe.transpose(bank[1 + h // 4][0:T, h % 4 * P:(h % 4 + 1) * P], probs[n % 2][:, h, 0:T], core.ident[:, :])
                    mm.then_inc(S["pT_in_psum"], 1)

                def turn_o(n, u):
                    pe.wait_ge(S["o_ready"], u + 1)
                    if not (isinstance(u, int) and u == 0):
                        pe.wait_ge(S["x_done"], u)
                    pe.transpose(bank[3][:, 0:P], o[n % 2][:, :], core.ident[:, :]).then_inc(S["oT_in_psum"], 1)

                def scores(n, u):
                    pe.wait_ge(S["kd_ready"], u + 1)
                    for half in range(2):
                        mm = pe.matmul(bank[4 + 2 * (n % 2) + half][:, :], q[n % 2][:, :],
                                       kd[n % 2][:, half * 4:half * 4 + 4, :].rearrange("p h m -> p (h m)"), start=True, stop=True)
                    mm.then_inc(S["scores_ready"], 1)

                run(pe, [(5, out_proj), (3, values), (2, turn_probs), (4, turn_o), (0, scores)])

            @block.scalar
            def _(act):
                act.preload_act_table_set("exp_and_others")

                def copy_xT(g, n):
                    act.wait_ge(S["xT_in_psum"], g + 3)
                    act.copy(flat(xT[n]), bank[n][:, :]).then_inc(S["xT_ready"], 1)

                def copy_projected(g, n, first):
                    for src, dst, ready, bk in (("q_in_psum", qT, "q_ready", 2), ("k_in_psum", kT, "k_ready", 3), ("v_in_psum", v, "v_ready", 4)):
                        act.wait_ge(S[src], g + 1)
                        act.copy(dst[:, bass.ds(first, GB), :].rearrange("p b d -> p (b d)"), bank[bk + 3 * n][:, :]).then_inc(S[ready], 1)

                copy_xT(0, 0)
                with act.Fori(0, NG // 2 - 1) as i:
                    for n in range(2):
                        copy_xT(i * 2 + n + 1, 1 - n)
                        copy_projected(i * 2 + n, n, i * 2 * GB + n * GB)
                copy_xT(NG - 1, 1)
                for n in range(2):
                    copy_projected(NG - 2 + n, n, (NG - 2 + n) * GB)

                def softmax(n, u):
                    act.wait_ge(S["nmax_ready"], u + 1)
                    for h in range(NH):
                        ex = act.activation(probs[n % 2][:, h, 0:T], bank[4 + 2 * (n % 2) + h // 4][:, h % 4 * P:h % 4 * P + T], ACT.Exp,
                                            bias=nmax[:, n % 2, h:h + 1], scale=SCALE, accum_out=den[:, n, h:h + 1])
                    ex.then_inc(S["probs_ready"], 1)

                def copy_probs(n, u):
                    act.wait_ge(S["pT_in_psum"], u + 1)
                    act.copy(pT[0:T, :, :].rearrange("p h m -> p (h m)"), core.banks[0:T, 512:3 * 512]).then_inc(S["pT_ready"], 1)

                def copy_o(n, u):
                    act.wait_ge(S["oT_in_psum"], u + 1)
                    act.copy(oT[n % 2][:, :], bank[3][:, 0:P]).then_inc(S["oT_ready"], 1)

                run(act, [(2, softmax), (3, copy_probs), (4, copy_o)])

            @block.vector
            def _(dve):
                step = Chain(dve, S["chain"])
                dve.wait_ge(S["w_loaded"], 6 * 16)
                dve.wait_ge(S["consts_ready"], 3)
                wide = lambda ap: ap[:, :].unsqueeze(1).to_broadcast([P, GB, D])
                with dve.Fori(0, NG // 2) as i:
                    step.enter(i, 2)
                    for n in range(2):
                        g = i * 2 + n
                        dve.wait_ge(S["xT_in_psum"], g + 1)
                        step(dve.tensor_tensor(x1[n][:, :, :], xn[:, bass.ds(i * 2 * GB + n * GB, GB), :], wide(g_all), ALU.mult))
                        dve.tensor_tensor(x1[n][:, :, :], x1[n][:, :, :], wide(b_all), ALU.add).then_inc(S["x1_ready"], 1)
                    step.leave(NG // 2)
                dve.wait_ge(S["q_ready"], NG)
                dve.wait_ge(S["k_ready"], NG)
                at = lambda t, u: t[:, bass.ds(u, 1), :].rearrange("p a d -> p (a d)")

                def spread_keys(n, u):
                    dve.tensor_copy(q[n % 2][:, :], at(qT, u))
                    dve.tensor_tensor(kd[n % 2][:, :, :], kT[:, bass.ds(u, 1), :].to_broadcast([P, NH, P]),
                                      head[:, :].unsqueeze(2).to_broadcast([P, NH, P]), ALU.mult).then_inc(S["kd_ready"], 1)

                def add_out(n, u):
                    dve.wait_ge(S["out_in_psum"], u + 1)
                    dve.tensor_tensor(at(x, u), bank[3][:, P:2 * P], at(x, u), ALU.add).then_inc(S["x_done"], 1)

                def divide(n, u):
                    dve.wait_ge(S["o_in_psum"], u + 1)
                    dve.reciprocal(rden[:, :], den[:, n, :]).then_inc(S["rden_ready"], 1)
                    dve.wait_ge(S["rden_ready"], u + 1)
                    dve.tensor_tensor(o[n % 2][:, :].rearrange("p (h d) -> p h d", h=NH), bank[0][:, 0:P].rearrange("p (h d) -> p h d", h=NH),
                                      rden[:, :].unsqueeze(2).to_broadcast([P, NH, DH]), ALU.mult).then_inc(S["o_ready"], 1)

                def maximum(n, u):
                    dve.wait_ge(S["scores_ready"], u + 1)
                    first = 4 + 2 * (n % 2)
                    dve.tensor_reduce(top[:, :], core.banks[:, first * 512:(first + 2) * 512].rearrange("p (h m) -> p h m", h=NH)[:, :, 0:T], X, ALU.max).then_inc(S["top_ready"], 1)
                    dve.wait_ge(S["top_ready"], u + 1)
                    dve.tensor_scalar(nmax[:, n % 2, :], top[:, :], -SCALE, None, ALU.mult).then_inc(S["nmax_ready"], 1)

                run(dve, [(0, spread_keys), (5, add_out), (3, divide), (0, maximum)])


class Dispatch:
    E, TOPK, C, CAP = 64, 2, 254, 256
    F = 512
    ROWS = E * CAP + TOPK * B * P


def route_two_of_64(core, xn, w, x2, put, take, gate):
    nc = core.nc
    core.phase = "route1_"
    Z = Dispatch
    E, K = Z.E, Z.TOPK
    W = E + 8 - 1
    FAR = 1e30
    PER = 49
    with ExitStack() as c:
        sb = lambda n, s, d=F32: core.sbuf(n, s, d, c)
        sem = lambda n: core.sem(n, c)
        wr = sb("wr", [D, E])
        g_all, b_all = sb("g_all", [P, D]), sb("b_all", [P, D])
        before, ones = sb("before", [P, P]), sb("ones", [P, P])
        real = sb("real", [P, 1])
        base = sb("base", [P, E])
        spill = sb("spill", [P, B, K])
        sentinels = sb("sentinels", [P, 7])
        stage, xT = sb("stage", [P, GB, D]), sb("xT", [P, GB, P])
        probs, expo = sb("probs", [P, GB, W]), sb("expo", [P, GB, E])
        top, total = sb("top", [P, GB]), sb("total", [P, GB])
        best = sb("best", [P, GB, 8])
        v12 = sb("v12", [P, GB, K])
        marked = [sb(f"marked{k}", [P, GB, W]) for k in range(K)]
        sel = sb("sel", [P, GB, E])
        seen = sb("seen", [P, GB + 1, E])
        pos, row, prod = sb("pos", [P, GB, E]), sb("row", [P, GB, E]), sb("prod", [P, GB, E])
        p_k, r_k, keep, over = (sb(n, [P, GB, K]) for n in ("p_k", "r_k", "keep", "over"))
        waiter = sb("waiter", [1, 1])
        names = ("w_loaded", "consts_ready", "staged", "xT_in_psum", "xT_ready", "logits_ready", "shifted", "exp_ready",
                 "sel_ready", "pos_in_psum", "group_done", "chain", "pool_chain")
        S = {n: sem(n) for n in names}
        flat = lambda ap: ap[:, :, :].rearrange("p b d -> p (b d)")
        bank = core.bank
        with nc.Block() as block:

            @block.sync
            def _(sp):
                sp.dma_start(wr[:, :], w["wr"]).then_inc(S["w_loaded"], 16)
                sp.dma_start(g_all[:, :], across(w["ln2_g"], P)).then_inc(S["w_loaded"], 16)
                sp.dma_start(b_all[:, :], across(w["ln2_b"], P)).then_inc(S["w_loaded"], 16)

            @block.gpsimd
            def _(pool):
                step = Chain(pool, S["pool_chain"])
                step(pool.memset(before[:, :], 1.0))
                step(pool.affine_select(out=before[:, :], in_=before[:, :], compare_op=ALU.is_gt, fill=0.0, base=0,
                                        pattern=[[1, P]], channel_multiplier=-1))
                step(pool.memset(ones[:, :], 1.0))
                step(pool.memset(real[:, :], 1.0))
                step(pool.affine_select(out=real[:, :], in_=real[:, :], compare_op=ALU.is_gt, fill=0.0, base=T,
                                        pattern=[[0, 1]], channel_multiplier=-1))
                step(pool.iota(base[:, :], pattern=[[Z.CAP, E]], base=0, channel_multiplier=0, allow_small_or_imprecise_dtypes=True))
                step(pool.iota(spill[:, :, :], pattern=[[K * P, B], [P, K]], base=E * Z.CAP, channel_multiplier=1, allow_small_or_imprecise_dtypes=True))
                for n in range(7):
                    step(pool.memset(sentinels[:, n:n + 1], -FAR * (n + 1)))
                pool.memset(seen[:, :, :], 0.0).then_inc(S["consts_ready"], 1)

            @block.tensor
            def _(pe):
                pe.wait_ge(S["w_loaded"], 3 * 16)
                pe.wait_ge(S["consts_ready"], 1)
                with pe.Fori(0, NG) as g:
                    pe.wait_ge(S["staged"], g + 1)
                    for b in range(GB):
                        mm = pe.transpose(bank[0][:, b * P:(b + 1) * P], stage[:, b, :], core.ident[:, :])
                    mm.then_inc(S["xT_in_psum"], 1)
                    pe.wait_ge(S["xT_ready"], g + 1)
                    for b in range(GB):
                        mm = pe.matmul(bank[1][:, b * E:(b + 1) * E], xT[:, b, :], wr[:, :], start=True, stop=True)
                    mm.then_inc(S["logits_ready"], 1)
                    pe.wait_ge(S["sel_ready"], g + 1)
                    pe.matmul(bank[2][:, 0:GB * E], before[:, :], flat(sel), start=True, stop=False)
                    pe.matmul(bank[2][:, 0:GB * E], ones[:, :], seen[:, 0:GB, :].rearrange("p b e -> p (b e)"), start=False, stop=True).then_inc(S["pos_in_psum"], 1)

            @block.scalar
            def _(act):
                act.preload_act_table_set("exp_and_others")
                with act.Fori(0, NG) as g:
                    act.wait_ge(S["xT_in_psum"], g + 1)
                    act.copy(flat(xT), bank[0][:, :]).then_inc(S["xT_ready"], 1)
                    act.wait_ge(S["shifted"], g + 1)
                    act.activation(flat(expo), flat(expo), ACT.Exp).then_inc(S["exp_ready"], 1)

            @block.vector
            def _(dve):
                step = Chain(dve, S["chain"])
                dve.wait_ge(S["w_loaded"], 3 * 16)
                dve.wait_ge(S["consts_ready"], 1)
                wide = lambda ap: ap[:, :].unsqueeze(1).to_broadcast([P, GB, D])
                each = lambda ap, n: ap.unsqueeze(2).to_broadcast([P, GB, n])
                step(dve.tensor_copy(probs[:, :, E:W], sentinels[:, :].unsqueeze(1).to_broadcast([P, GB, 7])))
                with dve.Fori(0, NG) as g:
                    step.enter(g, PER)
                    tiles = bass.ds(g * GB, GB)
                    step(dve.tensor_tensor(stage[:, :, :], xn[:, tiles, :], wide(g_all), ALU.mult))
                    dve.tensor_tensor(stage[:, :, :], stage[:, :, :], wide(b_all), ALU.add).then_inc(S["staged"], 1)
                    dve.wait_ge(S["staged"], g + 1)
                    step.tick(dve.tensor_copy(x2[:, tiles, :], stage[:, :, :]))
                    dve.wait_ge(S["logits_ready"], g + 1)
                    lg = bank[1][:, 0:GB * E].rearrange("p (b e) -> p b e", b=GB)
                    step(dve.tensor_reduce(top[:, :], lg, X, ALU.max))
                    dve.tensor_tensor(expo[:, :, :], lg, each(top[:, :], E), ALU.subtract).then_inc(S["shifted"], 1)
                    dve.wait_ge(S["exp_ready"], g + 1)
                    step(dve.tensor_reduce(total[:, :], expo[:, :, :], X, ALU.add))
                    step(dve.reciprocal(total[:, :], total[:, :]))
                    step(dve.tensor_tensor(probs[:, :, 0:E], expo[:, :, :], each(total[:, :], E), ALU.mult))
                    dve.memset(waiter[:, :], 0.0)
                    for b in range(GB):
                        step.tick(dve.max(best[:, b, :], probs[:, b, 0:E]))
                    step.settle()
                    step(dve.tensor_copy(v12[:, :, :], best[:, :, 0:K]))
                    for k in reversed(range(K)):
                        step(dve.tensor_copy(best[:, :, k + 1:8], sentinels[:, 0:7 - k].unsqueeze(1).to_broadcast([P, GB, 7 - k])))
                        dve.memset(waiter[:, :], 0.0)
                        for b in range(GB):
                            step.tick(dve.match_replace(marked[k][:, b, :], best[:, b, :], probs[:, b, :], FAR))
                        step.settle()
                    for k in range(K):
                        step.tick(dve.tensor_scalar(marked[k][:, :, 0:E], marked[k][:, :, 0:E], FAR, real[:, :], ALU.is_ge, ALU.mult))
                    step.settle()
                    step(dve.tensor_copy(sel[:, :, :], marked[1][:, :, 0:E]))
                    step.tick(dve.tensor_tensor(marked[1][:, :, 0:E], marked[1][:, :, 0:E], marked[0][:, :, 0:E], ALU.subtract))
                    for b in range(GB):
                        ins = dve.tensor_tensor(seen[:, b + 1, :], seen[:, b, :], sel[:, b, :], ALU.add)
                        if b < GB - 1:
                            step(ins)
                    ins.then_inc(S["sel_ready"], 1)
                    dve.wait_ge(S["pos_in_psum"], g + 1)
                    step.tick(dve.tensor_copy(seen[:, 0, :], seen[:, GB, :]))
                    step(dve.tensor_copy(pos[:, :, :], bank[2][:, 0:GB * E].rearrange("p (b e) -> p b e", b=GB)))
                    step(dve.tensor_tensor(row[:, :, :], pos[:, :, :], base[:, :].unsqueeze(1).to_broadcast([P, GB, E]), ALU.add))
                    for k in range(K):
                        for src, dst in ((pos, p_k), (row, r_k)):
                            step(dve.tensor_tensor(prod[:, :, :], marked[k][:, :, 0:E], src[:, :, :], ALU.mult))
                            step(dve.tensor_reduce(dst[:, :, k], prod[:, :, :], X, ALU.add))
                    step.tick(dve.tensor_scalar(keep[:, :, :], p_k[:, :, :], float(Z.C), real[:, :], ALU.is_lt, ALU.mult))
                    step(dve.tensor_scalar(over[:, :, :], p_k[:, :, :], float(1 - Z.C), 0.0, ALU.add, ALU.max))
                    step(dve.tensor_tensor(take[:, tiles, :], r_k[:, :, :], over[:, :, :], ALU.subtract))
                    step(dve.tensor_tensor(r_k[:, :, :], r_k[:, :, :], spill[:, tiles, :], ALU.subtract))
                    step(dve.tensor_tensor(r_k[:, :, :], r_k[:, :, :], keep[:, :, :], ALU.mult))
                    step(dve.tensor_tensor(put[:, tiles, :], r_k[:, :, :], spill[:, tiles, :], ALU.add))
                    step(dve.tensor_tensor(total[:, :], v12[:, :, 0], v12[:, :, 1], ALU.add))
                    step(dve.reciprocal(total[:, :], total[:, :]))
                    step(dve.tensor_tensor(v12[:, :, :], v12[:, :, :], each(total[:, :], K), ALU.mult))
                    step(dve.tensor_tensor(gate[:, tiles, :], v12[:, :, :], keep[:, :, :], ALU.mult))
                    step.leave(NG)


def experts_dispatched(core, x, x2, put, take, gate, w, buf, results):
    nc = core.nc
    core.phase = "experts1_"
    Z = Dispatch
    E, K, F = Z.E, Z.TOPK, Z.F
    FC = F // P
    R = Z.CAP // P
    with ExitStack() as c:
        sb = lambda n, s, d=F32: core.sbuf(n, s, d, c)
        sem = lambda n: core.sem(n, c)
        put_i, take_i = sb("put_i", [P, B, K], U32), sb("take_i", [P, B, K], U32)
        b1, b1T = sb("b1", [E, F]), sb("b1T", [P, FC, E])
        b2 = sb("b2", [1, E * D])
        ones = sb("ones", [1, P])
        w1 = [sb(f"w1_{n}", [D, F]) for n in range(2)]
        w2 = [sb(f"w2_{n}", [P, FC, D]) for n in range(2)]
        xe = [sb(f"xe{n}", [P, R, D]) for n in range(2)]
        xT = [sb(f"xT{n}", [D, R * P]) for n in range(2)]
        hT = [sb(f"hT{n}", [P, FC, R * P]) for n in range(2)]
        y = [sb(f"y{n}", [P, R, D]) for n in range(2)]
        back = [sb(f"back{n}", [P, K, D]) for n in range(4)]
        names = ("consts_loaded", "index_ready", "scattered", "b1T_in_psum", "b1T_ready", "ones_ready", "xT_in_psum", "xT_ready",
                 "up_in_psum", "h_ready", "y_in_psum", "y_ready", "chain")
        S = {n: sem(n) for n in names}
        w1_loaded, w2_loaded = ([sem(f"{w}_loaded{n}") for n in range(2)] for w in ("w1", "w2"))
        x_loaded = [sem(f"x_loaded{n}") for n in range(2)]
        y_stored = [sem(f"y_stored{n}") for n in range(2)]
        gathered = [sem(f"gathered{n}") for n in range(4)]
        bank = core.bank
        with nc.Block() as block:

            @block.gpsimd
            def _(pool):
                pool.wait_ge(S["index_ready"], 2)
                for b in range(B):
                    for k in range(K):
                        pool.indirect_dma_start(out=buf, out_offset=bass.IndirectOffsetOnAxis(ap=put_i[:, b, k:k + 1], axis=0),
                                                in_=x2[:, b, :], in_offset=None).then_inc(S["scattered"], 16)

            @block.sync
            def _(sp):
                sp.dma_start(b1[:, :], w["b1"]).then_inc(S["consts_loaded"], 16)
                sp.dma_start(b2[:, :], w["b2"].rearrange("(a e) d -> a (e d)", a=1)).then_inc(S["consts_loaded"], 16)

                def load_w1(e, n):
                    sp.dma_start(w1[n][:, :], w["w1"][bass.ds(e, 1), :, :].rearrange("e c f -> (e c) f")).then_inc(w1_loaded[n], 16)

                def load_w2(e, n):
                    sp.dma_start(w2[n][:, :, :], w["w2"][bass.ds(e, 1), :, :].rearrange("e (k f) c -> (e f) k c", k=FC)).then_inc(w2_loaded[n], 16)

                def load_x(e, n):
                    sp.dma_start(xe[n][:, :, :], buf[bass.ds(e * Z.CAP, Z.CAP), :].rearrange("(p r) d -> p r d", r=R)).then_inc(x_loaded[n], 16)

                def store(e, n):
                    sp.wait_ge(S["y_ready"], e + 1)
                    sp.dma_start(results[bass.ds(e * Z.CAP, Z.CAP), :].rearrange("(p r) d -> p r d", r=R), y[n][:, :, :]).then_inc(y_stored[n], 16)

                for n in range(2):
                    sp.sem_inc(y_stored[n], 16)
                    load_w1(n, n)
                    load_w2(n, n)
                sp.wait_ge(S["scattered"], 16 * B * K)
                for n in range(2):
                    load_x(n, n)
                with sp.Fori(0, E // 2 - 1) as i:
                    for n in range(2):
                        e = i * 2 + n
                        sp.wait_ge(S["xT_in_psum"], e + 1)
                        load_x(e + 2, n)
                        sp.wait_ge(S["up_in_psum"], e * 2 + 2)
                        load_w1(e + 2, n)
                        store(e, n)
                        load_w2(e + 2, n)
                for n in range(2):
                    store(E - 2 + n, n)
                for n in range(2):
                    sp.wait_ge(y_stored[n], 16 * (E // 2 + 1))

            @block.tensor
            def _(pe):
                pe.wait_ge(S["consts_loaded"], 32)
                for k in range(FC):
                    mm = pe.transpose(bank[0][:, k * E:(k + 1) * E], b1[:, k * P:(k + 1) * P], core.ident[0:E, 0:E])
                mm.then_inc(S["b1T_in_psum"], 1)
                pe.wait_ge(S["b1T_ready"], 1)
                pe.wait_ge(S["ones_ready"], 1)

                def front(e, n, times):
                    pe.wait_ge(x_loaded[n], times * 16)
                    for r in range(R):
                        mm = pe.transpose(bank[n][:, r * P:(r + 1) * P], xe[n][:, r, :], core.ident[:, :])
                    mm.then_inc(S["xT_in_psum"], 1)
                    pe.wait_ge(w1_loaded[n], times * 16)
                    pe.wait_ge(S["xT_ready"], e + 1)
                    for k in range(FC):
                        mm = pe.matmul(bank[2 + 2 * n + k // 2][:, k % 2 * R * P:(k % 2 + 1) * R * P], w1[n][:, k * P:(k + 1) * P], xT[n][:, :],
                                       start=True, stop=True)
                        if k % 2 == 1:
                            mm.then_inc(S["up_in_psum"], 1)

                def down(e, n, times):
                    pe.wait_ge(w2_loaded[n], times * 16)
                    for r in range(R):
                        pe.matmul(bank[6 + n][:, r * D:(r + 1) * D], ones[:, :], b2[:, bass.ds(e * D, D)], start=True, stop=False)
                        if r == 0:
                            pe.wait_ge(S["h_ready"], e + 1)
                        for k in range(FC):
                            mm = pe.matmul(bank[6 + n][:, r * D:(r + 1) * D], hT[n][:, k, r * P:(r + 1) * P], w2[n][:, k, :],
                                           start=False, stop=(k == FC - 1))
                    mm.then_inc(S["y_in_psum"], 1)

                front(0, 0, 1)
                with pe.Fori(0, E // 2 - 1) as i:
                    front(i * 2 + 1, 1, i + 1)
                    down(i * 2, 0, i + 1)
                    front(i * 2 + 2, 0, i + 2)
                    down(i * 2 + 1, 1, i + 1)
                front(E - 1, 1, E // 2)
                down(E - 2, 0, E // 2)
                down(E - 1, 1, E // 2)

            @block.scalar
            def _(act):
                act.preload_act_table_set("gelu_apprx_tanh_and_others")
                act.wait_ge(S["b1T_in_psum"], 1)
                act.copy(b1T[:, :, :].rearrange("p k e -> p (k e)"), bank[0][:, 0:FC * E]).then_inc(S["b1T_ready"], 1)
                act.wait_ge(S["b1T_ready"], 1)
                with act.Fori(0, E // 2) as i:
                    for n in range(2):
                        e = i * 2 + n
                        for k in range(FC):
                            act.wait_ge(S["up_in_psum"], i * 4 + n * 2 + k // 2 + 1)
                            ac = act.activation(hT[n][:, k, :], bank[2 + 2 * n + k // 2][:, k % 2 * R * P:(k % 2 + 1) * R * P], ACT.Gelu_apprx_tanh,
                                                bias=b1T[:, k, bass.ds(e, 1)])
                        ac.then_inc(S["h_ready"], 1)

            @block.vector
            def _(dve):
                dve.tensor_copy(put_i[:, :, :], put[:, :, :]).then_inc(S["index_ready"], 1)
                dve.tensor_copy(take_i[:, :, :], take[:, :, :]).then_inc(S["index_ready"], 1)
                dve.memset(ones[:, :], 1.0).then_inc(S["ones_ready"], 1)

                def copy_x(e, n):
                    dve.wait_ge(S["xT_in_psum"], e + 1)
                    dve.tensor_copy(xT[n][:, :], bank[n][:, 0:R * P]).then_inc(S["xT_ready"], 1)

                def copy_y(e, n, times):
                    dve.wait_ge(y_stored[n], times * 16)
                    dve.wait_ge(S["y_in_psum"], e + 1)
                    dve.tensor_copy(y[n][:, :, :].rearrange("p r d -> p (r d)"), bank[6 + n][:, 0:R * D]).then_inc(S["y_ready"], 1)

                copy_x(0, 0)
                with dve.Fori(0, E // 2 - 1) as i:
                    copy_x(i * 2 + 1, 1)
                    copy_y(i * 2, 0, i + 1)
                    copy_x(i * 2 + 2, 0)
                    copy_y(i * 2 + 1, 1, i + 1)
                copy_x(E - 1, 1)
                copy_y(E - 2, 0, E // 2)
                copy_y(E - 1, 1, E // 2)

        with nc.Block() as block:

            @block.gpsimd
            def _(pool):
                for b in range(B):
                    if b >= 4:
                        pool.wait_ge(S["chain"], 3 * (b - 3))
                    for k in range(K):
                        pool.indirect_dma_start(out=back[b % 4][:, k, :], out_offset=None, in_=results,
                                                in_offset=bass.IndirectOffsetOnAxis(ap=take_i[:, b, k:k + 1], axis=0)).then_inc(gathered[b % 4], 16)

            @block.vector
            def _(dve):
                step = Chain(dve, S["chain"])
                for b in range(B):
                    step(dve.tensor_tensor(core.hidden[:, b, :], core.hidden[:, b, :], x[:, b, :], ALU.add))
                    dve.wait_ge(gathered[b % 4], 32 * (b // 4 + 1))
                    for k in range(K):
                        step(dve.scalar_tensor_tensor(out=core.hidden[:, b, :], in0=back[b % 4][:, k, :], scalar=gate[:, b, k:k + 1],
                                                      in1=core.hidden[:, b, :], op0=ALU.mult, op1=ALU.add))


def audio_tower(nc, w, out):
    l1 = {k[len("L1_attn_"):]: v for k, v in w.items() if k.startswith("L1_attn_")}
    record = nc.dram_tensor("record", (P, B, ScanShapes.F), F32, kind="Internal").ap()
    record_part = nc.dram_tensor("record_part", (P, ScanShapes.J, B, 2 * ScanShapes.V), F32, kind="Internal").ap()
    reads = nc.dram_tensor("reads", (P, ScanShapes.J, B, ScanShapes.V), F32, kind="Internal").ap()
    states = nc.dram_tensor("states", (P, B, ScanShapes.H), F32, kind="Internal").ap()
    buf = nc.dram_tensor("dispatched", (Dispatch.ROWS, D), F32, kind="Internal").ap()
    results = nc.dram_tensor("results", (Dispatch.E * Dispatch.CAP, D), F32, kind="Internal").ap()
    buf0 = nc.dram_tensor("dispatched0", (Sparse.ROWS, D), F32, kind="Internal").ap()
    results0 = nc.dram_tensor("results0", (Sparse.TILES * P, D), F32, kind="Internal").ap()
    with ExitStack() as ctx:
        core = Core(nc, ctx)
        embed_patches(core, w["x"], w["L0_tok_W"], w["L0_tok_b"])
        with ExitStack() as c:
            core.phase = ""
            xn = core.sbuf("xn", [P, B, D], F32, c)
            with ExitStack() as cc:
                sq = core.sbuf("sq", [P, B, D], F32, cc)
                normalize(core, "ln0", core.hidden, xn, sq)
                channel_attention(core, xn, w["L0_attn_W_qkv"], w["L0_attn_W_o"],
                                  [buf0[0:Sparse.ROUTED * P, :], buf[0:Dispatch.E * Dispatch.CAP, :]])
        core.phase = ""
        l0f = {k[len("L0_ffn_"):]: v for k, v in w.items() if k.startswith("L0_ffn_")}
        with ExitStack() as c:
            E, H, HS = Sparse.E, Sparse.H, Sparse.HS
            w_up = core.sbuf("w_up", [P, E + 1, 2 * H], F32, c)
            tile_expert = core.sbuf("tile_expert", [1, Sparse.TILES + 8], I32, c)
            take = core.sbuf("take0", [P, B, Sparse.TOPK], F32, c)
            weight = core.sbuf("weight0", [P, B, Sparse.TOPK], F32, c)
            with ExitStack() as cc:
                xn = core.sbuf("xn0", [P, B, D], F32, cc)
                with ExitStack() as ccc:
                    sq = core.sbuf("sq1", [P, B, D], F32, ccc)
                    normalize(core, "ln1", core.hidden, xn, sq)
                core.phase = ""
                combine = core.sbuf("combine", [P, B, E], F32, cc)
                route_six_of_64(core, xn, combine, l0f["router_w"], l0f["bias_corr"],
                                [(w_up[:, 0:E, 0:H], l0f["Wg"].rearrange("e c h -> c e h")),
                                 (w_up[:, 0:E, H:2 * H], l0f["Wu"].rearrange("e c h -> c e h")),
                                 (w_up[:, E, 0:HS], l0f["sWg"]), (w_up[:, E, H:H + HS], l0f["sWu"])],
                                [w_up[:, E, HS:H], w_up[:, E, H + HS:2 * H]])
                dispatch_six(core, xn, combine, buf0, take, weight, tile_expert)
            experts_sparse(core, l0f, w_up, buf0, results0, tile_expert)
            collect_six(core, take, weight, results0)
        with ExitStack() as c:
            core.phase = ""
            xn = core.sbuf("xn2", [P, B, D], F32, c)
            with ExitStack() as cc:
                core.phase = ""
                sq = core.sbuf("sq2", [P, B, D], F32, cc)
                normalize(core, "ln2", core.hidden, xn, sq)
            scan_inputs(core, xn, l1, record_part, record)
        scan_tokens(core, l1, record_part, record, reads, states)
        scan_outputs(core, l1, reads, states)
        l1f = {k[len("L1_ffn_"):]: v for k, v in w.items() if k.startswith("L1_ffn_")}
        with ExitStack() as c:
            core.phase = ""
            x = core.sbuf("x", [P, B, D], F32, c)
            x2 = core.sbuf("x2", [P, B, D], F32, c)
            put, take, gate = (core.sbuf(n, [P, B, Dispatch.TOPK], F32, c) for n in ("put", "take", "gate"))
            with ExitStack() as cc:
                x1 = core.sbuf("x1", [P, B, D], F32, cc)
                normalize(core, "ln3", core.hidden, x, x2)
                normalize(core, "ln4", x, x1, x2)
                self_attention(core, x, x1, l1f["ln1_g"], l1f["ln1_b"], l1f["wq"], l1f["wk"], l1f["wv"], l1f["wo"])
                normalize(core, "ln5", x, x1, x2)
                route_two_of_64(core, x1, l1f, x2, put, take, gate)
            experts_dispatched(core, x, x2, put, take, gate, l1f, buf, results)
        store_hidden(core, out)


def kernel(**inputs):
    import numpy as _np
    import concourse.bacc as _bacc
    from concourse import mybir as _mybir
    from concourse.bass_utils import run_bass_kernel_spmd as _run

    nc = _bacc.Bacc("TRN2", target_bir_lowering=False, num_devices=1)
    arrays, aps = {}, {}
    for name, value in inputs.items():
        a = _np.ascontiguousarray(value)
        arrays[f"in_{name}_dram"] = a
        aps[name] = nc.dram_tensor(f"in_{name}_dram", a.shape, _mybir.dt.from_np(a.dtype), kind="ExternalInput").ap()
    out = nc.dram_tensor("out_0_dram", (32, 127, 128), _mybir.dt.float32, kind="ExternalOutput").ap()
    audio_tower(nc, aps, out)
    r = _run(nc, [arrays], core_ids=[0])
    return r.results[0]["out_0_dram"]
```
